# Optimizing a Trainium2 kernel written in Bass

```python
import numpy as np
import jax
import jax.numpy as jnp

def _softmax(x, axis=-1):
    return jax.nn.softmax(x, axis=axis)

def _gelu(x):
    return jax.nn.gelu(x, approximate=True)

def _silu(x):
    return jax.nn.silu(x)

def _sigmoid(x):
    return jax.nn.sigmoid(x)

def _layernorm(x, axis=-1, eps=1e-05):
    m = jnp.mean(x, axis=axis, keepdims=True)
    v = jnp.var(x, axis=axis, keepdims=True)
    return (x - m) / jnp.sqrt(v + eps)

def _scatter_add(tgt, idx, src, axis=0):
    return tgt.at[idx].add(src)

def _segment_sum(src, seg, n):
    return jax.ops.segment_sum(src, seg, n)
kernel_name = 'mk_flamingo_gated_d4_seqx_r8_a955c2'

def setup_inputs(seed: int=0):
    np.random.seed(seed)
    _w = jnp.asarray

    def _rec_inputs():
        import jax
        import jax.numpy as jnp
        _rk = jax.random.key(seed)
        x = -0.0003929 + 0.9999 * jax.random.normal(jax.random.fold_in(_rk, 1), (32, 128, 128), jnp.float32)
        _lenS = 128 - jax.random.randint(jax.random.fold_in(_rk, 7), (32,), 0, max(1, 128 // 4) + 1, jnp.int32)
        _lenS2 = 128 - jax.random.randint(jax.random.fold_in(_rk, 8), (32,), 0, max(1, 128 // 4) + 1, jnp.int32)
        _ctx_768P = jax.random.normal(jax.random.fold_in(_rk, 11), (32, 16, 96), jnp.float32)
        _ctx_768c = jax.random.dirichlet(jax.random.fold_in(_rk, 511), 0.3 * jnp.ones((16,), jnp.float32), (32, 128))
        _ctx_768t = jnp.einsum('bsk,bkd->bsd', _ctx_768c, _ctx_768P)
        _ctx_768t = _ctx_768t * jax.lax.rsqrt(jnp.mean(jnp.square(_ctx_768t)) + 1e-12) * 0.953939
        ctx_768 = -7.36909e-05 + 0.999899 * (_ctx_768t + 0.3 * jax.random.normal(jax.random.fold_in(_rk, 611), (32, 128, 96), jnp.float32))
        _validS = jnp.arange(128)[None, :] < _lenS[:, None]
        _validS2 = jnp.arange(128)[None, :] < _lenS2[:, None]
        _causal = jnp.tril(jnp.ones((128, 128), dtype=bool))
        mask_BxS_bf1 = jnp.ones((32, 128), dtype=bool)
        mask_BxS2_bf1 = jnp.ones((32, 128), dtype=bool)
        _g = jax.random.normal(jax.random.fold_in(_rk, 9001), (2, 4), jnp.float32)
        _g = jnp.sign(_g) * jnp.maximum(jnp.abs(_g), 1.0) + (_g == 0) * 1.0
        g_xattn = _g[0]
        g_ffn = _g[1]
        return (x, ctx_768, mask_BxS_bf1, mask_BxS2_bf1, g_xattn, g_ffn)
    x, ctx_768, mask_BxS_bf1, mask_BxS2_bf1, g_xattn, g_ffn = _rec_inputs()

    def _L0_xattn_setup():
        import jax, jax.numpy as jnp
        import numpy as np
        EPS = 1e-08
        key = jax.random.key(seed)
        kv, kt, k1, k2, k3, k4 = jax.random.split(key, 6)
        B, S = (16, 128)
        VD, TD, H = (128, 96, 64)
        visual_features = jax.random.normal(kv, (B, S, VD), dtype=jnp.float32)
        text_features = jax.random.normal(kt, (B, S, TD), dtype=jnp.float32)
        Wv = jax.random.normal(k1, (H, VD), dtype=jnp.float32) * (1.0 / np.sqrt(VD))
        bv = jax.random.normal(k2, (H,), dtype=jnp.float32) * 0.01
        Wt = jax.random.normal(k3, (H, TD), dtype=jnp.float32) * (1.0 / np.sqrt(TD))
        bt = jax.random.normal(k4, (H,), dtype=jnp.float32) * 0.01
        return {'visual_features': visual_features, 'text_features': text_features, 'Wv': Wv, 'bv': bv, 'Wt': Wt, 'bt': bt}
    _L0_xattn_all = _L0_xattn_setup()
    _L0_xattn_in = {k: v for k, v in _L0_xattn_all.items() if k in ('Wv', 'bv', 'Wt', 'bt')}
    del _L0_xattn_all

    def _L0_ffn_setup():
        import jax, jax.numpy as jnp
        import numpy as np
        NUM_EXPERTS = 8
        TOP_K = 2
        N_EMBD = 128
        B, T = (4, 256)
        key = jax.random.key(seed)
        k_x, k_g, k_e = jax.random.split(key, 3)
        x = jax.random.normal(k_x, (B, T, N_EMBD), dtype=jnp.float32)
        scale = 1.0 / np.sqrt(N_EMBD)
        gate_w = jax.random.uniform(k_g, (NUM_EXPERTS, N_EMBD), dtype=jnp.float32, minval=-scale, maxval=scale)
        expert_w = jax.random.uniform(k_e, (NUM_EXPERTS, N_EMBD, N_EMBD), dtype=jnp.float32, minval=-scale, maxval=scale)
        return {'x': x, 'gate_w': gate_w, 'expert_w': expert_w}
    _L0_ffn_all = _L0_ffn_setup()
    _L0_ffn_in = {k: v for k, v in _L0_ffn_all.items() if k in ('gate_w', 'expert_w')}
    del _L0_ffn_all

    def _L1_xattn_setup():
        import jax, jax.numpy as jnp
        import numpy as np
        B, T, DT, G, DV = (16, 64, 128, 72, 96)
        H, DH = (4, 32)
        INNER = H * DH
        HID = 4 * DT
        N_STATE = 64
        K_TOP = 32

        def layernorm(x, g, b, eps=1e-05):
            m = x.mean(-1, keepdims=True)
            v = x.var(-1, keepdims=True)
            return (x - m) * jax.lax.rsqrt(v + eps) * g + b

        def s4d(x, log_dt, A_re, A_im, C_re, C_im, D_skip):
            Bb, L, D = x.shape
            dt = jnp.exp(log_dt)
            A = A_re + 1j * A_im
            C = C_re + 1j * C_im
            dtA = dt[:, None] * A
            dC = C * (jnp.exp(dtA) - 1.0) / A
            powers = jnp.exp(dtA[:, :, None] * jnp.arange(L))
            K = 2.0 * jnp.einsum('dn,dnl->dl', dC, powers).real
            n = 2 * L
            Kf = jnp.fft.rfft(K, n=n, axis=-1)
            xf = jnp.fft.rfft(x, n=n, axis=1)
            y = jnp.fft.irfft(xf * Kf.T[None], n=n, axis=1)[:, :L]
            return y + x * D_skip
        key = jax.random.key(seed)
        ks = jax.random.split(key, 16)
        s = 0.02
        inp = {'x_text': jax.random.normal(ks[0], (B, T, DT), jnp.float32), 'x_vision': jax.random.normal(ks[1], (B, G, DV), jnp.float32), 'text_mask': jnp.ones((B, T), bool), 'vision_mask': jnp.ones((B, G), bool), 'Wq': jax.random.normal(ks[2], (DT, INNER), jnp.float32) * s, 'Wk': jax.random.normal(ks[3], (DV, INNER), jnp.float32) * s, 'Wv': jax.random.normal(ks[4], (DV, DT), jnp.float32) * s, 'W_film_in': jax.random.normal(ks[5], (DT, 2 * DT), jnp.float32) * s, 'b_film_in': jnp.zeros((2 * DT,), jnp.float32), 'W_film_out': jax.random.normal(ks[6], (DT, 2 * DT), jnp.float32) * s, 'b_film_out': jnp.zeros((2 * DT,), jnp.float32), 'g_norm_in': jnp.ones((DT,), jnp.float32), 'b_norm_in': jnp.zeros((DT,), jnp.float32), 'g_norm_out': jnp.ones((DT,), jnp.float32), 'b_norm_out': jnp.zeros((DT,), jnp.float32), 'g_ffn': jnp.ones((DT,), jnp.float32), 'b_ffn': jnp.zeros((DT,), jnp.float32), 'W1': jax.random.normal(ks[7], (DT, HID), jnp.float32) * s, 'b1': jnp.zeros((HID,), jnp.float32), 'W2': jax.random.normal(ks[8], (HID, DT), jnp.float32) * s, 'b2': jnp.zeros((DT,), jnp.float32), 'log_dt': jnp.log(0.001) + jax.random.uniform(ks[9], (DT,), jnp.float32) * (jnp.log(0.1) - jnp.log(0.001)), 'A_re': -0.5 * jnp.ones((DT, N_STATE), jnp.float32), 'A_im': jnp.tile(jnp.pi * jnp.arange(N_STATE, dtype=jnp.float32), (DT, 1)), 'C_re': jax.random.normal(ks[10], (DT, N_STATE), jnp.float32) * 0.5 ** 0.5, 'C_im': jax.random.normal(ks[11], (DT, N_STATE), jnp.float32) * 0.5 ** 0.5, 'D_skip': jax.random.normal(ks[12], (DT,), jnp.float32), 'mod_gate': jnp.array(0.5, jnp.float32)}
        return inp
    _L1_xattn_all = _L1_xattn_setup()
    _L1_xattn_in = {k: v for k, v in _L1_xattn_all.items() if k in ('Wq', 'Wk', 'Wv', 'W_film_in', 'b_film_in', 'W_film_out', 'b_film_out', 'g_norm_in', 'b_norm_in', 'g_norm_out', 'b_norm_out', 'g_ffn', 'b_ffn', 'W1', 'b1', 'W2', 'b2', 'log_dt', 'A_re', 'A_im', 'C_re', 'C_im', 'D_skip', 'mod_gate')}
    del _L1_xattn_all

    def _L1_ffn_setup():
        import jax, jax.numpy as jnp
        import numpy as np
        E = 8
        D = 128
        DO = 128
        R = 64
        H = 32
        B, T = (8, 256)
        key = jax.random.key(seed)
        ks = jax.random.split(key, 12)
        s = lambda k, shape, fan: jax.random.normal(k, shape, jnp.float32) / np.sqrt(fan)
        return {'x': jax.random.normal(ks[0], (B, T, D), jnp.float32), 'W_base': s(ks[1], (D, DO), D), 'b_base': jnp.zeros((DO,), jnp.float32), 'Wd1': s(ks[2], (E, D, H), D), 'bd1': jnp.zeros((E, H), jnp.float32), 'Wd2': s(ks[3], (E, H, D), H), 'bd2': jnp.zeros((E, D), jnp.float32), 'Wa_down': s(ks[4], (E, D, R), D), 'ba_down': jnp.zeros((E, R), jnp.float32), 'Wa_up': s(ks[5], (E, R, DO), R), 'ba_up': jnp.zeros((E, DO), jnp.float32)}
    _L1_ffn_all = _L1_ffn_setup()
    _L1_ffn_in = {k: v for k, v in _L1_ffn_all.items() if k in ('W_base', 'b_base', 'Wd1', 'bd1', 'Wd2', 'bd2', 'Wa_down', 'ba_down', 'Wa_up', 'ba_up')}
    del _L1_ffn_all

    def _L2_xattn_setup():
        import math
        import jax, jax.numpy as jnp
        import numpy as np
        B, SQ, SKV = (4, 256, 256)
        D_EMBED, D_CROSS, D_ATT, N_HEADS = (128, 96, 128, 16)
        D_HEAD = D_ATT // N_HEADS

        def _split_heads(t):
            b, s, _ = t.shape
            return t.reshape(b, s, N_HEADS, D_HEAD).transpose(0, 2, 1, 3)
        key = jax.random.key(seed)
        ks = jax.random.split(key, 10)
        s_e = 1.0 / math.sqrt(D_EMBED)
        s_c = 1.0 / math.sqrt(D_CROSS)
        s_a = 1.0 / math.sqrt(D_ATT)
        return {'x': jax.random.normal(ks[0], (B, SQ, D_EMBED), jnp.float32), 'y': jax.random.normal(ks[1], (B, SKV, D_CROSS), jnp.float32), 'Wq': jax.random.normal(ks[2], (D_EMBED, D_ATT), jnp.float32) * s_e, 'bq': jax.random.normal(ks[3], (D_ATT,), jnp.float32) * 0.01, 'Wk': jax.random.normal(ks[4], (D_CROSS, D_ATT), jnp.float32) * s_c, 'bk': jax.random.normal(ks[5], (D_ATT,), jnp.float32) * 0.01, 'Wv': jax.random.normal(ks[6], (D_CROSS, D_ATT), jnp.float32) * s_c, 'bv': jax.random.normal(ks[7], (D_ATT,), jnp.float32) * 0.01, 'Wo': jax.random.normal(ks[8], (D_ATT, D_EMBED), jnp.float32) * s_a, 'bo': jax.random.normal(ks[9], (D_EMBED,), jnp.float32) * 0.01}
    _L2_xattn_all = _L2_xattn_setup()
    _L2_xattn_in = {k: v for k, v in _L2_xattn_all.items() if k in ('Wq', 'bq', 'Wk', 'bk', 'Wv', 'bv', 'Wo', 'bo')}
    del _L2_xattn_all

    def _L2_ffn_setup():
        import jax, jax.numpy as jnp
        import numpy as np
        FP8_E4M3_MAX = 448.0

        def fake_quant_fp8(t):
            amax = jnp.max(jnp.abs(t))
            scale = FP8_E4M3_MAX / jnp.maximum(amax, 1e-12)
            q = (t * scale).astype(jnp.float8_e4m3fn).astype(jnp.float32)
            return q / scale
        key = jax.random.key(seed)
        k1, k2, k3 = jax.random.split(key, 3)
        d_in, d_out = (128, 128)
        x = jax.random.normal(k1, (4, 1024, d_in), dtype=jnp.float32)
        weight = jax.random.normal(k2, (d_out, d_in), dtype=jnp.float32) * (1.0 / np.sqrt(d_in))
        bias = jax.random.normal(k3, (d_out,), dtype=jnp.float32) * 0.01
        return {'x': x, 'weight': weight, 'bias': bias}
    _L2_ffn_all = _L2_ffn_setup()
    _L2_ffn_in = {k: v for k, v in _L2_ffn_all.items() if k in ('weight', 'bias')}
    del _L2_ffn_all

    def _L3_xattn_setup():
        import jax, jax.numpy as jnp
        import numpy as np
        HEADS = 8
        DIM_HEAD = 64
        SCALE = DIM_HEAD ** (-0.5)
        key = jax.random.key(seed)
        ks = jax.random.split(key, 7)
        B, Nq, Nc = (4, 256, 256)
        Dq, Dc = (128, 96)
        inner = HEADS * DIM_HEAD
        x = jax.random.normal(ks[0], (B, Nq, Dq), dtype=jnp.float32)
        context = jax.random.normal(ks[1], (B, Nc, Dc), dtype=jnp.float32)
        Wq = jax.random.normal(ks[2], (Dq, inner), dtype=jnp.float32) * Dq ** (-0.5)
        Wk = jax.random.normal(ks[3], (Dc, inner), dtype=jnp.float32) * Dc ** (-0.5)
        Wv = jax.random.normal(ks[4], (Dc, inner), dtype=jnp.float32) * Dc ** (-0.5)
        Wo = jax.random.normal(ks[5], (inner, Dq), dtype=jnp.float32) * inner ** (-0.5)
        bo = jax.random.normal(ks[6], (Dq,), dtype=jnp.float32) * 0.01
        return {'x': x, 'context': context, 'Wq': Wq, 'Wk': Wk, 'Wv': Wv, 'Wo': Wo, 'bo': bo}
    _L3_xattn_all = _L3_xattn_setup()
    _L3_xattn_in = {k: v for k, v in _L3_xattn_all.items() if k in ('Wq', 'Wk', 'Wv', 'Wo', 'bo')}
    del _L3_xattn_all

    def _L3_ffn_setup():
        import jax, jax.numpy as jnp
        import numpy as np
        B, S, D, H, E, K = (4, 256, 128, 256, 8, 2)
        TEMP = 5.0
        EPS = 1e-09
        key = jax.random.key(seed)
        k_x, k_wg, k_w1, k_w2 = jax.random.split(key, 4)
        scale = 0.02
        return {'x': jax.random.normal(k_x, (B, S, D), dtype=jnp.float32), 'Wg': jax.random.normal(k_wg, (D, E), dtype=jnp.float32) * scale, 'bg': jnp.zeros((E,), dtype=jnp.float32), 'W1': jax.random.normal(k_w1, (E, D, H), dtype=jnp.float32) * scale, 'b1': jnp.zeros((E, H), dtype=jnp.float32), 'W2': jax.random.normal(k_w2, (E, H, D), dtype=jnp.float32) * scale, 'b2': jnp.zeros((E, D), dtype=jnp.float32)}
    _L3_ffn_all = _L3_ffn_setup()
    _L3_ffn_in = {k: v for k, v in _L3_ffn_all.items() if k in ('Wg', 'bg', 'W1', 'b1', 'W2', 'b2')}
    del _L3_ffn_all
    return {'x': x, 'ctx_768': ctx_768, 'mask_BxS_bf1': mask_BxS_bf1, 'mask_BxS2_bf1': mask_BxS2_bf1, 'g_xattn': g_xattn, 'g_ffn': g_ffn, 'L0_xattn_Wv': _L0_xattn_in['Wv'], 'L0_xattn_bv': _L0_xattn_in['bv'], 'L0_xattn_Wt': _L0_xattn_in['Wt'], 'L0_xattn_bt': _L0_xattn_in['bt'], 'L0_ffn_gate_w': _L0_ffn_in['gate_w'], 'L0_ffn_expert_w': _L0_ffn_in['expert_w'], 'L1_xattn_Wq': _L1_xattn_in['Wq'], 'L1_xattn_Wk': _L1_xattn_in['Wk'], 'L1_xattn_Wv': _L1_xattn_in['Wv'], 'L1_xattn_W_film_in': _L1_xattn_in['W_film_in'], 'L1_xattn_b_film_in': _L1_xattn_in['b_film_in'], 'L1_xattn_W_film_out': _L1_xattn_in['W_film_out'], 'L1_xattn_b_film_out': _L1_xattn_in['b_film_out'], 'L1_xattn_g_norm_in': _L1_xattn_in['g_norm_in'], 'L1_xattn_b_norm_in': _L1_xattn_in['b_norm_in'], 'L1_xattn_g_norm_out': _L1_xattn_in['g_norm_out'], 'L1_xattn_b_norm_out': _L1_xattn_in['b_norm_out'], 'L1_xattn_g_ffn': _L1_xattn_in['g_ffn'], 'L1_xattn_b_ffn': _L1_xattn_in['b_ffn'], 'L1_xattn_W1': _L1_xattn_in['W1'], 'L1_xattn_b1': _L1_xattn_in['b1'], 'L1_xattn_W2': _L1_xattn_in['W2'], 'L1_xattn_b2': _L1_xattn_in['b2'], 'L1_xattn_log_dt': _L1_xattn_in['log_dt'], 'L1_xattn_A_re': _L1_xattn_in['A_re'], 'L1_xattn_A_im': _L1_xattn_in['A_im'], 'L1_xattn_C_re': _L1_xattn_in['C_re'], 'L1_xattn_C_im': _L1_xattn_in['C_im'], 'L1_xattn_D_skip': _L1_xattn_in['D_skip'], 'L1_xattn_mod_gate': _L1_xattn_in['mod_gate'], 'L1_ffn_W_base': _L1_ffn_in['W_base'], 'L1_ffn_b_base': _L1_ffn_in['b_base'], 'L1_ffn_Wd1': _L1_ffn_in['Wd1'], 'L1_ffn_bd1': _L1_ffn_in['bd1'], 'L1_ffn_Wd2': _L1_ffn_in['Wd2'], 'L1_ffn_bd2': _L1_ffn_in['bd2'], 'L1_ffn_Wa_down': _L1_ffn_in['Wa_down'], 'L1_ffn_ba_down': _L1_ffn_in['ba_down'], 'L1_ffn_Wa_up': _L1_ffn_in['Wa_up'], 'L1_ffn_ba_up': _L1_ffn_in['ba_up'], 'L2_xattn_Wq': _L2_xattn_in['Wq'], 'L2_xattn_bq': _L2_xattn_in['bq'], 'L2_xattn_Wk': _L2_xattn_in['Wk'], 'L2_xattn_bk': _L2_xattn_in['bk'], 'L2_xattn_Wv': _L2_xattn_in['Wv'], 'L2_xattn_bv': _L2_xattn_in['bv'], 'L2_xattn_Wo': _L2_xattn_in['Wo'], 'L2_xattn_bo': _L2_xattn_in['bo'], 'L2_ffn_weight': _L2_ffn_in['weight'], 'L2_ffn_bias': _L2_ffn_in['bias'], 'L3_xattn_Wq': _L3_xattn_in['Wq'], 'L3_xattn_Wk': _L3_xattn_in['Wk'], 'L3_xattn_Wv': _L3_xattn_in['Wv'], 'L3_xattn_Wo': _L3_xattn_in['Wo'], 'L3_xattn_bo': _L3_xattn_in['bo'], 'L3_ffn_Wg': _L3_ffn_in['Wg'], 'L3_ffn_bg': _L3_ffn_in['bg'], 'L3_ffn_W1': _L3_ffn_in['W1'], 'L3_ffn_b1': _L3_ffn_in['b1'], 'L3_ffn_W2': _L3_ffn_in['W2'], 'L3_ffn_b2': _L3_ffn_in['b2']}

def reference(x, ctx_768, mask_BxS_bf1, mask_BxS2_bf1, g_xattn, g_ffn, L0_xattn_Wv, L0_xattn_bv, L0_xattn_Wt, L0_xattn_bt, L0_ffn_gate_w, L0_ffn_expert_w, L1_xattn_Wq, L1_xattn_Wk, L1_xattn_Wv, L1_xattn_W_film_in, L1_xattn_b_film_in, L1_xattn_W_film_out, L1_xattn_b_film_out, L1_xattn_g_norm_in, L1_xattn_b_norm_in, L1_xattn_g_norm_out, L1_xattn_b_norm_out, L1_xattn_g_ffn, L1_xattn_b_ffn, L1_xattn_W1, L1_xattn_b1, L1_xattn_W2, L1_xattn_b2, L1_xattn_log_dt, L1_xattn_A_re, L1_xattn_A_im, L1_xattn_C_re, L1_xattn_C_im, L1_xattn_D_skip, L1_xattn_mod_gate, L1_ffn_W_base, L1_ffn_b_base, L1_ffn_Wd1, L1_ffn_bd1, L1_ffn_Wd2, L1_ffn_bd2, L1_ffn_Wa_down, L1_ffn_ba_down, L1_ffn_Wa_up, L1_ffn_ba_up, L2_xattn_Wq, L2_xattn_bq, L2_xattn_Wk, L2_xattn_bk, L2_xattn_Wv, L2_xattn_bv, L2_xattn_Wo, L2_xattn_bo, L2_ffn_weight, L2_ffn_bias, L3_xattn_Wq, L3_xattn_Wk, L3_xattn_Wv, L3_xattn_Wo, L3_xattn_bo, L3_ffn_Wg, L3_ffn_bg, L3_ffn_W1, L3_ffn_b1, L3_ffn_W2, L3_ffn_b2):
    import jax
    import jax.numpy as jnp

    def _L0_xattn_ref(visual_features, text_features, Wv, bv, Wt, bt):
        import jax, jax.numpy as jnp
        import numpy as np
        EPS = 1e-08
        v = jnp.einsum('bsd,hd->bsh', visual_features, Wv) + bv
        t = jnp.einsum('bsd,hd->bsh', text_features, Wt) + bt
        dots = jnp.einsum('bih,bjh->bij', v, t)
        vn = jnp.linalg.norm(v, axis=-1)
        tn = jnp.linalg.norm(t, axis=-1)
        denom = jnp.maximum(vn[:, :, None] * tn[:, None, :], EPS)
        return dots / denom

    def _L0_ffn_ref(x, gate_w, expert_w):
        import jax, jax.numpy as jnp
        import numpy as np
        NUM_EXPERTS = 8
        TOP_K = 2
        N_EMBD = 128
        B, T = (4, 256)
        Bb, Tt, C = x.shape
        xf = x.reshape(Bb * Tt, C)
        logits = xf @ gate_w.T
        w, sel = jax.lax.top_k(logits, TOP_K)
        w = jax.nn.softmax(w.astype(jnp.float32), axis=1).astype(xf.dtype)
        n = xf.shape[0]
        w_full = jnp.zeros((n, NUM_EXPERTS), dtype=xf.dtype)
        w_full = w_full.at[jnp.arange(n)[:, None], sel].add(w)
        expert_out = jnp.einsum('nc,edc->ned', xf, expert_w)
        out = jnp.einsum('ne,ned->nd', w_full, expert_out)
        return out.reshape(Bb, Tt, C)

    def _L1_xattn_ref(x_text, x_vision, text_mask, vision_mask, Wq, Wk, Wv, W_film_in, b_film_in, W_film_out, b_film_out, g_norm_in, b_norm_in, g_norm_out, b_norm_out, g_ffn, b_ffn, W1, b1, W2, b2, log_dt, A_re, A_im, C_re, C_im, D_skip, mod_gate):
        import jax, jax.numpy as jnp
        import numpy as np
        B, T, DT, G, DV = (16, 64, 128, 72, 96)
        H, DH = (4, 32)
        INNER = H * DH
        HID = 4 * DT
        N_STATE = 64
        K_TOP = 32

        def layernorm(x, g, b, eps=1e-05):
            m = x.mean(-1, keepdims=True)
            v = x.var(-1, keepdims=True)
            return (x - m) * jax.lax.rsqrt(v + eps) * g + b

        def s4d(x, log_dt, A_re, A_im, C_re, C_im, D_skip):
            Bb, L, D = x.shape
            dt = jnp.exp(log_dt)
            A = A_re + 1j * A_im
            C = C_re + 1j * C_im
            dtA = dt[:, None] * A
            dC = C * (jnp.exp(dtA) - 1.0) / A
            powers = jnp.exp(dtA[:, :, None] * jnp.arange(L))
            K = 2.0 * jnp.einsum('dn,dnl->dl', dC, powers).real
            n = 2 * L
            Kf = jnp.fft.rfft(K, n=n, axis=-1)
            xf = jnp.fft.rfft(x, n=n, axis=1)
            y = jnp.fft.irfft(xf * Kf.T[None], n=n, axis=1)[:, :L]
            return y + x * D_skip
        Bb, Tt, D = x_text.shape
        Gg = x_vision.shape[1]
        Q = (x_text @ Wq).reshape(Bb, Tt, H, DH)
        K = (x_vision @ Wk).reshape(Bb, Gg, H, DH)
        scores = jnp.einsum('bthd,bghd->bhtg', Q, K) / np.sqrt(DH).astype(np.float32)
        scores = jnp.where(vision_mask[:, None, None, :], scores, -jnp.inf)
        topv, topi = jax.lax.top_k(scores, K_TOP)
        probs = jax.nn.softmax(topv, axis=-1)
        bi = jnp.arange(Bb)[:, None, None, None]
        hi = jnp.arange(H)[None, :, None, None]
        ti = jnp.arange(Tt)[None, None, :, None]
        attn = jnp.zeros_like(scores).at[bi, hi, ti, topi].set(probs)
        attn_mean = attn.mean(axis=1)
        V = x_vision @ Wv
        c_t = jnp.einsum('btg,bgd->btd', attn_mean, V)
        c_t = c_t * text_mask[..., None]
        x = layernorm(x_text, g_norm_in, b_norm_in)
        scale_in, shift_in = jnp.split(c_t @ W_film_in + b_film_in, 2, axis=-1)
        x = x * (1.0 + mod_gate * scale_in) + mod_gate * shift_in
        y = s4d(x, log_dt, A_re, A_im, C_re, C_im, D_skip)
        scale_out, shift_out = jnp.split(c_t @ W_film_out + b_film_out, 2, axis=-1)
        y = y * (1.0 + mod_gate * scale_out) + mod_gate * shift_out
        xt = x_text + y
        h = layernorm(xt, g_ffn, b_ffn)
        h = jax.nn.gelu(h @ W1 + b1, approximate=False) @ W2 + b2
        xt = xt + h
        return layernorm(xt, g_norm_out, b_norm_out)

    def _L1_ffn_ref(x, W_base, b_base, Wd1, bd1, Wd2, bd2, Wa_down, ba_down, Wa_up, ba_up):
        import jax, jax.numpy as jnp
        import numpy as np
        E = 8
        D = 128
        DO = 128
        R = 64
        H = 32
        B, T = (8, 256)
        base = jnp.einsum('btd,do->bto', x, W_base) + b_base
        h = jax.nn.relu(jnp.einsum('btd,edh->ebth', x, Wd1) + bd1[:, None, None, :])
        recon = jnp.einsum('ebth,ehd->ebtd', h, Wd2) + bd2[:, None, None, :]
        losses = jnp.mean((recon - x[None]) ** 2, axis=(2, 3))
        idx = jnp.argmin(losses, axis=0)
        a = jax.nn.relu(jnp.einsum('btd,bdr->btr', x, Wa_down[idx]) + ba_down[idx][:, None, :])
        adapter_out = jnp.einsum('btr,bro->bto', a, Wa_up[idx]) + ba_up[idx][:, None, :]
        return base + adapter_out

    def _L2_xattn_ref(x, y, Wq, bq, Wk, bk, Wv, bv, Wo, bo):
        import math
        import jax, jax.numpy as jnp
        import numpy as np
        B, SQ, SKV = (4, 256, 256)
        D_EMBED, D_CROSS, D_ATT, N_HEADS = (128, 96, 128, 16)
        D_HEAD = D_ATT // N_HEADS

        def _split_heads(t):
            b, s, _ = t.shape
            return t.reshape(b, s, N_HEADS, D_HEAD).transpose(0, 2, 1, 3)
        q = _split_heads(x @ Wq + bq)
        k = _split_heads(y @ Wk + bk)
        v = _split_heads(y @ Wv + bv)
        scale = 1.0 / math.sqrt(D_HEAD)
        scores = jnp.einsum('bhqd,bhkd->bhqk', q, k) * scale
        weights = jax.nn.softmax(scores, axis=-1)
        out = jnp.einsum('bhqk,bhkd->bhqd', weights, v)
        out = out.transpose(0, 2, 1, 3).reshape(x.shape[0], x.shape[1], D_ATT)
        return out @ Wo + bo

    def _L2_ffn_ref(x, weight, bias):
        import jax, jax.numpy as jnp
        import numpy as np
        FP8_E4M3_MAX = 448.0

        def fake_quant_fp8(t):
            amax = jnp.max(jnp.abs(t))
            scale = FP8_E4M3_MAX / jnp.maximum(amax, 1e-12)
            q = (t * scale).astype(jnp.float8_e4m3fn).astype(jnp.float32)
            return q / scale
        xq = fake_quant_fp8(x)
        wq = fake_quant_fp8(weight)
        return jnp.einsum('bsd,od->bso', xq, wq) + bias

    def _L3_xattn_ref(x, context, Wq, Wk, Wv, Wo, bo):
        import jax, jax.numpy as jnp
        import numpy as np
        HEADS = 8
        DIM_HEAD = 64
        SCALE = DIM_HEAD ** (-0.5)
        B, Nq, _ = x.shape
        q = (x @ Wq).reshape(B, Nq, HEADS, DIM_HEAD)
        k = (context @ Wk).reshape(B, context.shape[1], HEADS, DIM_HEAD)
        v = (context @ Wv).reshape(B, context.shape[1], HEADS, DIM_HEAD)
        sim = jnp.einsum('bihd,bjhd->bhij', q, k) * SCALE
        attn = jax.nn.softmax(sim, axis=-1)
        out = jnp.einsum('bhij,bjhd->bihd', attn, v)
        out = out.reshape(B, Nq, HEADS * DIM_HEAD)
        return out @ Wo + bo

    def _L3_ffn_ref(x, Wg, bg, W1, b1, W2, b2):
        import jax, jax.numpy as jnp
        import numpy as np
        B, S, D, H, E, K = (4, 256, 128, 256, 8, 2)
        TEMP = 5.0
        EPS = 1e-09
        logits = jnp.einsum('bsd,de->bse', x, Wg) + bg
        probs = jax.nn.softmax(logits / TEMP, axis=-1)
        vals, idx = jax.lax.top_k(probs, K)
        onehot = jax.nn.one_hot(idx, E, dtype=x.dtype)
        mask = jnp.einsum('bske,bsk->bse', onehot, vals)
        gates = mask / (jnp.sum(mask, axis=-1, keepdims=True) + EPS)
        h = jax.nn.gelu(jnp.einsum('bsd,edh->besh', x, W1) + b1[None, :, None, :], approximate=False)
        out = jnp.einsum('besh,ehd->besd', h, W2) + b2[None, :, None, :]
        y = jnp.einsum('bse,besd->bsd', gates, out)
        return y
    x = x + jnp.tanh(g_xattn[0]) * _L0_xattn_ref(_layernorm(x, axis=-1), ctx_768, L0_xattn_Wv, L0_xattn_bv, L0_xattn_Wt, L0_xattn_bt)
    x = x + jnp.tanh(g_ffn[0]) * _L0_ffn_ref(_layernorm(x, axis=-1), L0_ffn_gate_w, L0_ffn_expert_w)
    x = x + jnp.tanh(g_xattn[1]) * _L1_xattn_ref(_layernorm(x, axis=-1), ctx_768, mask_BxS_bf1, mask_BxS2_bf1, L1_xattn_Wq, L1_xattn_Wk, L1_xattn_Wv, L1_xattn_W_film_in, L1_xattn_b_film_in, L1_xattn_W_film_out, L1_xattn_b_film_out, L1_xattn_g_norm_in, L1_xattn_b_norm_in, L1_xattn_g_norm_out, L1_xattn_b_norm_out, L1_xattn_g_ffn, L1_xattn_b_ffn, L1_xattn_W1, L1_xattn_b1, L1_xattn_W2, L1_xattn_b2, L1_xattn_log_dt, L1_xattn_A_re, L1_xattn_A_im, L1_xattn_C_re, L1_xattn_C_im, L1_xattn_D_skip, L1_xattn_mod_gate)
    x = x + jnp.tanh(g_ffn[1]) * _L1_ffn_ref(_layernorm(x, axis=-1), L1_ffn_W_base, L1_ffn_b_base, L1_ffn_Wd1, L1_ffn_bd1, L1_ffn_Wd2, L1_ffn_bd2, L1_ffn_Wa_down, L1_ffn_ba_down, L1_ffn_Wa_up, L1_ffn_ba_up)
    x = x + jnp.tanh(g_xattn[2]) * _L2_xattn_ref(_layernorm(x, axis=-1), ctx_768, L2_xattn_Wq, L2_xattn_bq, L2_xattn_Wk, L2_xattn_bk, L2_xattn_Wv, L2_xattn_bv, L2_xattn_Wo, L2_xattn_bo)
    x = x + jnp.tanh(g_ffn[2]) * _L2_ffn_ref(_layernorm(x, axis=-1), L2_ffn_weight, L2_ffn_bias)
    x = x + jnp.tanh(g_xattn[3]) * _L3_xattn_ref(_layernorm(x, axis=-1), ctx_768, L3_xattn_Wq, L3_xattn_Wk, L3_xattn_Wv, L3_xattn_Wo, L3_xattn_bo)
    x = x + jnp.tanh(g_ffn[3]) * _L3_ffn_ref(_layernorm(x, axis=-1), L3_ffn_Wg, L3_ffn_bg, L3_ffn_W1, L3_ffn_b1, L3_ffn_W2, L3_ffn_b2)
    return x

_drawn_inputs = setup_inputs


def setup_inputs(seed=0):
    import zlib

    import numpy as np

    out = dict(_drawn_inputs(seed))
    spreads = {'L1_xattn_b_film_in': (0.0, 0.1),
     'L1_xattn_b_film_out': (0.0, 0.1),
     'L1_xattn_g_norm_in': (1.0, 0.2),
     'L1_xattn_b_norm_in': (0.0, 0.1),
     'L1_xattn_g_norm_out': (1.0, 0.2),
     'L1_xattn_b_norm_out': (0.0, 0.1),
     'L1_xattn_g_ffn': (1.0, 0.6),
     'L1_xattn_b_ffn': (0.0, 0.8),
     'L1_xattn_b1': (0.0, 0.1),
     'L1_xattn_b2': (0.0, 0.1),
     'L1_xattn_A_re': (-0.5, 0.2),
     'L1_ffn_b_base': (0.0, 0.1),
     'L1_ffn_bd1': (0.0, 0.1),
     'L1_ffn_bd2': (0.0, 0.1),
     'L1_ffn_ba_down': (0.0, 0.1),
     'L1_ffn_ba_up': (0.0, 0.1),
     'L3_ffn_bg': (0.0, 0.1),
     'L3_ffn_b1': (0.0, 0.8),
     'L3_ffn_b2': (0.0, 0.1)}
    factors = {'L0_xattn_bv': 6.816,
     'L0_xattn_bt': 8.0,
     'L1_xattn_Wq': 5.816,
     'L1_xattn_Wk': 6.16,
     'L1_xattn_W_film_in': 3.034,
     'L1_xattn_W_film_out': 3.703,
     'L2_xattn_bq': 8.0,
     'L2_xattn_bk': 8.0,
     'L2_xattn_bv': 5.726,
     'L2_xattn_bo': 5.557,
     'L2_ffn_bias': 8.0,
     'L3_xattn_bo': 8.0,
     'L3_ffn_W1': 3.836,
     'L3_ffn_W2': 3.549}
    for name, (base, spread) in spreads.items():
        noise = np.random.default_rng([zlib.crc32(name.encode()), seed]).standard_normal(out[name].shape)
        drawn = base * np.exp(spread * noise) if base else spread * noise
        out[name] = jnp.asarray(drawn.astype(out[name].dtype))
    for name, factor in factors.items():
        out[name] = (out[name] * factor).astype(out[name].dtype)
    return out
```

```python
from contextlib import ExitStack

import concourse.bass as bass
from concourse import mybir

F32 = mybir.dt.float32
BF16 = mybir.dt.bfloat16
U8 = mybir.dt.uint8
I32 = mybir.dt.int32
U32 = mybir.dt.uint32
ACT = mybir.ActivationFunctionType
ALU = mybir.AluOpType
AX = mybir.AxisListType

B, S, D = 32, 128, 128
C = 96
G = 4
W = G * S
PAIR = 2 * G
TURNS = B // PAIR
EPS = 1e-5


class Signal:

    def __init__(self, sem, base, per, apart):
        self.sem, self.base, self.per, self.apart = sem, base, per, apart

    def wait(self, eng, turn, n):
        eng.wait_ge(self.sem, turn * self.per + (self.base + n))

    def wait_apart(self, eng, turn, n):
        self.wait(eng, turn, n)
        eng.sem_inc(self.apart, 1)


def signals(nc, k, phase, turns=TURNS, **per):
    s = {}
    for name, n in per.items():
        if name not in k.sems:
            k.sems[name] = [k.ctx.enter_context(nc.semaphore(name)), 1]
            nc.gpsimd.sem_inc(k.sems[name][0], 1)
        sem, base = k.sems[name]
        s[name] = Signal(sem, base, n, k.apart)
        k.sems[name][1] += n * turns
    return s


class OneTime:

    def __init__(self, nc, prefix):
        self.nc, self.prefix, self.sems = nc, prefix, []

    def __call__(self, name):
        self.sems.append(self.nc.alloc_semaphore(self.prefix + name))
        return self.sems[-1]

    def __enter__(self):
        return self

    def __exit__(self, *_):
        self.nc.clear_and_free_semaphores(self.sems)
        self.nc.all_engine_barrier()


class Norm:

    def __init__(self, sb, name):
        self.stats = sb(name + "_stats", [128, 2 * G, 2, 3])
        self.diff = sb(name + "_diff", [128, 2 * G])
        self.m2 = sb(name + "_m2", [128, 2 * G])
        self.d2 = sb(name + "_d2", [128, 2 * G])
        self.mean = sb(name + "_mean", [128, 2, G])
        self.ve = sb(name + "_ve", [128, 2, G])
        self.rstd = sb(name + "_rstd", [128, 2, G])


def norm_stats(dve, nm, s, t, src):
    for u in range(2):
        for j in range(G):
            dve.bn_stats(nm.stats[:, u * G + j].rearrange("p a b -> p (a b)"), src(u, j)).then_inc(s["stats"].sem, 1)
    s["stats"].wait(dve, t, 2 * G)
    dve.tensor_tensor(nm.diff[:], nm.stats[:, :, 0, 1], nm.stats[:, :, 1, 1], ALU.subtract).then_inc(s["halves"].sem, 1)
    dve.tensor_tensor(nm.m2[:], nm.stats[:, :, 0, 2], nm.stats[:, :, 1, 2], ALU.add).then_inc(s["halves"].sem, 1)
    mean = nm.mean[:].rearrange("p u j -> p (u j)")
    dve.tensor_tensor(mean, nm.stats[:, :, 0, 1], nm.stats[:, :, 1, 1], ALU.add).then_inc(s["halves"].sem, 1)
    s["halves"].wait(dve, t, 3)
    dve.tensor_tensor(nm.d2[:], nm.diff[:], nm.diff[:], ALU.mult).then_inc(s["square"].sem, 1)
    dve.tensor_scalar(mean, mean, 0.5, None, ALU.mult).then_inc(s["mean"].sem, 1)
    s["square"].wait(dve, t, 1)
    dve.scalar_tensor_tensor(out=nm.m2[:], in0=nm.d2[:], scalar=D / 4.0, in1=nm.m2[:], op0=ALU.mult,
                             op1=ALU.add).then_inc(s["square"].sem, 1)
    s["square"].wait(dve, t, 2)
    dve.tensor_scalar(nm.ve[:].rearrange("p u j -> p (u j)"), nm.m2[:], 1.0 / D, EPS, ALU.mult,
                      ALU.add).then_inc(s["ve"].sem, 1)


def norm_rstd(pool, nm, s, t, half):
    s["ve"].wait(pool, t, 1)
    pool.tensor_tensor(nm.rstd[:].rearrange("p u j -> p (u j)"), nm.ve[:].rearrange("p u j -> p (u j)"), half,
                       ALU.pow).then_inc(s["rstd"].sem, 1)


def norm_apply(dve, nm, s, t, u, src, xn):
    s["rstd"].wait(dve, t, 1)
    s["mean"].wait(dve, t, 1)
    for j in range(G):
        dve.tensor_scalar(xn[:, u, j, :], src(u, j), nm.mean[:, u, j:j + 1], nm.rstd[:, u, j:j + 1],
                          ALU.subtract, ALU.mult).then_inc(s["xn"].sem, 1)


NORM = dict(stats=2 * G, halves=3, square=2, mean=1, ve=1, rstd=1, xn=2 * G)


def transpose_tokens(pe, s, t, u, xn, bank, ident):
    s["xn"].wait(pe, t, G * (u + 1))
    for j in range(G):
        m = pe.transpose(bank[:, j * S:(j + 1) * S], xn[:, u, j, :], ident)
    m.then_inc(s["xnT_ps"].sem, 1)


def row_of(ap):
    return ap.rearrange("(a d) -> a d", a=1)


def setup_weights(nc, w, ps, k):
    with ExitStack() as ctx:
        def tmp(name, shape, dt=F32):
            return ctx.enter_context(nc.sbuf_tensor(name, shape, dt))

        sem = ctx.enter_context(OneTime(nc, "setup_"))

        nat_wv0 = tmp("nat_wv0", [64, 128])
        nat_wt0 = tmp("nat_wt0", [64, C])
        nat_gate = tmp("nat_gate", [8, 128])
        nat_exp = tmp("nat_exp", [128, 8, 128])
        nat_wv1 = tmp("nat_wv1", [C, 128])
        wv1T = tmp("wv1T", [128, C])
        wfilm = tmp("wfilm", [128, 2, 256])
        mgate = tmp("mgate", [128, 1])
        graw = tmp("graw", [128, 8])
        vmask8 = tmp("vmask8", [128, B * S], U8)
        tmask8 = tmp("tmask8", [B, S], U8)
        tmaskf = tmp("tmaskf", [B, S])
        rowraw = tmp("rowraw", [128, 2, 128])
        iraw = tmp("iraw", [128, 8], I32)
        nat_bd2 = tmp("nat_bd2", [8, 128])
        nat_wd2 = tmp("nat_wd2", [128, 2, 128])
        wd2T = tmp("wd2T", [128, 2, 128])
        bd2bc = tmp("bd2bc", [128, 2, 128])
        junk = tmp("setup_junk", [128, 128])
        wq2 = tmp("wq2", [128, 4, 4, 8])
        wk2 = tmp("wk2", [C, 4, 4, 8])
        bq2 = tmp("bq2", [128, 4])
        bbase = tmp("bbase", [128, 8, 128])

        loads = sem("loads")
        ident_zero, ident_done = sem("ident_zero"), sem("ident_done")
        pool_done, turned, copied = sem("pool_done"), sem("turned"), sem("copied")
        vec_done, act_done = sem("vec_done"), sem("act_done")
        film_ps, gram_ps = sem("film_ps"), sem("gram_ps")

        block = ctx.enter_context(nc.Block())

        x_dram = w["x"].rearrange("b s d -> s b d")
        plan = [(k.X[:, 8 * i:8 * i + 8, :], x_dram[:, 8 * i:8 * i + 8, :]) for i in range(4)]
        plan += [
            (nat_wv0[:], w["L0_xattn_Wv"]), (nat_wt0[:], w["L0_xattn_Wt"]), (nat_gate[:], w["L0_ffn_gate_w"]),
            (nat_exp[:], w["L0_ffn_expert_w"].rearrange("e d c -> d e c")),
            (nat_wv1[:], w["L1_xattn_Wv"]),
            (wfilm[:, 0, :], w["L1_xattn_W_film_in"]), (wfilm[:, 1, :], w["L1_xattn_W_film_out"]),
            (mgate[:], w["L1_xattn_mod_gate"].broadcast_to([128, 1])),
            (k.wfilm[C:C + 1, 0:256], row_of(w["L1_xattn_b_film_in"])),
            (k.wfilm[C:C + 1, 256:512], row_of(w["L1_xattn_b_film_out"])),
            (graw[:, 0:4], row_of(w["g_xattn"]).broadcast_to([128, 4])),
            (graw[:, 4:8], row_of(w["g_ffn"]).broadcast_to([128, 4])),
            (vmask8[:], w["mask_BxS2_bf1"].rearrange("(a b) s -> a (b s)", a=1).broadcast_to([128, B * S])),
            (tmask8[:], w["mask_BxS_bf1"]),
            (k.bv0[:], w["L0_xattn_bv"].rearrange("(h a) -> h a", a=1)),
            (k.bt0[:], w["L0_xattn_bt"].rearrange("(h a) -> h a", a=1)),
            (k.wq1[:], w["L1_xattn_Wq"]), (k.wk1[:], w["L1_xattn_Wk"]),
            (k.w1_1[:], w["L1_xattn_W1"]), (k.w2_1[:], w["L1_xattn_W2"].rearrange("(q p) d -> p q d", p=128)),
            (k.b1_1[:], w["L1_xattn_b1"].rearrange("(q p) -> p q", p=128)),
            (k.gffn1[:], w["L1_xattn_g_ffn"].rearrange("(p a) -> p a", a=1)),
            (k.bffn1[:], w["L1_xattn_b_ffn"].rearrange("(p a) -> p a", a=1)),
            (k.b2_1[:], row_of(w["L1_xattn_b2"]).broadcast_to([128, 128])),
            (k.gin1[:], row_of(w["L1_xattn_g_norm_in"]).broadcast_to([128, 128])),
            (k.bin1[:], row_of(w["L1_xattn_b_norm_in"]).broadcast_to([128, 128])),
            (rowraw[:, 0, :], row_of(w["L1_xattn_g_norm_out"]).broadcast_to([128, 128])),
            (rowraw[:, 1, :], row_of(w["L1_xattn_b_norm_out"]).broadcast_to([128, 128])),
            (k.wbase[:], w["L1_ffn_W_base"]),
            (k.wd1[:], w["L1_ffn_Wd1"].rearrange("e d h -> d e h")),
            (k.bd1[:], w["L1_ffn_bd1"].rearrange("(a e) h -> a (e h)", a=1).broadcast_to([128, 256])),
            (nat_bd2[:], w["L1_ffn_bd2"]),
            (nat_wd2[:], w["L1_ffn_Wd2"].rearrange("(q e) h d -> (e h) q d", q=2)),
            (k.wdown[:], w["L1_ffn_Wa_down"].rearrange("e d r -> d e r")),
            (k.bdown[:], w["L1_ffn_ba_down"].rearrange("(a e) r -> a e r", a=1)),
            (k.wup[0:64], w["L1_ffn_Wa_up"].rearrange("e r o -> r e o")),
            (k.wup[64:65], w["L1_ffn_ba_up"].rearrange("(a e) o -> a e o", a=1)),
            (bbase[64:65], row_of(w["L1_ffn_b_base"]).rearrange("a (e o) -> a e o", e=1).broadcast_to([1, 8, 128])),
            (wq2[:], w["L2_xattn_Wq"].rearrange("p (j i d) -> p j i d", i=4, d=8)),
            (wk2[:], w["L2_xattn_Wk"].rearrange("p (j i d) -> p j i d", i=4, d=8)),
            (k.wv2[:], w["L2_xattn_Wv"]), (k.wo2[:], w["L2_xattn_Wo"]),
            (k.bv2[:], row_of(w["L2_xattn_bv"]).broadcast_to([128, 128])),
            (k.bo2[:], row_of(w["L2_xattn_bo"]).broadcast_to([128, 128])),
            (k.wq8[:], w["L2_ffn_weight"]),
            (k.bias8[:], row_of(w["L2_ffn_bias"]).broadcast_to([128, 128])),
            (k.wq3[:], w["L3_xattn_Wq"]), (k.wk3[:], w["L3_xattn_Wk"]), (k.wv3[:], w["L3_xattn_Wv"]),
            (k.wo3[:], w["L3_xattn_Wo"].rearrange("(q p) d -> p q d", p=128)),
            (k.bo3[:], row_of(w["L3_xattn_bo"]).broadcast_to([128, 128])),
            (k.wg3[:], w["L3_ffn_Wg"]), (k.bg3[:], row_of(w["L3_ffn_bg"]).broadcast_to([128, 8])),
            (k.w1_3[:], w["L3_ffn_W1"].rearrange("e d h -> d e h")),
            (k.w2_3[:], w["L3_ffn_W2"].rearrange("e (q p) d -> p e q d", p=128)),
            (k.b1_3[:], w["L3_ffn_b1"].rearrange("e (q p) -> p (e q)", p=128)),
            (k.b2_3[:], w["L3_ffn_b2"]),
        ]
        plan += [(bd2bc[32 * (e % 4):32 * (e % 4) + 32, e // 4, :],
                  w["L1_ffn_bd2"][e:e + 1, :].broadcast_to([32, 128])) for e in range(8)]
        plan += [(k.bq2[32 * i:32 * i + 8, :],
                  w["L2_xattn_bq"].rearrange("(j i d) -> i d j", i=4, d=8)[i]) for i in range(4)]
        plan += [(k.bk2[32 * i:32 * i + 8, :],
                  w["L2_xattn_bk"].rearrange("(j i d) -> i d j", i=4, d=8)[i]) for i in range(4)]
        n_loads = 16 * len(plan)

        zeroed = sem("zeroed")

        ctx.enter_context(nc.allow_non_contiguous_dma(reason="small vectors, once"))

        @block.sync
        def _(sp):
            sp.wait_ge(zeroed, 2)
            for dst, src in plan:
                sp.dma_start(dst, src).then_inc(loads, 16)

        @block.gpsimd
        def _(pool):
            pool.memset(k.bq2[:], 0.0).then_inc(zeroed, 1)
            pool.memset(k.bk2[:], 0.0).then_inc(zeroed, 1)
            pool.memset(k.ident[:], 0.0).then_inc(ident_zero, 1)
            pool.wait_ge(ident_zero, 1)
            pool.affine_select(out=k.ident[:], in_=k.ident[:], compare_op=ALU.not_equal, fill=1.0, base=0,
                               pattern=[[-1, 128]], channel_multiplier=1).then_inc(ident_done, 1)
            pool.memset(k.flip[:], 0.0).then_inc(ident_zero, 1)
            pool.wait_ge(ident_zero, 2)
            pool.affine_select(out=k.flip[:], in_=k.flip[:], compare_op=ALU.not_equal, fill=1.0, base=-127,
                               pattern=[[1, 128]], channel_multiplier=1)
            pool.memset(k.half[:], -0.5).then_inc(pool_done, 1)
            pool.memset(k.ones[:], 1.0).then_inc(pool_done, 1)
            pool.iota(iraw[:], pattern=[[1, 8]], base=0, channel_multiplier=0).then_inc(pool_done, 1)
            pool.memset(k.indic[:], 0.0).then_inc(pool_done, 1)
            pool.memset(k.dcoef[:], 0.0).then_inc(pool_done, 1)
            pool.memset(k.wq2p[:], 0.0).then_inc(pool_done, 1)
            pool.memset(k.wk2p[:], 0.0).then_inc(pool_done, 1)
            pool.wait_ge(pool_done, 7)
            pool.tensor_copy(k.iota8[:], iraw[:]).then_inc(pool_done, 1)
            for e in range(4):
                for q in range(2):
                    pool.wait_ge(pool_done, 8 + 2 * e + q)
                    pool.memset(k.indic[32 * e:32 * e + 32, q, 4 * q + e:4 * q + e + 1], 1.0).then_inc(pool_done, 1)

        turns = [(nat_exp[:, e, :], 128, 128, e // 4, (e % 4) * 128) for e in range(8)]
        turns += [(nat_wv0[:], 64, 128, 2, 0), (nat_wt0[:], 64, C, 2, 64), (nat_gate[:], 8, 128, 2, 128),
                  (nat_wv1[:], C, 128, 2, 136), (nat_bd2[:], 8, 128, 2, 232), (tmaskf[:], B, S, 2, 240)]
        turns += [(nat_wd2[:, q, :], 128, 128, 3, 128 * q) for q in range(2)]

        @block.tensor
        def _(pe):
            pe.wait_ge(loads, n_loads)
            pe.wait_ge(ident_done, 1)
            pe.wait_ge(vec_done, 1)
            for src, rows, cols, bank, col in turns:
                m = pe.transpose(ps[0:cols, bank, col:col + rows], src, k.ident[0:rows, 0:rows])
            m.then_inc(turned, 1)
            pe.wait_ge(copied, 4)
            pe.matmul(ps[0:C, 4, :], wv1T[:], wfilm[:].rearrange("p a n -> p (a n)"),
                      start=True, stop=True).then_inc(film_ps, 1)
            for q in range(2):
                m = pe.matmul(ps[:, 5, 128 * q:128 * q + 128], wd2T[:, q, :], wd2T[:, q, :],
                              start=True, stop=True)
            m.then_inc(gram_ps, 1)

        @block.scalar
        def _(act):
            act.wait_ge(loads, n_loads)
            act.activation(k.tg[:], graw[:], ACT.Tanh).then_inc(act_done, 1)

        @block.vector
        def _(dve):
            dve.wait_ge(loads, n_loads)
            dve.tensor_copy(tmaskf[:], tmask8[:]).then_inc(vec_done, 1)
            dve.tensor_scalar(k.vmask[:].rearrange("p b s -> p (b s)"), vmask8[:], 1.0, 1e30,
                              ALU.subtract, ALU.mult)
            dve.wait_ge(act_done, 1)
            dve.tensor_scalar(k.gout1[:], rowraw[:, 0, :], k.tg[:, 1:2], None, ALU.mult)
            dve.tensor_scalar(k.bout1[:], rowraw[:, 1, :], k.tg[:, 1:2], None, ALU.mult)
            dve.tensor_tensor(k.wup[64:65], k.wup[64:65], bbase[64:65], ALU.add)
            dve.wait_ge(pool_done, 16)
            for i in range(4):
                dve.tensor_copy(k.wq2p[:, :, 32 * i:32 * i + 8], wq2[:, :, i, :])
                dve.tensor_copy(k.wk2p[:, :, 32 * i:32 * i + 8], wk2[:, :, i, :])
            row = k.wfilm[C:C + 1, :].rearrange("p (a n) -> p a n", a=2)
            dve.tensor_scalar(row, row, mgate[C:C + 1, 0:1], None, ALU.mult).then_inc(vec_done, 1)
            dve.wait_ge(vec_done, 2)
            dve.tensor_scalar(row[:, :, 0:128], row[:, :, 0:128], 1.0, None, ALU.add)
            dve.wait_ge(turned, 1)
            dve.tensor_copy(wv1T[:], ps[:, 2, 136:136 + C]).then_inc(copied, 1)
            dve.tensor_copy(wd2T[:], ps[:, 3, 0:256].rearrange("p (q n) -> p q n", q=2)).then_inc(copied, 1)
            dve.tensor_copy(k.wv0T[:], ps[:, 2, 0:64]).then_inc(copied, 1)
            dve.tensor_copy(k.wt0T[:], ps[0:C, 2, 64:128]).then_inc(copied, 1)
            dve.tensor_copy(k.gateT[:], ps[:, 2, 128:136])
            dve.tensor_scalar(k.bd2T[:], ps[:, 2, 232:240], -2.0, None, ALU.mult).then_inc(vec_done, 1)
            dve.tensor_copy(k.tmask[:], ps[:, 2, 240:240 + B])
            for h in range(2):
                dve.tensor_copy(k.expT[:, 4 * h:4 * h + 4, :],
                                ps[:, h, :].rearrange("p (e d) -> p e d", e=4))
            dve.wait_ge(vec_done, 3)
            dve.scalar_tensor_tensor(out=k.bd2q[:], in0=k.bd2T[:], scalar=S / 4.0, in1=k.bd2T[:], op0=ALU.mult,
                                     op1=ALU.mult)
            dve.wait_ge(gram_ps, 1)
            for q in range(2):
                g0, o0, x0 = ((0, 128, 129), (129, 0, 1))[q]
                for e in range(4):
                    p = slice(32 * e, 32 * e + 32)
                    dve.tensor_copy(k.dcoef[p, q, g0 + 32 * e:g0 + 32 * e + 32],
                                    ps[p, 5, 128 * q + 32 * e:128 * q + 32 * e + 32])
                dve.tensor_scalar(k.dcoef[:, q, x0:x0 + 128], nat_wd2[:, q, :], -2.0, None, ALU.mult)
                dve.scalar_tensor_tensor(out=junk[:], in0=nat_wd2[:, q, :], scalar=2.0, in1=bd2bc[:, q, :],
                                         op0=ALU.mult, op1=ALU.mult,
                                         accum_out=k.dcoef[:, q, o0:o0 + 1]).then_inc(vec_done, 1)
                dve.wait_ge(vec_done, 4 + q)
            dve.wait_ge(film_ps, 1)
            dve.tensor_scalar(k.wfilm[0:C, :], ps[0:C, 4, :], mgate[0:C, 0:1], None, ALU.mult)


def stage_cosine(nc, w, ps, k):
    with ExitStack() as ctx:
        def tmp(name, shape, dt=F32):
            return ctx.enter_context(nc.sbuf_tensor("a_" + name, shape, dt))

        nm = Norm(lambda n, s: ctx.enter_context(nc.sbuf_tensor(n, s, F32)), "a")
        xn, xnT = tmp("xn", [128, 2, G, 128]), tmp("xnT", [128, 2, W])
        cx = tmp("cx", [128, 2, G, C])
        vT, tT = tmp("vT", [64, 2, W]), tmp("tT", [64, 2, W])
        v2, t2 = tmp("v2", [64, 2, W]), tmp("t2", [64, 2, W])
        nv2 = tmp("nv2", [128, 2, G])
        den, prod = tmp("den", [128, 2, W]), tmp("prod", [128, 2, W])
        s = signals(nc, k, "a", **NORM, cx0=16, cx1=16, xnT_ps=2, cT_ps=2, xnT=2, cT=2, vt_ps=4, vt=8, norms=2,
                    nv2=2, den=2 * G, root=2, dots=2, rden=2, prod=2, x=2)
        block = ctx.enter_context(nc.Block())
        c_dram = w["ctx_768"].rearrange("b s c -> s b c")

        @block.sync
        def _(sp):
            with sp.Fori(0, TURNS) as t:
                for u in range(2):
                    s["cT_ps"].wait(sp, t, 0)
                    sp.dma_start(cx[:, u], c_dram[:, bass.ds(t * PAIR + u * G, G), :]).then_inc(s[f"cx{u}"].sem, 16)

        @block.gpsimd
        def _(pool):
            with pool.Fori(0, TURNS) as t:
                norm_rstd(pool, nm, s, t, k.half[:])

        @block.tensor
        def _(pe):
            with pe.Fori(0, TURNS) as t:
                for u in range(2):
                    s[f"cx{u}"].wait(pe, t, 16)
                    s["x"].wait(pe, t, 0)
                    for j in range(G):
                        m = pe.transpose(ps[0:C, 4 * u + 1, j * S:(j + 1) * S], cx[:, u, j, :], k.ident[:])
                    m.then_inc(s["cT_ps"].sem, 1)
                    transpose_tokens(pe, s, t, u, xn, ps[:, 4 * u, :], k.ident[:])
                for u in range(2):
                    s["cT"].wait(pe, t, u + 1)
                    s["xnT"].wait(pe, t, u + 1)
                    pe.matmul(ps[0:64, 4 * u + 2, :], k.wv0T[:], xnT[:, u], start=True,
                              stop=True).then_inc(s["vt_ps"].sem, 1)
                    pe.matmul(ps[0:64, 4 * u + 3, :], k.wt0T[:], k.cT[:, bass.ds(t * 2 * W + u * W, W)],
                              start=True, stop=True).then_inc(s["vt_ps"].sem, 1)
                for u in range(2):
                    s["vt"].wait(pe, t, 4 * (u + 1))
                    pe.matmul(ps[:, 4 * u + 1, :], k.ones[0:64, :], t2[:, u], start=True, stop=True)
                    for j in range(G):
                        m = pe.matmul(ps[:, 4 * u, j:j + 1], v2[:, u, j * S:(j + 1) * S], k.ones[0:64, 0:1],
                                      start=True, stop=True)
                    m.then_inc(s["norms"].sem, 1)
                    for j in range(G):
                        m = pe.matmul(ps[:, 4 * u + 2, j * S:(j + 1) * S], vT[:, u, j * S:(j + 1) * S],
                                      tT[:, u, j * S:(j + 1) * S], start=True, stop=True)
                    m.then_inc(s["dots"].sem, 1)

        @block.scalar
        def _(act):
            with act.Fori(0, TURNS) as t:
                for u in range(2):
                    s["xnT_ps"].wait(act, t, u + 1)
                    act.activation(xnT[:, u], ps[:, 4 * u, :], ACT.Identity).then_inc(s["xnT"].sem, 1)
                for u in range(2):
                    s["vt_ps"].wait(act, t, 2 * u + 2)
                    for dst, func, bank, bias in ((vT, ACT.Identity, 2, k.bv0), (v2, ACT.Square, 2, k.bv0),
                                                  (tT, ACT.Identity, 3, k.bt0), (t2, ACT.Square, 3, k.bt0)):
                        act.activation(dst[:, u], ps[0:64, 4 * u + bank, :], func,
                                       bias=bias[:]).then_inc(s["vt"].sem, 1)
                for u in range(2):
                    s["den"].wait(act, t, G * (u + 1))
                    act.activation(den[:, u], den[:, u], ACT.Sqrt).then_inc(s["root"].sem, 1)

        @block.vector
        def _(dve):
            with dve.Fori(0, TURNS) as t:
                xj = [[k.X[:, bass.ds(t * PAIR + u * G + j, 1), :] for j in range(G)] for u in range(2)]
                norm_stats(dve, nm, s, t, lambda u, j: xj[u][j])
                for u in range(2):
                    norm_apply(dve, nm, s, t, u, lambda u, j: xj[u][j], xn)
                for u in range(2):
                    s["cT_ps"].wait(dve, t, u + 1)
                    dve.tensor_copy(k.cT[:, bass.ds(t * 2 * W + u * W, W)],
                                    ps[0:C, 4 * u + 1, :]).then_inc(s["cT"].sem, 1)
                for u in range(2):
                    s["norms"].wait(dve, t, u + 1)
                    dve.tensor_copy(nv2[:, u], ps[:, 4 * u, 0:G]).then_inc(s["nv2"].sem, 1)
                    s["nv2"].wait(dve, t, u + 1)
                    for j in range(G):
                        dve.tensor_scalar(den[:, u, j * S:(j + 1) * S], ps[:, 4 * u + 1, j * S:(j + 1) * S],
                                          nv2[:, u, j:j + 1], 1e-16, ALU.mult, ALU.max).then_inc(s["den"].sem, 1)
                for u in range(2):
                    s["root"].wait(dve, t, u + 1)
                    dve.reciprocal(den[:, u], den[:, u]).then_inc(s["rden"].sem, 1)
                    s["rden"].wait(dve, t, u + 1)
                    s["dots"].wait(dve, t, u + 1)
                    dve.tensor_tensor(prod[:, u], ps[:, 4 * u + 2, :], den[:, u],
                                      ALU.mult).then_inc(s["prod"].sem, 1)
                    s["prod"].wait(dve, t, u + 1)
                    xg = k.X[:, bass.ds(t * PAIR + u * G, G), :]
                    dve.scalar_tensor_tensor(out=xg, in0=prod[:, u].rearrange("p (j d) -> p j d", j=G),
                                             scalar=k.tg[:, 0:1], in1=xg, op0=ALU.mult,
                                             op1=ALU.add).then_inc(s["x"].sem, 1)


def stage_experts(nc, w, ps, k):
    with ExitStack() as ctx:
        def tmp(name, shape, dt=F32):
            return ctx.enter_context(nc.sbuf_tensor("b_" + name, shape, dt))

        nm = Norm(lambda n, s: ctx.enter_context(nc.sbuf_tensor(n, s, F32)), "b")
        xn, xnT = tmp("xn", [128, 2, G, 128]), tmp("xnT", [128, 2, W])
        lg, top = tmp("lg", [128, 2, G, 8]), tmp("top", [128, 2, G, 8])
        at, atf = tmp("at", [128, 2, G, 8], U32), tmp("atf", [128, 2, G, 2])
        gap, e2, tot = tmp("gap", [128, 2, G]), tmp("e2", [128, 2, G]), tmp("tot", [128, 2, G])
        wt = tmp("wt", [128, 2, G, 2])
        hit, wf = tmp("hit", [128, 2, G, 2, 8]), tmp("wf", [128, 2, G, 8])
        s = signals(nc, k, "b", **NORM, xnT_ps=2, xnT=2, lg_ps=2, lg=2, top=2 * G, at=2 * G, atf=2, gap=2,
                    e2=2, tot=2, rtot=2, w1=2, w2=2, hit=4, whit=4, wf=2, out_ps=2 * G, x=2 * G * 8)
        block = ctx.enter_context(nc.Block())

        @block.gpsimd
        def _(pool):
            with pool.Fori(0, TURNS) as t:
                norm_rstd(pool, nm, s, t, k.half[:])

        @block.tensor
        def _(pe):
            with pe.Fori(0, TURNS) as t:
                for u in range(2):
                    s["x"].wait(pe, t, 0)
                    transpose_tokens(pe, s, t, u, xn, ps[:, 4 * u, :], k.ident[:])
                for u in range(2):
                    s["xnT"].wait(pe, t, u + 1)
                    for j in range(G):
                        m = pe.matmul(ps[:, 4 * u + 1, 8 * j:8 * j + 8], xnT[:, u, j * S:(j + 1) * S],
                                      k.gateT[:], start=True, stop=True)
                    m.then_inc(s["lg_ps"].sem, 1)
                for u in range(2):
                    s["lg"].wait(pe, t, u + 1)
                    for j in range(G):
                        bank = 4 * u + (2, 0)[j % 2]
                        if j >= 2:
                            s["x"].wait(pe, t, 8 * (G * u + j - 1))
                        for h in range(2):
                            m = pe.matmul(ps[:, bank + h, :], xnT[:, u, j * S:(j + 1) * S],
                                          k.expT[:, 4 * h:4 * h + 4, :].rearrange("p e d -> p (e d)"),
                                          start=True, stop=True)
                        m.then_inc(s["out_ps"].sem, 1)

        @block.scalar
        def _(act):
            with act.Fori(0, TURNS) as t:
                for u in range(2):
                    s["xnT_ps"].wait(act, t, u + 1)
                    act.activation(xnT[:, u], ps[:, 4 * u, :], ACT.Identity).then_inc(s["xnT"].sem, 1)
                for u in range(2):
                    s["gap"].wait(act, t, u + 1)
                    act.activation(e2[:, u], gap[:, u], ACT.Exp).then_inc(s["e2"].sem, 1)

        @block.vector
        def _(dve):
            with dve.Fori(0, TURNS) as t:
                xj = [[k.X[:, bass.ds(t * PAIR + u * G + j, 1), :] for j in range(G)] for u in range(2)]
                norm_stats(dve, nm, s, t, lambda u, j: xj[u][j])
                for u in range(2):
                    norm_apply(dve, nm, s, t, u, lambda u, j: xj[u][j], xn)
                for u in range(2):
                    s["lg_ps"].wait(dve, t, u + 1)
                    dve.tensor_copy(lg[:, u].rearrange("p j e -> p (j e)"),
                                    ps[:, 4 * u + 1, 0:8 * G]).then_inc(s["lg"].sem, 1)
                    s["lg"].wait_apart(dve, t, u + 1)
                    for j in range(G):
                        dve.max(top[:, u, j, :], lg[:, u, j, :]).then_inc(s["top"].sem, 1)
                    s["top"].wait_apart(dve, t, G * (u + 1))
                    for j in range(G):
                        dve.max_index(at[:, u, j, :], top[:, u, j, :], lg[:, u, j, :]).then_inc(s["at"].sem, 1)
                    dve.tensor_tensor(gap[:, u], top[:, u, :, 1], top[:, u, :, 0],
                                      ALU.subtract).then_inc(s["gap"].sem, 1)
                for u in range(2):
                    s["at"].wait(dve, t, G * (u + 1))
                    dve.tensor_copy(atf[:, u], at[:, u, :, 0:2]).then_inc(s["atf"].sem, 1)
                    s["e2"].wait(dve, t, u + 1)
                    dve.tensor_scalar(tot[:, u], e2[:, u], 1.0, None, ALU.add).then_inc(s["tot"].sem, 1)
                    s["tot"].wait(dve, t, u + 1)
                    dve.reciprocal(tot[:, u], tot[:, u]).then_inc(s["rtot"].sem, 1)
                    s["rtot"].wait(dve, t, u + 1)
                    dve.tensor_scalar(wt[:, u, :, 0], tot[:, u], k.tg[:, 4:5], None,
                                      ALU.mult).then_inc(s["w1"].sem, 1)
                    s["w1"].wait(dve, t, u + 1)
                    dve.tensor_tensor(wt[:, u, :, 1], wt[:, u, :, 0], e2[:, u],
                                      ALU.mult).then_inc(s["w2"].sem, 1)
                    s["w2"].wait(dve, t, u + 1)
                    s["atf"].wait(dve, t, u + 1)
                    for i in range(2):
                        dve.tensor_tensor(hit[:, u, :, i, :], k.iota8[:].rearrange("p (j e) -> p j e", j=1).broadcast_to([128, G, 8]),
                                          atf[:, u, :, i:i + 1].broadcast_to([128, G, 8]),
                                          ALU.is_equal).then_inc(s["hit"].sem, 1)
                    s["hit"].wait(dve, t, 2 * u + 2)
                    for i in range(2):
                        dve.tensor_tensor(hit[:, u, :, i, :], hit[:, u, :, i, :],
                                          wt[:, u, :, i:i + 1].broadcast_to([128, G, 8]),
                                          ALU.mult).then_inc(s["whit"].sem, 1)
                    s["whit"].wait(dve, t, 2 * u + 2)
                    dve.tensor_tensor(wf[:, u], hit[:, u, :, 0, :], hit[:, u, :, 1, :],
                                      ALU.add).then_inc(s["wf"].sem, 1)
                for u in range(2):
                    s["wf"].wait(dve, t, u + 1)
                    for j in range(G):
                        bank = 4 * u + (2, 0)[j % 2]
                        s["out_ps"].wait(dve, t, G * u + j + 1)
                        for e in range(8):
                            if e:
                                s["x"].wait(dve, t, 8 * (G * u + j) + e)
                            dve.scalar_tensor_tensor(
                                out=xj[u][j], in0=ps[:, bank + e // 4, 128 * (e % 4):128 * (e % 4) + 128],
                                scalar=wf[:, u, j, e:e + 1], in1=xj[u][j], op0=ALU.mult,
                                op1=ALU.add).then_inc(s["x"].sem, 1)


def setup_kernel(nc, w, ps, k):
    N, NA, NB = 64, 8, 16
    M = NA + NB + NA + 1
    PI = 3.14159265358979
    TWO_PI = (6.28125, 1.9340515136718750e-3, 1.2556659146e-6)
    ROUND = 1.5 * 2.0 ** 23
    with ExitStack() as ctx:
        def tmp(name, shape, dt=F32):
            return ctx.enter_context(nc.sbuf_tensor("s4_" + name, shape, dt))

        sem = ctx.enter_context(OneTime(nc, "s4_"))

        nat = tmp("nat", [128, 4, 2, N])
        par = tmp("par", [128, 4, 128])
        ldt, drow = tmp("ldt", [128, 128]), tmp("drow", [1, 128])
        mi, mf = tmp("mi", [128, M], I32), tmp("mf", [128, M])
        ph = tmp("ph", [128, 2])
        sgn = tmp("sgn", [128, 1])
        dta = tmp("dta", [128, 2, 128])
        arg, kk, ex = tmp("arg", [128, 128, M]), tmp("kk", [128, 128, M]), tmp("ex", [128, 128, M])
        tt = kk
        sm = tmp("sm", [128, 12, 128])
        pq, pq2 = tmp("pq", [128, 128, NA]), tmp("pq2", [128, 128, NA])
        k2 = tmp("k2", [NA, 128, NB])
        zero = tmp("zero", [128, 127])
        loads, consts, turned, kps = sem("loads"), sem("consts"), sem("turned"), sem("kps")
        act_dt, vec_arg, act_ex, vec_red, act_sin = (sem(n) for n in ("act_dt", "vec_arg", "act_ex", "vec_red",
                                                                     "act_sin"))
        chain, vec_pq, vec_k2, stored = sem("chain"), sem("vec_pq"), sem("vec_k2"), sem("stored")
        block = ctx.enter_context(nc.Block())

        @block.sync
        def _(sp):
            for i, name in enumerate(("A_re", "A_im", "C_re", "C_im")):
                for h in range(2):
                    sp.dma_start(nat[:, i, h, :], w["L1_xattn_" + name]).then_inc(loads, 16)
            sp.dma_start(ldt[:], row_of(w["L1_xattn_log_dt"]).broadcast_to([128, 128])).then_inc(loads, 16)
            sp.dma_start(drow[:], row_of(w["L1_xattn_D_skip"])).then_inc(loads, 16)
            sp.wait_ge(consts, 9)
            sp.dma_start(k.kpad[:, 0:127], zero[:]).then_inc(stored, 16)
            sp.wait_ge(vec_k2, 1)
            sp.dma_start(k.kpad[:, 127:255].rearrange("d (a b) -> a d b", b=NB), k2[:]).then_inc(stored, 16)
            sp.wait_ge(stored, 32)

        @block.gpsimd
        def _(pool):
            pool.iota(mi[:, 0:8], pattern=[[16, 8]], base=0, channel_multiplier=0).then_inc(consts, 1)
            pool.iota(mi[:, 8:24], pattern=[[1, 16]], base=0, channel_multiplier=0).then_inc(consts, 1)
            pool.iota(mi[:, 24:32], pattern=[[16, 8]], base=0, channel_multiplier=0).then_inc(consts, 1)
            pool.iota(mi[:, 32:33], pattern=[[1, 1]], base=1, channel_multiplier=0).then_inc(consts, 1)
            pool.memset(ph[:], 0.0).then_inc(consts, 1)
            pool.memset(sgn[:], 1.0).then_inc(consts, 1)
            pool.wait_ge(consts, 6)
            pool.memset(ph[0:N, 0:1], PI / 2).then_inc(consts, 1)
            pool.wait_ge(consts, 7)
            pool.memset(ph[N:128, 1:2], PI / 2).then_inc(consts, 1)
            pool.wait_ge(consts, 8)
            pool.memset(zero[:], 0.0).then_inc(consts, 1)
            pool.wait_ge(consts, 9)
            pool.memset(sgn[N:128], -1.0).then_inc(consts, 1)

        @block.tensor
        def _(pe):
            pe.wait_ge(loads, 160)
            for i in range(4):
                m = pe.transpose(ps[:, 0, 128 * i:128 * i + 128], nat[:, i].rearrange("p h n -> p (h n)"), k.ident[:])
            m.then_inc(turned, 1)
            pe.wait_ge(vec_pq, 1)
            for d in range(128):
                m = pe.matmul(ps[0:NA, 1 + d // 32, NB * (d % 32):NB * (d % 32) + NB], pq[:, d, :],
                              tt[:, d, NA:NA + NB], start=True, stop=True)
            m.then_inc(kps, 1)

        @block.scalar
        def _(act):
            act.wait_ge(loads, 160)
            act.activation(ldt[:], ldt[:], ACT.Exp).then_inc(act_dt, 1)
            act.wait_ge(vec_arg, 1)
            act.activation(ex[:], ex[:], ACT.Exp).then_inc(act_ex, 1)
            act.wait_ge(vec_red, 1)
            act.activation(tt[:], arg[:], ACT.Sin).then_inc(act_sin, 1)

        @block.vector
        def _(dve):
            n = [0]

            def link(ins):
                n[0] += 1
                ins.then_inc(chain, 1)
                dve.wait_ge(chain, n[0])

            dve.wait_ge(consts, 10)
            link(dve.tensor_copy(mf[:], mi[:]))
            dve.wait_ge(turned, 1)
            link(dve.tensor_copy(par[:].rearrange("p i d -> p (i d)"), ps[:, 0, :]))
            dve.wait_ge(act_dt, 1)
            for i in range(2):
                link(dve.tensor_tensor(dta[:, i, :], par[:, i, :], ldt[:], ALU.mult))
            mb = mf[:].rearrange("p (o m) -> p o m", o=1).broadcast_to([128, 128, M])

            def per_channel(t):
                return t.rearrange("p (d o) -> p d o", o=1)

            dve.tensor_tensor(ex[:], per_channel(dta[:, 0, :]).broadcast_to([128, 128, M]), mb,
                              ALU.mult).then_inc(vec_arg, 1)
            link(dve.tensor_tensor(arg[:], per_channel(dta[:, 1, :]).broadcast_to([128, 128, M]), mb, ALU.mult))
            for lo, hi, i in ((0, 24, 0), (24, M, 1)):
                a, q = arg[:, :, lo:hi], kk[:, :, lo:hi]
                link(dve.tensor_scalar(q, a, ph[:, i:i + 1], 1 / (2 * PI), ALU.add, ALU.mult))
                link(dve.tensor_scalar(q, q, ROUND, ROUND, ALU.add, ALU.subtract))
            for c in TWO_PI:
                link(dve.scalar_tensor_tensor(out=arg[:], in0=kk[:], scalar=-c, in1=arg[:], op0=ALU.mult,
                                              op1=ALU.add))
            for lo, hi, i in ((0, 24, 0), (24, M, 1)):
                a = arg[:, :, lo:hi]
                link(dve.tensor_scalar(a, a, ph[:, i:i + 1], 3.1415925, ALU.add, ALU.min))
            dve.tensor_scalar(arg[:], arg[:], -3.1415925, None, ALU.max).then_inc(vec_red, 1)
            dve.wait_ge(act_sin, 1)
            dve.wait_ge(act_ex, 1)
            cos, sin = sm[:, 0, :], sm[:, 1, :]
            dve.tensor_copy(sm[0:N, 0, :], tt[0:N, :, NA + 1])
            dve.tensor_copy(sm[N:128, 0, :], tt[N:128, :, M - 1])
            dve.tensor_copy(sm[0:N, 1, :], tt[0:N, :, M - 1])
            link(dve.tensor_copy(sm[N:128, 1, :], tt[N:128, :, NA + 1]))
            link(dve.tensor_tensor(tt[:], tt[:], ex[:], ALU.mult))
            e1 = ex[:, :, M - 1]
            ar, ai, cr, ci = (par[:, i, :] for i in range(4))
            r = [sm[:, i, :] for i in range(12)]

            def tt_(out, a, b, op):
                link(dve.tensor_tensor(out, a, b, op))

            tt_(r[2], cos, e1, ALU.mult)
            link(dve.tensor_scalar(r[2], r[2], 1.0, None, ALU.subtract))
            tt_(r[3], sin, e1, ALU.mult)
            tt_(r[4], cr, r[2], ALU.mult)
            tt_(r[5], ci, r[3], ALU.mult)
            tt_(r[4], r[4], r[5], ALU.subtract)
            tt_(r[5], cr, r[3], ALU.mult)
            tt_(r[6], ci, r[2], ALU.mult)
            tt_(r[5], r[5], r[6], ALU.add)
            tt_(r[6], ar, ar, ALU.mult)
            tt_(r[7], ai, ai, ALU.mult)
            tt_(r[6], r[6], r[7], ALU.add)
            link(dve.reciprocal(r[6], r[6]))
            tt_(r[7], r[4], ar, ALU.mult)
            tt_(r[8], r[5], ai, ALU.mult)
            tt_(r[7], r[7], r[8], ALU.add)
            tt_(r[8], r[5], ar, ALU.mult)
            tt_(r[9], r[4], ai, ALU.mult)
            tt_(r[8], r[8], r[9], ALU.subtract)
            tt_(r[7], r[7], r[6], ALU.mult)
            tt_(r[8], r[8], r[6], ALU.mult)
            link(dve.tensor_scalar(r[7], r[7], sgn[:, 0:1], 2.0, ALU.mult, ALU.mult))
            link(dve.tensor_scalar(r[8], r[8], 2.0, None, ALU.mult))
            tt_(pq[:], tt[:, :, 0:NA], per_channel(r[7]).broadcast_to([128, 128, NA]), ALU.mult)
            tt_(pq2[:], tt[:, :, NA + NB:NA + NB + NA], per_channel(r[8]).broadcast_to([128, 128, NA]), ALU.mult)
            dve.tensor_tensor(pq[:], pq[:], pq2[:], ALU.subtract).then_inc(vec_pq, 1)
            dve.wait_ge(kps, 1)
            for b in range(4):
                link(dve.tensor_copy(k2[:, 32 * b:32 * b + 32, :].rearrange("p d b -> p (d b)"),
                                     ps[0:NA, 1 + b, :]))
            dve.tensor_tensor(k2[0:1, :, 0], k2[0:1, :, 0], drow[:], ALU.add).then_inc(vec_k2, 1)


def stage_film(nc, w, ps, k):
    film_in(nc, w, ps, k)
    convolve(nc, w, ps, k)
    film_out(nc, w, ps, k)


def film_in(nc, w, ps, k):
    H, DH, ROUNDS = 4, 32, 4
    SCALE = DH ** -0.5
    TAKEN = -3e38
    with ExitStack() as ctx:
        def tmp(name, shape, dt=F32):
            return ctx.enter_context(nc.sbuf_tensor("c_" + name, shape, dt))

        nm = Norm(lambda n, s: ctx.enter_context(nc.sbuf_tensor(n, s, F32)), "c")
        xn, xnT = tmp("xn", [128, 2, G, 128]), tmp("xnT", [128, 2, W])
        rstd2 = tmp("rstd2", [128, 2 * G])
        cx = tmp("cx", [128, 2, G, C])
        qT, kT = tmp("qT", [128, 2, W]), tmp("kT", [128, 2, W])
        sc, left = tmp("sc", [128, 2, H, 128]), tmp("left", [128, 2, H, 128])
        first, top = tmp("first", [128, 2, H, 8]), tmp("top", [128, 2, H, 8])
        shift, total = tmp("shift", [128, 2, H]), tmp("total", [128, 2, H])
        ex = tmp("ex", [128, 2, H, 128])
        mean_w = tmp("mean_w", [128, 2, G, 128])
        wT, aT = tmp("wT", [128, 2, W]), tmp("aT", [C + 1, 2, W])
        x2 = tmp("x2", [128, 2, G, 128])
        fo = tmp("fo", [128, 2, G, 512])
        NB_ = 2 * G
        s = signals(nc, k, "c", **NORM, rr=1, vr=1, ve2=1, rstd2=1, kept=2, cx0=16, cx1=16, xnT_ps=2, xnT=2,
                    qk_ps=2, qT=2, kT=2, sc_ps=2, sc=NB_, top=NB_ * H * ROUNDS, left=NB_ * H * ROUNDS,
                    shift=NB_, ex=NB_ * H, keep=NB_ * H, rtot=NB_, share=NB_, mean_sum=NB_ * H, wT_ps=2, wT=2,
                    aT_ps=2, aT=2, film_ps=NB_, x2a=2 * G, x2b=2 * G, x2c=2 * G, x3=2 * G, fo=2 * G,
                    fo_out0=16, fo_out1=16)
        ones = ctx.enter_context(OneTime(nc, "c_"))("ones")
        block = ctx.enter_context(nc.Block())
        c_dram = w["ctx_768"].rearrange("b s c -> s b c")

        @block.sync
        def _(sp):
            with sp.Fori(0, TURNS) as t:
                for u in range(2):
                    s["aT_ps"].wait(sp, t, 0)
                    sp.dma_start(cx[:, u], c_dram[:, bass.ds(t * PAIR + u * G, G), :]).then_inc(s[f"cx{u}"].sem, 16)
                for u in range(2):
                    s["fo"].wait(sp, t, G * (u + 1))
                    sp.dma_start(k.fo_dram[:, bass.ds(t * PAIR + u * G, G), :],
                                 fo[:, u, :, 256:512]).then_inc(s[f"fo_out{u}"].sem, 16)
            for u in range(2):
                s[f"fo_out{u}"].wait(sp, TURNS - 1, 16)

        @block.gpsimd
        def _(pool):
            pool.memset(aT[C:C + 1], 1.0).then_inc(ones, 1)
            pool.wait_ge(ones, 1)
            with pool.Fori(0, TURNS) as t:
                norm_rstd(pool, nm, s, t, k.half[:])
                s["ve2"].wait(pool, t, 1)
                pool.tensor_tensor(rstd2[:], rstd2[:], k.half[:], ALU.pow).then_inc(s["rstd2"].sem, 1)

        @block.tensor
        def _(pe):
            pe.wait_ge(ones, 1)
            with pe.Fori(0, TURNS) as t:
                for u in range(2):
                    s["x3"].wait(pe, t, 0)
                    s["fo"].wait(pe, t, 0)
                    transpose_tokens(pe, s, t, u, xn, ps[:, 4 * u, :], k.ident[:])
                for u in range(2):
                    s["xnT"].wait(pe, t, u + 1)
                    pe.matmul(ps[:, 4 * u + 1, :], k.wq1[:], xnT[:, u], start=True, stop=True)
                    pe.matmul(ps[:, 4 * u + 2, :], k.wk1[:], k.cT[:, bass.ds(t * 2 * W + u * W, W)],
                              start=True, stop=True).then_inc(s["qk_ps"].sem, 1)
                for u in range(2):
                    s["qT"].wait(pe, t, u + 1)
                    s["kT"].wait(pe, t, u + 1)
                    for j in range(G):
                        for h in range(H):
                            r = slice(DH * h, DH * h + DH)
                            m = pe.matmul(ps[:, 4 * u + h, j * S:j * S + S], qT[r, u, j * S:j * S + S],
                                          kT[r, u, j * S:j * S + S], start=True, stop=True,
                                          tile_position=(DH * h, 0))
                    m.then_inc(s["sc_ps"].sem, 1)
                for u in range(2):
                    s["mean_sum"].wait(pe, t, H * (2 * (G - 1) + u + 1))
                    for j in range(G):
                        m = pe.transpose(ps[:, 4 * u + 1, j * S:j * S + S], mean_w[:, u, j, :], k.ident[:])
                    m.then_inc(s["wT_ps"].sem, 1)
                for u in range(2):
                    s["wT"].wait(pe, t, u + 1)
                    s[f"cx{u}"].wait(pe, t, 16)
                    for j in range(G):
                        m = pe.matmul(ps[0:C, 4 * u + 2, j * S:j * S + S], cx[:, u, j, :],
                                      wT[:, u, j * S:j * S + S], start=True, stop=True)
                    m.then_inc(s["aT_ps"].sem, 1)
                for u in range(2):
                    s["aT"].wait(pe, t, u + 1)
                    for j in range(G):
                        if j >= 2:
                            s["fo"].wait(pe, t, G * u + j - 1)
                        pe.matmul(ps[:, 4 * u + (3, 0)[j % 2], :], aT[:, u, j * S:j * S + S], k.wfilm[:],
                                  start=True, stop=True).then_inc(s["film_ps"].sem, 1)

        @block.scalar
        def _(act):
            with act.Fori(0, TURNS) as t:
                for u in range(2):
                    s["xnT_ps"].wait(act, t, u + 1)
                    act.activation(xnT[:, u], ps[:, 4 * u, :], ACT.Identity).then_inc(s["xnT"].sem, 1)
                for u in range(2):
                    s["qk_ps"].wait(act, t, u + 1)
                    act.activation(qT[:, u], ps[:, 4 * u + 1, :], ACT.Identity).then_inc(s["qT"].sem, 1)
                    act.activation(kT[:, u], ps[:, 4 * u + 2, :], ACT.Identity).then_inc(s["kT"].sem, 1)
                for i in range(NB_):
                    u = i % 2
                    s["shift"].wait(act, t, i + 1)
                    for h in range(H):
                        act.activation(ex[:, u, h, :], sc[:, u, h, :], ACT.Exp, bias=shift[:, u, h:h + 1],
                                       scale=SCALE).then_inc(s["ex"].sem, 1)
                for u in range(2):
                    s["wT_ps"].wait(act, t, u + 1)
                    act.activation(wT[:, u], ps[:, 4 * u + 1, :], ACT.Identity).then_inc(s["wT"].sem, 1)
                for u in range(2):
                    s["aT_ps"].wait(act, t, u + 1)
                    act.activation(aT[0:C, u], ps[0:C, 4 * u + 2, :], ACT.Identity).then_inc(s["aT"].sem, 1)
                for u in range(2):
                    s[f"fo_out{u}"].wait(act, t, 0)
                    s["x3"].wait(act, t, 0)
                    for j in range(G):
                        s["film_ps"].wait(act, t, G * u + j + 1)
                        act.activation(fo[:, u, j, :], ps[:, 4 * u + (3, 0)[j % 2], :],
                                       ACT.Identity).then_inc(s["fo"].sem, 1)

        @block.vector
        def _(dve):
            with dve.Fori(0, TURNS) as t:
                xj = [[k.X[:, bass.ds(t * PAIR + u * G + j, 1), :] for j in range(G)] for u in range(2)]
                norm_stats(dve, nm, s, t, lambda u, j: xj[u][j])
                for u in range(2):
                    norm_apply(dve, nm, s, t, u, lambda u, j: xj[u][j], xn)
                rs, ve = nm.rstd[:].rearrange("p u j -> p (u j)"), nm.ve[:].rearrange("p u j -> p (u j)")
                dve.tensor_tensor(rstd2[:], rs, rs, ALU.mult).then_inc(s["rr"].sem, 1)
                s["rr"].wait(dve, t, 1)
                dve.scalar_tensor_tensor(out=rstd2[:], in0=ve, scalar=EPS, in1=rstd2[:], op0=ALU.subtract,
                                         op1=ALU.mult).then_inc(s["vr"].sem, 1)
                s["vr"].wait(dve, t, 1)
                dve.tensor_scalar(rstd2[:], rstd2[:], EPS, None, ALU.add).then_inc(s["ve2"].sem, 1)
                dve.tensor_copy(k.mean1[:, bass.ds(t * PAIR, PAIR)],
                                nm.mean[:].rearrange("p u j -> p (u j)")).then_inc(s["kept"].sem, 1)
                dve.tensor_copy(k.rstd1[:, bass.ds(t * PAIR, PAIR)], rs).then_inc(s["kept"].sem, 1)
                for i in range(NB_):
                    j, u = i // 2, i % 2
                    b = t * PAIR + u * G + j
                    s["sc_ps"].wait(dve, t, u + 1)
                    dve.tensor_tensor(sc[:, u], ps[:, 4 * u:4 * u + H, j * S:j * S + S],
                                      k.vmask[:, bass.ds(b, 1), :].broadcast_to([128, H, 128]),
                                      ALU.add).then_inc(s["sc"].sem, 1)
                    s["sc"].wait_apart(dve, t, i + 1)
                    for r in range(ROUNDS):
                        if r:
                            s["left"].wait_apart(dve, t, H * (ROUNDS * i + r))
                        for h in range(H):
                            dve.max((first if r == 0 else top)[:, u, h, :],
                                    (sc if r == 0 else left)[:, u, h, :]).then_inc(s["top"].sem, 1)
                        s["top"].wait_apart(dve, t, H * (ROUNDS * i + r + 1))
                        if r == 0:
                            dve.tensor_scalar(shift[:, u, :], first[:, u, :, 0], -SCALE, None,
                                              ALU.mult).then_inc(s["shift"].sem, 1)
                        for h in range(H):
                            dve.match_replace(left[:, u, h, :], (first if r == 0 else top)[:, u, h, :],
                                              (sc if r == 0 else left)[:, u, h, :],
                                              TAKEN).then_inc(s["left"].sem, 1)
                    s["left"].wait(dve, t, H * ROUNDS * (i + 1))
                    s["ex"].wait(dve, t, H * (i + 1))
                    for h in range(H):
                        dve.scalar_tensor_tensor(out=ex[:, u, h, :], in0=left[:, u, h, :], scalar=TAKEN * 0.5,
                                                 in1=ex[:, u, h, :], op0=ALU.is_le, op1=ALU.mult,
                                                 accum_out=total[:, u, h:h + 1]).then_inc(s["keep"].sem, 1)
                    s["keep"].wait(dve, t, H * (i + 1))
                    dve.reciprocal(total[:, u, :], total[:, u, :]).then_inc(s["rtot"].sem, 1)
                    s["rtot"].wait(dve, t, i + 1)
                    dve.scalar_tensor_tensor(out=total[:, u, :], in0=total[:, u, :], scalar=1.0 / H,
                                             in1=k.tmask[:, bass.ds(b, 1)].broadcast_to([128, H]),
                                             op0=ALU.mult, op1=ALU.mult).then_inc(s["share"].sem, 1)
                    s["share"].wait(dve, t, i + 1)
                    for h in range(H):
                        if h == 0:
                            m = dve.tensor_scalar(mean_w[:, u, j, :], ex[:, u, h, :], total[:, u, h:h + 1], None,
                                                  ALU.mult)
                        else:
                            s["mean_sum"].wait(dve, t, H * i + h)
                            m = dve.scalar_tensor_tensor(out=mean_w[:, u, j, :], in0=ex[:, u, h, :],
                                                         scalar=total[:, u, h:h + 1], in1=mean_w[:, u, j, :],
                                                         op0=ALU.mult, op1=ALU.add)
                        m.then_inc(s["mean_sum"].sem, 1)
                s["rstd2"].wait(dve, t, 1)
                for u in range(2):
                    for j in range(G):
                        dve.scalar_tensor_tensor(out=x2[:, u, j, :], in0=xn[:, u, j, :],
                                                 scalar=rstd2[:, u * G + j:u * G + j + 1], in1=k.gin1[:],
                                                 op0=ALU.mult, op1=ALU.mult).then_inc(s["x2a"].sem, 1)
                s["x2a"].wait(dve, t, 2 * G)
                for u in range(2):
                    for j in range(G):
                        dve.tensor_tensor(x2[:, u, j, :], x2[:, u, j, :], k.bin1[:],
                                          ALU.add).then_inc(s["x2b"].sem, 1)
                s["x2b"].wait(dve, t, 2 * G)
                for u in range(2):
                    for j in range(G):
                        s["fo"].wait(dve, t, G * u + j + 1)
                        dve.tensor_tensor(x2[:, u, j, :], x2[:, u, j, :], fo[:, u, j, 0:128],
                                          ALU.mult).then_inc(s["x2c"].sem, 1)
                        s["x2c"].wait(dve, t, G * u + j + 1)
                        dve.tensor_tensor(k.x3[:, :, bass.ds(t * PAIR + u * G + j, 1)],
                                          x2[:, u, j, :].rearrange("p (c o) -> p c o", o=1),
                                          fo[:, u, j, 128:256].rearrange("p (c o) -> p c o", o=1),
                                          ALU.add).then_inc(s["x3"].sem, 1)


def convolve(nc, w, ps, k):
    CH = 16
    CHUNKS = D // CH
    with ExitStack() as ctx:
        toep = ctx.enter_context(nc.sbuf_tensor("v_toep", [128, CHUNKS, CH, 128], F32))
        once = ctx.enter_context(OneTime(nc, "v_"))
        toep_in = [once(f"toep_in{i}") for i in range(CHUNKS)]
        flip_ps, flipped, y_ps = once("flip_ps"), once("flipped"), once("y_ps")
        block = ctx.enter_context(nc.Block())

        def chunk(c):
            return k.x3[:, CH * c:CH * c + CH, :].rearrange("p c b -> p (c b)")

        @block.sync
        def _(sp):
            for c in range(CHUNKS):
                src = bass.AP(tensor=k.kpad.tensor, offset=256 * CH * c, ap=[[1, 128], [256, CH], [1, 128]])
                sp.dma_start(toep[:, c], src).then_inc(toep_in[c], 16)

        @block.tensor
        def _(pe):
            for c in range(CHUNKS):
                pe.matmul(ps[:, c, :], k.flip[:], chunk(c), start=True, stop=True).then_inc(flip_ps, 1)
            for c in range(CHUNKS):
                pe.wait_ge(flipped, c + 1)
                pe.wait_ge(toep_in[c], 16)
                for i in range(CH):
                    m = pe.matmul(ps[:, c, B * i:B * i + B], toep[:, c, i, :], k.x3[:, CH * c + i, :],
                                  start=True, stop=True)
                m.then_inc(y_ps, 1)

        @block.scalar
        def _(act):
            for c in range(CHUNKS):
                act.wait_ge(flip_ps, c + 1)
                act.activation(chunk(c), ps[:, c, :], ACT.Identity).then_inc(flipped, 1)

        @block.vector
        def _(dve):
            for c in range(CHUNKS):
                dve.wait_ge(y_ps, c + 1)
                dve.tensor_copy(chunk(c), ps[:, c, :])


def film_out(nc, w, ps, k):
    with ExitStack() as ctx:
        def tmp(name, shape, dt=F32):
            return ctx.enter_context(nc.sbuf_tensor("d_" + name, shape, dt))

        nm1 = Norm(lambda n, s: ctx.enter_context(nc.sbuf_tensor(n, s, F32)), "d1")
        nm2 = Norm(lambda n, s: ctx.enter_context(nc.sbuf_tensor(n, s, F32)), "d2")
        fo = tmp("fo", [128, 2, G, 256])
        z, xt = tmp("z", [128, 2, G, 128]), tmp("xt", [128, 2, G, 128])
        xn, hT = tmp("xn", [128, 2, G, 128]), tmp("hT", [128, 2, W])
        hid = tmp("hid", [128, 2, 4, W])
        s = signals(nc, k, "d", fo_in0=16, fo_in1=16, xt=2 * G, zs=2, zh=2, z=2, xnT_ps=2, hT=2,
                    hid_ps=8, hid=8, mlp_ps=2, zm=2, zb=2, og=2, ob=2, x=2)
        s1 = signals(nc, k, "d1", **NORM)
        s2 = {n[3:]: v for n, v in signals(nc, k, "d2", **{"n2_" + n: v for n, v in NORM.items()}).items()}
        s1["xnT_ps"] = s["xnT_ps"]
        block = ctx.enter_context(nc.Block())

        @block.sync
        def _(sp):
            with sp.Fori(0, TURNS) as t:
                for u in range(2):
                    s["zh"].wait(sp, t, 0)
                    sp.dma_start(fo[:, u], k.fo_dram[:, bass.ds(t * PAIR + u * G, G), :]).then_inc(s[f"fo_in{u}"].sem, 16)

        @block.gpsimd
        def _(pool):
            with pool.Fori(0, TURNS) as t:
                norm_rstd(pool, nm1, s1, t, k.half[:])
                norm_rstd(pool, nm2, s2, t, k.half[:])

        @block.tensor
        def _(pe):
            with pe.Fori(0, TURNS) as t:
                for u in range(2):
                    s["zm"].wait(pe, t, 0)
                    transpose_tokens(pe, s1, t, u, xn, ps[:, 4 * u, :], k.ident[:])
                for u in range(2):
                    s["hT"].wait(pe, t, u + 1)
                    for q in range(4):
                        pe.matmul(ps[:, 4 * u + (q + 1) % 4, :], k.w1_1[:, 128 * q:128 * q + 128], hT[:, u],
                                  start=True, stop=True).then_inc(s["hid_ps"].sem, 1)
                for u in range(2):
                    s["hid"].wait(pe, t, 4 * (u + 1))
                    for j in range(G):
                        for q in range(4):
                            m = pe.matmul(ps[:, 4 * u + 1, j * S:j * S + S], hid[:, u, q, j * S:j * S + S],
                                          k.w2_1[:, q, :], start=q == 0, stop=q == 3)
                    m.then_inc(s["mlp_ps"].sem, 1)

        @block.scalar
        def _(act):
            with act.Fori(0, TURNS) as t:
                for u in range(2):
                    s["xnT_ps"].wait(act, t, u + 1)
                    act.activation(hT[:, u], ps[:, 4 * u, :], ACT.Identity, bias=k.bffn1[:],
                                   scale=k.gffn1[:]).then_inc(s["hT"].sem, 1)
                for u in range(2):
                    for q in range(4):
                        s["hid_ps"].wait(act, t, 4 * u + q + 1)
                        act.activation(hid[:, u, q, :], ps[:, 4 * u + (q + 1) % 4, :], ACT.Gelu,
                                       bias=k.b1_1[:, q:q + 1]).then_inc(s["hid"].sem, 1)

        @block.vector
        def _(dve):
            with dve.Fori(0, TURNS) as t:
                xg = [k.X[:, bass.ds(t * PAIR + u * G, G), :] for u in range(2)]
                yg = [k.x3[:, :, bass.ds(t * PAIR + u * G, G)].rearrange("p c b -> p b c") for u in range(2)]

                def rows(v):
                    return v[:].rearrange("p (j d) -> p j d", j=1).broadcast_to([128, G, 128])

                s["x"].wait(dve, t, 0)
                for u in range(2):
                    for j in range(G):
                        b = t * PAIR + u * G + j
                        dve.tensor_scalar(xt[:, u, j, :], k.X[:, bass.ds(b, 1), :], k.mean1[:, bass.ds(b, 1)],
                                          k.rstd1[:, bass.ds(b, 1)], ALU.subtract,
                                          ALU.mult).then_inc(s["xt"].sem, 1)
                for u in range(2):
                    s[f"fo_in{u}"].wait(dve, t, 16)
                    dve.tensor_tensor(z[:, u], yg[u], fo[:, u, :, 0:128], ALU.mult).then_inc(s["zs"].sem, 1)
                    s["zs"].wait(dve, t, u + 1)
                    dve.tensor_tensor(z[:, u], z[:, u], fo[:, u, :, 128:256], ALU.add).then_inc(s["zh"].sem, 1)
                    s["zh"].wait(dve, t, u + 1)
                    s["xt"].wait(dve, t, G * (u + 1))
                    dve.tensor_tensor(z[:, u], z[:, u], xt[:, u], ALU.add).then_inc(s["z"].sem, 1)
                s["z"].wait(dve, t, 2)
                norm_stats(dve, nm1, s1, t, lambda u, j: z[:, u, j, :])
                for u in range(2):
                    norm_apply(dve, nm1, s1, t, u, lambda u, j: z[:, u, j, :], xn)
                for u in range(2):
                    s["mlp_ps"].wait(dve, t, u + 1)
                    dve.tensor_tensor(z[:, u].rearrange("p j d -> p (j d)"), z[:, u].rearrange("p j d -> p (j d)"),
                                      ps[:, 4 * u + 1, :], ALU.add).then_inc(s["zm"].sem, 1)
                    s["zm"].wait(dve, t, u + 1)
                    dve.tensor_tensor(z[:, u], z[:, u], rows(k.b2_1), ALU.add).then_inc(s["zb"].sem, 1)
                s["zb"].wait(dve, t, 2)
                norm_stats(dve, nm2, s2, t, lambda u, j: z[:, u, j, :])
                for u in range(2):
                    norm_apply(dve, nm2, s2, t, u, lambda u, j: z[:, u, j, :], xt)
                for u in range(2):
                    s2["xn"].wait(dve, t, G * (u + 1))
                    dve.tensor_tensor(xt[:, u], xt[:, u], rows(k.gout1), ALU.mult).then_inc(s["og"].sem, 1)
                    s["og"].wait(dve, t, u + 1)
                    dve.tensor_tensor(xt[:, u], xt[:, u], rows(k.bout1), ALU.add).then_inc(s["ob"].sem, 1)
                    s["ob"].wait(dve, t, u + 1)
                    dve.tensor_tensor(xg[u], xg[u], xt[:, u], ALU.add).then_inc(s["x"].sem, 1)


def stage_adapters(nc, w, ps, k):
    R = 64
    NB_ = 2 * G
    with ExitStack() as ctx:
        def tmp(name, shape, dt=F32):
            return ctx.enter_context(nc.sbuf_tensor("e_" + name, shape, dt))

        nm = Norm(lambda n, s: ctx.enter_context(nc.sbuf_tensor(n, s, F32)), "e")
        hx = tmp("hx", [128, 2, G, 514])
        xn = hx[:, :, :, 129:257]
        xnT, sx = tmp("xnT", [128, 2, W]), tmp("sx", [128, NB_])
        loss = tmp("loss", [128, 2, NB_])
        junk = tmp("junk", [128, 2, 257])
        gain, best = tmp("gain", [NB_, 8]), tmp("best", [NB_, 8])
        at, atf = tmp("at", [NB_, 8], U32), tmp("atf", [NB_, 1])
        pick = tmp("pick", [1, NB_], I32)
        a, aT = tmp("a", [128, 2, G, R]), tmp("aT", [R + 1, 2, W])
        s = signals(nc, k, "e", **NORM, xnT_ps=2, xnT=2, sx=2, h_ps=2, hb=NB_, h=NB_, gram_ps=NB_, loss=2 * NB_,
                    sum_ps=1, gain=1, best=1, at=1, atf=1, pick_ps=1, pick=1, a_ps=2, a=2, aT_ps=2, aT=2,
                    out_ps=2, x=2)
        ones = ctx.enter_context(OneTime(nc, "e_"))("ones")
        block = ctx.enter_context(nc.Block())

        @block.gpsimd
        def _(pool):
            pool.memset(hx[:, :, :, 128:129], 1.0).then_inc(ones, 1)
            pool.wait_ge(ones, 1)
            pool.memset(aT[R:R + 1], 1.0).then_inc(ones, 1)
            pool.wait_ge(ones, 2)
            with pool.Fori(0, TURNS) as t:
                norm_rstd(pool, nm, s, t, k.half[:])

        @block.tensor
        def _(pe):
            pe.wait_ge(ones, 2)
            with pe.Fori(0, TURNS) as t:
                for u in range(2):
                    s["x"].wait(pe, t, 0)
                    transpose_tokens(pe, s, t, u, xn, ps[:, 4 * u, :], k.ident[:])
                for u in range(2):
                    s["xnT"].wait(pe, t, u + 1)
                    for j in range(G):
                        m = pe.matmul(ps[:, 4 * u + 1 + j // 2, 256 * (j % 2):256 * (j % 2) + 256],
                                      xnT[:, u, j * S:j * S + S], k.wd1[:].rearrange("p e h -> p (e h)"),
                                      start=True, stop=True)
                    m.then_inc(s["h_ps"].sem, 1)
                for u in range(2):
                    s["hb"].wait(pe, t, G * (u + 1))
                    for j in range(G):
                        s["h"].wait(pe, t, G * u + j + 1)
                        if j >= 2:
                            s["loss"].wait(pe, t, 2 * (G * u + j - 1))
                        for q in range(2):
                            m = pe.matmul(ps[:, 4 * u + ((3, 0), (1, 2))[j % 2][q], 0:257],
                                          hx[:, u, j, 257 * q:257 * q + 128],
                                          hx[:, u, j, 128 * q:128 * q + 257], start=True, stop=True)
                        m.then_inc(s["gram_ps"].sem, 1)
                s["loss"].wait(pe, t, 2 * NB_)
                s["sx"].wait(pe, t, 2)
                pe.matmul(ps[0:NB_, 0, 0:8], loss[:, 0, :], k.indic[:, 0, :], start=True, stop=False)
                pe.matmul(ps[0:NB_, 0, 0:8], loss[:, 1, :], k.indic[:, 1, :], start=False, stop=False)
                pe.matmul(ps[0:NB_, 0, 0:8], sx[:], k.bd2T[:], start=False, stop=False)
                pe.matmul(ps[0:NB_, 0, 0:8], k.ones[:, 0:NB_], k.bd2q[:], start=False,
                          stop=True).then_inc(s["sum_ps"].sem, 1)
                s["atf"].wait_apart(pe, t, 1)
                pe.transpose(ps[0:1, 1, 0:NB_], atf[:], k.ident[0:NB_, 0:NB_]).then_inc(s["pick_ps"].sem, 1)
                s["pick"].wait_apart(pe, t, 1)
                chosen = [pe.value_load(pick[0:1, i:i + 1], min_val=0, max_val=7) for i in range(NB_)]
                for u in range(2):
                    for j in range(G):
                        e = chosen[G * u + j]
                        o = ps[:, 4 * u + 2, R * j:R * j + R]
                        pe.matmul(o, xnT[:, u, j * S:j * S + S],
                                  k.wdown[:, bass.ds(e, 1), :].rearrange("p e r -> p (e r)"), start=True, stop=False)
                        m = pe.matmul(o, k.ones[0:1, :], k.bdown[:, bass.ds(e, 1), :].rearrange("p e r -> p (e r)"),
                                      start=False, stop=True)
                    m.then_inc(s["a_ps"].sem, 1)
                for u in range(2):
                    s["a"].wait_apart(pe, t, u + 1)
                    for j in range(G):
                        m = pe.transpose(ps[0:R, 4 * u + 3, j * S:j * S + S], a[:, u, j, :], k.ident[:])
                    m.then_inc(s["aT_ps"].sem, 1)
                for u in range(2):
                    s["aT"].wait(pe, t, u + 1)
                    for j in range(G):
                        e = chosen[G * u + j]
                        o = ps[:, 4 * u + 2, j * S:j * S + S]
                        pe.matmul(o, xnT[:, u, j * S:j * S + S], k.wbase[:], start=True, stop=False)
                        m = pe.matmul(o, aT[:, u, j * S:j * S + S],
                                      k.wup[:, bass.ds(e, 1), :].rearrange("p e r -> p (e r)"), start=False, stop=True)
                    m.then_inc(s["out_ps"].sem, 1)

        @block.scalar
        def _(act):
            with act.Fori(0, TURNS) as t:
                for u in range(2):
                    s["xnT_ps"].wait(act, t, u + 1)
                    act.activation(xnT[:, u], ps[:, 4 * u, :], ACT.Identity).then_inc(s["xnT"].sem, 1)
                for u in range(2):
                    for j in range(G):
                        s["hb"].wait(act, t, G * u + j + 1)
                        h = hx[:, u, j, :].rearrange("p (q n) -> p q n", q=2)[:, :, 0:128]
                        act.activation(h, h, ACT.Relu).then_inc(s["h"].sem, 1)
                for u in range(2):
                    s["a_ps"].wait(act, t, u + 1)
                    act.activation(a[:, u].rearrange("p j r -> p (j r)"), ps[:, 4 * u + 2, 0:G * R],
                                   ACT.Relu).then_inc(s["a"].sem, 1)
                for u in range(2):
                    s["aT_ps"].wait(act, t, u + 1)
                    act.activation(aT[0:R, u], ps[0:R, 4 * u + 3, :], ACT.Identity).then_inc(s["aT"].sem, 1)

        @block.vector
        def _(dve):
            dve.wait_ge(ones, 2)
            with dve.Fori(0, TURNS) as t:
                xj = [[k.X[:, bass.ds(t * PAIR + u * G + j, 1), :] for j in range(G)] for u in range(2)]
                norm_stats(dve, nm, s, t, lambda u, j: xj[u][j])
                for u in range(2):
                    norm_apply(dve, nm, s, t, u, lambda u, j: xj[u][j], xn)
                for u in range(2):
                    s["h_ps"].wait(dve, t, u + 1)
                    for j in range(G):
                        h = hx[:, u, j, :].rearrange("p (q n) -> p q n", q=2)[:, :, 0:128]
                        dve.tensor_tensor(h, ps[:, 4 * u + 1 + j // 2, 256 * (j % 2):256 * (j % 2) + 256]
                                          .rearrange("p (q n) -> p q n", q=2),
                                          k.bd1[:].rearrange("p (q n) -> p q n", q=2),
                                          ALU.add).then_inc(s["hb"].sem, 1)
                for u in range(2):
                    s["xnT"].wait(dve, t, u + 1)
                    dve.tensor_reduce(sx[:, G * u:G * u + G], xnT[:, u].rearrange("p (j t) -> p j t", j=G),
                                      AX.X, ALU.add).then_inc(s["sx"].sem, 1)
                for u in range(2):
                    for j in range(G):
                        i = G * u + j
                        s["gram_ps"].wait(dve, t, i + 1)
                        if i:
                            s["loss"].wait(dve, t, 2 * i)
                        for q in range(2):
                            dve.scalar_tensor_tensor(out=junk[:, q, :], in0=ps[:, 4 * u + ((3, 0), (1, 2))[j % 2][q], 0:257],
                                                     scalar=1.0, in1=k.dcoef[:, q, :], op0=ALU.mult, op1=ALU.mult,
                                                     accum_out=loss[:, q, i:i + 1]).then_inc(s["loss"].sem, 1)
                s["sum_ps"].wait(dve, t, 1)
                dve.tensor_scalar(gain[:], ps[0:NB_, 0, 0:8], -1.0, None, ALU.mult).then_inc(s["gain"].sem, 1)
                s["gain"].wait_apart(dve, t, 1)
                dve.max(best[:], gain[:]).then_inc(s["best"].sem, 1)
                s["best"].wait_apart(dve, t, 1)
                dve.max_index(at[:], best[:], gain[:]).then_inc(s["at"].sem, 1)
                s["at"].wait(dve, t, 1)
                dve.tensor_copy(atf[:], at[:, 0:1]).then_inc(s["atf"].sem, 1)
                s["pick_ps"].wait(dve, t, 1)
                dve.tensor_copy(pick[:], ps[0:1, 1, 0:NB_]).then_inc(s["pick"].sem, 1)
                for u in range(2):
                    s["out_ps"].wait(dve, t, u + 1)
                    xg = k.X[:, bass.ds(t * PAIR + u * G, G), :]
                    dve.scalar_tensor_tensor(out=xg, in0=ps[:, 4 * u + 2, :].rearrange("p (j d) -> p j d", j=G),
                                             scalar=k.tg[:, 5:6], in1=xg, op0=ALU.mult,
                                             op1=ALU.add).then_inc(s["x"].sem, 1)


def stage_attention16(nc, w, ps, k):
    H, DH = 16, 8
    SCALE = DH ** -0.5
    NB_ = 2 * G
    with ExitStack() as ctx:
        def tmp(name, shape, dt=F32):
            return ctx.enter_context(nc.sbuf_tensor("g_" + name, shape, dt))

        nm = Norm(lambda n, s: ctx.enter_context(nc.sbuf_tensor(n, s, F32)), "g")
        xn, xnT, ct = tmp("xn", [128, 2, G, 128]), tmp("xnT", [128, 2, W]), tmp("ct", [C, 2, W])
        qT, kT = tmp("qT", [128, 2, 4, W]), tmp("kT", [128, 2, 4, W])
        v = tmp("v", [128, 2, G, H, DH + 1])
        top = tmp("top", [128, 2, H])
        p, pT = tmp("p", [128, 2, H, 128]), tmp("pT", [128, 2, H, 128])
        rsum, o, oT = tmp("rsum", [128, 2, H]), tmp("o", [128, 2, 128]), tmp("oT", [128, 2, 128])
        bo, bv = tmp("bo", [128, 128]), tmp("bv", [128, W])
        s = signals(nc, k, "g", **NORM, ct0=16, ct1=16, xnT_ps=2, xnT=2, q_ps=2, q=8, k_ps=2, kT=8, v_ps=2, v=2,
                    sc_ps=NB_, top=NB_, sub=NB_, p=NB_, pT_ps=NB_, pT=2 * NB_, av_ps=NB_, rsum=NB_, o=NB_,
                    oT_ps=NB_, oT=NB_, out_ps=NB_, x=NB_, xb=NB_)
        once = ctx.enter_context(OneTime(nc, "g_"))
        ones, bo_done = once("ones"), once("bo")
        block = ctx.enter_context(nc.Block())

        @block.sync
        def _(sp):
            with sp.Fori(0, TURNS) as t:
                for u in range(2):
                    s["v_ps"].wait(sp, t, 0)
                    s["k_ps"].wait(sp, t, 0)
                    sp.dma_start(ct[:, u], k.cT[:, bass.ds(t * 2 * W + u * W, W)]).then_inc(s[f"ct{u}"].sem, 16)

        @block.gpsimd
        def _(pool):
            pool.memset(v[:, :, :, :, DH:DH + 1], 1.0).then_inc(ones, 1)
            pool.wait_ge(ones, 1)
            with pool.Fori(0, TURNS) as t:
                norm_rstd(pool, nm, s, t, k.half[:])

        @block.tensor
        def _(pe):
            pe.wait_ge(ones, 1)
            with pe.Fori(0, TURNS) as t:
                for u in range(2):
                    s["xb"].wait(pe, t, 0)
                    s["x"].wait(pe, t, 0)
                    s[f"ct{u}"].wait(pe, t, 16)
                    for b in range(4):
                        m = pe.matmul(ps[:, 4 * u + b, :], k.wk2p[:, b, :], ct[:, u], start=True, stop=True)
                    m.then_inc(s["k_ps"].sem, 1)
                for u in range(2):
                    s["kT"].wait(pe, t, 4 * (u + 1))
                    for j in range(G):
                        m = pe.matmul(ps[:, 4 * u + 1, j * S:j * S + S], ct[:, u, j * S:j * S + S], k.wv2[:],
                                      start=True, stop=True)
                    m.then_inc(s["v_ps"].sem, 1)
                    transpose_tokens(pe, s, t, u, xn, ps[:, 4 * u, :], k.ident[:])
                for u in range(2):
                    s["xnT"].wait(pe, t, u + 1)
                    s["v"].wait(pe, t, u + 1)
                    for b in range(4):
                        m = pe.matmul(ps[:, 4 * u + b, :], k.wq2p[:, b, :], xnT[:, u], start=True, stop=True)
                    m.then_inc(s["q_ps"].sem, 1)
                for stage in range(NB_ + 1):
                    if stage < NB_:
                        i = stage
                        j, u = i // 2, i % 2
                        if j == 0:
                            s["q"].wait(pe, t, 4 * (u + 1))
                        else:
                            s["x"].wait(pe, t, i - 1)
                        for b in range(4):
                            for r in range(4):
                                m = pe.matmul(ps[:, 4 * u + r, 128 * b:128 * b + 128],
                                              qT[32 * r:32 * r + DH, u, b, j * S:j * S + S],
                                              kT[32 * r:32 * r + DH, u, b, j * S:j * S + S],
                                              start=True, stop=True, tile_position=(32 * r, 0))
                        m.then_inc(s["sc_ps"].sem, 1)
                    if stage >= 1:
                        i = stage - 1
                        j, u = i // 2, i % 2
                        s["p"].wait(pe, t, i + 1)
                        for h in range(H):
                            m = pe.transpose(ps[:, 4 * u + h // 4, 128 * (h % 4):128 * (h % 4) + 128], p[:, u, h, :],
                                             k.ident[:])
                        m.then_inc(s["pT_ps"].sem, 1)
                        s["pT"].wait(pe, t, 2 * (i + 1))
                        for h in range(H):
                            m = pe.matmul(ps[:, 4 * u, 9 * h:9 * h + 9], pT[:, u, 4 * (h % 4) + h // 4, :],
                                          v[:, u, j, h, :], start=True, stop=True)
                        m.then_inc(s["av_ps"].sem, 1)
                        s["o"].wait(pe, t, i + 1)
                        pe.transpose(ps[:, 4 * u + 1, 0:128], o[:, u], k.ident[:]).then_inc(s["oT_ps"].sem, 1)
                        s["oT"].wait(pe, t, i + 1)
                        pe.matmul(ps[:, 4 * u + 2, 0:128], oT[:, u], k.wo2[:], start=True,
                                  stop=True).then_inc(s["out_ps"].sem, 1)

        @block.scalar
        def _(act):
            with act.Fori(0, TURNS) as t:
                for u in range(2):
                    s["k_ps"].wait(act, t, u + 1)
                    for b in range(4):
                        act.activation(kT[:, u, b, :], ps[:, 4 * u + b, :], ACT.Identity,
                                       bias=k.bk2[:, b:b + 1]).then_inc(s["kT"].sem, 1)
                for u in range(2):
                    s["xnT_ps"].wait(act, t, u + 1)
                    act.activation(xnT[:, u], ps[:, 4 * u, :], ACT.Identity).then_inc(s["xnT"].sem, 1)
                for u in range(2):
                    s["q_ps"].wait(act, t, u + 1)
                    for b in range(4):
                        act.activation(qT[:, u, b, :], ps[:, 4 * u + b, :], ACT.Identity,
                                       bias=k.bq2[:, b:b + 1]).then_inc(s["q"].sem, 1)
                for i in range(NB_):
                    u = i % 2
                    s["sub"].wait(act, t, i + 1)
                    act.activation(p[:, u], p[:, u], ACT.Exp, scale=SCALE).then_inc(s["p"].sem, 1)
                    s["pT_ps"].wait(act, t, i + 1)
                    act.activation(pT[:, u, 0:8, :], ps[:, 4 * u:4 * u + 2, :].rearrange("p a (b c) -> p (a b) c", b=4),
                                   ACT.Identity).then_inc(s["pT"].sem, 1)
                    s["oT_ps"].wait(act, t, i + 1)
                    act.activation(oT[:, u], ps[:, 4 * u + 1, 0:128], ACT.Identity).then_inc(s["oT"].sem, 1)

        @block.vector
        def _(dve):
            dve.tensor_scalar(bo[:], k.bo2[:], k.tg[:, 2:3], None, ALU.mult).then_inc(bo_done, 1)
            dve.tensor_copy(bv[:].rearrange("p (j n) -> p j n", j=G), k.bv2[:].rearrange("p (j n) -> p j n", j=1)
                            .broadcast_to([128, G, 128])).then_inc(bo_done, 1)
            dve.wait_ge(bo_done, 2)
            dve.wait_ge(ones, 1)
            with dve.Fori(0, TURNS) as t:
                xj = [[k.X[:, bass.ds(t * PAIR + u * G + j, 1), :] for j in range(G)] for u in range(2)]
                norm_stats(dve, nm, s, t, lambda u, j: xj[u][j])
                for u in range(2):
                    norm_apply(dve, nm, s, t, u, lambda u, j: xj[u][j], xn)
                for u in range(2):
                    s["v_ps"].wait(dve, t, u + 1)
                    dve.tensor_tensor(v[:, u, :, :, 0:DH].rearrange("p j h d -> p (j h) d"),
                                      ps[:, 4 * u + 1, :].rearrange("p (n d) -> p n d", d=DH),
                                      bv[:].rearrange("p (n d) -> p n d", d=DH),
                                      ALU.add).then_inc(s["v"].sem, 1)
                for i in range(NB_ + 1):
                    if i < NB_:
                        u = i % 2
                        sc = ps[:, 4 * u:4 * u + 4, :].rearrange("p a (b c) -> p (a b) c", b=4)
                        s["sc_ps"].wait(dve, t, i + 1)
                        dve.tensor_reduce(top[:, u, :], sc, AX.X, ALU.max).then_inc(s["top"].sem, 1)
                        s["top"].wait(dve, t, i + 1)
                        dve.tensor_tensor(p[:, u], sc, top[:, u, :].rearrange("p (h o) -> p h o", o=1)
                                          .broadcast_to([128, H, 128]), ALU.subtract).then_inc(s["sub"].sem, 1)
                    if i >= 1:
                        n = i - 1
                        j, u = n // 2, n % 2
                        s["pT_ps"].wait(dve, t, n + 1)
                        dve.tensor_copy(pT[:, u, 8:16, :].rearrange("p (a b) c -> p a (b c)", a=2),
                                        ps[:, 4 * u + 2:4 * u + 4, :]).then_inc(s["pT"].sem, 1)
                        s["av_ps"].wait(dve, t, n + 1)
                        av = ps[:, 4 * u, 0:9 * H].rearrange("p (h d) -> p h d", d=9)
                        dve.reciprocal(rsum[:, u, :], av[:, :, DH]).then_inc(s["rsum"].sem, 1)
                        s["rsum"].wait(dve, t, n + 1)
                        dve.tensor_tensor(o[:, u].rearrange("p (h d) -> p h d", h=H), av[:, :, 0:DH],
                                          rsum[:, u, :].rearrange("p (h o) -> p h o", o=1)
                                          .broadcast_to([128, H, DH]), ALU.mult).then_inc(s["o"].sem, 1)
                        s["out_ps"].wait(dve, t, n + 1)
                        x_ = k.X[:, bass.ds(t * PAIR + u * G + j, 1), :].rearrange("p o d -> p (o d)")
                        dve.scalar_tensor_tensor(out=x_, in0=ps[:, 4 * u + 2, 0:128], scalar=k.tg[:, 2:3], in1=x_,
                                                 op0=ALU.mult, op1=ALU.add).then_inc(s["x"].sem, 1)
                        s["x"].wait(dve, t, n + 1)
                        dve.tensor_tensor(x_, x_, bo[:], ALU.add).then_inc(s["xb"].sem, 1)


def stage_fp8(nc, w, ps, k):
    with ExitStack() as ctx:
        k.amax = ctx.enter_context(nc.sbuf_tensor("h_amax", [128, 2], F32))
        k.scale = ctx.enter_context(nc.sbuf_tensor("h_scale", [128, 2], F32))
        k.unscale = ctx.enter_context(nc.sbuf_tensor("h_unscale", [128, 1], F32))
        k.wqT = ctx.enter_context(nc.sbuf_tensor("h_wqT", [128, 128], BF16))
        k.identb = ctx.enter_context(nc.sbuf_tensor("h_identb", [128, 128], BF16))
        k.bias8t = ctx.enter_context(nc.sbuf_tensor("h_bias8t", [128, 128], F32))
        norm_all(nc, w, ps, k)
        fp8_scales(nc, w, ps, k)
        fp8_product(nc, w, ps, k)


def norm_all(nc, w, ps, k):
    with ExitStack() as ctx:
        nm = Norm(lambda n, s: ctx.enter_context(nc.sbuf_tensor(n, s, F32)), "h")
        xall = k.x3[:].rearrange("p a b -> p (a b)").rearrange("p (b c) -> p b c", b=B)
        now = ctx.enter_context(nc.sbuf_tensor("h_now", [128, PAIR], F32))
        most = ctx.enter_context(nc.sbuf_tensor("h_most", [128, PAIR], F32))
        s = signals(nc, k, "h", **NORM, now=1, most=1)
        once = ctx.enter_context(OneTime(nc, "h_"))
        zeroed, final = once("zeroed"), once("final")
        block = ctx.enter_context(nc.Block())

        @block.gpsimd
        def _(pool):
            with pool.Fori(0, TURNS) as t:
                norm_rstd(pool, nm, s, t, k.half[:])

        @block.vector
        def _(dve):
            dve.memset(most[:], 0.0).then_inc(zeroed, 1)
            dve.wait_ge(zeroed, 1)
            with dve.Fori(0, TURNS) as t:
                xj = [[k.X[:, bass.ds(t * PAIR + u * G + j, 1), :] for j in range(G)] for u in range(2)]
                norm_stats(dve, nm, s, t, lambda u, j: xj[u][j])
                s["rstd"].wait(dve, t, 1)
                s["mean"].wait(dve, t, 1)
                for u in range(2):
                    for j in range(G):
                        dve.tensor_scalar(xall[:, bass.ds(t * PAIR + u * G + j, 1), :], xj[u][j],
                                          nm.mean[:, u, j:j + 1], nm.rstd[:, u, j:j + 1], ALU.subtract,
                                          ALU.mult).then_inc(s["xn"].sem, 1)
                s["most"].wait(dve, t, 0)
                s["xn"].wait_apart(dve, t, 2 * G)
                dve.tensor_reduce(now[:], xall[:, bass.ds(t * PAIR, PAIR), :], AX.X, ALU.max,
                                  apply_absolute_value=True).then_inc(s["now"].sem, 1)
                s["now"].wait(dve, t, 1)
                dve.tensor_tensor(most[:], most[:], now[:], ALU.max).then_inc(s["most"].sem, 1)
            s["most"].wait(dve, TURNS - 1, 1)
            dve.tensor_reduce(k.amax[:, 0:1], most[:], AX.X, ALU.max).then_inc(final, 1)
            dve.tensor_reduce(k.amax[:, 1:2], k.wq8[:], AX.X, ALU.max, apply_absolute_value=True).then_inc(final, 1)


E4M3 = dict(top=448.0, least=2.0 ** -6, magic=1.5 * 2.0 ** 20, exponent=0x7F800000)


def fp8_scales(nc, w, ps, k):
    with ExitStack() as ctx:
        def tmp(name, shape, dt=F32):
            return ctx.enter_context(nc.sbuf_tensor("i_" + name, shape, dt))

        row, inv = tmp("row", [1, 2]), tmp("inv", [128, 2])
        q, mag, wq = tmp("q", [128, 128]), tmp("mag", [128, 128]), tmp("wq", [128, 128], BF16)
        once = ctx.enter_context(OneTime(nc, "i_"))
        chain, amax_T, rows, amax_b, wq_done, wT = (once(n) for n in (
            "chain", "amax_T", "rows", "amax_b", "wq_done", "wT"))
        block = ctx.enter_context(nc.Block())

        @block.tensor
        def _(pe):
            for i in range(2):
                m = pe.transpose(ps[0:1, 0, 128 * i:128 * i + 128], k.amax[:, i:i + 1], k.ident[:])
            m.then_inc(amax_T, 1)
            pe.wait_ge(rows, 1)
            pe.matmul(ps[:, 1, 0:2], k.ones[0:1, :], row[:], start=True, stop=True).then_inc(amax_b, 1)
            pe.wait_ge(wq_done, 1)
            pe.transpose(ps[:, 2, 0:64].bitcast(BF16), wq[:], k.identb[:]).then_inc(wT, 1)

        @block.vector
        def _(dve):
            n = [0]

            def link(ins):
                n[0] += 1
                ins.then_inc(chain, 1)
                dve.wait_ge(chain, n[0])

            dve.wait_ge(amax_T, 1)
            dve.tensor_reduce(row[:], ps[0:1, 0, 0:256].rearrange("p (a b) -> p a b", a=2), AX.X,
                              ALU.max).then_inc(rows, 1)
            link(dve.tensor_copy(k.identb[:], k.ident[:]))
            dve.tensor_scalar(k.bias8t[:], k.bias8[:], k.tg[:, 6:7], None, ALU.mult)
            dve.wait_ge(amax_b, 1)
            link(dve.tensor_scalar(k.scale[:], ps[:, 1, 0:2], 1e-12, None, ALU.max))
            link(dve.reciprocal(inv[:], k.scale[:]))
            link(dve.tensor_scalar(k.scale[:], inv[:], E4M3["top"], None, ALU.mult))
            link(dve.reciprocal(inv[:], k.scale[:]))
            link(dve.tensor_tensor(k.unscale[:], inv[:, 0:1], inv[:, 1:2], ALU.mult))
            link(dve.tensor_tensor(k.unscale[:], k.tg[:, 6:7], k.unscale[:], ALU.mult))
            link(dve.tensor_scalar(q[:], k.wq8[:], k.scale[:, 1:2], None, ALU.mult))
            link(dve.tensor_scalar(mag[:].bitcast(I32), q[:].bitcast(I32), E4M3["exponent"], None, ALU.bitwise_and))
            link(dve.tensor_scalar(mag[:], mag[:], E4M3["least"], E4M3["magic"], ALU.max, ALU.mult))
            link(dve.tensor_tensor(q[:], q[:], mag[:], ALU.add))
            dve.tensor_tensor(wq[:], q[:], mag[:], ALU.subtract).then_inc(wq_done, 1)
            dve.wait_ge(wT, 1)
            dve.tensor_copy(k.wqT[:], ps[:, 2, 0:64].bitcast(BF16))


def fp8_product(nc, w, ps, k):
    with ExitStack() as ctx:
        def tmp(name, shape, dt=F32):
            return ctx.enter_context(nc.sbuf_tensor("j_" + name, shape, dt))

        xall = k.x3[:].rearrange("p a b -> p (a b)").rearrange("p (b c) -> p b c", b=B)
        q, mag = tmp("q", [128, 2, W]), tmp("mag", [128, 2, W])
        xq, xqT = tmp("xq", [128, 2, W], BF16), tmp("xqT", [128, 2, W], BF16)
        s = signals(nc, k, "j", q=2, exponent=2, magic=2, sum=2, xq=2, xqT_ps=2, xqT=2, out_ps=2, x=2, xb=2)
        block = ctx.enter_context(nc.Block())

        @block.tensor
        def _(pe):
            with pe.Fori(0, TURNS) as t:
                for u in range(2):
                    s["xq"].wait(pe, t, u + 1)
                    s["xqT"].wait(pe, t, 0)
                    for j in range(G):
                        m = pe.transpose(ps[:, 4 * u, 64 * j:64 * j + 64].bitcast(BF16), xq[:, u, j * S:j * S + S],
                                         k.identb[:])
                    m.then_inc(s["xqT_ps"].sem, 1)
                for u in range(2):
                    s["xqT"].wait(pe, t, u + 1)
                    s["x"].wait(pe, t, 0)
                    for j in range(G):
                        m = pe.matmul(ps[:, 4 * u + 1, j * S:j * S + S], xqT[:, u, j * S:j * S + S], k.wqT[:],
                                      start=True, stop=True)
                    m.then_inc(s["out_ps"].sem, 1)

        @block.scalar
        def _(act):
            with act.Fori(0, TURNS) as t:
                for u in range(2):
                    s["xqT_ps"].wait(act, t, u + 1)
                    s["out_ps"].wait(act, t, 0)
                    act.activation(xqT[:, u], ps[:, 4 * u, 0:256].bitcast(BF16), ACT.Identity).then_inc(s["xqT"].sem, 1)

        @block.vector
        def _(dve):
            with dve.Fori(0, TURNS) as t:
                for u in range(2):
                    s["xqT_ps"].wait(dve, t, 0)
                    s["xq"].wait(dve, t, 0)
                    dve.tensor_scalar(q[:, u].rearrange("p (j c) -> p j c", j=G),
                                      xall[:, bass.ds(t * PAIR + u * G, G), :], k.scale[:, 0:1], None,
                                      ALU.mult).then_inc(s["q"].sem, 1)
                for u in range(2):
                    s["q"].wait(dve, t, u + 1)
                    dve.tensor_scalar(mag[:, u].bitcast(I32), q[:, u].bitcast(I32), E4M3["exponent"], None,
                                      ALU.bitwise_and).then_inc(s["exponent"].sem, 1)
                for u in range(2):
                    s["exponent"].wait(dve, t, u + 1)
                    dve.tensor_scalar(mag[:, u], mag[:, u], E4M3["least"], E4M3["magic"], ALU.max,
                                      ALU.mult).then_inc(s["magic"].sem, 1)
                for u in range(2):
                    s["magic"].wait(dve, t, u + 1)
                    dve.tensor_tensor(q[:, u], q[:, u], mag[:, u], ALU.add).then_inc(s["sum"].sem, 1)
                for u in range(2):
                    s["sum"].wait(dve, t, u + 1)
                    dve.tensor_tensor(xq[:, u], q[:, u], mag[:, u], ALU.subtract).then_inc(s["xq"].sem, 1)
                for u in range(2):
                    s["out_ps"].wait(dve, t, u + 1)
                    xg = k.X[:, bass.ds(t * PAIR + u * G, G), :]
                    dve.scalar_tensor_tensor(out=xg, in0=ps[:, 4 * u + 1, :].rearrange("p (j d) -> p j d", j=G),
                                             scalar=k.unscale[:, 0:1], in1=xg, op0=ALU.mult,
                                             op1=ALU.add).then_inc(s["x"].sem, 1)
                for u in range(2):
                    s["x"].wait(dve, t, u + 1)
                    xg = k.X[:, bass.ds(t * PAIR + u * G, G), :]
                    dve.tensor_tensor(xg, xg, k.bias8t[:].rearrange("p (j d) -> p j d", j=1)
                                      .broadcast_to([128, G, 128]), ALU.add).then_inc(s["xb"].sem, 1)


def stage_attention8(nc, w, ps, k):
    H, DH = 8, 64
    SCALE = DH ** -0.5
    NB_ = 2 * G
    with ExitStack() as ctx:
        def tmp(name, shape, dt=F32):
            return ctx.enter_context(nc.sbuf_tensor("l_" + name, shape, dt))

        nm = Norm(lambda n, s: ctx.enter_context(nc.sbuf_tensor(n, s, F32)), "l")
        xn, xnT, ct = tmp("xn", [128, 2, G, 128]), tmp("xnT", [128, 2, W]), tmp("ct", [C, 2, W])
        qT, kT = tmp("qT", [128, 2, 4, W]), tmp("kT", [128, 2, 4, W])
        v = tmp("v", [128, 2, H * DH])
        shift, total = tmp("shift", [128, 2, H]), tmp("total", [128, 2, H])
        top = tmp("top", [128, 2, H])
        p, pT = tmp("p", [128, 2, H, 128]), tmp("pT", [128, 2, H, 128])
        o, oT = tmp("o", [128, 2, H * DH]), tmp("oT", [128, 2, 4, 128])
        bo = tmp("bo", [128, 128])
        s = signals(nc, k, "l", **NORM, ct0=16, ct1=16, xnT_ps=2, xnT=2, q_ps=2, q=8, k_ps=2, kT=8,
                    sc_ps=NB_, top=NB_, shift=NB_, p=NB_ * H, v_ps=NB_, v=NB_, pT_ps=NB_, pT=2 * NB_, av_ps=NB_,
                    rsum=NB_, o=NB_, oT_ps=NB_, oT=NB_, out_ps=NB_, x=NB_, xb=NB_)
        bo_done = ctx.enter_context(OneTime(nc, "l_"))("bo")
        block = ctx.enter_context(nc.Block())

        @block.sync
        def _(sp):
            with sp.Fori(0, TURNS) as t:
                for u in range(2):
                    s["v_ps"].wait(sp, t, 0)
                    sp.dma_start(ct[:, u], k.cT[:, bass.ds(t * 2 * W + u * W, W)]).then_inc(s[f"ct{u}"].sem, 16)

        @block.gpsimd
        def _(pool):
            with pool.Fori(0, TURNS) as t:
                norm_rstd(pool, nm, s, t, k.half[:])

        @block.tensor
        def _(pe):
            with pe.Fori(0, TURNS) as t:
                for u in range(2):
                    s["xb"].wait(pe, t, 0)
                    s[f"ct{u}"].wait(pe, t, 16)
                    for b in range(4):
                        m = pe.matmul(ps[:, 4 * u + b, :], k.wk3[:, 128 * b:128 * b + 128], ct[:, u], start=True,
                                      stop=True)
                    m.then_inc(s["k_ps"].sem, 1)
                for u in range(2):
                    s["kT"].wait(pe, t, 4 * (u + 1))
                    transpose_tokens(pe, s, t, u, xn, ps[:, 4 * u, :], k.ident[:])
                for u in range(2):
                    s["xnT"].wait(pe, t, u + 1)
                    for b in range(4):
                        m = pe.matmul(ps[:, 4 * u + b, :], k.wq3[:, 128 * b:128 * b + 128], xnT[:, u], start=True,
                                      stop=True)
                    m.then_inc(s["q_ps"].sem, 1)
                for stage in range(NB_ + 1):
                    if stage < NB_:
                        i = stage
                        j, u = i // 2, i % 2
                        if j == 0:
                            s["q"].wait(pe, t, 4 * (u + 1))
                        else:
                            s["x"].wait(pe, t, i - 1)
                        for h in range(H):
                            r = DH * (h % 2)
                            m = pe.matmul(ps[:, 4 * u + h % 2, 128 * (h // 2):128 * (h // 2) + 128],
                                          qT[r:r + DH, u, h // 2, j * S:j * S + S],
                                          kT[r:r + DH, u, h // 2, j * S:j * S + S], start=True, stop=True,
                                          tile_position=(r, 0))
                        m.then_inc(s["sc_ps"].sem, 1)
                        pe.matmul(ps[:, 4 * u + 2, :], ct[:, u, j * S:j * S + S], k.wv3[:], start=True,
                                  stop=True).then_inc(s["v_ps"].sem, 1)
                    if stage >= 1:
                        i = stage - 1
                        j, u = i // 2, i % 2
                        s["p"].wait(pe, t, H * (i + 1))
                        s["v"].wait(pe, t, i + 1)
                        for n in range(H):
                            m = pe.transpose(ps[:, 4 * u + 2 + n // 4, 128 * (n % 4):128 * (n % 4) + 128], p[:, u, n, :],
                                             k.ident[:])
                        m.then_inc(s["pT_ps"].sem, 1)
                        s["pT"].wait(pe, t, 2 * (i + 1))
                        for h in range(H):
                            n = 4 * (h % 2) + h // 2
                            m = pe.matmul(ps[:, 4 * u, DH * h:DH * h + DH], pT[:, u, n, :], v[:, u, DH * h:DH * h + DH],
                                          start=True, stop=True)
                        m.then_inc(s["av_ps"].sem, 1)
                        s["o"].wait(pe, t, i + 1)
                        for b in range(4):
                            m = pe.transpose(ps[:, 4 * u + 1, 128 * b:128 * b + 128], o[:, u, 128 * b:128 * b + 128],
                                             k.ident[:])
                        m.then_inc(s["oT_ps"].sem, 1)
                        s["oT"].wait(pe, t, i + 1)
                        for b in range(4):
                            m = pe.matmul(ps[:, 4 * u + 3, 0:128], oT[:, u, b, :], k.wo3[:, b, :], start=b == 0,
                                          stop=b == 3)
                        m.then_inc(s["out_ps"].sem, 1)

        @block.scalar
        def _(act):
            with act.Fori(0, TURNS) as t:
                for u in range(2):
                    s["k_ps"].wait(act, t, u + 1)
                    for b in range(4):
                        act.activation(kT[:, u, b, :], ps[:, 4 * u + b, :], ACT.Identity).then_inc(s["kT"].sem, 1)
                for u in range(2):
                    s["xnT_ps"].wait(act, t, u + 1)
                    act.activation(xnT[:, u], ps[:, 4 * u, :], ACT.Identity).then_inc(s["xnT"].sem, 1)
                for u in range(2):
                    s["q_ps"].wait(act, t, u + 1)
                    for b in range(4):
                        act.activation(qT[:, u, b, :], ps[:, 4 * u + b, :], ACT.Identity).then_inc(s["q"].sem, 1)
                for i in range(NB_):
                    u = i % 2
                    s["shift"].wait(act, t, i + 1)
                    for n in range(H):
                        act.activation(p[:, u, n, :], ps[:, 4 * u + n // 4, 128 * (n % 4):128 * (n % 4) + 128], ACT.Exp,
                                       bias=shift[:, u, n:n + 1], scale=SCALE,
                                       accum_out=total[:, u, n:n + 1]).then_inc(s["p"].sem, 1)
                    s["pT_ps"].wait(act, t, i + 1)
                    act.activation(pT[:, u, 0:4, :].rearrange("p a b -> p (a b)"), ps[:, 4 * u + 2, :],
                                   ACT.Identity).then_inc(s["pT"].sem, 1)
                    s["oT_ps"].wait(act, t, i + 1)
                    act.activation(oT[:, u].rearrange("p a b -> p (a b)"), ps[:, 4 * u + 1, :],
                                   ACT.Identity).then_inc(s["oT"].sem, 1)

        @block.vector
        def _(dve):
            dve.tensor_scalar(bo[:], k.bo3[:], k.tg[:, 3:4], None, ALU.mult).then_inc(bo_done, 1)
            dve.wait_ge(bo_done, 1)
            with dve.Fori(0, TURNS) as t:
                xj = [[k.X[:, bass.ds(t * PAIR + u * G + j, 1), :] for j in range(G)] for u in range(2)]
                norm_stats(dve, nm, s, t, lambda u, j: xj[u][j])
                for u in range(2):
                    norm_apply(dve, nm, s, t, u, lambda u, j: xj[u][j], xn)
                for i in range(NB_ + 1):
                    if i < NB_:
                        u = i % 2
                        s["sc_ps"].wait(dve, t, i + 1)
                        dve.tensor_reduce(top[:, u, :], ps[:, 4 * u:4 * u + 2, :].rearrange("p a (b c) -> p (a b) c", b=4),
                                          AX.X, ALU.max).then_inc(s["top"].sem, 1)
                        s["top"].wait(dve, t, i + 1)
                        dve.tensor_scalar(shift[:, u, :], top[:, u, :], -SCALE, None,
                                          ALU.mult).then_inc(s["shift"].sem, 1)
                        s["v_ps"].wait(dve, t, i + 1)
                        dve.tensor_copy(v[:, u], ps[:, 4 * u + 2, :]).then_inc(s["v"].sem, 1)
                    if i >= 1:
                        n = i - 1
                        j, u = n // 2, n % 2
                        s["pT_ps"].wait(dve, t, n + 1)
                        dve.tensor_copy(pT[:, u, 4:8, :].rearrange("p a b -> p (a b)"),
                                        ps[:, 4 * u + 3, :]).then_inc(s["pT"].sem, 1)
                        s["p"].wait(dve, t, H * (n + 1))
                        dve.reciprocal(total[:, u, :], total[:, u, :]).then_inc(s["rsum"].sem, 1)
                        s["rsum"].wait(dve, t, n + 1)
                        s["av_ps"].wait(dve, t, n + 1)
                        dve.tensor_tensor(o[:, u].rearrange("p (b a d) -> p a b d", a=2, d=DH),
                                          ps[:, 4 * u, :].rearrange("p (b a d) -> p a b d", a=2, d=DH),
                                          total[:, u, :].rearrange("p (a b o) -> p a b o", a=2, o=1)
                                          .broadcast_to([128, 2, 4, DH]), ALU.mult).then_inc(s["o"].sem, 1)
                        s["out_ps"].wait(dve, t, n + 1)
                        x_ = k.X[:, bass.ds(t * PAIR + u * G + j, 1), :].rearrange("p o d -> p (o d)")
                        dve.scalar_tensor_tensor(out=x_, in0=ps[:, 4 * u + 3, 0:128], scalar=k.tg[:, 3:4], in1=x_,
                                                 op0=ALU.mult, op1=ALU.add).then_inc(s["x"].sem, 1)
                        s["x"].wait(dve, t, n + 1)
                        dve.tensor_tensor(x_, x_, bo[:], ALU.add).then_inc(s["xb"].sem, 1)


def stage_moe(nc, w, ps, k):
    E, TEMP, TINY = 8, 5.0, 1e-9
    with ExitStack() as ctx:
        def tmp(name, shape, dt=F32):
            return ctx.enter_context(nc.sbuf_tensor("m_" + name, shape, dt))

        nm = Norm(lambda n, s: ctx.enter_context(nc.sbuf_tensor(n, s, F32)), "m")
        xn, xnT = tmp("xn", [128, 2, G, 128]), tmp("xnT", [128, 2, W])
        lg, pr, top = tmp("lg", [128, 2, G, E]), tmp("pr", [128, 2, G, E]), tmp("top", [128, 2, G, 8])
        big, tot = tmp("big", [128, 2, G]), tmp("tot", [128, 2, G])
        at, atf = tmp("at", [128, 2, G, 8], U32), tmp("atf", [128, 2, G, 2])
        hit, gt = tmp("hit", [128, 2, G, 2, E]), tmp("gt", [128, 2, G, E])
        gtT = tmp("gtT", [E, 2, W])
        hid = tmp("hid", [128, 2, 2, W])
        s = signals(nc, k, "m", **NORM, xnT_ps=2, xnT=2, lg_ps=2, lg=2, big=2, less=2, ex=2, tot=2, rtot=2,
                    pr=2, top=2 * G, at=2 * G, atf=2, pair=2, rpair=4, two=2, hit=4, whit=4, gt=2, gT_ps=2, gT=2,
                    hid_ps=4 * E, hid=4 * E, out_ps=2 * E, x=2 * G * E, b_ps=2, xb=2)
        block = ctx.enter_context(nc.Block())

        @block.gpsimd
        def _(pool):
            with pool.Fori(0, TURNS) as t:
                norm_rstd(pool, nm, s, t, k.half[:])

        @block.tensor
        def _(pe):
            with pe.Fori(0, TURNS) as t:
                for u in range(2):
                    s["xb"].wait(pe, t, 0)
                    transpose_tokens(pe, s, t, u, xn, ps[:, 4 * u, :], k.ident[:])
                for u in range(2):
                    s["xnT"].wait(pe, t, u + 1)
                    for j in range(G):
                        m = pe.matmul(ps[:, 4 * u + 3, E * j:E * j + E], xnT[:, u, j * S:j * S + S], k.wg3[:],
                                      start=True, stop=True)
                    m.then_inc(s["lg_ps"].sem, 1)
                s["lg"].wait(pe, t, 2)
                for n in range(2 * E + 2):
                    if n < 2 * E:
                        e, u = n // 2, n % 2
                        for q in range(2):
                            if e:
                                s["hid"].wait(pe, t, 4 * (e - 1) + 2 * u + q + 1)
                            pe.matmul(ps[:, 4 * u + q, :], k.w1_3[:, e, 128 * q:128 * q + 128], xnT[:, u], start=True,
                                      stop=True).then_inc(s["hid_ps"].sem, 1)
                    if n >= 2:
                        e, u = (n - 2) // 2, n % 2
                        s["hid"].wait(pe, t, 4 * e + 2 * u + 2)
                        if e >= 2:
                            s["x"].wait(pe, t, G * (2 * (e - 2) + u + 1))
                        for j in range(G):
                            for q in range(2):
                                m = pe.matmul(ps[:, 4 * u + 2 + e % 2, j * S:j * S + S], hid[:, u, q, j * S:j * S + S],
                                              k.w2_3[:, e, q, :], start=q == 0, stop=q == 1)
                        m.then_inc(s["out_ps"].sem, 1)
                for u in range(2):
                    s["gt"].wait(pe, t, u + 1)
                    for j in range(G):
                        m = pe.transpose(ps[0:E, 4 * u, j * S:j * S + S], gt[:, u, j, :], k.ident[:])
                    m.then_inc(s["gT_ps"].sem, 1)
                for u in range(2):
                    s["gT"].wait(pe, t, u + 1)
                    for j in range(G):
                        m = pe.matmul(ps[:, 4 * u + 1, j * S:j * S + S], gtT[:, u, j * S:j * S + S], k.b2_3[:],
                                      start=True, stop=True)
                    m.then_inc(s["b_ps"].sem, 1)

        @block.scalar
        def _(act):
            with act.Fori(0, TURNS) as t:
                for u in range(2):
                    s["xnT_ps"].wait(act, t, u + 1)
                    act.activation(xnT[:, u], ps[:, 4 * u, :], ACT.Identity).then_inc(s["xnT"].sem, 1)
                for u in range(2):
                    s["less"].wait(act, t, u + 1)
                    act.activation(pr[:, u], lg[:, u], ACT.Exp, scale=1.0 / TEMP).then_inc(s["ex"].sem, 1)
                for n in range(2 * E):
                    e, u = n // 2, n % 2
                    for q in range(2):
                        s["hid_ps"].wait(act, t, 2 * n + q + 1)
                        if e:
                            s["out_ps"].wait(act, t, n - 1)
                        act.activation(hid[:, u, q, :], ps[:, 4 * u + q, :], ACT.Gelu,
                                       bias=k.b1_3[:, 2 * e + q:2 * e + q + 1]).then_inc(s["hid"].sem, 1)
                for u in range(2):
                    s["gT_ps"].wait(act, t, u + 1)
                    act.activation(gtT[:, u], ps[0:E, 4 * u, :], ACT.Identity).then_inc(s["gT"].sem, 1)

        @block.vector
        def _(dve):
            with dve.Fori(0, TURNS) as t:
                xj = [[k.X[:, bass.ds(t * PAIR + u * G + j, 1), :] for j in range(G)] for u in range(2)]
                norm_stats(dve, nm, s, t, lambda u, j: xj[u][j])
                for u in range(2):
                    norm_apply(dve, nm, s, t, u, lambda u, j: xj[u][j], xn)

                def each(ap):
                    return ap.rearrange("p (j o) -> p j o", o=1).broadcast_to([128, G, E])

                for u in range(2):
                    s["lg_ps"].wait(dve, t, u + 1)
                    dve.tensor_tensor(lg[:, u], ps[:, 4 * u + 3, 0:E * G].rearrange("p (j e) -> p j e", e=E),
                                      k.bg3[:].rearrange("p (j e) -> p j e", j=1).broadcast_to([128, G, E]),
                                      ALU.add).then_inc(s["lg"].sem, 1)
                    s["lg"].wait(dve, t, u + 1)
                    dve.tensor_reduce(big[:, u], lg[:, u], AX.X, ALU.max).then_inc(s["big"].sem, 1)
                    s["big"].wait(dve, t, u + 1)
                    dve.tensor_tensor(lg[:, u], lg[:, u], each(big[:, u]), ALU.subtract).then_inc(s["less"].sem, 1)
                for u in range(2):
                    s["ex"].wait(dve, t, u + 1)
                    dve.tensor_reduce(tot[:, u], pr[:, u], AX.X, ALU.add).then_inc(s["tot"].sem, 1)
                    s["tot"].wait(dve, t, u + 1)
                    dve.reciprocal(tot[:, u], tot[:, u]).then_inc(s["rtot"].sem, 1)
                    s["rtot"].wait(dve, t, u + 1)
                    dve.tensor_tensor(pr[:, u], pr[:, u], each(tot[:, u]), ALU.mult).then_inc(s["pr"].sem, 1)
                    s["pr"].wait_apart(dve, t, u + 1)
                    for j in range(G):
                        dve.max(top[:, u, j, :], pr[:, u, j, :]).then_inc(s["top"].sem, 1)
                    s["top"].wait_apart(dve, t, G * (u + 1))
                    for j in range(G):
                        dve.max_index(at[:, u, j, :], top[:, u, j, :], pr[:, u, j, :]).then_inc(s["at"].sem, 1)
                    dve.tensor_tensor(tot[:, u], top[:, u, :, 0], top[:, u, :, 1], ALU.add).then_inc(s["pair"].sem, 1)
                    s["pair"].wait(dve, t, u + 1)
                    dve.tensor_scalar(tot[:, u], tot[:, u], TINY, None, ALU.add).then_inc(s["rpair"].sem, 1)
                    s["rpair"].wait(dve, t, 2 * u + 1)
                    dve.reciprocal(tot[:, u], tot[:, u]).then_inc(s["rpair"].sem, 1)
                    s["rpair"].wait(dve, t, 2 * u + 2)
                    dve.scalar_tensor_tensor(out=top[:, u, :, 0:2], in0=top[:, u, :, 0:2], scalar=k.tg[:, 7:8],
                                             in1=tot[:, u].rearrange("p (j o) -> p j o", o=1).broadcast_to([128, G, 2]),
                                             op0=ALU.mult, op1=ALU.mult).then_inc(s["two"].sem, 1)
                    s["at"].wait(dve, t, G * (u + 1))
                    dve.tensor_copy(atf[:, u], at[:, u, :, 0:2]).then_inc(s["atf"].sem, 1)
                    s["atf"].wait(dve, t, u + 1)
                    for i in range(2):
                        dve.tensor_tensor(hit[:, u, :, i, :],
                                          k.iota8[:].rearrange("p (j e) -> p j e", j=1).broadcast_to([128, G, E]),
                                          atf[:, u, :, i:i + 1].broadcast_to([128, G, E]),
                                          ALU.is_equal).then_inc(s["hit"].sem, 1)
                    s["hit"].wait(dve, t, 2 * u + 2)
                    s["two"].wait(dve, t, u + 1)
                    for i in range(2):
                        dve.tensor_tensor(hit[:, u, :, i, :], hit[:, u, :, i, :],
                                          top[:, u, :, i:i + 1].broadcast_to([128, G, E]),
                                          ALU.mult).then_inc(s["whit"].sem, 1)
                    s["whit"].wait(dve, t, 2 * u + 2)
                    dve.tensor_tensor(gt[:, u], hit[:, u, :, 0, :], hit[:, u, :, 1, :], ALU.add).then_inc(s["gt"].sem, 1)
                s["gt"].wait(dve, t, 2)
                for n in range(2 * E):
                    e, u = n // 2, n % 2
                    s["out_ps"].wait(dve, t, n + 1)
                    if e:
                        s["x"].wait(dve, t, G * (n - 1))
                    for j in range(G):
                        dve.scalar_tensor_tensor(out=xj[u][j], in0=ps[:, 4 * u + 2 + e % 2, j * S:j * S + S],
                                                 scalar=gt[:, u, j, e:e + 1], in1=xj[u][j], op0=ALU.mult,
                                                 op1=ALU.add).then_inc(s["x"].sem, 1)
                s["x"].wait(dve, t, 2 * G * E)
                for u in range(2):
                    s["b_ps"].wait(dve, t, u + 1)
                    xg = k.X[:, bass.ds(t * PAIR + u * G, G), :]
                    dve.tensor_tensor(xg, xg, ps[:, 4 * u + 1, :].rearrange("p (j d) -> p j d", j=G),
                                      ALU.add).then_inc(s["xb"].sem, 1)


class Kept:

    def __init__(self, keep):
        self.X = keep("X", [128, B, 128])
        self.cT = keep("cT", [C, B * S])
        self.ident = keep("ident", [128, 128])
        self.flip = keep("flip", [128, 128])
        self.half = keep("half", [128, 8])
        self.ones = keep("ones", [128, 128])
        self.iota8 = keep("iota8", [128, 8])
        self.tg = keep("tg", [128, 8])
        self.tmask = keep("tmask", [128, B])
        self.wv0T = keep("wv0T", [128, 64])
        self.wt0T = keep("wt0T", [C, 64])
        self.bv0 = keep("bv0", [64, 1])
        self.bt0 = keep("bt0", [64, 1])
        self.gateT = keep("gateT", [128, 8])
        self.expT = keep("expT", [128, 8, 128])
        self.wq1 = keep("wq1", [128, 128])
        self.wk1 = keep("wk1", [C, 128])
        self.wfilm = keep("wfilm", [C + 1, 512])
        self.gin1 = keep("gin1", [128, 128])
        self.bin1 = keep("bin1", [128, 128])
        self.w1_1 = keep("w1_1", [128, 512])
        self.w2_1 = keep("w2_1", [128, 4, 128])
        self.b1_1 = keep("b1_1", [128, 4])
        self.gffn1 = keep("gffn1", [128, 1])
        self.bffn1 = keep("bffn1", [128, 1])
        self.b2_1 = keep("b2_1", [128, 128])
        self.gout1 = keep("gout1", [128, 128])
        self.bout1 = keep("bout1", [128, 128])
        self.wbase = keep("wbase", [128, 128])
        self.wd1 = keep("wd1", [128, 8, 32])
        self.bd1 = keep("bd1", [128, 256])
        self.dcoef = keep("dcoef", [128, 2, 257])
        self.indic = keep("indic", [128, 2, 8])
        self.bd2T = keep("bd2T", [128, 8])
        self.bd2q = keep("bd2q", [128, 8])
        self.wdown = keep("wdown", [128, 8, 64])
        self.bdown = keep("bdown", [1, 8, 64])
        self.wup = keep("wup", [65, 8, 128])
        self.wq2p = keep("wq2p", [128, 4, 128])
        self.wk2p = keep("wk2p", [C, 4, 128])
        self.bq2 = keep("bq2", [128, 4])
        self.bk2 = keep("bk2", [128, 4])
        self.wv2 = keep("wv2", [C, 128])
        self.bv2 = keep("bv2", [128, 128])
        self.wo2 = keep("wo2", [128, 128])
        self.bo2 = keep("bo2", [128, 128])
        self.wq8 = keep("wq8", [128, 128])
        self.bias8 = keep("bias8", [128, 128])
        self.wq3 = keep("wq3", [128, 512])
        self.wk3 = keep("wk3", [C, 512])
        self.wv3 = keep("wv3", [C, 512])
        self.wo3 = keep("wo3", [128, 4, 128])
        self.bo3 = keep("bo3", [128, 128])
        self.wg3 = keep("wg3", [128, 8])
        self.bg3 = keep("bg3", [128, 8])
        self.w1_3 = keep("w1_3", [128, 8, 256])
        self.w2_3 = keep("w2_3", [128, 8, 2, 128])
        self.b1_3 = keep("b1_3", [128, 16])
        self.b2_3 = keep("b2_3", [8, 128])
        self.x3 = keep("x3", [128, 128, B])
        self.mean1 = keep("mean1", [128, B])
        self.rstd1 = keep("rstd1", [128, B])


def build(nc, w, out):
    with ExitStack() as ctx:
        def keep(name, shape, dt=F32):
            return ctx.enter_context(nc.sbuf_tensor("k_" + name, shape, dt))

        k = Kept(keep)
        k.ctx, k.sems, k.apart = ctx, {}, ctx.enter_context(nc.semaphore("apart"))
        k.vmask = keep("vmask", [128, B, S], BF16)
        k.kpad = nc.dram_tensor("kpad", (128, 256), F32, kind="Internal").ap()
        ps = ctx.enter_context(nc.psum_tensor("ps", [128, 8, 512], F32))

        k.fo_dram = nc.dram_tensor("fo_dram", (128, B, 256), F32, kind="Internal").ap()
        setup_weights(nc, w, ps, k)
        setup_kernel(nc, w, ps, k)
        stages = [stage_cosine, stage_experts, stage_film, stage_adapters, stage_attention16, stage_fp8,
                  stage_attention8, stage_moe]
        for stage in stages:
            stage(nc, w, ps, k)
        store(nc, k, out)


def store(nc, k, out):
    with ExitStack() as ctx:
        stored = ctx.enter_context(OneTime(nc, ""))("stored")
        block = ctx.enter_context(nc.Block())

        @block.sync
        def _(sp):
            o = out.rearrange("b s d -> s b d")
            for i in range(4):
                sp.dma_start(o[:, 8 * i:8 * i + 8, :], k.X[:, 8 * i:8 * i + 8, :]).then_inc(stored, 16)
            sp.wait_ge(stored, 64)


def kernel(**inputs):
    import numpy as np
    import concourse.bacc as bacc
    from concourse.bass_utils import run_bass_kernel_spmd

    nc = bacc.Bacc("TRN2", target_bir_lowering=False, num_devices=1)
    arrays, aps = {}, {}
    for name, value in inputs.items():
        a = np.ascontiguousarray(value)
        if a.ndim == 0:
            a = a.reshape(1, 1)
        arrays["in_" + name] = a
        aps[name] = nc.dram_tensor("in_" + name, a.shape, mybir.dt.from_np(a.dtype), kind="ExternalInput").ap()
    out = nc.dram_tensor("out", (B, S, D), F32, kind="ExternalOutput").ap()
    build(nc, aps, out)
    r = run_bass_kernel_spmd(nc, [arrays], core_ids=[0])
    return r.results[0]["out"]
```

```python
from contextlib import ExitStack

import concourse.bass as bass
from concourse import mybir

F32 = mybir.dt.float32
BF16 = mybir.dt.bfloat16
U8 = mybir.dt.uint8
I32 = mybir.dt.int32
U32 = mybir.dt.uint32
ACT = mybir.ActivationFunctionType
ALU = mybir.AluOpType
AX = mybir.AxisListType

B, S, D = 32, 128, 128
C = 96
G = 4
W = G * S
PAIR = 2 * G
TURNS = B // PAIR
EPS = 1e-5


class Signal:

    def __init__(self, sem, base, per, apart):
        self.sem, self.base, self.per, self.apart = sem, base, per, apart

    def wait(self, eng, turn, n):
        eng.wait_ge(self.sem, turn * self.per + (self.base + n))

    def wait_apart(self, eng, turn, n):
        self.wait(eng, turn, n)
        eng.sem_inc(self.apart, 1)


def signals(nc, k, phase, turns=TURNS, **per):
    s = {}
    for name, n in per.items():
        if name not in k.sems:
            k.sems[name] = [k.ctx.enter_context(nc.semaphore(name)), 1]
            nc.gpsimd.sem_inc(k.sems[name][0], 1)
        sem, base = k.sems[name]
        s[name] = Signal(sem, base, n, k.apart)
        k.sems[name][1] += n * turns
    return s


class OneTime:

    def __init__(self, nc, prefix):
        self.nc, self.prefix, self.sems = nc, prefix, []

    def __call__(self, name):
        self.sems.append(self.nc.alloc_semaphore(self.prefix + name))
        return self.sems[-1]

    def __enter__(self):
        return self

    def __exit__(self, *_):
        self.nc.clear_and_free_semaphores(self.sems)
        self.nc.all_engine_barrier()


class Norm:

    def __init__(self, sb, name):
        self.stats = sb(name + "_stats", [128, 2 * G, 2, 3])
        self.diff = sb(name + "_diff", [128, 2 * G])
        self.m2 = sb(name + "_m2", [128, 2 * G])
        self.d2 = sb(name + "_d2", [128, 2 * G])
        self.mean = sb(name + "_mean", [128, 2, G])
        self.ve = sb(name + "_ve", [128, 2, G])
        self.rstd = sb(name + "_rstd", [128, 2, G])


def norm_stats(dve, nm, s, t, src):
    for u in range(2):
        for j in range(G):
            dve.bn_stats(nm.stats[:, u * G + j].rearrange("p a b -> p (a b)"), src(u, j)).then_inc(s["stats"].sem, 1)
    s["stats"].wait(dve, t, 2 * G)
    dve.tensor_tensor(nm.diff[:], nm.stats[:, :, 0, 1], nm.stats[:, :, 1, 1], ALU.subtract).then_inc(s["halves"].sem, 1)
    dve.tensor_tensor(nm.m2[:], nm.stats[:, :, 0, 2], nm.stats[:, :, 1, 2], ALU.add).then_inc(s["halves"].sem, 1)
    mean = nm.mean[:].rearrange("p u j -> p (u j)")
    dve.tensor_tensor(mean, nm.stats[:, :, 0, 1], nm.stats[:, :, 1, 1], ALU.add).then_inc(s["halves"].sem, 1)
    s["halves"].wait(dve, t, 3)
    dve.tensor_tensor(nm.d2[:], nm.diff[:], nm.diff[:], ALU.mult).then_inc(s["square"].sem, 1)
    dve.tensor_scalar(mean, mean, 0.5, None, ALU.mult).then_inc(s["mean"].sem, 1)
    s["square"].wait(dve, t, 1)
    dve.scalar_tensor_tensor(out=nm.m2[:], in0=nm.d2[:], scalar=D / 4.0, in1=nm.m2[:], op0=ALU.mult,
                             op1=ALU.add).then_inc(s["square"].sem, 1)
    s["square"].wait(dve, t, 2)
    dve.tensor_scalar(nm.ve[:].rearrange("p u j -> p (u j)"), nm.m2[:], 1.0 / D, EPS, ALU.mult,
                      ALU.add).then_inc(s["ve"].sem, 1)


def norm_rstd(pool, nm, s, t, half):
    s["ve"].wait(pool, t, 1)
    pool.tensor_tensor(nm.rstd[:].rearrange("p u j -> p (u j)"), nm.ve[:].rearrange("p u j -> p (u j)"), half,
                       ALU.pow).then_inc(s["rstd"].sem, 1)


def norm_apply(dve, nm, s, t, u, src, xn):
    s["rstd"].wait(dve, t, 1)
    s["mean"].wait(dve, t, 1)
    for j in range(G):
        dve.tensor_scalar(xn[:, u, j, :], src(u, j), nm.mean[:, u, j:j + 1], nm.rstd[:, u, j:j + 1],
                          ALU.subtract, ALU.mult).then_inc(s["xn"].sem, 1)


NORM = dict(stats=2 * G, halves=3, square=2, mean=1, ve=1, rstd=1, xn=2 * G)


def transpose_tokens(pe, s, t, u, xn, bank, ident):
    s["xn"].wait(pe, t, G * (u + 1))
    for j in range(G):
        m = pe.transpose(bank[:, j * S:(j + 1) * S], xn[:, u, j, :], ident)
    m.then_inc(s["xnT_ps"].sem, 1)


def row_of(ap):
    return ap.rearrange("(a d) -> a d", a=1)


def setup_weights(nc, w, ps, k):
    with ExitStack() as ctx:
        def tmp(name, shape, dt=F32):
            return ctx.enter_context(nc.sbuf_tensor(name, shape, dt))

        sem = ctx.enter_context(OneTime(nc, "setup_"))

        nat_wv0 = tmp("nat_wv0", [64, 128])
        nat_wt0 = tmp("nat_wt0", [64, C])
        nat_gate = tmp("nat_gate", [8, 128])
        nat_exp = tmp("nat_exp", [128, 8, 128])
        nat_wv1 = tmp("nat_wv1", [C, 128])
        wv1T = tmp("wv1T", [128, C])
        wfilm = tmp("wfilm", [128, 2, 256])
        mgate = tmp("mgate", [128, 1])
        graw = tmp("graw", [128, 8])
        vmask8 = tmp("vmask8", [128, B * S], U8)
        tmask8 = tmp("tmask8", [B, S], U8)
        tmaskf = tmp("tmaskf", [B, S])
        rowraw = tmp("rowraw", [128, 2, 128])
        iraw = tmp("iraw", [128, 8], I32)
        nat_bd2 = tmp("nat_bd2", [8, 128])
        nat_wd2 = tmp("nat_wd2", [128, 2, 128])
        wd2T = tmp("wd2T", [128, 2, 128])
        bd2bc = tmp("bd2bc", [128, 2, 128])
        junk = tmp("setup_junk", [128, 128])
        bbase = tmp("bbase", [128, 8, 128])

        loads = sem("loads")
        ident_zero, ident_done = sem("ident_zero"), sem("ident_done")
        pool_done, turned, copied = sem("pool_done"), sem("turned"), sem("copied")
        vec_done, act_done = sem("vec_done"), sem("act_done")
        film_ps, gram_ps = sem("film_ps"), sem("gram_ps")

        block = ctx.enter_context(nc.Block())

        x_dram = w["x"].rearrange("b s d -> s b d")
        plan = [(k.X[:, 8 * i:8 * i + 8, :], x_dram[:, 8 * i:8 * i + 8, :]) for i in range(4)]
        plan += [
            (nat_wv0[:], w["L0_xattn_Wv"]), (nat_wt0[:], w["L0_xattn_Wt"]), (nat_gate[:], w["L0_ffn_gate_w"]),
            (nat_exp[:], w["L0_ffn_expert_w"].rearrange("e d c -> d e c")),
            (nat_wv1[:], w["L1_xattn_Wv"]),
            (wfilm[:, 0, :], w["L1_xattn_W_film_in"]), (wfilm[:, 1, :], w["L1_xattn_W_film_out"]),
            (mgate[:], w["L1_xattn_mod_gate"].broadcast_to([128, 1])),
            (k.wfilm[C:C + 1, 0:256], row_of(w["L1_xattn_b_film_in"])),
            (k.wfilm[C:C + 1, 256:512], row_of(w["L1_xattn_b_film_out"])),
            (graw[:, 0:4], row_of(w["g_xattn"]).broadcast_to([128, 4])),
            (graw[:, 4:8], row_of(w["g_ffn"]).broadcast_to([128, 4])),
            (vmask8[:], w["mask_BxS2_bf1"].rearrange("(a b) s -> a (b s)", a=1).broadcast_to([128, B * S])),
            (tmask8[:], w["mask_BxS_bf1"]),
            (k.bv0[:], w["L0_xattn_bv"].rearrange("(h a) -> h a", a=1)),
            (k.bt0[:], w["L0_xattn_bt"].rearrange("(h a) -> h a", a=1)),
            (k.wq1[:], w["L1_xattn_Wq"]), (k.wk1[:], w["L1_xattn_Wk"]),
            (k.w1_1[:], w["L1_xattn_W1"]), (k.w2_1[:], w["L1_xattn_W2"].rearrange("(q p) d -> p q d", p=128)),
            (k.b1_1[:], w["L1_xattn_b1"].rearrange("(q p) -> p q", p=128)),
            (k.gffn1[:], w["L1_xattn_g_ffn"].rearrange("(p a) -> p a", a=1)),
            (k.bffn1[:], w["L1_xattn_b_ffn"].rearrange("(p a) -> p a", a=1)),
            (k.b2_1[:], row_of(w["L1_xattn_b2"]).broadcast_to([128, 128])),
            (k.gin1[:], row_of(w["L1_xattn_g_norm_in"]).broadcast_to([128, 128])),
            (k.bin1[:], row_of(w["L1_xattn_b_norm_in"]).broadcast_to([128, 128])),
            (rowraw[:, 0, :], row_of(w["L1_xattn_g_norm_out"]).broadcast_to([128, 128])),
            (rowraw[:, 1, :], row_of(w["L1_xattn_b_norm_out"]).broadcast_to([128, 128])),
            (k.wbase[:], w["L1_ffn_W_base"]),
            (k.wd1[:], w["L1_ffn_Wd1"].rearrange("e d h -> d e h")),
            (k.bd1[:], w["L1_ffn_bd1"].rearrange("(a e) h -> a (e h)", a=1).broadcast_to([128, 256])),
            (nat_bd2[:], w["L1_ffn_bd2"]),
            (nat_wd2[:], w["L1_ffn_Wd2"].rearrange("(q e) h d -> (e h) q d", q=2)),
            (k.wdown[:], w["L1_ffn_Wa_down"].rearrange("e d r -> d e r")),
            (k.bdown[:], w["L1_ffn_ba_down"].rearrange("(a e) r -> a e r", a=1)),
            (k.wup[0:64], w["L1_ffn_Wa_up"].rearrange("e r o -> r e o")),
            (k.wup[64:65], w["L1_ffn_ba_up"].rearrange("(a e) o -> a e o", a=1)),
            (bbase[64:65], row_of(w["L1_ffn_b_base"]).rearrange("a (e o) -> a e o", e=1).broadcast_to([1, 8, 128])),
            (k.wq2[:], w["L2_xattn_Wq"]), (k.wk2[:], w["L2_xattn_Wk"]),
            (k.bq2[:], w["L2_xattn_bq"].rearrange("(p a) -> p a", a=1)),
            (k.bk2[:], w["L2_xattn_bk"].rearrange("(p a) -> p a", a=1)),
            (k.wv2[:], w["L2_xattn_Wv"]), (k.wo2[:], w["L2_xattn_Wo"]),
            (k.bv2[:], row_of(w["L2_xattn_bv"]).broadcast_to([128, 128])),
            (k.bo2[:], row_of(w["L2_xattn_bo"]).broadcast_to([128, 128])),
            (k.wq8[:], w["L2_ffn_weight"]),
            (k.bias8[:], row_of(w["L2_ffn_bias"]).broadcast_to([128, 128])),
            (k.wq3[:], w["L3_xattn_Wq"]), (k.wk3[:], w["L3_xattn_Wk"]), (k.wv3[:], w["L3_xattn_Wv"]),
            (k.wo3[:], w["L3_xattn_Wo"].rearrange("(q p) d -> p q d", p=128)),
            (k.bo3[:], row_of(w["L3_xattn_bo"]).broadcast_to([128, 128])),
            (k.wg3[:], w["L3_ffn_Wg"]), (k.bg3[:], row_of(w["L3_ffn_bg"]).broadcast_to([128, 8])),
            (k.w1_3[:], w["L3_ffn_W1"].rearrange("e d h -> d e h")),
            (k.w2_3[:], w["L3_ffn_W2"].rearrange("e (q p) d -> p e q d", p=128)),
            (k.b1_3[:], w["L3_ffn_b1"].rearrange("e (q p) -> p (e q)", p=128)),
            (k.b2_3[:], w["L3_ffn_b2"]),
        ]
        plan += [(bd2bc[32 * (e % 4):32 * (e % 4) + 32, e // 4, :],
                  w["L1_ffn_bd2"][e:e + 1, :].broadcast_to([32, 128])) for e in range(8)]
        n_loads = 16 * len(plan)

        ctx.enter_context(nc.allow_non_contiguous_dma(reason="small vectors, once"))

        @block.sync
        def _(sp):
            for dst, src in plan:
                sp.dma_start(dst, src).then_inc(loads, 16)

        @block.gpsimd
        def _(pool):
            pool.memset(k.ident[:], 0.0).then_inc(ident_zero, 1)
            pool.wait_ge(ident_zero, 1)
            pool.affine_select(out=k.ident[:], in_=k.ident[:], compare_op=ALU.not_equal, fill=1.0, base=0,
                               pattern=[[-1, 128]], channel_multiplier=1).then_inc(ident_done, 1)
            pool.memset(k.flip[:], 0.0).then_inc(ident_zero, 1)
            pool.wait_ge(ident_zero, 2)
            pool.affine_select(out=k.flip[:], in_=k.flip[:], compare_op=ALU.not_equal, fill=1.0, base=-127,
                               pattern=[[1, 128]], channel_multiplier=1)
            pool.memset(k.half[:], -0.5).then_inc(pool_done, 1)
            pool.memset(k.ones[:], 1.0).then_inc(pool_done, 1)
            pool.iota(iraw[:], pattern=[[1, 8]], base=0, channel_multiplier=0).then_inc(pool_done, 1)
            pool.memset(k.indic[:], 0.0).then_inc(pool_done, 1)
            pool.memset(k.dcoef[:], 0.0).then_inc(pool_done, 1)
            pool.wait_ge(pool_done, 5)
            pool.tensor_copy(k.iota8[:], iraw[:]).then_inc(pool_done, 1)
            for e in range(4):
                for q in range(2):
                    pool.wait_ge(pool_done, 6 + 2 * e + q)
                    pool.memset(k.indic[32 * e:32 * e + 32, q, 4 * q + e:4 * q + e + 1], 1.0).then_inc(pool_done, 1)

        turns = [(nat_exp[:, e, :], 128, 128, e // 4, (e % 4) * 128) for e in range(8)]
        turns += [(nat_wv0[:], 64, 128, 2, 0), (nat_wt0[:], 64, C, 2, 64), (nat_gate[:], 8, 128, 2, 128),
                  (nat_wv1[:], C, 128, 2, 136), (nat_bd2[:], 8, 128, 2, 232), (tmaskf[:], B, S, 2, 240)]
        turns += [(nat_wd2[:, q, :], 128, 128, 3, 128 * q) for q in range(2)]

        @block.tensor
        def _(pe):
            pe.wait_ge(loads, n_loads)
            pe.wait_ge(ident_done, 1)
            pe.wait_ge(vec_done, 1)
            for src, rows, cols, bank, col in turns:
                m = pe.transpose(ps[0:cols, bank, col:col + rows], src, k.ident[0:rows, 0:rows])
            m.then_inc(turned, 1)
            pe.wait_ge(copied, 4)
            pe.matmul(ps[0:C, 4, :], wv1T[:], wfilm[:].rearrange("p a n -> p (a n)"),
                      start=True, stop=True).then_inc(film_ps, 1)
            for q in range(2):
                m = pe.matmul(ps[:, 5, 128 * q:128 * q + 128], wd2T[:, q, :], wd2T[:, q, :],
                              start=True, stop=True)
            m.then_inc(gram_ps, 1)

        @block.scalar
        def _(act):
            act.wait_ge(loads, n_loads)
            act.activation(k.tg[:], graw[:], ACT.Tanh).then_inc(act_done, 1)

        @block.vector
        def _(dve):
            dve.wait_ge(loads, n_loads)
            dve.tensor_copy(tmaskf[:], tmask8[:]).then_inc(vec_done, 1)
            dve.tensor_scalar(k.vmask[:].rearrange("p b s -> p (b s)"), vmask8[:], 1.0, 1e30,
                              ALU.subtract, ALU.mult)
            dve.wait_ge(act_done, 1)
            dve.tensor_scalar(k.gout1[:], rowraw[:, 0, :], k.tg[:, 1:2], None, ALU.mult)
            dve.tensor_scalar(k.bout1[:], rowraw[:, 1, :], k.tg[:, 1:2], None, ALU.mult)
            dve.tensor_tensor(k.wup[64:65], k.wup[64:65], bbase[64:65], ALU.add)
            dve.wait_ge(pool_done, 14)
            row = k.wfilm[C:C + 1, :].rearrange("p (a n) -> p a n", a=2)
            dve.tensor_scalar(row, row, mgate[C:C + 1, 0:1], None, ALU.mult).then_inc(vec_done, 1)
            dve.wait_ge(vec_done, 2)
            dve.tensor_scalar(row[:, :, 0:128], row[:, :, 0:128], 1.0, None, ALU.add)
            dve.wait_ge(turned, 1)
            dve.tensor_copy(wv1T[:], ps[:, 2, 136:136 + C]).then_inc(copied, 1)
            dve.tensor_copy(wd2T[:], ps[:, 3, 0:256].rearrange("p (q n) -> p q n", q=2)).then_inc(copied, 1)
            dve.tensor_copy(k.wv0T[:], ps[:, 2, 0:64]).then_inc(copied, 1)
            dve.tensor_copy(k.wt0T[:], ps[0:C, 2, 64:128]).then_inc(copied, 1)
            dve.tensor_copy(k.gateT[:], ps[:, 2, 128:136])
            dve.tensor_scalar(k.bd2T[:], ps[:, 2, 232:240], -2.0, None, ALU.mult).then_inc(vec_done, 1)
            dve.tensor_copy(k.tmask[:], ps[:, 2, 240:240 + B])
            for h in range(2):
                dve.tensor_copy(k.expT[:, 4 * h:4 * h + 4, :],
                                ps[:, h, :].rearrange("p (e d) -> p e d", e=4))
            dve.wait_ge(vec_done, 3)
            dve.scalar_tensor_tensor(out=k.bd2q[:], in0=k.bd2T[:], scalar=S / 4.0, in1=k.bd2T[:], op0=ALU.mult,
                                     op1=ALU.mult)
            dve.wait_ge(gram_ps, 1)
            for q in range(2):
                g0, o0, x0 = ((0, 128, 129), (129, 0, 1))[q]
                for e in range(4):
                    p = slice(32 * e, 32 * e + 32)
                    dve.tensor_copy(k.dcoef[p, q, g0 + 32 * e:g0 + 32 * e + 32],
                                    ps[p, 5, 128 * q + 32 * e:128 * q + 32 * e + 32])
                dve.tensor_scalar(k.dcoef[:, q, x0:x0 + 128], nat_wd2[:, q, :], -2.0, None, ALU.mult)
                dve.scalar_tensor_tensor(out=junk[:], in0=nat_wd2[:, q, :], scalar=2.0, in1=bd2bc[:, q, :],
                                         op0=ALU.mult, op1=ALU.mult,
                                         accum_out=k.dcoef[:, q, o0:o0 + 1]).then_inc(vec_done, 1)
                dve.wait_ge(vec_done, 4 + q)
            dve.wait_ge(film_ps, 1)
            dve.tensor_scalar(k.wfilm[0:C, :], ps[0:C, 4, :], mgate[0:C, 0:1], None, ALU.mult)


def stage_cosine(nc, w, ps, k):
    with ExitStack() as ctx:
        def tmp(name, shape, dt=F32):
            return ctx.enter_context(nc.sbuf_tensor("a_" + name, shape, dt))

        nm = Norm(lambda n, s: ctx.enter_context(nc.sbuf_tensor(n, s, F32)), "a")
        xn, xnT = tmp("xn", [128, 2, G, 128]), tmp("xnT", [128, 2, W])
        cx = tmp("cx", [128, 2, G, C])
        vT, tT = tmp("vT", [64, 2, W]), tmp("tT", [64, 2, W])
        v2, t2 = tmp("v2", [64, 2, W]), tmp("t2", [64, 2, W])
        nv2 = tmp("nv2", [128, 2, G])
        den, prod = tmp("den", [128, 2, W]), tmp("prod", [128, 2, W])
        s = signals(nc, k, "a", **NORM, cx0=16, cx1=16, xnT_ps=2, cT_ps=2, xnT=2, cT=2, vt_ps=4, vt=8, norms=2,
                    nv2=2, den=2 * G, root=2, dots=2, rden=2, prod=2, x=2)
        block = ctx.enter_context(nc.Block())
        c_dram = w["ctx_768"].rearrange("b s c -> s b c")

        @block.sync
        def _(sp):
            with sp.Fori(0, TURNS) as t:
                for u in range(2):
                    s["cT_ps"].wait(sp, t, 0)
                    sp.dma_start(cx[:, u], c_dram[:, bass.ds(t * PAIR + u * G, G), :]).then_inc(s[f"cx{u}"].sem, 16)

        @block.gpsimd
        def _(pool):
            with pool.Fori(0, TURNS) as t:
                norm_rstd(pool, nm, s, t, k.half[:])

        @block.tensor
        def _(pe):
            with pe.Fori(0, TURNS) as t:
                for u in range(2):
                    s[f"cx{u}"].wait(pe, t, 16)
                    s["x"].wait(pe, t, 0)
                    for j in range(G):
                        m = pe.transpose(ps[0:C, 4 * u + 1, j * S:(j + 1) * S], cx[:, u, j, :], k.ident[:])
                    m.then_inc(s["cT_ps"].sem, 1)
                    transpose_tokens(pe, s, t, u, xn, ps[:, 4 * u, :], k.ident[:])
                for u in range(2):
                    s["cT"].wait(pe, t, u + 1)
                    s["xnT"].wait(pe, t, u + 1)
                    pe.matmul(ps[0:64, 4 * u + 2, :], k.wv0T[:], xnT[:, u], start=True,
                              stop=True).then_inc(s["vt_ps"].sem, 1)
                    pe.matmul(ps[0:64, 4 * u + 3, :], k.wt0T[:], k.cT[:, bass.ds(t * 2 * W + u * W, W)],
                              start=True, stop=True).then_inc(s["vt_ps"].sem, 1)
                for u in range(2):
                    s["vt"].wait(pe, t, 4 * (u + 1))
                    pe.matmul(ps[:, 4 * u + 1, :], k.ones[0:64, :], t2[:, u], start=True, stop=True)
                    for j in range(G):
                        m = pe.matmul(ps[:, 4 * u, j:j + 1], v2[:, u, j * S:(j + 1) * S], k.ones[0:64, 0:1],
                                      start=True, stop=True)
                    m.then_inc(s["norms"].sem, 1)
                    for j in range(G):
                        m = pe.matmul(ps[:, 4 * u + 2, j * S:(j + 1) * S], vT[:, u, j * S:(j + 1) * S],
                                      tT[:, u, j * S:(j + 1) * S], start=True, stop=True)
                    m.then_inc(s["dots"].sem, 1)

        @block.scalar
        def _(act):
            with act.Fori(0, TURNS) as t:
                for u in range(2):
                    s["xnT_ps"].wait(act, t, u + 1)
                    act.activation(xnT[:, u], ps[:, 4 * u, :], ACT.Identity).then_inc(s["xnT"].sem, 1)
                for u in range(2):
                    s["vt_ps"].wait(act, t, 2 * u + 2)
                    for dst, func, bank, bias in ((vT, ACT.Identity, 2, k.bv0), (v2, ACT.Square, 2, k.bv0),
                                                  (tT, ACT.Identity, 3, k.bt0), (t2, ACT.Square, 3, k.bt0)):
                        act.activation(dst[:, u], ps[0:64, 4 * u + bank, :], func,
                                       bias=bias[:]).then_inc(s["vt"].sem, 1)
                for u in range(2):
                    s["den"].wait(act, t, G * (u + 1))
                    act.activation(den[:, u], den[:, u], ACT.Sqrt).then_inc(s["root"].sem, 1)

        @block.vector
        def _(dve):
            with dve.Fori(0, TURNS) as t:
                xj = [[k.X[:, bass.ds(t * PAIR + u * G + j, 1), :] for j in range(G)] for u in range(2)]
                norm_stats(dve, nm, s, t, lambda u, j: xj[u][j])
                for u in range(2):
                    norm_apply(dve, nm, s, t, u, lambda u, j: xj[u][j], xn)
                for u in range(2):
                    s["cT_ps"].wait(dve, t, u + 1)
                    dve.tensor_copy(k.cT[:, bass.ds(t * 2 * W + u * W, W)],
                                    ps[0:C, 4 * u + 1, :]).then_inc(s["cT"].sem, 1)
                for u in range(2):
                    s["norms"].wait(dve, t, u + 1)
                    dve.tensor_copy(nv2[:, u], ps[:, 4 * u, 0:G]).then_inc(s["nv2"].sem, 1)
                    s["nv2"].wait(dve, t, u + 1)
                    for j in range(G):
                        dve.tensor_scalar(den[:, u, j * S:(j + 1) * S], ps[:, 4 * u + 1, j * S:(j + 1) * S],
                                          nv2[:, u, j:j + 1], 1e-16, ALU.mult, ALU.max).then_inc(s["den"].sem, 1)
                for u in range(2):
                    s["root"].wait(dve, t, u + 1)
                    dve.reciprocal(den[:, u], den[:, u]).then_inc(s["rden"].sem, 1)
                    s["rden"].wait(dve, t, u + 1)
                    s["dots"].wait(dve, t, u + 1)
                    dve.tensor_tensor(prod[:, u], ps[:, 4 * u + 2, :], den[:, u],
                                      ALU.mult).then_inc(s["prod"].sem, 1)
                    s["prod"].wait(dve, t, u + 1)
                    xg = k.X[:, bass.ds(t * PAIR + u * G, G), :]
                    dve.scalar_tensor_tensor(out=xg, in0=prod[:, u].rearrange("p (j d) -> p j d", j=G),
                                             scalar=k.tg[:, 0:1], in1=xg, op0=ALU.mult,
                                             op1=ALU.add).then_inc(s["x"].sem, 1)


def stage_experts(nc, w, ps, k):
    with ExitStack() as ctx:
        def tmp(name, shape, dt=F32):
            return ctx.enter_context(nc.sbuf_tensor("b_" + name, shape, dt))

        nm = Norm(lambda n, s: ctx.enter_context(nc.sbuf_tensor(n, s, F32)), "b")
        xn, xnT = tmp("xn", [128, 2, G, 128]), tmp("xnT", [128, 2, W])
        lg, top = tmp("lg", [128, 2, G, 8]), tmp("top", [128, 2, G, 8])
        at, atf = tmp("at", [128, 2, G, 8], U32), tmp("atf", [128, 2, G, 2])
        gap, e2, tot = tmp("gap", [128, 2, G]), tmp("e2", [128, 2, G]), tmp("tot", [128, 2, G])
        wt = tmp("wt", [128, 2, G, 2])
        hit, wf = tmp("hit", [128, 2, G, 2, 8]), tmp("wf", [128, 2, G, 8])
        s = signals(nc, k, "b", **NORM, xnT_ps=2, xnT=2, lg_ps=2, lg=2, top=2 * G, at=2 * G, atf=2, gap=2,
                    e2=2, tot=2, rtot=2, w1=2, w2=2, hit=4, whit=4, wf=2, out_ps=2 * G, x=2 * G * 8)
        block = ctx.enter_context(nc.Block())

        @block.gpsimd
        def _(pool):
            with pool.Fori(0, TURNS) as t:
                norm_rstd(pool, nm, s, t, k.half[:])

        @block.tensor
        def _(pe):
            with pe.Fori(0, TURNS) as t:
                for u in range(2):
                    s["x"].wait(pe, t, 0)
                    transpose_tokens(pe, s, t, u, xn, ps[:, 4 * u, :], k.ident[:])
                for u in range(2):
                    s["xnT"].wait(pe, t, u + 1)
                    for j in range(G):
                        m = pe.matmul(ps[:, 4 * u + 1, 8 * j:8 * j + 8], xnT[:, u, j * S:(j + 1) * S],
                                      k.gateT[:], start=True, stop=True)
                    m.then_inc(s["lg_ps"].sem, 1)
                for u in range(2):
                    s["lg"].wait(pe, t, u + 1)
                    for j in range(G):
                        bank = 4 * u + (2, 0)[j % 2]
                        if j >= 2:
                            s["x"].wait(pe, t, 8 * (G * u + j - 1))
                        for h in range(2):
                            m = pe.matmul(ps[:, bank + h, :], xnT[:, u, j * S:(j + 1) * S],
                                          k.expT[:, 4 * h:4 * h + 4, :].rearrange("p e d -> p (e d)"),
                                          start=True, stop=True)
                        m.then_inc(s["out_ps"].sem, 1)

        @block.scalar
        def _(act):
            with act.Fori(0, TURNS) as t:
                for u in range(2):
                    s["xnT_ps"].wait(act, t, u + 1)
                    act.activation(xnT[:, u], ps[:, 4 * u, :], ACT.Identity).then_inc(s["xnT"].sem, 1)
                for u in range(2):
                    s["gap"].wait(act, t, u + 1)
                    act.activation(e2[:, u], gap[:, u], ACT.Exp).then_inc(s["e2"].sem, 1)

        @block.vector
        def _(dve):
            with dve.Fori(0, TURNS) as t:
                xj = [[k.X[:, bass.ds(t * PAIR + u * G + j, 1), :] for j in range(G)] for u in range(2)]
                norm_stats(dve, nm, s, t, lambda u, j: xj[u][j])
                for u in range(2):
                    norm_apply(dve, nm, s, t, u, lambda u, j: xj[u][j], xn)
                for u in range(2):
                    s["lg_ps"].wait(dve, t, u + 1)
                    dve.tensor_copy(lg[:, u].rearrange("p j e -> p (j e)"),
                                    ps[:, 4 * u + 1, 0:8 * G]).then_inc(s["lg"].sem, 1)
                    s["lg"].wait_apart(dve, t, u + 1)
                    for j in range(G):
                        dve.max(top[:, u, j, :], lg[:, u, j, :]).then_inc(s["top"].sem, 1)
                    s["top"].wait_apart(dve, t, G * (u + 1))
                    for j in range(G):
                        dve.max_index(at[:, u, j, :], top[:, u, j, :], lg[:, u, j, :]).then_inc(s["at"].sem, 1)
                    dve.tensor_tensor(gap[:, u], top[:, u, :, 1], top[:, u, :, 0],
                                      ALU.subtract).then_inc(s["gap"].sem, 1)
                for u in range(2):
                    s["at"].wait(dve, t, G * (u + 1))
                    dve.tensor_copy(atf[:, u], at[:, u, :, 0:2]).then_inc(s["atf"].sem, 1)
                    s["e2"].wait(dve, t, u + 1)
                    dve.tensor_scalar(tot[:, u], e2[:, u], 1.0, None, ALU.add).then_inc(s["tot"].sem, 1)
                    s["tot"].wait(dve, t, u + 1)
                    dve.reciprocal(tot[:, u], tot[:, u]).then_inc(s["rtot"].sem, 1)
                    s["rtot"].wait(dve, t, u + 1)
                    dve.tensor_scalar(wt[:, u, :, 0], tot[:, u], k.tg[:, 4:5], None,
                                      ALU.mult).then_inc(s["w1"].sem, 1)
                    s["w1"].wait(dve, t, u + 1)
                    dve.tensor_tensor(wt[:, u, :, 1], wt[:, u, :, 0], e2[:, u],
                                      ALU.mult).then_inc(s["w2"].sem, 1)
                    s["w2"].wait(dve, t, u + 1)
                    s["atf"].wait(dve, t, u + 1)
                    for i in range(2):
                        dve.tensor_tensor(hit[:, u, :, i, :], k.iota8[:].rearrange("p (j e) -> p j e", j=1).broadcast_to([128, G, 8]),
                                          atf[:, u, :, i:i + 1].broadcast_to([128, G, 8]),
                                          ALU.is_equal).then_inc(s["hit"].sem, 1)
                    s["hit"].wait(dve, t, 2 * u + 2)
                    for i in range(2):
                        dve.tensor_tensor(hit[:, u, :, i, :], hit[:, u, :, i, :],
                                          wt[:, u, :, i:i + 1].broadcast_to([128, G, 8]),
                                          ALU.mult).then_inc(s["whit"].sem, 1)
                    s["whit"].wait(dve, t, 2 * u + 2)
                    dve.tensor_tensor(wf[:, u], hit[:, u, :, 0, :], hit[:, u, :, 1, :],
                                      ALU.add).then_inc(s["wf"].sem, 1)
                for u in range(2):
                    s["wf"].wait(dve, t, u + 1)
                    for j in range(G):
                        bank = 4 * u + (2, 0)[j % 2]
                        s["out_ps"].wait(dve, t, G * u + j + 1)
                        for e in range(8):
                            if e:
                                s["x"].wait(dve, t, 8 * (G * u + j) + e)
                            dve.scalar_tensor_tensor(
                                out=xj[u][j], in0=ps[:, bank + e // 4, 128 * (e % 4):128 * (e % 4) + 128],
                                scalar=wf[:, u, j, e:e + 1], in1=xj[u][j], op0=ALU.mult,
                                op1=ALU.add).then_inc(s["x"].sem, 1)


def setup_kernel(nc, w, ps, k):
    N, NA, NB = 64, 8, 16
    M = NA + NB + NA + 1
    PI = 3.14159265358979
    TWO_PI = (6.28125, 1.9340515136718750e-3, 1.2556659146e-6)
    ROUND = 1.5 * 2.0 ** 23
    with ExitStack() as ctx:
        def tmp(name, shape, dt=F32):
            return ctx.enter_context(nc.sbuf_tensor("s4_" + name, shape, dt))

        sem = ctx.enter_context(OneTime(nc, "s4_"))

        nat = tmp("nat", [128, 4, 2, N])
        par = tmp("par", [128, 4, 128])
        ldt, drow = tmp("ldt", [128, 128]), tmp("drow", [1, 128])
        mi, mf = tmp("mi", [128, M], I32), tmp("mf", [128, M])
        ph = tmp("ph", [128, 2])
        sgn = tmp("sgn", [128, 1])
        dta = tmp("dta", [128, 2, 128])
        arg, kk, ex = tmp("arg", [128, 128, M]), tmp("kk", [128, 128, M]), tmp("ex", [128, 128, M])
        tt = kk
        sm = tmp("sm", [128, 12, 128])
        pq, pq2 = tmp("pq", [128, 128, NA]), tmp("pq2", [128, 128, NA])
        k2 = tmp("k2", [NA, 128, NB])
        zero = tmp("zero", [128, 127])
        loads, consts, turned, kps = sem("loads"), sem("consts"), sem("turned"), sem("kps")
        act_dt, vec_arg, act_ex, vec_red, act_sin = (sem(n) for n in ("act_dt", "vec_arg", "act_ex", "vec_red",
                                                                     "act_sin"))
        chain, vec_pq, vec_k2, stored = sem("chain"), sem("vec_pq"), sem("vec_k2"), sem("stored")
        block = ctx.enter_context(nc.Block())

        @block.sync
        def _(sp):
            for i, name in enumerate(("A_re", "A_im", "C_re", "C_im")):
                for h in range(2):
                    sp.dma_start(nat[:, i, h, :], w["L1_xattn_" + name]).then_inc(loads, 16)
            sp.dma_start(ldt[:], row_of(w["L1_xattn_log_dt"]).broadcast_to([128, 128])).then_inc(loads, 16)
            sp.dma_start(drow[:], row_of(w["L1_xattn_D_skip"])).then_inc(loads, 16)
            sp.wait_ge(consts, 9)
            sp.dma_start(k.kpad[:, 0:127], zero[:]).then_inc(stored, 16)
            sp.wait_ge(vec_k2, 1)
            sp.dma_start(k.kpad[:, 127:255].rearrange("d (a b) -> a d b", b=NB), k2[:]).then_inc(stored, 16)
            sp.wait_ge(stored, 32)

        @block.gpsimd
        def _(pool):
            pool.iota(mi[:, 0:8], pattern=[[16, 8]], base=0, channel_multiplier=0).then_inc(consts, 1)
            pool.iota(mi[:, 8:24], pattern=[[1, 16]], base=0, channel_multiplier=0).then_inc(consts, 1)
            pool.iota(mi[:, 24:32], pattern=[[16, 8]], base=0, channel_multiplier=0).then_inc(consts, 1)
            pool.iota(mi[:, 32:33], pattern=[[1, 1]], base=1, channel_multiplier=0).then_inc(consts, 1)
            pool.memset(ph[:], 0.0).then_inc(consts, 1)
            pool.memset(sgn[:], 1.0).then_inc(consts, 1)
            pool.wait_ge(consts, 6)
            pool.memset(ph[0:N, 0:1], PI / 2).then_inc(consts, 1)
            pool.wait_ge(consts, 7)
            pool.memset(ph[N:128, 1:2], PI / 2).then_inc(consts, 1)
            pool.wait_ge(consts, 8)
            pool.memset(zero[:], 0.0).then_inc(consts, 1)
            pool.wait_ge(consts, 9)
            pool.memset(sgn[N:128], -1.0).then_inc(consts, 1)

        @block.tensor
        def _(pe):
            pe.wait_ge(loads, 160)
            for i in range(4):
                m = pe.transpose(ps[:, 0, 128 * i:128 * i + 128], nat[:, i].rearrange("p h n -> p (h n)"), k.ident[:])
            m.then_inc(turned, 1)
            pe.wait_ge(vec_pq, 1)
            for d in range(128):
                m = pe.matmul(ps[0:NA, 1 + d // 32, NB * (d % 32):NB * (d % 32) + NB], pq[:, d, :],
                              tt[:, d, NA:NA + NB], start=True, stop=True)
            m.then_inc(kps, 1)

        @block.scalar
        def _(act):
            act.wait_ge(loads, 160)
            act.activation(ldt[:], ldt[:], ACT.Exp).then_inc(act_dt, 1)
            act.wait_ge(vec_arg, 1)
            act.activation(ex[:], ex[:], ACT.Exp).then_inc(act_ex, 1)
            act.wait_ge(vec_red, 1)
            act.activation(tt[:], arg[:], ACT.Sin).then_inc(act_sin, 1)

        @block.vector
        def _(dve):
            n = [0]

            def link(ins):
                n[0] += 1
                ins.then_inc(chain, 1)
                dve.wait_ge(chain, n[0])

            dve.wait_ge(consts, 10)
            link(dve.tensor_copy(mf[:], mi[:]))
            dve.wait_ge(turned, 1)
            link(dve.tensor_copy(par[:].rearrange("p i d -> p (i d)"), ps[:, 0, :]))
            dve.wait_ge(act_dt, 1)
            for i in range(2):
                link(dve.tensor_tensor(dta[:, i, :], par[:, i, :], ldt[:], ALU.mult))
            mb = mf[:].rearrange("p (o m) -> p o m", o=1).broadcast_to([128, 128, M])

            def per_channel(t):
                return t.rearrange("p (d o) -> p d o", o=1)

            dve.tensor_tensor(ex[:], per_channel(dta[:, 0, :]).broadcast_to([128, 128, M]), mb,
                              ALU.mult).then_inc(vec_arg, 1)
            link(dve.tensor_tensor(arg[:], per_channel(dta[:, 1, :]).broadcast_to([128, 128, M]), mb, ALU.mult))
            for lo, hi, i in ((0, 24, 0), (24, M, 1)):
                a, q = arg[:, :, lo:hi], kk[:, :, lo:hi]
                link(dve.tensor_scalar(q, a, ph[:, i:i + 1], 1 / (2 * PI), ALU.add, ALU.mult))
                link(dve.tensor_scalar(q, q, ROUND, ROUND, ALU.add, ALU.subtract))
            for c in TWO_PI:
                link(dve.scalar_tensor_tensor(out=arg[:], in0=kk[:], scalar=-c, in1=arg[:], op0=ALU.mult,
                                              op1=ALU.add))
            for lo, hi, i in ((0, 24, 0), (24, M, 1)):
                a = arg[:, :, lo:hi]
                link(dve.tensor_scalar(a, a, ph[:, i:i + 1], 3.1415925, ALU.add, ALU.min))
            dve.tensor_scalar(arg[:], arg[:], -3.1415925, None, ALU.max).then_inc(vec_red, 1)
            dve.wait_ge(act_sin, 1)
            dve.wait_ge(act_ex, 1)
            cos, sin = sm[:, 0, :], sm[:, 1, :]
            dve.tensor_copy(sm[0:N, 0, :], tt[0:N, :, NA + 1])
            dve.tensor_copy(sm[N:128, 0, :], tt[N:128, :, M - 1])
            dve.tensor_copy(sm[0:N, 1, :], tt[0:N, :, M - 1])
            link(dve.tensor_copy(sm[N:128, 1, :], tt[N:128, :, NA + 1]))
            link(dve.tensor_tensor(tt[:], tt[:], ex[:], ALU.mult))
            e1 = ex[:, :, M - 1]
            ar, ai, cr, ci = (par[:, i, :] for i in range(4))
            r = [sm[:, i, :] for i in range(12)]

            def tt_(out, a, b, op):
                link(dve.tensor_tensor(out, a, b, op))

            tt_(r[2], cos, e1, ALU.mult)
            link(dve.tensor_scalar(r[2], r[2], 1.0, None, ALU.subtract))
            tt_(r[3], sin, e1, ALU.mult)
            tt_(r[4], cr, r[2], ALU.mult)
            tt_(r[5], ci, r[3], ALU.mult)
            tt_(r[4], r[4], r[5], ALU.subtract)
            tt_(r[5], cr, r[3], ALU.mult)
            tt_(r[6], ci, r[2], ALU.mult)
            tt_(r[5], r[5], r[6], ALU.add)
            tt_(r[6], ar, ar, ALU.mult)
            tt_(r[7], ai, ai, ALU.mult)
            tt_(r[6], r[6], r[7], ALU.add)
            link(dve.reciprocal(r[6], r[6]))
            tt_(r[7], r[4], ar, ALU.mult)
            tt_(r[8], r[5], ai, ALU.mult)
            tt_(r[7], r[7], r[8], ALU.add)
            tt_(r[8], r[5], ar, ALU.mult)
            tt_(r[9], r[4], ai, ALU.mult)
            tt_(r[8], r[8], r[9], ALU.subtract)
            tt_(r[7], r[7], r[6], ALU.mult)
            tt_(r[8], r[8], r[6], ALU.mult)
            link(dve.tensor_scalar(r[7], r[7], sgn[:, 0:1], 2.0, ALU.mult, ALU.mult))
            link(dve.tensor_scalar(r[8], r[8], 2.0, None, ALU.mult))
            tt_(pq[:], tt[:, :, 0:NA], per_channel(r[7]).broadcast_to([128, 128, NA]), ALU.mult)
            tt_(pq2[:], tt[:, :, NA + NB:NA + NB + NA], per_channel(r[8]).broadcast_to([128, 128, NA]), ALU.mult)
            dve.tensor_tensor(pq[:], pq[:], pq2[:], ALU.subtract).then_inc(vec_pq, 1)
            dve.wait_ge(kps, 1)
            for b in range(4):
                link(dve.tensor_copy(k2[:, 32 * b:32 * b + 32, :].rearrange("p d b -> p (d b)"),
                                     ps[0:NA, 1 + b, :]))
            dve.tensor_tensor(k2[0:1, :, 0], k2[0:1, :, 0], drow[:], ALU.add).then_inc(vec_k2, 1)


def stage_film(nc, w, ps, k):
    film_in(nc, w, ps, k)
    convolve(nc, w, ps, k)
    film_out(nc, w, ps, k)


def film_in(nc, w, ps, k):
    H, DH, ROUNDS = 4, 32, 4
    SCALE = DH ** -0.5
    TAKEN = -3e38
    with ExitStack() as ctx:
        def tmp(name, shape, dt=F32):
            return ctx.enter_context(nc.sbuf_tensor("c_" + name, shape, dt))

        nm = Norm(lambda n, s: ctx.enter_context(nc.sbuf_tensor(n, s, F32)), "c")
        xn, xnT = tmp("xn", [128, 2, G, 128]), tmp("xnT", [128, 2, W])
        rstd2 = tmp("rstd2", [128, 2 * G])
        cx = tmp("cx", [128, 2, G, C])
        qT, kT = tmp("qT", [128, 2, W]), tmp("kT", [128, 2, W])
        sc, left = tmp("sc", [128, 2, H, 128]), tmp("left", [128, 2, H, 128])
        first, top = tmp("first", [128, 2, H, 8]), tmp("top", [128, 2, H, 8])
        shift, total = tmp("shift", [128, 2, H]), tmp("total", [128, 2, H])
        ex = tmp("ex", [128, 2, H, 128])
        mean_w = tmp("mean_w", [128, 2, G, 128])
        wT, aT = tmp("wT", [128, 2, W]), tmp("aT", [C + 1, 2, W])
        x2 = tmp("x2", [128, 2, G, 128])
        fo = tmp("fo", [128, 2, G, 512])
        NB_ = 2 * G
        s = signals(nc, k, "c", **NORM, rr=1, vr=1, ve2=1, rstd2=1, kept=2, cx0=16, cx1=16, xnT_ps=2, xnT=2,
                    qk_ps=2, qT=2, kT=2, sc_ps=2, sc=NB_, top=NB_ * H * ROUNDS, left=NB_ * H * ROUNDS,
                    shift=NB_, ex=NB_ * H, keep=NB_ * H, rtot=NB_, share=NB_, mean_sum=NB_ * H, wT_ps=2, wT=2,
                    aT_ps=2, aT=2, film_ps=NB_, x2a=2 * G, x2b=2 * G, x2c=2 * G, x3=2 * G, fo=2 * G,
                    fo_out0=16, fo_out1=16)
        ones = ctx.enter_context(OneTime(nc, "c_"))("ones")
        block = ctx.enter_context(nc.Block())
        c_dram = w["ctx_768"].rearrange("b s c -> s b c")

        @block.sync
        def _(sp):
            with sp.Fori(0, TURNS) as t:
                for u in range(2):
                    s["aT_ps"].wait(sp, t, 0)
                    sp.dma_start(cx[:, u], c_dram[:, bass.ds(t * PAIR + u * G, G), :]).then_inc(s[f"cx{u}"].sem, 16)
                for u in range(2):
                    s["fo"].wait(sp, t, G * (u + 1))
                    sp.dma_start(k.fo_dram[:, bass.ds(t * PAIR + u * G, G), :],
                                 fo[:, u, :, 256:512]).then_inc(s[f"fo_out{u}"].sem, 16)
            for u in range(2):
                s[f"fo_out{u}"].wait(sp, TURNS - 1, 16)

        @block.gpsimd
        def _(pool):
            pool.memset(aT[C:C + 1], 1.0).then_inc(ones, 1)
            pool.wait_ge(ones, 1)
            with pool.Fori(0, TURNS) as t:
                norm_rstd(pool, nm, s, t, k.half[:])
                s["ve2"].wait(pool, t, 1)
                pool.tensor_tensor(rstd2[:], rstd2[:], k.half[:], ALU.pow).then_inc(s["rstd2"].sem, 1)

        @block.tensor
        def _(pe):
            pe.wait_ge(ones, 1)
            with pe.Fori(0, TURNS) as t:
                for u in range(2):
                    s["x3"].wait(pe, t, 0)
                    s["fo"].wait(pe, t, 0)
                    transpose_tokens(pe, s, t, u, xn, ps[:, 4 * u, :], k.ident[:])
                for u in range(2):
                    s["xnT"].wait(pe, t, u + 1)
                    pe.matmul(ps[:, 4 * u + 1, :], k.wq1[:], xnT[:, u], start=True, stop=True)
                    pe.matmul(ps[:, 4 * u + 2, :], k.wk1[:], k.cT[:, bass.ds(t * 2 * W + u * W, W)],
                              start=True, stop=True).then_inc(s["qk_ps"].sem, 1)
                for u in range(2):
                    s["qT"].wait(pe, t, u + 1)
                    s["kT"].wait(pe, t, u + 1)
                    for j in range(G):
                        for h in range(H):
                            r = slice(DH * h, DH * h + DH)
                            m = pe.matmul(ps[:, 4 * u + h, j * S:j * S + S], qT[r, u, j * S:j * S + S],
                                          kT[r, u, j * S:j * S + S], start=True, stop=True,
                                          tile_position=(DH * h, 0))
                    m.then_inc(s["sc_ps"].sem, 1)
                for u in range(2):
                    s["mean_sum"].wait(pe, t, H * (2 * (G - 1) + u + 1))
                    for j in range(G):
                        m = pe.transpose(ps[:, 4 * u + 1, j * S:j * S + S], mean_w[:, u, j, :], k.ident[:])
                    m.then_inc(s["wT_ps"].sem, 1)
                for u in range(2):
                    s["wT"].wait(pe, t, u + 1)
                    s[f"cx{u}"].wait(pe, t, 16)
                    for j in range(G):
                        m = pe.matmul(ps[0:C, 4 * u + 2, j * S:j * S + S], cx[:, u, j, :],
                                      wT[:, u, j * S:j * S + S], start=True, stop=True)
                    m.then_inc(s["aT_ps"].sem, 1)
                for u in range(2):
                    s["aT"].wait(pe, t, u + 1)
                    for j in range(G):
                        if j >= 2:
                            s["fo"].wait(pe, t, G * u + j - 1)
                        pe.matmul(ps[:, 4 * u + (3, 0)[j % 2], :], aT[:, u, j * S:j * S + S], k.wfilm[:],
                                  start=True, stop=True).then_inc(s["film_ps"].sem, 1)

        @block.scalar
        def _(act):
            with act.Fori(0, TURNS) as t:
                for u in range(2):
                    s["xnT_ps"].wait(act, t, u + 1)
                    act.activation(xnT[:, u], ps[:, 4 * u, :], ACT.Identity).then_inc(s["xnT"].sem, 1)
                for u in range(2):
                    s["qk_ps"].wait(act, t, u + 1)
                    act.activation(qT[:, u], ps[:, 4 * u + 1, :], ACT.Identity).then_inc(s["qT"].sem, 1)
                    act.activation(kT[:, u], ps[:, 4 * u + 2, :], ACT.Identity).then_inc(s["kT"].sem, 1)
                for i in range(NB_):
                    u = i % 2
                    s["shift"].wait(act, t, i + 1)
                    for h in range(H):
                        act.activation(ex[:, u, h, :], sc[:, u, h, :], ACT.Exp, bias=shift[:, u, h:h + 1],
                                       scale=SCALE).then_inc(s["ex"].sem, 1)
                for u in range(2):
                    s["wT_ps"].wait(act, t, u + 1)
                    act.activation(wT[:, u], ps[:, 4 * u + 1, :], ACT.Identity).then_inc(s["wT"].sem, 1)
                for u in range(2):
                    s["aT_ps"].wait(act, t, u + 1)
                    act.activation(aT[0:C, u], ps[0:C, 4 * u + 2, :], ACT.Identity).then_inc(s["aT"].sem, 1)
                for u in range(2):
                    s[f"fo_out{u}"].wait(act, t, 0)
                    s["x3"].wait(act, t, 0)
                    for j in range(G):
                        s["film_ps"].wait(act, t, G * u + j + 1)
                        act.activation(fo[:, u, j, :], ps[:, 4 * u + (3, 0)[j % 2], :],
                                       ACT.Identity).then_inc(s["fo"].sem, 1)

        @block.vector
        def _(dve):
            with dve.Fori(0, TURNS) as t:
                xj = [[k.X[:, bass.ds(t * PAIR + u * G + j, 1), :] for j in range(G)] for u in range(2)]
                norm_stats(dve, nm, s, t, lambda u, j: xj[u][j])
                for u in range(2):
                    norm_apply(dve, nm, s, t, u, lambda u, j: xj[u][j], xn)
                rs, ve = nm.rstd[:].rearrange("p u j -> p (u j)"), nm.ve[:].rearrange("p u j -> p (u j)")
                dve.tensor_tensor(rstd2[:], rs, rs, ALU.mult).then_inc(s["rr"].sem, 1)
                s["rr"].wait(dve, t, 1)
                dve.scalar_tensor_tensor(out=rstd2[:], in0=ve, scalar=EPS, in1=rstd2[:], op0=ALU.subtract,
                                         op1=ALU.mult).then_inc(s["vr"].sem, 1)
                s["vr"].wait(dve, t, 1)
                dve.tensor_scalar(rstd2[:], rstd2[:], EPS, None, ALU.add).then_inc(s["ve2"].sem, 1)
                dve.tensor_copy(k.mean1[:, bass.ds(t * PAIR, PAIR)],
                                nm.mean[:].rearrange("p u j -> p (u j)")).then_inc(s["kept"].sem, 1)
                dve.tensor_copy(k.rstd1[:, bass.ds(t * PAIR, PAIR)], rs).then_inc(s["kept"].sem, 1)
                for i in range(NB_):
                    j, u = i // 2, i % 2
                    b = t * PAIR + u * G + j
                    s["sc_ps"].wait(dve, t, u + 1)
                    dve.tensor_tensor(sc[:, u], ps[:, 4 * u:4 * u + H, j * S:j * S + S],
                                      k.vmask[:, bass.ds(b, 1), :].broadcast_to([128, H, 128]),
                                      ALU.add).then_inc(s["sc"].sem, 1)
                    s["sc"].wait_apart(dve, t, i + 1)
                    for r in range(ROUNDS):
                        if r:
                            s["left"].wait_apart(dve, t, H * (ROUNDS * i + r))
                        for h in range(H):
                            dve.max((first if r == 0 else top)[:, u, h, :],
                                    (sc if r == 0 else left)[:, u, h, :]).then_inc(s["top"].sem, 1)
                        s["top"].wait_apart(dve, t, H * (ROUNDS * i + r + 1))
                        if r == 0:
                            dve.tensor_scalar(shift[:, u, :], first[:, u, :, 0], -SCALE, None,
                                              ALU.mult).then_inc(s["shift"].sem, 1)
                        for h in range(H):
                            dve.match_replace(left[:, u, h, :], (first if r == 0 else top)[:, u, h, :],
                                              (sc if r == 0 else left)[:, u, h, :],
                                              TAKEN).then_inc(s["left"].sem, 1)
                    s["left"].wait(dve, t, H * ROUNDS * (i + 1))
                    s["ex"].wait(dve, t, H * (i + 1))
                    for h in range(H):
                        dve.scalar_tensor_tensor(out=ex[:, u, h, :], in0=left[:, u, h, :], scalar=TAKEN * 0.5,
                                                 in1=ex[:, u, h, :], op0=ALU.is_le, op1=ALU.mult,
                                                 accum_out=total[:, u, h:h + 1]).then_inc(s["keep"].sem, 1)
                    s["keep"].wait(dve, t, H * (i + 1))
                    dve.reciprocal(total[:, u, :], total[:, u, :]).then_inc(s["rtot"].sem, 1)
                    s["rtot"].wait(dve, t, i + 1)
                    dve.scalar_tensor_tensor(out=total[:, u, :], in0=total[:, u, :], scalar=1.0 / H,
                                             in1=k.tmask[:, bass.ds(b, 1)].broadcast_to([128, H]),
                                             op0=ALU.mult, op1=ALU.mult).then_inc(s["share"].sem, 1)
                    s["share"].wait(dve, t, i + 1)
                    for h in range(H):
                        if h == 0:
                            m = dve.tensor_scalar(mean_w[:, u, j, :], ex[:, u, h, :], total[:, u, h:h + 1], None,
                                                  ALU.mult)
                        else:
                            s["mean_sum"].wait(dve, t, H * i + h)
                            m = dve.scalar_tensor_tensor(out=mean_w[:, u, j, :], in0=ex[:, u, h, :],
                                                         scalar=total[:, u, h:h + 1], in1=mean_w[:, u, j, :],
                                                         op0=ALU.mult, op1=ALU.add)
                        m.then_inc(s["mean_sum"].sem, 1)
                s["rstd2"].wait(dve, t, 1)
                for u in range(2):
                    for j in range(G):
                        dve.scalar_tensor_tensor(out=x2[:, u, j, :], in0=xn[:, u, j, :],
                                                 scalar=rstd2[:, u * G + j:u * G + j + 1], in1=k.gin1[:],
                                                 op0=ALU.mult, op1=ALU.mult).then_inc(s["x2a"].sem, 1)
                s["x2a"].wait(dve, t, 2 * G)
                for u in range(2):
                    for j in range(G):
                        dve.tensor_tensor(x2[:, u, j, :], x2[:, u, j, :], k.bin1[:],
                                          ALU.add).then_inc(s["x2b"].sem, 1)
                s["x2b"].wait(dve, t, 2 * G)
                for u in range(2):
                    for j in range(G):
                        s["fo"].wait(dve, t, G * u + j + 1)
                        dve.tensor_tensor(x2[:, u, j, :], x2[:, u, j, :], fo[:, u, j, 0:128],
                                          ALU.mult).then_inc(s["x2c"].sem, 1)
                        s["x2c"].wait(dve, t, G * u + j + 1)
                        dve.tensor_tensor(k.x3[:, :, bass.ds(t * PAIR + u * G + j, 1)],
                                          x2[:, u, j, :].rearrange("p (c o) -> p c o", o=1),
                                          fo[:, u, j, 128:256].rearrange("p (c o) -> p c o", o=1),
                                          ALU.add).then_inc(s["x3"].sem, 1)


def convolve(nc, w, ps, k):
    CH = 16
    CHUNKS = D // CH
    with ExitStack() as ctx:
        toep = ctx.enter_context(nc.sbuf_tensor("v_toep", [128, CHUNKS, CH, 128], F32))
        once = ctx.enter_context(OneTime(nc, "v_"))
        toep_in = [once(f"toep_in{i}") for i in range(CHUNKS)]
        flip_ps, flipped, y_ps = once("flip_ps"), once("flipped"), once("y_ps")
        block = ctx.enter_context(nc.Block())

        def chunk(c):
            return k.x3[:, CH * c:CH * c + CH, :].rearrange("p c b -> p (c b)")

        @block.sync
        def _(sp):
            for c in range(CHUNKS):
                src = bass.AP(tensor=k.kpad.tensor, offset=256 * CH * c, ap=[[1, 128], [256, CH], [1, 128]])
                sp.dma_start(toep[:, c], src).then_inc(toep_in[c], 16)

        @block.tensor
        def _(pe):
            for c in range(CHUNKS):
                pe.matmul(ps[:, c, :], k.flip[:], chunk(c), start=True, stop=True).then_inc(flip_ps, 1)
            for c in range(CHUNKS):
                pe.wait_ge(flipped, c + 1)
                pe.wait_ge(toep_in[c], 16)
                for i in range(CH):
                    m = pe.matmul(ps[:, c, B * i:B * i + B], toep[:, c, i, :], k.x3[:, CH * c + i, :],
                                  start=True, stop=True)
                m.then_inc(y_ps, 1)

        @block.scalar
        def _(act):
            for c in range(CHUNKS):
                act.wait_ge(flip_ps, c + 1)
                act.activation(chunk(c), ps[:, c, :], ACT.Identity).then_inc(flipped, 1)

        @block.vector
        def _(dve):
            for c in range(CHUNKS):
                dve.wait_ge(y_ps, c + 1)
                dve.tensor_copy(chunk(c), ps[:, c, :])


def film_out(nc, w, ps, k):
    with ExitStack() as ctx:
        def tmp(name, shape, dt=F32):
            return ctx.enter_context(nc.sbuf_tensor("d_" + name, shape, dt))

        nm1 = Norm(lambda n, s: ctx.enter_context(nc.sbuf_tensor(n, s, F32)), "d1")
        nm2 = Norm(lambda n, s: ctx.enter_context(nc.sbuf_tensor(n, s, F32)), "d2")
        fo = tmp("fo", [128, 2, G, 256])
        z, xt = tmp("z", [128, 2, G, 128]), tmp("xt", [128, 2, G, 128])
        xn, hT = tmp("xn", [128, 2, G, 128]), tmp("hT", [128, 2, W])
        hid = tmp("hid", [128, 2, 4, W])
        s = signals(nc, k, "d", fo_in0=16, fo_in1=16, xt=2 * G, zs=2, zh=2, z=2, xnT_ps=2, hT=2,
                    hid_ps=8, hid=8, mlp_ps=2, zm=2, zb=2, og=2, ob=2, x=2)
        s1 = signals(nc, k, "d1", **NORM)
        s2 = {n[3:]: v for n, v in signals(nc, k, "d2", **{"n2_" + n: v for n, v in NORM.items()}).items()}
        s1["xnT_ps"] = s["xnT_ps"]
        block = ctx.enter_context(nc.Block())

        @block.sync
        def _(sp):
            with sp.Fori(0, TURNS) as t:
                for u in range(2):
                    s["zh"].wait(sp, t, 0)
                    sp.dma_start(fo[:, u], k.fo_dram[:, bass.ds(t * PAIR + u * G, G), :]).then_inc(s[f"fo_in{u}"].sem, 16)

        @block.gpsimd
        def _(pool):
            with pool.Fori(0, TURNS) as t:
                norm_rstd(pool, nm1, s1, t, k.half[:])
                norm_rstd(pool, nm2, s2, t, k.half[:])

        @block.tensor
        def _(pe):
            with pe.Fori(0, TURNS) as t:
                for u in range(2):
                    s["zm"].wait(pe, t, 0)
                    transpose_tokens(pe, s1, t, u, xn, ps[:, 4 * u, :], k.ident[:])
                for u in range(2):
                    s["hT"].wait(pe, t, u + 1)
                    for q in range(4):
                        pe.matmul(ps[:, 4 * u + (q + 1) % 4, :], k.w1_1[:, 128 * q:128 * q + 128], hT[:, u],
                                  start=True, stop=True).then_inc(s["hid_ps"].sem, 1)
                for u in range(2):
                    s["hid"].wait(pe, t, 4 * (u + 1))
                    for j in range(G):
                        for q in range(4):
                            m = pe.matmul(ps[:, 4 * u + 1, j * S:j * S + S], hid[:, u, q, j * S:j * S + S],
                                          k.w2_1[:, q, :], start=q == 0, stop=q == 3)
                    m.then_inc(s["mlp_ps"].sem, 1)

        @block.scalar
        def _(act):
            with act.Fori(0, TURNS) as t:
                for u in range(2):
                    s["xnT_ps"].wait(act, t, u + 1)
                    act.activation(hT[:, u], ps[:, 4 * u, :], ACT.Identity, bias=k.bffn1[:],
                                   scale=k.gffn1[:]).then_inc(s["hT"].sem, 1)
                for u in range(2):
                    for q in range(4):
                        s["hid_ps"].wait(act, t, 4 * u + q + 1)
                        act.activation(hid[:, u, q, :], ps[:, 4 * u + (q + 1) % 4, :], ACT.Gelu,
                                       bias=k.b1_1[:, q:q + 1]).then_inc(s["hid"].sem, 1)

        @block.vector
        def _(dve):
            with dve.Fori(0, TURNS) as t:
                xg = [k.X[:, bass.ds(t * PAIR + u * G, G), :] for u in range(2)]
                yg = [k.x3[:, :, bass.ds(t * PAIR + u * G, G)].rearrange("p c b -> p b c") for u in range(2)]

                def rows(v):
                    return v[:].rearrange("p (j d) -> p j d", j=1).broadcast_to([128, G, 128])

                s["x"].wait(dve, t, 0)
                for u in range(2):
                    for j in range(G):
                        b = t * PAIR + u * G + j
                        dve.tensor_scalar(xt[:, u, j, :], k.X[:, bass.ds(b, 1), :], k.mean1[:, bass.ds(b, 1)],
                                          k.rstd1[:, bass.ds(b, 1)], ALU.subtract,
                                          ALU.mult).then_inc(s["xt"].sem, 1)
                for u in range(2):
                    s[f"fo_in{u}"].wait(dve, t, 16)
                    dve.tensor_tensor(z[:, u], yg[u], fo[:, u, :, 0:128], ALU.mult).then_inc(s["zs"].sem, 1)
                    s["zs"].wait(dve, t, u + 1)
                    dve.tensor_tensor(z[:, u], z[:, u], fo[:, u, :, 128:256], ALU.add).then_inc(s["zh"].sem, 1)
                    s["zh"].wait(dve, t, u + 1)
                    s["xt"].wait(dve, t, G * (u + 1))
                    dve.tensor_tensor(z[:, u], z[:, u], xt[:, u], ALU.add).then_inc(s["z"].sem, 1)
                s["z"].wait(dve, t, 2)
                norm_stats(dve, nm1, s1, t, lambda u, j: z[:, u, j, :])
                for u in range(2):
                    norm_apply(dve, nm1, s1, t, u, lambda u, j: z[:, u, j, :], xn)
                for u in range(2):
                    s["mlp_ps"].wait(dve, t, u + 1)
                    dve.tensor_tensor(z[:, u].rearrange("p j d -> p (j d)"), z[:, u].rearrange("p j d -> p (j d)"),
                                      ps[:, 4 * u + 1, :], ALU.add).then_inc(s["zm"].sem, 1)
                    s["zm"].wait(dve, t, u + 1)
                    dve.tensor_tensor(z[:, u], z[:, u], rows(k.b2_1), ALU.add).then_inc(s["zb"].sem, 1)
                s["zb"].wait(dve, t, 2)
                norm_stats(dve, nm2, s2, t, lambda u, j: z[:, u, j, :])
                for u in range(2):
                    norm_apply(dve, nm2, s2, t, u, lambda u, j: z[:, u, j, :], xt)
                for u in range(2):
                    s2["xn"].wait(dve, t, G * (u + 1))
                    dve.tensor_tensor(xt[:, u], xt[:, u], rows(k.gout1), ALU.mult).then_inc(s["og"].sem, 1)
                    s["og"].wait(dve, t, u + 1)
                    dve.tensor_tensor(xt[:, u], xt[:, u], rows(k.bout1), ALU.add).then_inc(s["ob"].sem, 1)
                    s["ob"].wait(dve, t, u + 1)
                    dve.tensor_tensor(xg[u], xg[u], xt[:, u], ALU.add).then_inc(s["x"].sem, 1)


def stage_adapters(nc, w, ps, k):
    R = 64
    NB_ = 2 * G
    with ExitStack() as ctx:
        def tmp(name, shape, dt=F32):
            return ctx.enter_context(nc.sbuf_tensor("e_" + name, shape, dt))

        nm = Norm(lambda n, s: ctx.enter_context(nc.sbuf_tensor(n, s, F32)), "e")
        hx = tmp("hx", [128, 2, G, 514])
        xn = hx[:, :, :, 129:257]
        xnT, sx = tmp("xnT", [128, 2, W]), tmp("sx", [128, NB_])
        loss = tmp("loss", [128, 2, NB_])
        junk = tmp("junk", [128, 2, 257])
        gain, best = tmp("gain", [NB_, 8]), tmp("best", [NB_, 8])
        at, atf = tmp("at", [NB_, 8], U32), tmp("atf", [NB_, 1])
        pick = tmp("pick", [1, NB_], I32)
        a, aT = tmp("a", [128, 2, G, R]), tmp("aT", [R + 1, 2, W])
        s = signals(nc, k, "e", **NORM, xnT_ps=2, xnT=2, sx=2, h_ps=2, hb=NB_, h=NB_, gram_ps=NB_, loss=2 * NB_,
                    sum_ps=1, gain=1, best=1, at=1, atf=1, pick_ps=1, pick=1, a_ps=2, a=2, aT_ps=2, aT=2,
                    out_ps=2, x=2)
        ones = ctx.enter_context(OneTime(nc, "e_"))("ones")
        block = ctx.enter_context(nc.Block())

        @block.gpsimd
        def _(pool):
            pool.memset(hx[:, :, :, 128:129], 1.0).then_inc(ones, 1)
            pool.wait_ge(ones, 1)
            pool.memset(aT[R:R + 1], 1.0).then_inc(ones, 1)
            pool.wait_ge(ones, 2)
            with pool.Fori(0, TURNS) as t:
                norm_rstd(pool, nm, s, t, k.half[:])

        @block.tensor
        def _(pe):
            pe.wait_ge(ones, 2)
            with pe.Fori(0, TURNS) as t:
                for u in range(2):
                    s["x"].wait(pe, t, 0)
                    transpose_tokens(pe, s, t, u, xn, ps[:, 4 * u, :], k.ident[:])
                for u in range(2):
                    s["xnT"].wait(pe, t, u + 1)
                    for j in range(G):
                        m = pe.matmul(ps[:, 4 * u + 1 + j // 2, 256 * (j % 2):256 * (j % 2) + 256],
                                      xnT[:, u, j * S:j * S + S], k.wd1[:].rearrange("p e h -> p (e h)"),
                                      start=True, stop=True)
                    m.then_inc(s["h_ps"].sem, 1)
                for u in range(2):
                    s["hb"].wait(pe, t, G * (u + 1))
                    for j in range(G):
                        s["h"].wait(pe, t, G * u + j + 1)
                        if j >= 2:
                            s["loss"].wait(pe, t, 2 * (G * u + j - 1))
                        for q in range(2):
                            m = pe.matmul(ps[:, 4 * u + ((3, 0), (1, 2))[j % 2][q], 0:257],
                                          hx[:, u, j, 257 * q:257 * q + 128],
                                          hx[:, u, j, 128 * q:128 * q + 257], start=True, stop=True)
                        m.then_inc(s["gram_ps"].sem, 1)
                s["loss"].wait(pe, t, 2 * NB_)
                s["sx"].wait(pe, t, 2)
                pe.matmul(ps[0:NB_, 0, 0:8], loss[:, 0, :], k.indic[:, 0, :], start=True, stop=False)
                pe.matmul(ps[0:NB_, 0, 0:8], loss[:, 1, :], k.indic[:, 1, :], start=False, stop=False)
                pe.matmul(ps[0:NB_, 0, 0:8], sx[:], k.bd2T[:], start=False, stop=False)
                pe.matmul(ps[0:NB_, 0, 0:8], k.ones[:, 0:NB_], k.bd2q[:], start=False,
                          stop=True).then_inc(s["sum_ps"].sem, 1)
                s["atf"].wait_apart(pe, t, 1)
                pe.transpose(ps[0:1, 1, 0:NB_], atf[:], k.ident[0:NB_, 0:NB_]).then_inc(s["pick_ps"].sem, 1)
                s["pick"].wait_apart(pe, t, 1)
                chosen = [pe.value_load(pick[0:1, i:i + 1], min_val=0, max_val=7) for i in range(NB_)]
                for u in range(2):
                    for j in range(G):
                        e = chosen[G * u + j]
                        o = ps[:, 4 * u + 2, R * j:R * j + R]
                        pe.matmul(o, xnT[:, u, j * S:j * S + S],
                                  k.wdown[:, bass.ds(e, 1), :].rearrange("p e r -> p (e r)"), start=True, stop=False)
                        m = pe.matmul(o, k.ones[0:1, :], k.bdown[:, bass.ds(e, 1), :].rearrange("p e r -> p (e r)"),
                                      start=False, stop=True)
                    m.then_inc(s["a_ps"].sem, 1)
                for u in range(2):
                    s["a"].wait_apart(pe, t, u + 1)
                    for j in range(G):
                        m = pe.transpose(ps[0:R, 4 * u + 3, j * S:j * S + S], a[:, u, j, :], k.ident[:])
                    m.then_inc(s["aT_ps"].sem, 1)
                for u in range(2):
                    s["aT"].wait(pe, t, u + 1)
                    for j in range(G):
                        e = chosen[G * u + j]
                        o = ps[:, 4 * u + 2, j * S:j * S + S]
                        pe.matmul(o, xnT[:, u, j * S:j * S + S], k.wbase[:], start=True, stop=False)
                        m = pe.matmul(o, aT[:, u, j * S:j * S + S],
                                      k.wup[:, bass.ds(e, 1), :].rearrange("p e r -> p (e r)"), start=False, stop=True)
                    m.then_inc(s["out_ps"].sem, 1)

        @block.scalar
        def _(act):
            with act.Fori(0, TURNS) as t:
                for u in range(2):
                    s["xnT_ps"].wait(act, t, u + 1)
                    act.activation(xnT[:, u], ps[:, 4 * u, :], ACT.Identity).then_inc(s["xnT"].sem, 1)
                for u in range(2):
                    for j in range(G):
                        s["hb"].wait(act, t, G * u + j + 1)
                        h = hx[:, u, j, :].rearrange("p (q n) -> p q n", q=2)[:, :, 0:128]
                        act.activation(h, h, ACT.Relu).then_inc(s["h"].sem, 1)
                for u in range(2):
                    s["a_ps"].wait(act, t, u + 1)
                    act.activation(a[:, u].rearrange("p j r -> p (j r)"), ps[:, 4 * u + 2, 0:G * R],
                                   ACT.Relu).then_inc(s["a"].sem, 1)
                for u in range(2):
                    s["aT_ps"].wait(act, t, u + 1)
                    act.activation(aT[0:R, u], ps[0:R, 4 * u + 3, :], ACT.Identity).then_inc(s["aT"].sem, 1)

        @block.vector
        def _(dve):
            dve.wait_ge(ones, 2)
            with dve.Fori(0, TURNS) as t:
                xj = [[k.X[:, bass.ds(t * PAIR + u * G + j, 1), :] for j in range(G)] for u in range(2)]
                norm_stats(dve, nm, s, t, lambda u, j: xj[u][j])
                for u in range(2):
                    norm_apply(dve, nm, s, t, u, lambda u, j: xj[u][j], xn)
                for u in range(2):
                    s["h_ps"].wait(dve, t, u + 1)
                    for j in range(G):
                        h = hx[:, u, j, :].rearrange("p (q n) -> p q n", q=2)[:, :, 0:128]
                        dve.tensor_tensor(h, ps[:, 4 * u + 1 + j // 2, 256 * (j % 2):256 * (j % 2) + 256]
                                          .rearrange("p (q n) -> p q n", q=2),
                                          k.bd1[:].rearrange("p (q n) -> p q n", q=2),
                                          ALU.add).then_inc(s["hb"].sem, 1)
                for u in range(2):
                    s["xnT"].wait(dve, t, u + 1)
                    dve.tensor_reduce(sx[:, G * u:G * u + G], xnT[:, u].rearrange("p (j t) -> p j t", j=G),
                                      AX.X, ALU.add).then_inc(s["sx"].sem, 1)
                for u in range(2):
                    for j in range(G):
                        i = G * u + j
                        s["gram_ps"].wait(dve, t, i + 1)
                        if i:
                            s["loss"].wait(dve, t, 2 * i)
                        for q in range(2):
                            dve.scalar_tensor_tensor(out=junk[:, q, :], in0=ps[:, 4 * u + ((3, 0), (1, 2))[j % 2][q], 0:257],
                                                     scalar=1.0, in1=k.dcoef[:, q, :], op0=ALU.mult, op1=ALU.mult,
                                                     accum_out=loss[:, q, i:i + 1]).then_inc(s["loss"].sem, 1)
                s["sum_ps"].wait(dve, t, 1)
                dve.tensor_scalar(gain[:], ps[0:NB_, 0, 0:8], -1.0, None, ALU.mult).then_inc(s["gain"].sem, 1)
                s["gain"].wait_apart(dve, t, 1)
                dve.max(best[:], gain[:]).then_inc(s["best"].sem, 1)
                s["best"].wait_apart(dve, t, 1)
                dve.max_index(at[:], best[:], gain[:]).then_inc(s["at"].sem, 1)
                s["at"].wait(dve, t, 1)
                dve.tensor_copy(atf[:], at[:, 0:1]).then_inc(s["atf"].sem, 1)
                s["pick_ps"].wait(dve, t, 1)
                dve.tensor_copy(pick[:], ps[0:1, 1, 0:NB_]).then_inc(s["pick"].sem, 1)
                for u in range(2):
                    s["out_ps"].wait(dve, t, u + 1)
                    xg = k.X[:, bass.ds(t * PAIR + u * G, G), :]
                    dve.scalar_tensor_tensor(out=xg, in0=ps[:, 4 * u + 2, :].rearrange("p (j d) -> p j d", j=G),
                                             scalar=k.tg[:, 5:6], in1=xg, op0=ALU.mult,
                                             op1=ALU.add).then_inc(s["x"].sem, 1)


def stage_attention16(nc, w, ps, k):
    H, DH = 16, 8
    SCALE = DH ** -0.5
    HU = H // 2
    NB_ = PAIR
    UNITS = 2 * NB_
    AHEAD = 3
    with ExitStack() as ctx:
        def tmp(name, shape, dt=F32):
            return ctx.enter_context(nc.sbuf_tensor("g_" + name, shape, dt))

        nm = Norm(lambda n, s: ctx.enter_context(nc.sbuf_tensor(n, s, F32)), "g")
        xn, xnT, ct = tmp("xn", [128, 2, G, 128]), tmp("xnT", [128, 2, W]), tmp("ct", [C, 2, W])
        qT, kT = tmp("qT", [128, 2, W]), tmp("kT", [128, 2, W])
        hmask = tmp("hmask", [128, H])
        km = tmp("km", [128, AHEAD, H, 128])
        v = tmp("v", [128, NB_, 4, 160])
        sel = tmp("sel", [128, 160])
        top = tmp("top", [128, 2, HU])
        p, pT = tmp("p", [128, 2, HU, 128]), tmp("pT", [128, 2, HU, 128])
        rsum, oT = tmp("rsum", [128, 128]), tmp("oT", [128, 2, 128])
        bo = tmp("bo", [128, 128])
        s = signals(nc, k, "g", **NORM, ct0=16, ct1=16, xnT_ps=2, xnT=2, q_ps=2, q=2, k_ps=2, kT=2, km=NB_,
                    v_ps=2, v=NB_, xb=2, sc_ps=UNITS, top=UNITS, sub=UNITS, p=UNITS, pT_ps=UNITS, pT=2 * UNITS,
                    av_ps=UNITS, rsum=NB_, oT=NB_, out_ps=NB_, x=NB_)
        once = ctx.enter_context(OneTime(nc, "g_"))
        consts, bo_done = once("consts"), once("bo")
        block = ctx.enter_context(nc.Block())

        @block.sync
        def _(sp):
            with sp.Fori(0, TURNS) as t:
                for u in range(2):
                    s["v_ps"].wait(sp, t, 0)
                    s["k_ps"].wait(sp, t, 0)
                    sp.dma_start(ct[:, u], k.cT[:, bass.ds(t * 2 * W + u * W, W)]).then_inc(s[f"ct{u}"].sem, 16)

        @block.gpsimd
        def _(pool):
            pool.memset(v[:], 0.0).then_inc(consts, 1)
            pool.memset(sel[:], 0.0).then_inc(consts, 1)
            pool.memset(hmask[:], 1.0).then_inc(consts, 1)
            pool.wait_ge(consts, 3)
            pool.memset(sel[:].rearrange("p (b x) -> p b x", x=40)[:, :, 0:DH], 1.0).then_inc(consts, 1)
            pool.affine_select(out=hmask[:], in_=hmask[:], compare_op=ALU.is_ge, fill=0.0, base=0,
                               pattern=[[-DH, H]], channel_multiplier=1).then_inc(consts, 1)
            pool.wait_ge(consts, 5)
            pool.affine_select(out=hmask[:], in_=hmask[:], compare_op=ALU.is_ge, fill=0.0, base=DH - 1,
                               pattern=[[DH, H]], channel_multiplier=-1).then_inc(consts, 1)
            pool.wait_ge(consts, 6)
            with pool.Fori(0, TURNS) as t:
                norm_rstd(pool, nm, s, t, k.half[:])
                for i in range(NB_):
                    u, j = i // G, i % G
                    s["kT"].wait(pool, t, u + 1)
                    s["sc_ps"].wait(pool, t, 2 * max(i - AHEAD + 1, 0))
                    pool.tensor_tensor(km[:, i % AHEAD],
                                       kT[:, u, j * S:j * S + S].rearrange("p (h t) -> p h t", h=1)
                                       .broadcast_to([128, H, 128]),
                                       hmask[:].rearrange("p (h o) -> p h o", o=1).broadcast_to([128, H, 128]),
                                       ALU.mult).then_inc(s["km"].sem, 1)

        @block.tensor
        def _(pe):
            pe.wait_ge(consts, 6)
            with pe.Fori(0, TURNS) as t:
                s["sub"].wait(pe, t, 0)
                for u in range(2):
                    s[f"ct{u}"].wait(pe, t, 16)
                    pe.matmul(ps[:, u, :], k.wk2[:], ct[:, u], start=True, stop=True).then_inc(s["k_ps"].sem, 1)
                for u in range(2):
                    for j in range(G):
                        m = pe.matmul(ps[:, 2 + u, j * S:j * S + S], ct[:, u, j * S:j * S + S], k.wv2[:],
                                      start=True, stop=True)
                    m.then_inc(s["v_ps"].sem, 1)
                s["pT"].wait(pe, t, 0)
                for u in range(2):
                    transpose_tokens(pe, s, t, u, xn, ps[:, 4 + u, :], k.ident[:])
                s["x"].wait(pe, t, 0)
                for u in range(2):
                    s["xnT"].wait(pe, t, u + 1)
                    pe.matmul(ps[:, 6 + u, :], k.wq2[:], xnT[:, u], start=True, stop=True).then_inc(s["q_ps"].sem, 1)
                for n in range(UNITS + 3):
                    if n < UNITS:
                        i, half = n // 2, n % 2
                        u, j = i // G, i % G
                        if n % UNITS == 0 or n == UNITS // 2:
                            s["q"].wait(pe, t, u + 1)
                        if half == 0:
                            s["km"].wait(pe, t, i + 1)
                        if n == 0:
                            s["v"].wait(pe, t, NB_)
                        if n >= 2:
                            s["sub"].wait(pe, t, n - 1)
                        for a in range(2):
                            h = HU * half + 4 * a
                            m = pe.matmul(ps[:, 2 * half + a, :], qT[:, u, j * S:j * S + S],
                                          km[:, i % AHEAD, h:h + 4, :].rearrange("p h t -> p (h t)"),
                                          start=True, stop=True)
                        m.then_inc(s["sc_ps"].sem, 1)
                    if n % 2 == 0 and n >= 4:
                        i = n // 2 - 2
                        s["oT"].wait(pe, t, i + 1)
                        if i:
                            s["x"].wait(pe, t, i)
                        else:
                            s["q"].wait(pe, t, 2)
                        pe.matmul(ps[:, 7, 0:128], oT[:, i % 2], k.wo2[:], start=True,
                                  stop=True).then_inc(s["out_ps"].sem, 1)
                    if 1 <= n <= UNITS:
                        s["p"].wait(pe, t, n)
                        if n >= 2:
                            s["pT"].wait(pe, t, 2 * (n - 1))
                        for h in range(HU):
                            m = pe.transpose(ps[:, 4 + h // 4, 128 * (h % 4):128 * (h % 4) + 128],
                                             p[:, (n - 1) % 2, h, :], k.ident[:])
                        m.then_inc(s["pT_ps"].sem, 1)
                    if 2 <= n < UNITS + 2:
                        i, half = (n - 2) // 2, n % 2
                        s["pT"].wait(pe, t, 2 * (n - 1))
                        if half == 0 and i:
                            s["oT"].wait(pe, t, i)
                        for a in (2 * half, 2 * half + 1):
                            o = ps[32 * a:32 * a + 32, 6, :]
                            for b in range(4):
                                pe.matmul(o[:, 0:128], v[:, i, a, 32 * b:32 * b + 32],
                                          pT[:, half, 4 * (a % 2) + b, :], start=b == 0, stop=b == 3)
                            for b in range(4):
                                m = pe.matmul(o[:, 128:256], sel[:, 32 * b:32 * b + 32],
                                              pT[:, half, 4 * (a % 2) + b, :], start=b == 0, stop=b == 3)
                        m.then_inc(s["av_ps"].sem, 1)

        @block.scalar
        def _(act):
            with act.Fori(0, TURNS) as t:
                for u in range(2):
                    s["k_ps"].wait(act, t, u + 1)
                    act.activation(kT[:, u], ps[:, u, :], ACT.Identity, bias=k.bk2[:]).then_inc(s["kT"].sem, 1)
                for u in range(2):
                    s["xnT_ps"].wait(act, t, u + 1)
                    act.activation(xnT[:, u], ps[:, 4 + u, :], ACT.Identity).then_inc(s["xnT"].sem, 1)
                for u in range(2):
                    s["q_ps"].wait(act, t, u + 1)
                    act.activation(qT[:, u], ps[:, 6 + u, :], ACT.Identity, bias=k.bq2[:]).then_inc(s["q"].sem, 1)
                for n in range(UNITS + 1):
                    if n >= 1:
                        s["pT_ps"].wait(act, t, n)
                        if n >= 3:
                            s["av_ps"].wait(act, t, n - 2)
                        for a in range(2):
                            act.activation(pT[:, (n - 1) % 2, 4 * a:4 * a + 4, :].rearrange("p a b -> p (a b)"),
                                           ps[:, 4 + a, :], ACT.Identity).then_inc(s["pT"].sem, 1)
                    if n < UNITS:
                        s["sub"].wait(act, t, n + 1)
                        act.activation(p[:, n % 2], p[:, n % 2], ACT.Exp, scale=SCALE).then_inc(s["p"].sem, 1)

        @block.vector
        def _(dve):
            dve.tensor_scalar(bo[:], k.bo2[:], k.tg[:, 2:3], None, ALU.mult).then_inc(bo_done, 1)
            dve.wait_ge(bo_done, 1)
            dve.wait_ge(consts, 6)
            with dve.Fori(0, TURNS) as t:
                xj = [[k.X[:, bass.ds(t * PAIR + u * G + j, 1), :] for j in range(G)] for u in range(2)]
                norm_stats(dve, nm, s, t, lambda u, j: xj[u][j])
                for u in range(2):
                    norm_apply(dve, nm, s, t, u, lambda u, j: xj[u][j], xn)
                for i in range(NB_):
                    u, j = i // G, i % G
                    if j == 0:
                        s["v_ps"].wait(dve, t, u + 1)
                    dve.tensor_tensor(v[:, i].rearrange("p a (b x) -> p a b x", x=40)[:, :, :, 0:DH],
                                      ps[:, 2 + u, j * S:j * S + S].rearrange("p (a b d) -> p a b d", a=4, b=4),
                                      k.bv2[:].rearrange("p (a b d) -> p a b d", a=4, b=4),
                                      ALU.add).then_inc(s["v"].sem, 1)
                s["xn"].wait(dve, t, 2 * G)
                for u in range(2):
                    xg = k.X[:, bass.ds(t * PAIR + u * G, G), :]
                    dve.tensor_tensor(xg, xg, bo[:].rearrange("p (j d) -> p j d", j=1).broadcast_to([128, G, 128]),
                                      ALU.add).then_inc(s["xb"].sem, 1)
                s["xb"].wait(dve, t, 2)
                for n in range(UNITS + 3):
                    done = n // 2 - 2 if n % 2 == 0 and n >= 4 else None
                    if done is not None:
                        s["av_ps"].wait(dve, t, 2 * done + 2)
                        dve.reciprocal(rsum[:], ps[:, 6, 128:256]).then_inc(s["rsum"].sem, 1)
                        s["rsum"].wait(dve, t, done + 1)
                        dve.tensor_tensor(oT[:, done % 2], ps[:, 6, 0:128], rsum[:], ALU.mult).then_inc(s["oT"].sem, 1)
                    if n < UNITS:
                        half = n % 2
                        sc = ps[:, 2 * half:2 * half + 2, :].rearrange("p a (b c) -> p (a b) c", b=4)
                        s["sc_ps"].wait(dve, t, n + 1)
                        dve.tensor_reduce(top[:, half, :], sc, AX.X, ALU.max).then_inc(s["top"].sem, 1)
                        s["top"].wait(dve, t, n + 1)
                        if n >= 2:
                            s["pT_ps"].wait(dve, t, n - 1)
                        dve.tensor_tensor(p[:, half], sc, top[:, half, :].rearrange("p (h o) -> p h o", o=1)
                                          .broadcast_to([128, HU, 128]), ALU.subtract).then_inc(s["sub"].sem, 1)
                    if done is not None:
                        s["out_ps"].wait(dve, t, done + 1)
                        x_ = k.X[:, bass.ds(t * PAIR + done, 1), :].rearrange("p o d -> p (o d)")
                        dve.scalar_tensor_tensor(out=x_, in0=ps[:, 7, 0:128], scalar=k.tg[:, 2:3], in1=x_,
                                                 op0=ALU.mult, op1=ALU.add).then_inc(s["x"].sem, 1)


def stage_fp8(nc, w, ps, k):
    with ExitStack() as ctx:
        k.amax = ctx.enter_context(nc.sbuf_tensor("h_amax", [128, 2], F32))
        k.scale = ctx.enter_context(nc.sbuf_tensor("h_scale", [128, 2], F32))
        k.unscale = ctx.enter_context(nc.sbuf_tensor("h_unscale", [128, 1], F32))
        k.wqT = ctx.enter_context(nc.sbuf_tensor("h_wqT", [128, 128], BF16))
        k.identb = ctx.enter_context(nc.sbuf_tensor("h_identb", [128, 128], BF16))
        k.bias8t = ctx.enter_context(nc.sbuf_tensor("h_bias8t", [128, 128], F32))
        norm_all(nc, w, ps, k)
        fp8_scales(nc, w, ps, k)
        fp8_product(nc, w, ps, k)


def norm_all(nc, w, ps, k):
    with ExitStack() as ctx:
        nm = Norm(lambda n, s: ctx.enter_context(nc.sbuf_tensor(n, s, F32)), "h")
        xall = k.x3[:].rearrange("p a b -> p (a b)").rearrange("p (b c) -> p b c", b=B)
        now = ctx.enter_context(nc.sbuf_tensor("h_now", [128, PAIR], F32))
        most = ctx.enter_context(nc.sbuf_tensor("h_most", [128, PAIR], F32))
        s = signals(nc, k, "h", **NORM, now=1, most=1)
        once = ctx.enter_context(OneTime(nc, "h_"))
        zeroed, final = once("zeroed"), once("final")
        block = ctx.enter_context(nc.Block())

        @block.gpsimd
        def _(pool):
            with pool.Fori(0, TURNS) as t:
                norm_rstd(pool, nm, s, t, k.half[:])

        @block.vector
        def _(dve):
            dve.memset(most[:], 0.0).then_inc(zeroed, 1)
            dve.wait_ge(zeroed, 1)
            with dve.Fori(0, TURNS) as t:
                xj = [[k.X[:, bass.ds(t * PAIR + u * G + j, 1), :] for j in range(G)] for u in range(2)]
                norm_stats(dve, nm, s, t, lambda u, j: xj[u][j])
                s["rstd"].wait(dve, t, 1)
                s["mean"].wait(dve, t, 1)
                for u in range(2):
                    for j in range(G):
                        dve.tensor_scalar(xall[:, bass.ds(t * PAIR + u * G + j, 1), :], xj[u][j],
                                          nm.mean[:, u, j:j + 1], nm.rstd[:, u, j:j + 1], ALU.subtract,
                                          ALU.mult).then_inc(s["xn"].sem, 1)
                s["most"].wait(dve, t, 0)
                s["xn"].wait_apart(dve, t, 2 * G)
                dve.tensor_reduce(now[:], xall[:, bass.ds(t * PAIR, PAIR), :], AX.X, ALU.max,
                                  apply_absolute_value=True).then_inc(s["now"].sem, 1)
                s["now"].wait(dve, t, 1)
                dve.tensor_tensor(most[:], most[:], now[:], ALU.max).then_inc(s["most"].sem, 1)
            s["most"].wait(dve, TURNS - 1, 1)
            dve.tensor_reduce(k.amax[:, 0:1], most[:], AX.X, ALU.max).then_inc(final, 1)
            dve.tensor_reduce(k.amax[:, 1:2], k.wq8[:], AX.X, ALU.max, apply_absolute_value=True).then_inc(final, 1)


E4M3 = dict(top=448.0, least=2.0 ** -6, magic=1.5 * 2.0 ** 20, exponent=0x7F800000)


def fp8_scales(nc, w, ps, k):
    with ExitStack() as ctx:
        def tmp(name, shape, dt=F32):
            return ctx.enter_context(nc.sbuf_tensor("i_" + name, shape, dt))

        row, inv = tmp("row", [1, 2]), tmp("inv", [128, 2])
        q, mag, wq = tmp("q", [128, 128]), tmp("mag", [128, 128]), tmp("wq", [128, 128], BF16)
        once = ctx.enter_context(OneTime(nc, "i_"))
        chain, amax_T, rows, amax_b, wq_done, wT = (once(n) for n in (
            "chain", "amax_T", "rows", "amax_b", "wq_done", "wT"))
        block = ctx.enter_context(nc.Block())

        @block.tensor
        def _(pe):
            for i in range(2):
                m = pe.transpose(ps[0:1, 0, 128 * i:128 * i + 128], k.amax[:, i:i + 1], k.ident[:])
            m.then_inc(amax_T, 1)
            pe.wait_ge(rows, 1)
            pe.matmul(ps[:, 1, 0:2], k.ones[0:1, :], row[:], start=True, stop=True).then_inc(amax_b, 1)
            pe.wait_ge(wq_done, 1)
            pe.transpose(ps[:, 2, 0:64].bitcast(BF16), wq[:], k.identb[:]).then_inc(wT, 1)

        @block.vector
        def _(dve):
            n = [0]

            def link(ins):
                n[0] += 1
                ins.then_inc(chain, 1)
                dve.wait_ge(chain, n[0])

            dve.wait_ge(amax_T, 1)
            dve.tensor_reduce(row[:], ps[0:1, 0, 0:256].rearrange("p (a b) -> p a b", a=2), AX.X,
                              ALU.max).then_inc(rows, 1)
            link(dve.tensor_copy(k.identb[:], k.ident[:]))
            dve.tensor_scalar(k.bias8t[:], k.bias8[:], k.tg[:, 6:7], None, ALU.mult)
            dve.wait_ge(amax_b, 1)
            link(dve.tensor_scalar(k.scale[:], ps[:, 1, 0:2], 1e-12, None, ALU.max))
            link(dve.reciprocal(inv[:], k.scale[:]))
            link(dve.tensor_scalar(k.scale[:], inv[:], E4M3["top"], None, ALU.mult))
            link(dve.reciprocal(inv[:], k.scale[:]))
            link(dve.tensor_tensor(k.unscale[:], inv[:, 0:1], inv[:, 1:2], ALU.mult))
            link(dve.tensor_tensor(k.unscale[:], k.tg[:, 6:7], k.unscale[:], ALU.mult))
            link(dve.tensor_scalar(q[:], k.wq8[:], k.scale[:, 1:2], None, ALU.mult))
            link(dve.tensor_scalar(mag[:].bitcast(I32), q[:].bitcast(I32), E4M3["exponent"], None, ALU.bitwise_and))
            link(dve.tensor_scalar(mag[:], mag[:], E4M3["least"], E4M3["magic"], ALU.max, ALU.mult))
            link(dve.tensor_tensor(q[:], q[:], mag[:], ALU.add))
            dve.tensor_tensor(wq[:], q[:], mag[:], ALU.subtract).then_inc(wq_done, 1)
            dve.wait_ge(wT, 1)
            dve.tensor_copy(k.wqT[:], ps[:, 2, 0:64].bitcast(BF16))


def fp8_product(nc, w, ps, k):
    with ExitStack() as ctx:
        def tmp(name, shape, dt=F32):
            return ctx.enter_context(nc.sbuf_tensor("j_" + name, shape, dt))

        xall = k.x3[:].rearrange("p a b -> p (a b)").rearrange("p (b c) -> p b c", b=B)
        q, mag = tmp("q", [128, 2, W]), tmp("mag", [128, 2, W])
        xq, xqT = tmp("xq", [128, 2, W], BF16), tmp("xqT", [128, 2, W], BF16)
        s = signals(nc, k, "j", q=2, exponent=2, magic=2, sum=2, xq=2, xqT_ps=2, xqT=2, out_ps=2, x=2, xb=2)
        block = ctx.enter_context(nc.Block())

        @block.tensor
        def _(pe):
            with pe.Fori(0, TURNS) as t:
                for u in range(2):
                    s["xq"].wait(pe, t, u + 1)
                    s["xqT"].wait(pe, t, 0)
                    for j in range(G):
                        m = pe.transpose(ps[:, 4 * u, 64 * j:64 * j + 64].bitcast(BF16), xq[:, u, j * S:j * S + S],
                                         k.identb[:])
                    m.then_inc(s["xqT_ps"].sem, 1)
                for u in range(2):
                    s["xqT"].wait(pe, t, u + 1)
                    s["x"].wait(pe, t, 0)
                    for j in range(G):
                        m = pe.matmul(ps[:, 4 * u + 1, j * S:j * S + S], xqT[:, u, j * S:j * S + S], k.wqT[:],
                                      start=True, stop=True)
                    m.then_inc(s["out_ps"].sem, 1)

        @block.scalar
        def _(act):
            with act.Fori(0, TURNS) as t:
                for u in range(2):
                    s["xqT_ps"].wait(act, t, u + 1)
                    s["out_ps"].wait(act, t, 0)
                    act.activation(xqT[:, u], ps[:, 4 * u, 0:256].bitcast(BF16), ACT.Identity).then_inc(s["xqT"].sem, 1)

        @block.vector
        def _(dve):
            with dve.Fori(0, TURNS) as t:
                for u in range(2):
                    s["xqT_ps"].wait(dve, t, 0)
                    s["xq"].wait(dve, t, 0)
                    dve.tensor_scalar(q[:, u].rearrange("p (j c) -> p j c", j=G),
                                      xall[:, bass.ds(t * PAIR + u * G, G), :], k.scale[:, 0:1], None,
                                      ALU.mult).then_inc(s["q"].sem, 1)
                for u in range(2):
                    s["q"].wait(dve, t, u + 1)
                    dve.tensor_scalar(mag[:, u].bitcast(I32), q[:, u].bitcast(I32), E4M3["exponent"], None,
                                      ALU.bitwise_and).then_inc(s["exponent"].sem, 1)
                for u in range(2):
                    s["exponent"].wait(dve, t, u + 1)
                    dve.tensor_scalar(mag[:, u], mag[:, u], E4M3["least"], E4M3["magic"], ALU.max,
                                      ALU.mult).then_inc(s["magic"].sem, 1)
                for u in range(2):
                    s["magic"].wait(dve, t, u + 1)
                    dve.tensor_tensor(q[:, u], q[:, u], mag[:, u], ALU.add).then_inc(s["sum"].sem, 1)
                for u in range(2):
                    s["sum"].wait(dve, t, u + 1)
                    dve.tensor_tensor(xq[:, u], q[:, u], mag[:, u], ALU.subtract).then_inc(s["xq"].sem, 1)
                for u in range(2):
                    s["out_ps"].wait(dve, t, u + 1)
                    xg = k.X[:, bass.ds(t * PAIR + u * G, G), :]
                    dve.scalar_tensor_tensor(out=xg, in0=ps[:, 4 * u + 1, :].rearrange("p (j d) -> p j d", j=G),
                                             scalar=k.unscale[:, 0:1], in1=xg, op0=ALU.mult,
                                             op1=ALU.add).then_inc(s["x"].sem, 1)
                for u in range(2):
                    s["x"].wait(dve, t, u + 1)
                    xg = k.X[:, bass.ds(t * PAIR + u * G, G), :]
                    dve.tensor_tensor(xg, xg, k.bias8t[:].rearrange("p (j d) -> p j d", j=1)
                                      .broadcast_to([128, G, 128]), ALU.add).then_inc(s["xb"].sem, 1)


def stage_attention8(nc, w, ps, k):
    H, DH = 8, 64
    SCALE = DH ** -0.5
    NB_ = PAIR
    with ExitStack() as ctx:
        def tmp(name, shape, dt=F32):
            return ctx.enter_context(nc.sbuf_tensor("l_" + name, shape, dt))

        nm = Norm(lambda n, s: ctx.enter_context(nc.sbuf_tensor(n, s, F32)), "l")
        xn, xnT, ct = tmp("xn", [128, 2, G, 128]), tmp("xnT", [128, 2, W]), tmp("ct", [C, 2, W])
        qT, km = tmp("qT", [128, 2, 4, W]), tmp("km", [128, 2, 4, G, 2, 128])
        v = tmp("v", [128, 3, H * DH])
        shift, total, top = tmp("shift", [128, 2, H]), tmp("total", [128, 2, H]), tmp("top", [128, 2, H])
        p, pT = tmp("p", [128, 2, H, 128]), tmp("pT", [128, H, 128])
        oT = tmp("oT", [128, 4, 128])
        bo = tmp("bo", [128, 128])
        s = signals(nc, k, "l", **NORM, ct0=16, ct1=16, xnT_ps=2, xnT=2, q_ps=2, q0=4, q1=4, k_ps=2, kT0=8, kT1=8,
                    xb=2, sc_ps=NB_, top=NB_, shift=NB_, p=NB_ * H, rsum=NB_, share=NB_, v_ps=NB_, v=NB_,
                    pT_ps=NB_, pT=2 * NB_, av_ps=NB_, oT=NB_, out_ps=NB_, x=NB_)
        once = ctx.enter_context(OneTime(nc, "l_"))
        zeroed, bo_done = once("zeroed"), once("bo")
        block = ctx.enter_context(nc.Block())

        @block.sync
        def _(sp):
            with sp.Fori(0, TURNS) as t:
                for u in range(2):
                    s["v_ps"].wait(sp, t, 0)
                    sp.dma_start(ct[:, u], k.cT[:, bass.ds(t * 2 * W + u * W, W)]).then_inc(s[f"ct{u}"].sem, 16)

        @block.gpsimd
        def _(pool):
            pool.memset(km[:], 0.0).then_inc(zeroed, 1)
            with pool.Fori(0, TURNS) as t:
                norm_rstd(pool, nm, s, t, k.half[:])

        @block.tensor
        def _(pe):
            with pe.Fori(0, TURNS) as t:
                s["x"].wait(pe, t, 0)
                for u in range(2):
                    s[f"ct{u}"].wait(pe, t, 16)
                    for b in range(4):
                        m = pe.matmul(ps[:, 4 * u + b, :], k.wk3[:, 128 * b:128 * b + 128], ct[:, u], start=True,
                                      stop=True)
                    m.then_inc(s["k_ps"].sem, 1)
                for u in range(2):
                    s[f"kT{u}"].wait(pe, t, 8)
                    transpose_tokens(pe, s, t, u, xn, ps[:, 4 * u, :], k.ident[:])
                for u in range(2):
                    s["xnT"].wait(pe, t, u + 1)
                    for b in range(4):
                        m = pe.matmul(ps[:, 4 * u + b, :], k.wq3[:, 128 * b:128 * b + 128], xnT[:, u], start=True,
                                      stop=True)
                    m.then_inc(s["q_ps"].sem, 1)
                for n in range(NB_ + 3):
                    if n < NB_:
                        u, j = n // G, n % G
                        if n == 0:
                            s["q0"].wait(pe, t, 4)
                        if n == G:
                            s["q1"].wait(pe, t, 4)
                        if n >= 2:
                            s["p"].wait(pe, t, H * (n - 1))
                        for b in range(4):
                            m = pe.matmul(ps[:, 2 * (n % 2) + b // 2, 256 * (b % 2):256 * (b % 2) + 256],
                                          qT[:, u, b, j * S:j * S + S], km[:, u, b, j].rearrange("p h t -> p (h t)"),
                                          start=True, stop=True)
                        m.then_inc(s["sc_ps"].sem, 1)
                    if n >= 3:
                        s["oT"].wait(pe, t, n - 2)
                        if n <= NB_:
                            s["v"].wait(pe, t, n)
                        else:
                            s["x"].wait(pe, t, n - 3)
                        for b in range(4):
                            m = pe.matmul(ps[:, 7, 0:128], oT[:, b, :], k.wo3[:, b, :], start=b == 0, stop=b == 3)
                        m.then_inc(s["out_ps"].sem, 1)
                    if n < NB_:
                        if n == 0:
                            s["q1"].wait(pe, t, 4)
                        elif n < 3:
                            s["v"].wait(pe, t, n)
                        else:
                            s["x"].wait(pe, t, n - 2)
                        pe.matmul(ps[:, 7, :], ct[:, u, j * S:j * S + S], k.wv3[:], start=True,
                                  stop=True).then_inc(s["v_ps"].sem, 1)
                    if 2 <= n < NB_ + 2:
                        i = n - 2
                        s["pT"].wait(pe, t, 2 * (i + 1))
                        s["v"].wait(pe, t, i + 1)
                        if i:
                            s["oT"].wait(pe, t, i)
                        for h in range(H):
                            r = DH * (h % 2)
                            m = pe.matmul(ps[r:r + DH, 6, 128 * (h // 2):128 * (h // 2) + 128],
                                          v[:, i % 3, DH * h:DH * h + DH], pT[:, h, :], start=True, stop=True)
                        m.then_inc(s["av_ps"].sem, 1)
                    if 1 <= n <= NB_:
                        i = n - 1
                        s["share"].wait(pe, t, i + 1)
                        if i:
                            s["pT"].wait(pe, t, 2 * i)
                        else:
                            s["q1"].wait(pe, t, 4)
                        for h in range(H):
                            m = pe.transpose(ps[:, 4 + h // 4, 128 * (h % 4):128 * (h % 4) + 128], p[:, i % 2, h, :],
                                             k.ident[:])
                        m.then_inc(s["pT_ps"].sem, 1)

        @block.scalar
        def _(act):
            act.wait_ge(zeroed, 1)
            with act.Fori(0, TURNS) as t:
                s["k_ps"].wait(act, t, 1)
                for b in range(4):
                    for a in range(2):
                        r = slice(DH * a, DH * a + DH)
                        act.activation(km[r, 0, b, :, a, :], ps[r, b, :].rearrange("p (j t) -> p j t", j=G),
                                       ACT.Identity).then_inc(s["kT0"].sem, 1)
                for u in range(2):
                    s["xnT_ps"].wait(act, t, u + 1)
                    act.activation(xnT[:, u], ps[:, 4 * u, :], ACT.Identity).then_inc(s["xnT"].sem, 1)
                s["q_ps"].wait(act, t, 1)
                for b in range(4):
                    act.activation(qT[:, 0, b, :], ps[:, b, :], ACT.Identity).then_inc(s["q0"].sem, 1)
                for n in range(NB_ + 2):
                    if n >= 2:
                        i = n - 2
                        s["pT_ps"].wait(act, t, i + 1)
                        if i:
                            s["av_ps"].wait(act, t, i)
                        for a in range(2):
                            act.activation(pT[:, 4 * a:4 * a + 4, :].rearrange("p a b -> p (a b)"), ps[:, 4 + a, :],
                                           ACT.Identity).then_inc(s["pT"].sem, 1)
                    if n < NB_:
                        s["shift"].wait(act, t, n + 1)
                        if n >= 2:
                            s["pT_ps"].wait(act, t, n - 1)
                        for h in range(H):
                            act.activation(p[:, n % 2, h, :],
                                           ps[:, 2 * (n % 2) + h // 4, 128 * (h % 4):128 * (h % 4) + 128], ACT.Exp,
                                           bias=shift[:, n % 2, h:h + 1], scale=SCALE,
                                           accum_out=total[:, n % 2, h:h + 1]).then_inc(s["p"].sem, 1)
                    if n >= 2:
                        s["av_ps"].wait(act, t, i + 1)
                        if i:
                            s["out_ps"].wait(act, t, i)
                        act.activation(oT[:].rearrange("p a b -> p (a b)"), ps[:, 6, :],
                                       ACT.Identity).then_inc(s["oT"].sem, 1)

        @block.vector
        def _(dve):
            dve.tensor_scalar(bo[:], k.bo3[:], k.tg[:, 3:4], None, ALU.mult).then_inc(bo_done, 1)
            dve.wait_ge(bo_done, 1)
            dve.wait_ge(zeroed, 1)
            with dve.Fori(0, TURNS) as t:
                xj = [[k.X[:, bass.ds(t * PAIR + u * G + j, 1), :] for j in range(G)] for u in range(2)]
                norm_stats(dve, nm, s, t, lambda u, j: xj[u][j])
                for u in range(2):
                    norm_apply(dve, nm, s, t, u, lambda u, j: xj[u][j], xn)
                s["k_ps"].wait(dve, t, 2)
                for b in range(4):
                    for a in range(2):
                        r = slice(DH * a, DH * a + DH)
                        dve.tensor_copy(km[r, 1, b, :, a, :],
                                        ps[r, 4 + b, :].rearrange("p (j t) -> p j t", j=G)).then_inc(s["kT1"].sem, 1)
                s["xn"].wait(dve, t, 2 * G)
                for u in range(2):
                    xg = k.X[:, bass.ds(t * PAIR + u * G, G), :]
                    dve.tensor_tensor(xg, xg, bo[:].rearrange("p (j d) -> p j d", j=1).broadcast_to([128, G, 128]),
                                      ALU.add).then_inc(s["xb"].sem, 1)
                s["q_ps"].wait(dve, t, 2)
                for b in range(4):
                    dve.tensor_copy(qT[:, 1, b, :], ps[:, 4 + b, :]).then_inc(s["q1"].sem, 1)
                s["xb"].wait(dve, t, 2)
                for n in range(NB_ + 3):
                    if 1 <= n <= NB_:
                        i, a = n - 1, (n - 1) % 2
                        s["p"].wait(dve, t, H * (i + 1))
                        dve.reciprocal(total[:, a, :], total[:, a, :]).then_inc(s["rsum"].sem, 1)
                        s["rsum"].wait(dve, t, i + 1)
                        dve.tensor_tensor(p[:, a], p[:, a], total[:, a, :].rearrange("p (h o) -> p h o", o=1)
                                          .broadcast_to([128, H, 128]), ALU.mult).then_inc(s["share"].sem, 1)
                    if n < NB_:
                        a = n % 2
                        s["sc_ps"].wait(dve, t, n + 1)
                        dve.tensor_reduce(top[:, a, :],
                                          ps[:, 2 * a:2 * a + 2, :].rearrange("p a (b c) -> p (a b) c", b=4),
                                          AX.X, ALU.max).then_inc(s["top"].sem, 1)
                        s["top"].wait(dve, t, n + 1)
                        dve.tensor_scalar(shift[:, a, :], top[:, a, :], -SCALE, None,
                                          ALU.mult).then_inc(s["shift"].sem, 1)
                    if n >= 3:
                        i = n - 3
                        s["out_ps"].wait(dve, t, i + 1)
                        x_ = k.X[:, bass.ds(t * PAIR + i, 1), :].rearrange("p o d -> p (o d)")
                        dve.scalar_tensor_tensor(out=x_, in0=ps[:, 7, 0:128], scalar=k.tg[:, 3:4], in1=x_,
                                                 op0=ALU.mult, op1=ALU.add).then_inc(s["x"].sem, 1)
                    if n < NB_:
                        s["v_ps"].wait(dve, t, n + 1)
                        if n >= 3:
                            s["av_ps"].wait(dve, t, n - 2)
                        dve.tensor_copy(v[:, n % 3], ps[:, 7, :]).then_inc(s["v"].sem, 1)


def stage_moe(nc, w, ps, k):
    E, TEMP, TINY = 8, 5.0, 1e-9
    with ExitStack() as ctx:
        def tmp(name, shape, dt=F32):
            return ctx.enter_context(nc.sbuf_tensor("m_" + name, shape, dt))

        nm = Norm(lambda n, s: ctx.enter_context(nc.sbuf_tensor(n, s, F32)), "m")
        xn, xnT = tmp("xn", [128, 2, G, 128]), tmp("xnT", [128, 2, W])
        lg, pr, top = tmp("lg", [128, 2, G, E]), tmp("pr", [128, 2, G, E]), tmp("top", [128, 2, G, 8])
        big, tot = tmp("big", [128, 2, G]), tmp("tot", [128, 2, G])
        at, atf = tmp("at", [128, 2, G, 8], U32), tmp("atf", [128, 2, G, 2])
        hit, gt = tmp("hit", [128, 2, G, 2, E]), tmp("gt", [128, 2, G, E])
        gtT = tmp("gtT", [E, 2, W])
        hid = tmp("hid", [128, 2, 2, W])
        s = signals(nc, k, "m", **NORM, xnT_ps=2, xnT=2, lg_ps=2, lg=2, big=2, less=2, ex=2, tot=2, rtot=2,
                    pr=2, top=2 * G, at=2 * G, atf=2, pair=2, rpair=4, two=2, hit=4, whit=4, gt=2, gT_ps=2, gT=2,
                    hid_ps=4 * E, hid=4 * E, out_ps=2 * E, x=2 * G * E, b_ps=2, xb=2)
        block = ctx.enter_context(nc.Block())

        @block.gpsimd
        def _(pool):
            with pool.Fori(0, TURNS) as t:
                norm_rstd(pool, nm, s, t, k.half[:])

        @block.tensor
        def _(pe):
            with pe.Fori(0, TURNS) as t:
                for u in range(2):
                    s["xb"].wait(pe, t, 0)
                    transpose_tokens(pe, s, t, u, xn, ps[:, 4 * u, :], k.ident[:])
                for u in range(2):
                    s["xnT"].wait(pe, t, u + 1)
                    for j in range(G):
                        m = pe.matmul(ps[:, 4 * u + 3, E * j:E * j + E], xnT[:, u, j * S:j * S + S], k.wg3[:],
                                      start=True, stop=True)
                    m.then_inc(s["lg_ps"].sem, 1)
                s["lg"].wait(pe, t, 2)
                for n in range(2 * E + 2):
                    if n < 2 * E:
                        e, u = n // 2, n % 2
                        for q in range(2):
                            if e:
                                s["hid"].wait(pe, t, 4 * (e - 1) + 2 * u + q + 1)
                            pe.matmul(ps[:, 4 * u + q, :], k.w1_3[:, e, 128 * q:128 * q + 128], xnT[:, u], start=True,
                                      stop=True).then_inc(s["hid_ps"].sem, 1)
                    if n >= 2:
                        e, u = (n - 2) // 2, n % 2
                        s["hid"].wait(pe, t, 4 * e + 2 * u + 2)
                        if e >= 2:
                            s["x"].wait(pe, t, G * (2 * (e - 2) + u + 1))
                        for j in range(G):
                            for q in range(2):
                                m = pe.matmul(ps[:, 4 * u + 2 + e % 2, j * S:j * S + S], hid[:, u, q, j * S:j * S + S],
                                              k.w2_3[:, e, q, :], start=q == 0, stop=q == 1)
                        m.then_inc(s["out_ps"].sem, 1)
                for u in range(2):
                    s["gt"].wait(pe, t, u + 1)
                    for j in range(G):
                        m = pe.transpose(ps[0:E, 4 * u, j * S:j * S + S], gt[:, u, j, :], k.ident[:])
                    m.then_inc(s["gT_ps"].sem, 1)
                for u in range(2):
                    s["gT"].wait(pe, t, u + 1)
                    for j in range(G):
                        m = pe.matmul(ps[:, 4 * u + 1, j * S:j * S + S], gtT[:, u, j * S:j * S + S], k.b2_3[:],
                                      start=True, stop=True)
                    m.then_inc(s["b_ps"].sem, 1)

        @block.scalar
        def _(act):
            with act.Fori(0, TURNS) as t:
                for u in range(2):
                    s["xnT_ps"].wait(act, t, u + 1)
                    act.activation(xnT[:, u], ps[:, 4 * u, :], ACT.Identity).then_inc(s["xnT"].sem, 1)
                for u in range(2):
                    s["less"].wait(act, t, u + 1)
                    act.activation(pr[:, u], lg[:, u], ACT.Exp, scale=1.0 / TEMP).then_inc(s["ex"].sem, 1)
                for n in range(2 * E):
                    e, u = n // 2, n % 2
                    for q in range(2):
                        s["hid_ps"].wait(act, t, 2 * n + q + 1)
                        if e:
                            s["out_ps"].wait(act, t, n - 1)
                        act.activation(hid[:, u, q, :], ps[:, 4 * u + q, :], ACT.Gelu,
                                       bias=k.b1_3[:, 2 * e + q:2 * e + q + 1]).then_inc(s["hid"].sem, 1)
                for u in range(2):
                    s["gT_ps"].wait(act, t, u + 1)
                    act.activation(gtT[:, u], ps[0:E, 4 * u, :], ACT.Identity).then_inc(s["gT"].sem, 1)

        @block.vector
        def _(dve):
            with dve.Fori(0, TURNS) as t:
                xj = [[k.X[:, bass.ds(t * PAIR + u * G + j, 1), :] for j in range(G)] for u in range(2)]
                norm_stats(dve, nm, s, t, lambda u, j: xj[u][j])
                for u in range(2):
                    norm_apply(dve, nm, s, t, u, lambda u, j: xj[u][j], xn)

                def each(ap):
                    return ap.rearrange("p (j o) -> p j o", o=1).broadcast_to([128, G, E])

                for u in range(2):
                    s["lg_ps"].wait(dve, t, u + 1)
                    dve.tensor_tensor(lg[:, u], ps[:, 4 * u + 3, 0:E * G].rearrange("p (j e) -> p j e", e=E),
                                      k.bg3[:].rearrange("p (j e) -> p j e", j=1).broadcast_to([128, G, E]),
                                      ALU.add).then_inc(s["lg"].sem, 1)
                    s["lg"].wait(dve, t, u + 1)
                    dve.tensor_reduce(big[:, u], lg[:, u], AX.X, ALU.max).then_inc(s["big"].sem, 1)
                    s["big"].wait(dve, t, u + 1)
                    dve.tensor_tensor(lg[:, u], lg[:, u], each(big[:, u]), ALU.subtract).then_inc(s["less"].sem, 1)
                for u in range(2):
                    s["ex"].wait(dve, t, u + 1)
                    dve.tensor_reduce(tot[:, u], pr[:, u], AX.X, ALU.add).then_inc(s["tot"].sem, 1)
                    s["tot"].wait(dve, t, u + 1)
                    dve.reciprocal(tot[:, u], tot[:, u]).then_inc(s["rtot"].sem, 1)
                    s["rtot"].wait(dve, t, u + 1)
                    dve.tensor_tensor(pr[:, u], pr[:, u], each(tot[:, u]), ALU.mult).then_inc(s["pr"].sem, 1)
                    s["pr"].wait_apart(dve, t, u + 1)
                    for j in range(G):
                        dve.max(top[:, u, j, :], pr[:, u, j, :]).then_inc(s["top"].sem, 1)
                    s["top"].wait_apart(dve, t, G * (u + 1))
                    for j in range(G):
                        dve.max_index(at[:, u, j, :], top[:, u, j, :], pr[:, u, j, :]).then_inc(s["at"].sem, 1)
                    dve.tensor_tensor(tot[:, u], top[:, u, :, 0], top[:, u, :, 1], ALU.add).then_inc(s["pair"].sem, 1)
                    s["pair"].wait(dve, t, u + 1)
                    dve.tensor_scalar(tot[:, u], tot[:, u], TINY, None, ALU.add).then_inc(s["rpair"].sem, 1)
                    s["rpair"].wait(dve, t, 2 * u + 1)
                    dve.reciprocal(tot[:, u], tot[:, u]).then_inc(s["rpair"].sem, 1)
                    s["rpair"].wait(dve, t, 2 * u + 2)
                    dve.scalar_tensor_tensor(out=top[:, u, :, 0:2], in0=top[:, u, :, 0:2], scalar=k.tg[:, 7:8],
                                             in1=tot[:, u].rearrange("p (j o) -> p j o", o=1).broadcast_to([128, G, 2]),
                                             op0=ALU.mult, op1=ALU.mult).then_inc(s["two"].sem, 1)
                    s["at"].wait(dve, t, G * (u + 1))
                    dve.tensor_copy(atf[:, u], at[:, u, :, 0:2]).then_inc(s["atf"].sem, 1)
                    s["atf"].wait(dve, t, u + 1)
                    for i in range(2):
                        dve.tensor_tensor(hit[:, u, :, i, :],
                                          k.iota8[:].rearrange("p (j e) -> p j e", j=1).broadcast_to([128, G, E]),
                                          atf[:, u, :, i:i + 1].broadcast_to([128, G, E]),
                                          ALU.is_equal).then_inc(s["hit"].sem, 1)
                    s["hit"].wait(dve, t, 2 * u + 2)
                    s["two"].wait(dve, t, u + 1)
                    for i in range(2):
                        dve.tensor_tensor(hit[:, u, :, i, :], hit[:, u, :, i, :],
                                          top[:, u, :, i:i + 1].broadcast_to([128, G, E]),
                                          ALU.mult).then_inc(s["whit"].sem, 1)
                    s["whit"].wait(dve, t, 2 * u + 2)
                    dve.tensor_tensor(gt[:, u], hit[:, u, :, 0, :], hit[:, u, :, 1, :], ALU.add).then_inc(s["gt"].sem, 1)
                s["gt"].wait(dve, t, 2)
                for n in range(2 * E):
                    e, u = n // 2, n % 2
                    s["out_ps"].wait(dve, t, n + 1)
                    if e:
                        s["x"].wait(dve, t, G * (n - 1))
                    for j in range(G):
                        dve.scalar_tensor_tensor(out=xj[u][j], in0=ps[:, 4 * u + 2 + e % 2, j * S:j * S + S],
                                                 scalar=gt[:, u, j, e:e + 1], in1=xj[u][j], op0=ALU.mult,
                                                 op1=ALU.add).then_inc(s["x"].sem, 1)
                s["x"].wait(dve, t, 2 * G * E)
                for u in range(2):
                    s["b_ps"].wait(dve, t, u + 1)
                    xg = k.X[:, bass.ds(t * PAIR + u * G, G), :]
                    dve.tensor_tensor(xg, xg, ps[:, 4 * u + 1, :].rearrange("p (j d) -> p j d", j=G),
                                      ALU.add).then_inc(s["xb"].sem, 1)


class Kept:

    def __init__(self, keep):
        self.X = keep("X", [128, B, 128])
        self.cT = keep("cT", [C, B * S])
        self.ident = keep("ident", [128, 128])
        self.flip = keep("flip", [128, 128])
        self.half = keep("half", [128, 8])
        self.ones = keep("ones", [128, 128])
        self.iota8 = keep("iota8", [128, 8])
        self.tg = keep("tg", [128, 8])
        self.tmask = keep("tmask", [128, B])
        self.wv0T = keep("wv0T", [128, 64])
        self.wt0T = keep("wt0T", [C, 64])
        self.bv0 = keep("bv0", [64, 1])
        self.bt0 = keep("bt0", [64, 1])
        self.gateT = keep("gateT", [128, 8])
        self.expT = keep("expT", [128, 8, 128])
        self.wq1 = keep("wq1", [128, 128])
        self.wk1 = keep("wk1", [C, 128])
        self.wfilm = keep("wfilm", [C + 1, 512])
        self.gin1 = keep("gin1", [128, 128])
        self.bin1 = keep("bin1", [128, 128])
        self.w1_1 = keep("w1_1", [128, 512])
        self.w2_1 = keep("w2_1", [128, 4, 128])
        self.b1_1 = keep("b1_1", [128, 4])
        self.gffn1 = keep("gffn1", [128, 1])
        self.bffn1 = keep("bffn1", [128, 1])
        self.b2_1 = keep("b2_1", [128, 128])
        self.gout1 = keep("gout1", [128, 128])
        self.bout1 = keep("bout1", [128, 128])
        self.wbase = keep("wbase", [128, 128])
        self.wd1 = keep("wd1", [128, 8, 32])
        self.bd1 = keep("bd1", [128, 256])
        self.dcoef = keep("dcoef", [128, 2, 257])
        self.indic = keep("indic", [128, 2, 8])
        self.bd2T = keep("bd2T", [128, 8])
        self.bd2q = keep("bd2q", [128, 8])
        self.wdown = keep("wdown", [128, 8, 64])
        self.bdown = keep("bdown", [1, 8, 64])
        self.wup = keep("wup", [65, 8, 128])
        self.wq2 = keep("wq2", [128, 128])
        self.wk2 = keep("wk2", [C, 128])
        self.bq2 = keep("bq2", [128, 1])
        self.bk2 = keep("bk2", [128, 1])
        self.wv2 = keep("wv2", [C, 128])
        self.bv2 = keep("bv2", [128, 128])
        self.wo2 = keep("wo2", [128, 128])
        self.bo2 = keep("bo2", [128, 128])
        self.wq8 = keep("wq8", [128, 128])
        self.bias8 = keep("bias8", [128, 128])
        self.wq3 = keep("wq3", [128, 512])
        self.wk3 = keep("wk3", [C, 512])
        self.wv3 = keep("wv3", [C, 512])
        self.wo3 = keep("wo3", [128, 4, 128])
        self.bo3 = keep("bo3", [128, 128])
        self.wg3 = keep("wg3", [128, 8])
        self.bg3 = keep("bg3", [128, 8])
        self.w1_3 = keep("w1_3", [128, 8, 256])
        self.w2_3 = keep("w2_3", [128, 8, 2, 128])
        self.b1_3 = keep("b1_3", [128, 16])
        self.b2_3 = keep("b2_3", [8, 128])
        self.x3 = keep("x3", [128, 128, B])
        self.mean1 = keep("mean1", [128, B])
        self.rstd1 = keep("rstd1", [128, B])


def build(nc, w, out):
    with ExitStack() as ctx:
        def keep(name, shape, dt=F32):
            return ctx.enter_context(nc.sbuf_tensor("k_" + name, shape, dt))

        k = Kept(keep)
        k.ctx, k.sems, k.apart = ctx, {}, ctx.enter_context(nc.semaphore("apart"))
        k.vmask = keep("vmask", [128, B, S], BF16)
        k.kpad = nc.dram_tensor("kpad", (128, 256), F32, kind="Internal").ap()
        ps = ctx.enter_context(nc.psum_tensor("ps", [128, 8, 512], F32))

        k.fo_dram = nc.dram_tensor("fo_dram", (128, B, 256), F32, kind="Internal").ap()
        setup_weights(nc, w, ps, k)
        setup_kernel(nc, w, ps, k)
        stages = [stage_cosine, stage_experts, stage_film, stage_adapters, stage_attention16, stage_fp8,
                  stage_attention8, stage_moe]
        for stage in stages:
            stage(nc, w, ps, k)
        store(nc, k, out)


def store(nc, k, out):
    with ExitStack() as ctx:
        stored = ctx.enter_context(OneTime(nc, ""))("stored")
        block = ctx.enter_context(nc.Block())

        @block.sync
        def _(sp):
            o = out.rearrange("b s d -> s b d")
            for i in range(4):
                sp.dma_start(o[:, 8 * i:8 * i + 8, :], k.X[:, 8 * i:8 * i + 8, :]).then_inc(stored, 16)
            sp.wait_ge(stored, 64)


def kernel(**inputs):
    import numpy as np
    import concourse.bacc as bacc
    from concourse.bass_utils import run_bass_kernel_spmd

    nc = bacc.Bacc("TRN2", target_bir_lowering=False, num_devices=1)
    arrays, aps = {}, {}
    for name, value in inputs.items():
        a = np.ascontiguousarray(value)
        if a.ndim == 0:
            a = a.reshape(1, 1)
        arrays["in_" + name] = a
        aps[name] = nc.dram_tensor("in_" + name, a.shape, mybir.dt.from_np(a.dtype), kind="ExternalInput").ap()
    out = nc.dram_tensor("out", (B, S, D), F32, kind="ExternalOutput").ap()
    build(nc, aps, out)
    r = run_bass_kernel_spmd(nc, [arrays], core_ids=[0])
    return r.results[0]["out"]
```

```python
from contextlib import ExitStack

import concourse.bass as bass
from concourse import mybir

F32 = mybir.dt.float32
BF16 = mybir.dt.bfloat16
U8 = mybir.dt.uint8
I32 = mybir.dt.int32
U32 = mybir.dt.uint32
ACT = mybir.ActivationFunctionType
ALU = mybir.AluOpType
AX = mybir.AxisListType

B, S, D = 32, 128, 128
C = 96
G = 4
W = G * S
PAIR = 2 * G
TURNS = B // PAIR
EPS = 1e-5


class Signal:

    def __init__(self, sem, base, per, apart):
        self.sem, self.base, self.per, self.apart = sem, base, per, apart

    def wait(self, eng, turn, n):
        eng.wait_ge(self.sem, turn * self.per + (self.base + n))

    def wait_apart(self, eng, turn, n):
        self.wait(eng, turn, n)
        eng.sem_inc(self.apart, 1)


def signals(nc, k, phase, turns=TURNS, **per):
    s = {}
    for name, n in per.items():
        if name not in k.sems:
            k.sems[name] = [k.ctx.enter_context(nc.semaphore(name)), 1]
            nc.gpsimd.sem_inc(k.sems[name][0], 1)
        sem, base = k.sems[name]
        s[name] = Signal(sem, base, n, k.apart)
        k.sems[name][1] += n * turns
    return s


class OneTime:

    def __init__(self, nc, prefix):
        self.nc, self.prefix, self.sems = nc, prefix, []

    def __call__(self, name):
        self.sems.append(self.nc.alloc_semaphore(self.prefix + name))
        return self.sems[-1]

    def __enter__(self):
        return self

    def __exit__(self, *_):
        self.nc.clear_and_free_semaphores(self.sems)
        self.nc.all_engine_barrier()


class Norm:

    def __init__(self, sb, name):
        self.stats = sb(name + "_stats", [128, 2 * G, 2, 3])
        self.diff = sb(name + "_diff", [128, 2 * G])
        self.m2 = sb(name + "_m2", [128, 2 * G])
        self.d2 = sb(name + "_d2", [128, 2 * G])
        self.mean = sb(name + "_mean", [128, 2, G])
        self.ve = sb(name + "_ve", [128, 2, G])
        self.rstd = sb(name + "_rstd", [128, 2, G])


def norm_stats(dve, nm, s, t, src):
    for u in range(2):
        group_stats(dve, nm, s, u, src)
    norm_moments(dve, nm, s, t)


def group_stats(dve, nm, s, u, src):
    for j in range(G):
        dve.bn_stats(nm.stats[:, u * G + j].rearrange("p a b -> p (a b)"), src(u, j)).then_inc(s["stats"].sem, 1)


def norm_moments(dve, nm, s, t):
    s["stats"].wait(dve, t, 2 * G)
    dve.tensor_tensor(nm.diff[:], nm.stats[:, :, 0, 1], nm.stats[:, :, 1, 1], ALU.subtract).then_inc(s["halves"].sem, 1)
    dve.tensor_tensor(nm.m2[:], nm.stats[:, :, 0, 2], nm.stats[:, :, 1, 2], ALU.add).then_inc(s["halves"].sem, 1)
    mean = nm.mean[:].rearrange("p u j -> p (u j)")
    dve.tensor_tensor(mean, nm.stats[:, :, 0, 1], nm.stats[:, :, 1, 1], ALU.add).then_inc(s["halves"].sem, 1)
    s["halves"].wait(dve, t, 3)
    dve.tensor_tensor(nm.d2[:], nm.diff[:], nm.diff[:], ALU.mult).then_inc(s["square"].sem, 1)
    dve.tensor_scalar(mean, mean, 0.5, None, ALU.mult).then_inc(s["mean"].sem, 1)
    s["square"].wait(dve, t, 1)
    dve.scalar_tensor_tensor(out=nm.m2[:], in0=nm.d2[:], scalar=D / 4.0, in1=nm.m2[:], op0=ALU.mult,
                             op1=ALU.add).then_inc(s["square"].sem, 1)
    s["square"].wait(dve, t, 2)
    dve.tensor_scalar(nm.ve[:].rearrange("p u j -> p (u j)"), nm.m2[:], 1.0 / D, EPS, ALU.mult,
                      ALU.add).then_inc(s["ve"].sem, 1)


def norm_rstd(pool, nm, s, t, half):
    s["ve"].wait(pool, t, 1)
    pool.tensor_tensor(nm.rstd[:].rearrange("p u j -> p (u j)"), nm.ve[:].rearrange("p u j -> p (u j)"), half,
                       ALU.pow).then_inc(s["rstd"].sem, 1)


def norm_apply(dve, nm, s, t, u, src, xn):
    s["rstd"].wait(dve, t, 1)
    s["mean"].wait(dve, t, 1)
    for j in range(G):
        dve.tensor_scalar(xn[:, u, j, :], src(u, j), nm.mean[:, u, j:j + 1], nm.rstd[:, u, j:j + 1],
                          ALU.subtract, ALU.mult).then_inc(s["xn"].sem, 1)


def turns(eng, opening, body, parts=1):
    if parts == 1:
        opening(0)
    else:
        for part in range(parts):
            opening(0, part)
    with eng.Fori(0, TURNS - 1) as t:
        body(t, lambda *part: opening(t + 1, *part))
    body(TURNS - 1, lambda *part: None)


NORM_PARTS = 5


def norm_turn(dve, nm, s, t, part, k, xn):
    def src(u, j):
        return k.X[:, bass.ds(t * PAIR + u * G + j, 1), :]

    if part == 0:
        s["xn"].wait(dve, t, 0)
    if part < 2:
        group_stats(dve, nm, s, part, src)
    elif part == 2:
        norm_moments(dve, nm, s, t)
    else:
        s["xnT_ps"].wait(dve, t, 0)
        norm_apply(dve, nm, s, t, part - 3, src, xn)


NORM = dict(stats=2 * G, halves=3, square=2, mean=1, ve=1, rstd=1, xn=2 * G)


GROUP_NORM = dict(stats=2 * G, halves=6, square=4, mean=2, ve=2, rstd=2, xn=2 * G)


def group_moments(dve, nm, s, t, u):
    g = slice(u * G, u * G + G)
    even, odd = nm.stats[:, g, 0, :], nm.stats[:, g, 1, :]
    s["stats"].wait(dve, t, G * (u + 1))
    dve.tensor_tensor(nm.diff[:, g], even[:, :, 1], odd[:, :, 1], ALU.subtract).then_inc(s["halves"].sem, 1)
    dve.tensor_tensor(nm.m2[:, g], even[:, :, 2], odd[:, :, 2], ALU.add).then_inc(s["halves"].sem, 1)
    dve.tensor_tensor(nm.mean[:, u], even[:, :, 1], odd[:, :, 1], ALU.add).then_inc(s["halves"].sem, 1)
    s["halves"].wait(dve, t, 3 * (u + 1))
    dve.tensor_tensor(nm.d2[:, g], nm.diff[:, g], nm.diff[:, g], ALU.mult).then_inc(s["square"].sem, 1)
    dve.tensor_scalar(nm.mean[:, u], nm.mean[:, u], 0.5, None, ALU.mult).then_inc(s["mean"].sem, 1)
    s["square"].wait(dve, t, 2 * u + 1)
    dve.scalar_tensor_tensor(out=nm.m2[:, g], in0=nm.d2[:, g], scalar=D / 4.0, in1=nm.m2[:, g], op0=ALU.mult,
                             op1=ALU.add).then_inc(s["square"].sem, 1)
    s["square"].wait(dve, t, 2 * u + 2)
    dve.tensor_scalar(nm.ve[:, u], nm.m2[:, g], 1.0 / D, EPS, ALU.mult, ALU.add).then_inc(s["ve"].sem, 1)


def group_apply(dve, nm, s, t, u, src, xn):
    s["rstd"].wait(dve, t, u + 1)
    s["mean"].wait(dve, t, u + 1)
    for j in range(G):
        dve.tensor_scalar(xn[:, u, j, :], src(u, j), nm.mean[:, u, j:j + 1], nm.rstd[:, u, j:j + 1],
                          ALU.subtract, ALU.mult).then_inc(s["xn"].sem, 1)


def transpose_tokens(pe, s, t, u, xn, bank, ident):
    s["xn"].wait(pe, t, G * (u + 1))
    for j in range(G):
        m = pe.transpose(bank[:, j * S:(j + 1) * S], xn[:, u, j, :], ident)
    m.then_inc(s["xnT_ps"].sem, 1)


def row_of(ap):
    return ap.rearrange("(a d) -> a d", a=1)


def setup_weights(nc, w, ps, k):
    with ExitStack() as ctx:
        def tmp(name, shape, dt=F32):
            return ctx.enter_context(nc.sbuf_tensor(name, shape, dt))

        sem = ctx.enter_context(OneTime(nc, "setup_"))

        nat_wv0 = tmp("nat_wv0", [64, 128])
        nat_wt0 = tmp("nat_wt0", [64, C])
        nat_gate = tmp("nat_gate", [8, 128])
        nat_exp = tmp("nat_exp", [128, 8, 128])
        nat_wv1 = tmp("nat_wv1", [C, 128])
        wv1T = tmp("wv1T", [128, C])
        wfilm = tmp("wfilm", [128, 2, 256])
        mgate = tmp("mgate", [128, 1])
        graw = tmp("graw", [128, 8])
        vmask8 = tmp("vmask8", [128, B * S], U8)
        tmask8 = tmp("tmask8", [B, S], U8)
        tmaskf = tmp("tmaskf", [B, S])
        rowraw = tmp("rowraw", [128, 2, 128])
        iraw = tmp("iraw", [128, 8], I32)
        nat_bd2 = tmp("nat_bd2", [8, 128])
        nat_wd2 = tmp("nat_wd2", [128, 2, 128])
        wd2T = tmp("wd2T", [128, 2, 128])
        bd2bc = tmp("bd2bc", [128, 2, 128])
        junk = tmp("setup_junk", [128, 128])
        bbase = tmp("bbase", [128, 8, 128])

        loads = sem("loads")
        ident_zero, ident_done = sem("ident_zero"), sem("ident_done")
        pool_done, turned, copied = sem("pool_done"), sem("turned"), sem("copied")
        vec_done, act_done = sem("vec_done"), sem("act_done")
        film_ps, gram_ps = sem("film_ps"), sem("gram_ps")

        x_dram = w["x"].rearrange("b s d -> s b d")
        plan = [(k.X[:, 8 * i:8 * i + 8, :], x_dram[:, 8 * i:8 * i + 8, :]) for i in range(4)]
        plan += [
            (nat_wv0[:], w["L0_xattn_Wv"]), (nat_wt0[:], w["L0_xattn_Wt"]), (nat_gate[:], w["L0_ffn_gate_w"]),
            (nat_exp[:], w["L0_ffn_expert_w"].rearrange("e d c -> d e c")),
            (nat_wv1[:], w["L1_xattn_Wv"]),
            (wfilm[:, 0, :], w["L1_xattn_W_film_in"]), (wfilm[:, 1, :], w["L1_xattn_W_film_out"]),
            (mgate[:], w["L1_xattn_mod_gate"].broadcast_to([128, 1])),
            (k.wfilm[C:C + 1, 0:256], row_of(w["L1_xattn_b_film_in"])),
            (k.wfilm[C:C + 1, 256:512], row_of(w["L1_xattn_b_film_out"])),
            (graw[:, 0:4], row_of(w["g_xattn"]).broadcast_to([128, 4])),
            (graw[:, 4:8], row_of(w["g_ffn"]).broadcast_to([128, 4])),
            (vmask8[:], w["mask_BxS2_bf1"].rearrange("(a b) s -> a (b s)", a=1).broadcast_to([128, B * S])),
            (tmask8[:], w["mask_BxS_bf1"]),
            (k.bv0[:], w["L0_xattn_bv"].rearrange("(h a) -> h a", a=1)),
            (k.bt0[:], w["L0_xattn_bt"].rearrange("(h a) -> h a", a=1)),
            (k.wq1[:], w["L1_xattn_Wq"]), (k.wk1[:], w["L1_xattn_Wk"]),
            (k.w1_1[:], w["L1_xattn_W1"]), (k.w2_1[:], w["L1_xattn_W2"].rearrange("(q p) d -> p q d", p=128)),
            (k.b1_1[:], w["L1_xattn_b1"].rearrange("(q p) -> p q", p=128)),
            (k.gffn1[:], w["L1_xattn_g_ffn"].rearrange("(p a) -> p a", a=1)),
            (k.bffn1[:], w["L1_xattn_b_ffn"].rearrange("(p a) -> p a", a=1)),
            (k.b2_1[:], row_of(w["L1_xattn_b2"]).broadcast_to([128, 128])),
            (k.gin1[:], row_of(w["L1_xattn_g_norm_in"]).broadcast_to([128, 128])),
            (k.bin1[:], row_of(w["L1_xattn_b_norm_in"]).broadcast_to([128, 128])),
            (rowraw[:, 0, :], row_of(w["L1_xattn_g_norm_out"]).broadcast_to([128, 128])),
            (rowraw[:, 1, :], row_of(w["L1_xattn_b_norm_out"]).broadcast_to([128, 128])),
            (k.wbase[:], w["L1_ffn_W_base"]),
            (k.wd1[:], w["L1_ffn_Wd1"].rearrange("e d h -> d e h")),
            (k.bd1[:], w["L1_ffn_bd1"].rearrange("(a e) h -> a (e h)", a=1).broadcast_to([128, 256])),
            (nat_bd2[:], w["L1_ffn_bd2"]),
            (nat_wd2[:], w["L1_ffn_Wd2"].rearrange("(q e) h d -> (e h) q d", q=2)),
            (k.wdown[:], w["L1_ffn_Wa_down"].rearrange("e d r -> d e r")),
            (k.bdown[:], w["L1_ffn_ba_down"].rearrange("(a e) r -> a e r", a=1)),
            (k.wup[0:64], w["L1_ffn_Wa_up"].rearrange("e r o -> r e o")),
            (k.wup[64:65], w["L1_ffn_ba_up"].rearrange("(a e) o -> a e o", a=1)),
            (bbase[64:65], row_of(w["L1_ffn_b_base"]).rearrange("a (e o) -> a e o", e=1).broadcast_to([1, 8, 128])),
            (k.wq2[:], w["L2_xattn_Wq"]), (k.wk2[:], w["L2_xattn_Wk"]),
            (k.bq2[:], w["L2_xattn_bq"].rearrange("(p a) -> p a", a=1)),
            (k.bk2[:], w["L2_xattn_bk"].rearrange("(p a) -> p a", a=1)),
            (k.wv2[:], w["L2_xattn_Wv"]), (k.wo2[:], w["L2_xattn_Wo"]),
            (k.bv2[:], row_of(w["L2_xattn_bv"]).broadcast_to([128, 128])),
            (k.bo2[:], row_of(w["L2_xattn_bo"]).broadcast_to([128, 128])),
            (k.wq8[:], w["L2_ffn_weight"]),
            (k.bias8[:], row_of(w["L2_ffn_bias"]).broadcast_to([128, 128])),
            (k.wq3[:], w["L3_xattn_Wq"]), (k.wk3[:], w["L3_xattn_Wk"]), (k.wv3[:], w["L3_xattn_Wv"]),
            (k.wo3[:], w["L3_xattn_Wo"].rearrange("(q p) d -> p q d", p=128)),
            (k.bo3[:], row_of(w["L3_xattn_bo"]).broadcast_to([128, 128])),
            (k.wg3[:], w["L3_ffn_Wg"]), (k.bg3[:], row_of(w["L3_ffn_bg"]).broadcast_to([128, 8])),
            (k.w1_3[:], w["L3_ffn_W1"].rearrange("e d h -> d e h")),
            (k.w2_3[:], w["L3_ffn_W2"].rearrange("e (q p) d -> p e q d", p=128)),
            (k.b1_3[:], w["L3_ffn_b1"].rearrange("e (q p) -> p (e q)", p=128)),
            (k.b2_3[:], w["L3_ffn_b2"]),
        ]
        plan += [(bd2bc[32 * (e % 4):32 * (e % 4) + 32, e // 4, :],
                  w["L1_ffn_bd2"][e:e + 1, :].broadcast_to([32, 128])) for e in range(8)]
        n_loads = 16 * len(plan)

        ctx.enter_context(nc.allow_non_contiguous_dma(reason="small vectors, once"))

        with nc.Block() as block:
            @block.gpsimd
            def _(pool):
                pool.memset(k.ident[:], 0.0).then_inc(ident_zero, 1)
                pool.wait_ge(ident_zero, 1)
                pool.affine_select(out=k.ident[:], in_=k.ident[:], compare_op=ALU.not_equal, fill=1.0, base=0,
                                   pattern=[[-1, 128]], channel_multiplier=1).then_inc(ident_done, 1)
                pool.memset(k.flip[:], 0.0).then_inc(ident_zero, 1)
                pool.wait_ge(ident_zero, 2)
                pool.affine_select(out=k.flip[:], in_=k.flip[:], compare_op=ALU.not_equal, fill=1.0, base=-127,
                                   pattern=[[1, 128]], channel_multiplier=1)
                pool.memset(k.half[:], -0.5).then_inc(pool_done, 1)
                pool.memset(k.ones[:], 1.0).then_inc(pool_done, 1)
                pool.iota(iraw[:], pattern=[[1, 8]], base=0, channel_multiplier=0).then_inc(pool_done, 1)
                pool.memset(k.indic[:], 0.0).then_inc(pool_done, 1)
                pool.memset(k.dcoef[:], 0.0).then_inc(pool_done, 1)
                pool.wait_ge(pool_done, 5)
                pool.tensor_copy(k.iota8[:], iraw[:]).then_inc(pool_done, 1)
                for e in range(4):
                    for q in range(2):
                        pool.wait_ge(pool_done, 6 + 2 * e + q)
                        pool.memset(k.indic[32 * e:32 * e + 32, q, 4 * q + e:4 * q + e + 1], 1.0).then_inc(pool_done, 1)

        def start_loads(sp):
            for dst, src in plan:
                sp.dma_start(dst, src).then_inc(loads, 16)

        setup_kernel(nc, w, ps, k, start_loads)
        block = ctx.enter_context(nc.Block())

        turned_weights = [(nat_exp[:, e, :], 128, 128, e // 4, (e % 4) * 128) for e in range(8)]
        turned_weights += [(nat_wv0[:], 64, 128, 2, 0), (nat_wt0[:], 64, C, 2, 64), (nat_gate[:], 8, 128, 2, 128),
                  (nat_wv1[:], C, 128, 2, 136), (nat_bd2[:], 8, 128, 2, 232), (tmaskf[:], B, S, 2, 240)]
        turned_weights += [(nat_wd2[:, q, :], 128, 128, 3, 128 * q) for q in range(2)]

        @block.tensor
        def _(pe):
            pe.wait_ge(loads, n_loads)
            pe.wait_ge(ident_done, 1)
            pe.wait_ge(vec_done, 1)
            for src, rows, cols, bank, col in turned_weights:
                m = pe.transpose(ps[0:cols, bank, col:col + rows], src, k.ident[0:rows, 0:rows])
            m.then_inc(turned, 1)
            pe.wait_ge(copied, 4)
            pe.matmul(ps[0:C, 4, :], wv1T[:], wfilm[:].rearrange("p a n -> p (a n)"),
                      start=True, stop=True).then_inc(film_ps, 1)
            for q in range(2):
                m = pe.matmul(ps[:, 5, 128 * q:128 * q + 128], wd2T[:, q, :], wd2T[:, q, :],
                              start=True, stop=True)
            m.then_inc(gram_ps, 1)

        @block.scalar
        def _(act):
            act.wait_ge(loads, n_loads)
            act.activation(k.tg[:], graw[:], ACT.Tanh).then_inc(act_done, 1)

        @block.vector
        def _(dve):
            dve.wait_ge(loads, n_loads)
            dve.tensor_copy(tmaskf[:], tmask8[:]).then_inc(vec_done, 1)
            dve.tensor_scalar(k.vmask[:].rearrange("p b s -> p (b s)"), vmask8[:], 1.0, 1e30,
                              ALU.subtract, ALU.mult)
            dve.wait_ge(act_done, 1)
            dve.tensor_scalar(k.gout1[:], rowraw[:, 0, :], k.tg[:, 1:2], None, ALU.mult)
            dve.tensor_scalar(k.bout1[:], rowraw[:, 1, :], k.tg[:, 1:2], None, ALU.mult)
            dve.tensor_tensor(k.wup[64:65], k.wup[64:65], bbase[64:65], ALU.add)
            dve.wait_ge(pool_done, 14)
            row = k.wfilm[C:C + 1, :].rearrange("p (a n) -> p a n", a=2)
            dve.tensor_scalar(row, row, mgate[C:C + 1, 0:1], None, ALU.mult).then_inc(vec_done, 1)
            dve.wait_ge(vec_done, 2)
            dve.tensor_scalar(row[:, :, 0:128], row[:, :, 0:128], 1.0, None, ALU.add)
            dve.wait_ge(turned, 1)
            dve.tensor_copy(wv1T[:], ps[:, 2, 136:136 + C]).then_inc(copied, 1)
            dve.tensor_copy(wd2T[:], ps[:, 3, 0:256].rearrange("p (q n) -> p q n", q=2)).then_inc(copied, 1)
            dve.tensor_copy(k.wv0T[:], ps[:, 2, 0:64]).then_inc(copied, 1)
            dve.tensor_copy(k.wt0T[:], ps[0:C, 2, 64:128]).then_inc(copied, 1)
            dve.tensor_copy(k.gateT[:], ps[:, 2, 128:136])
            dve.tensor_scalar(k.bd2T[:], ps[:, 2, 232:240], -2.0, None, ALU.mult).then_inc(vec_done, 1)
            dve.tensor_copy(k.tmask[:], ps[:, 2, 240:240 + B])
            for h in range(2):
                dve.tensor_copy(k.expT[:, 4 * h:4 * h + 4, :],
                                ps[:, h, :].rearrange("p (e d) -> p e d", e=4))
            dve.wait_ge(vec_done, 3)
            dve.scalar_tensor_tensor(out=k.bd2q[:], in0=k.bd2T[:], scalar=S / 4.0, in1=k.bd2T[:], op0=ALU.mult,
                                     op1=ALU.mult)
            dve.wait_ge(gram_ps, 1)
            for q in range(2):
                g0, o0, x0 = ((0, 128, 129), (129, 0, 1))[q]
                for e in range(4):
                    p = slice(32 * e, 32 * e + 32)
                    dve.tensor_copy(k.dcoef[p, q, g0 + 32 * e:g0 + 32 * e + 32],
                                    ps[p, 5, 128 * q + 32 * e:128 * q + 32 * e + 32])
                dve.tensor_scalar(k.dcoef[:, q, x0:x0 + 128], nat_wd2[:, q, :], -2.0, None, ALU.mult)
                dve.scalar_tensor_tensor(out=junk[:], in0=nat_wd2[:, q, :], scalar=2.0, in1=bd2bc[:, q, :],
                                         op0=ALU.mult, op1=ALU.mult,
                                         accum_out=k.dcoef[:, q, o0:o0 + 1]).then_inc(vec_done, 1)
                dve.wait_ge(vec_done, 4 + q)
            dve.wait_ge(film_ps, 1)
            dve.tensor_scalar(k.wfilm[0:C, :], ps[0:C, 4, :], mgate[0:C, 0:1], None, ALU.mult)


def stage_cosine(nc, w, ps, k):
    LEAST = 1e-37
    with ExitStack() as ctx:
        def tmp(name, shape, dt=F32):
            return ctx.enter_context(nc.sbuf_tensor("a_" + name, shape, dt))

        nm = Norm(lambda n, s: ctx.enter_context(nc.sbuf_tensor(n, s, F32)), "a")
        xn, xnT = tmp("xn", [128, 2, G, 128]), tmp("xnT", [128, 2, W])
        cx = tmp("cx", [128, 2, G, C])
        vT, tT = tmp("vT", [64, 2, W]), tmp("tT", [64, 2, W])
        v2, t2 = tmp("v2", [64, 2, W]), tmp("t2", [64, 2, W])
        inv = tmp("inv", [128, 2, 2 * G])
        scale, prod = tmp("scale", [128, 2, W]), tmp("prod", [128, 2, W])
        s = signals(nc, k, "a", **NORM, cx0=16, cx1=16, xnT_ps=2, cT_ps=2, xnT=2, cT=2, vt_ps=4, vt=8, norms=2,
                    squares=2, inv=2, inv_t=2, dots=2, scale=2 * G, prod=2, x=2)
        block = ctx.enter_context(nc.Block())
        c_dram = w["ctx_768"].rearrange("b s c -> s b c")

        @block.sync
        def _(sp):
            with sp.Fori(0, TURNS) as t:
                for u in range(2):
                    s["cT_ps"].wait(sp, t, 0)
                    sp.dma_start(cx[:, u], c_dram[:, bass.ds(t * PAIR + u * G, G), :]).then_inc(s[f"cx{u}"].sem, 16)

        @block.gpsimd
        def _(pool):
            def body(t, next_rstd):
                for u in range(2):
                    s["squares"].wait(pool, t, u + 1)
                    pool.tensor_tensor(inv[:, u], inv[:, u], k.half[:], ALU.pow).then_inc(s["inv"].sem, 1)
                next_rstd()

            turns(pool, lambda t: norm_rstd(pool, nm, s, t, k.half[:]), body)

        @block.tensor
        def _(pe):
            with pe.Fori(0, TURNS) as t:
                for u in range(2):
                    s[f"cx{u}"].wait(pe, t, 16)
                    s["x"].wait(pe, t, 0)
                    for j in range(G):
                        m = pe.transpose(ps[0:C, 4 * u + 1, j * S:(j + 1) * S], cx[:, u, j, :], k.ident[:])
                    m.then_inc(s["cT_ps"].sem, 1)
                    transpose_tokens(pe, s, t, u, xn, ps[:, 4 * u, :], k.ident[:])
                for u in range(2):
                    s["cT"].wait(pe, t, u + 1)
                    s["xnT"].wait(pe, t, u + 1)
                    pe.matmul(ps[0:64, 4 * u + 2, :], k.wv0T[:], xnT[:, u], start=True,
                              stop=True).then_inc(s["vt_ps"].sem, 1)
                    pe.matmul(ps[0:64, 4 * u + 3, :], k.wt0T[:], k.cT[:, bass.ds(t * 2 * W + u * W, W)],
                              start=True, stop=True).then_inc(s["vt_ps"].sem, 1)
                for u in range(2):
                    s["vt"].wait(pe, t, 4 * (u + 1))
                    for i, sq in ((0, v2), (G, t2)):
                        for j in range(G):
                            m = pe.matmul(ps[:, 4 * u, i + j:i + j + 1], sq[:, u, j * S:(j + 1) * S],
                                          k.ones[0:64, 0:1], start=True, stop=True)
                    m.then_inc(s["norms"].sem, 1)
                    for j in range(G):
                        m = pe.matmul(ps[:, 4 * u + 2, j * S:(j + 1) * S], vT[:, u, j * S:(j + 1) * S],
                                      tT[:, u, j * S:(j + 1) * S], start=True, stop=True)
                    m.then_inc(s["dots"].sem, 1)
                for u in range(2):
                    s["inv"].wait(pe, t, u + 1)
                    for j in range(G):
                        m = pe.transpose(ps[:, 4 * u + 1, j * S:(j + 1) * S],
                                         inv[:, u, G + j:G + j + 1].broadcast_to([128, 128]), k.ident[:])
                    m.then_inc(s["inv_t"].sem, 1)

        @block.scalar
        def _(act):
            with act.Fori(0, TURNS) as t:
                for u in range(2):
                    s["xnT_ps"].wait(act, t, u + 1)
                    act.activation(xnT[:, u], ps[:, 4 * u, :], ACT.Identity).then_inc(s["xnT"].sem, 1)
                for u in range(2):
                    s["vt_ps"].wait(act, t, 2 * u + 2)
                    for dst, func, bank, bias in ((vT, ACT.Identity, 2, k.bv0), (v2, ACT.Square, 2, k.bv0),
                                                  (tT, ACT.Identity, 3, k.bt0), (t2, ACT.Square, 3, k.bt0)):
                        act.activation(dst[:, u], ps[0:64, 4 * u + bank, :], func,
                                       bias=bias[:]).then_inc(s["vt"].sem, 1)

        @block.vector
        def _(dve):
            def body(t, next_norm):
                for u in range(2):
                    s["cT_ps"].wait(dve, t, u + 1)
                    dve.tensor_copy(k.cT[:, bass.ds(t * 2 * W + u * W, W)],
                                    ps[0:C, 4 * u + 1, :]).then_inc(s["cT"].sem, 1)
                for part in range(3):
                    next_norm(part)
                for u in range(2):
                    s["norms"].wait(dve, t, u + 1)
                    dve.tensor_scalar(inv[:, u], ps[:, 4 * u, 0:2 * G], LEAST, None,
                                      ALU.max).then_inc(s["squares"].sem, 1)
                for part in range(3, NORM_PARTS):
                    next_norm(part)
                for u in range(2):
                    s["inv_t"].wait(dve, t, u + 1)
                    for j in range(G):
                        dve.tensor_scalar(scale[:, u, j * S:(j + 1) * S], ps[:, 4 * u + 1, j * S:(j + 1) * S],
                                          inv[:, u, j:j + 1], 1e8, ALU.mult, ALU.min).then_inc(s["scale"].sem, 1)
                    s["scale"].wait(dve, t, G * (u + 1))
                    s["dots"].wait(dve, t, u + 1)
                    dve.tensor_tensor(prod[:, u], ps[:, 4 * u + 2, :], scale[:, u],
                                      ALU.mult).then_inc(s["prod"].sem, 1)
                    s["prod"].wait(dve, t, u + 1)
                    xg = k.X[:, bass.ds(t * PAIR + u * G, G), :]
                    dve.scalar_tensor_tensor(out=xg, in0=prod[:, u].rearrange("p (j d) -> p j d", j=G),
                                             scalar=k.tg[:, 0:1], in1=xg, op0=ALU.mult,
                                             op1=ALU.add).then_inc(s["x"].sem, 1)

            turns(dve, lambda t, part: norm_turn(dve, nm, s, t, part, k, xn), body, NORM_PARTS)


def stage_experts(nc, w, ps, k):
    with ExitStack() as ctx:
        def tmp(name, shape, dt=F32):
            return ctx.enter_context(nc.sbuf_tensor("b_" + name, shape, dt))

        nm = Norm(lambda n, s: ctx.enter_context(nc.sbuf_tensor(n, s, F32)), "b")
        xn, xnT = tmp("xn", [128, 2, G, 128]), tmp("xnT", [128, 2, W])
        lg, top = tmp("lg", [128, 2, G, 8]), tmp("top", [128, 2, G, 8])
        at, atf = tmp("at", [128, 2, G, 8], U32), tmp("atf", [128, 2, G, 2])
        gap, e2, tot = tmp("gap", [128, 2, G]), tmp("e2", [128, 2, G]), tmp("tot", [128, 2, G])
        wt = tmp("wt", [128, 2, G, 2])
        hit, wf = tmp("hit", [128, 2, G, 2, 8]), tmp("wf", [128, 2, G, 8])
        part = tmp("part", [128, 2, 4, 128])
        half_sum, whole = tmp("half_sum", [128, 2, 128]), tmp("whole", [128, 128])
        s = signals(nc, k, "b", **NORM, xnT_ps=2, xnT=2, lg_ps=2, lg=2, top=2 * G, at=2 * G, atf=2, gap=2,
                    e2=2, tot=2, rtot=2, w1=2, w2=2, hit=4, whit=4, wf=2, out_ps=2 * G, x=2 * G * 4,
                    scaled=2 * G * 4, half_sum=2 * G, part=2 * G, xb=2 * G)
        block = ctx.enter_context(nc.Block())

        @block.gpsimd
        def _(pool):
            def body(t, next_rstd):
                for i in range(2 * G):
                    if i == 2 * G - 2:
                        next_rstd()
                    s["scaled"].wait(pool, t, 4 * (i + 1))
                    pool.tensor_tensor(half_sum[:], part[:, i % 2, 0:2], part[:, i % 2, 2:4],
                                       ALU.add).then_inc(s["half_sum"].sem, 1)
                    s["half_sum"].wait(pool, t, i + 1)
                    pool.tensor_tensor(whole[:], half_sum[:, 0], half_sum[:, 1], ALU.add).then_inc(s["part"].sem, 1)
                    s["part"].wait(pool, t, i + 1)
                    s["x"].wait_apart(pool, t, 4 * (i + 1))
                    x_ = k.X[:, bass.ds(t * PAIR + i, 1), :].rearrange("p o d -> p (o d)")
                    pool.tensor_tensor(x_, x_, whole[:], ALU.add).then_inc(s["xb"].sem, 1)
                    s["xb"].wait(pool, t, i + 1)

            turns(pool, lambda t: norm_rstd(pool, nm, s, t, k.half[:]), body)

        @block.tensor
        def _(pe):
            with pe.Fori(0, TURNS) as t:
                for u in range(2):
                    s["x"].wait(pe, t, 0)
                    s["scaled"].wait(pe, t, 0)
                    transpose_tokens(pe, s, t, u, xn, ps[:, 4 * u, :], k.ident[:])
                for u in range(2):
                    s["xnT"].wait(pe, t, u + 1)
                    for j in range(G):
                        m = pe.matmul(ps[:, 4 * u + 1, 8 * j:8 * j + 8], xnT[:, u, j * S:(j + 1) * S],
                                      k.gateT[:], start=True, stop=True)
                    m.then_inc(s["lg_ps"].sem, 1)
                for u in range(2):
                    s["lg"].wait(pe, t, u + 1)
                    for j in range(G):
                        bank = 4 * u + (2, 0)[j % 2]
                        if j >= 2:
                            s["x"].wait(pe, t, 4 * (G * u + j - 1))
                            s["scaled"].wait(pe, t, 4 * (G * u + j - 1))
                        for h in range(2):
                            m = pe.matmul(ps[:, bank + h, :], xnT[:, u, j * S:(j + 1) * S],
                                          k.expT[:, 4 * h:4 * h + 4, :].rearrange("p e d -> p (e d)"),
                                          start=True, stop=True)
                        m.then_inc(s["out_ps"].sem, 1)

        @block.scalar
        def _(act):
            with act.Fori(0, TURNS) as t:
                for u in range(2):
                    s["xnT_ps"].wait(act, t, u + 1)
                    act.activation(xnT[:, u], ps[:, 4 * u, :], ACT.Identity).then_inc(s["xnT"].sem, 1)
                for u in range(2):
                    s["gap"].wait(act, t, u + 1)
                    act.activation(e2[:, u], gap[:, u], ACT.Exp).then_inc(s["e2"].sem, 1)
                for u in range(2):
                    s["wf"].wait(act, t, u + 1)
                    for j in range(G):
                        i = G * u + j
                        s["out_ps"].wait(act, t, i + 1)
                        s["half_sum"].wait(act, t, max(i - 1, 0))
                        for e in range(4):
                            act.activation(part[:, i % 2, e, :],
                                           ps[:, 4 * u + (3, 1)[j % 2], 128 * e:128 * e + 128], ACT.Identity,
                                           scale=wf[:, u, j, 4 + e:5 + e]).then_inc(s["scaled"].sem, 1)

        @block.vector
        def _(dve):
            def body(t, next_norm):
                xj = [[k.X[:, bass.ds(t * PAIR + u * G + j, 1), :] for j in range(G)] for u in range(2)]
                for u in range(2):
                    s["lg_ps"].wait(dve, t, u + 1)
                    dve.tensor_copy(lg[:, u].rearrange("p j e -> p (j e)"),
                                    ps[:, 4 * u + 1, 0:8 * G]).then_inc(s["lg"].sem, 1)
                    s["lg"].wait_apart(dve, t, u + 1)
                    for j in range(G):
                        dve.max(top[:, u, j, :], lg[:, u, j, :]).then_inc(s["top"].sem, 1)
                    s["top"].wait_apart(dve, t, G * (u + 1))
                    for j in range(G):
                        dve.max_index(at[:, u, j, :], top[:, u, j, :], lg[:, u, j, :]).then_inc(s["at"].sem, 1)
                    dve.tensor_tensor(gap[:, u], top[:, u, :, 1], top[:, u, :, 0],
                                      ALU.subtract).then_inc(s["gap"].sem, 1)
                for u in range(2):
                    s["at"].wait(dve, t, G * (u + 1))
                    dve.tensor_copy(atf[:, u], at[:, u, :, 0:2]).then_inc(s["atf"].sem, 1)
                    s["e2"].wait(dve, t, u + 1)
                    dve.tensor_scalar(tot[:, u], e2[:, u], 1.0, None, ALU.add).then_inc(s["tot"].sem, 1)
                    s["tot"].wait(dve, t, u + 1)
                    dve.reciprocal(tot[:, u], tot[:, u]).then_inc(s["rtot"].sem, 1)
                    s["rtot"].wait(dve, t, u + 1)
                    dve.tensor_scalar(wt[:, u, :, 0], tot[:, u], k.tg[:, 4:5], None,
                                      ALU.mult).then_inc(s["w1"].sem, 1)
                    s["w1"].wait(dve, t, u + 1)
                    dve.tensor_tensor(wt[:, u, :, 1], wt[:, u, :, 0], e2[:, u],
                                      ALU.mult).then_inc(s["w2"].sem, 1)
                    s["w2"].wait(dve, t, u + 1)
                    s["atf"].wait(dve, t, u + 1)
                    for i in range(2):
                        dve.tensor_tensor(hit[:, u, :, i, :], k.iota8[:].rearrange("p (j e) -> p j e", j=1).broadcast_to([128, G, 8]),
                                          atf[:, u, :, i:i + 1].broadcast_to([128, G, 8]),
                                          ALU.is_equal).then_inc(s["hit"].sem, 1)
                    s["hit"].wait(dve, t, 2 * u + 2)
                    for i in range(2):
                        dve.tensor_tensor(hit[:, u, :, i, :], hit[:, u, :, i, :],
                                          wt[:, u, :, i:i + 1].broadcast_to([128, G, 8]),
                                          ALU.mult).then_inc(s["whit"].sem, 1)
                    s["whit"].wait(dve, t, 2 * u + 2)
                    s["scaled"].wait(dve, t, 0)
                    dve.tensor_tensor(wf[:, u], hit[:, u, :, 0, :], hit[:, u, :, 1, :],
                                      ALU.add).then_inc(s["wf"].sem, 1)
                for u in range(2):
                    s["wf"].wait(dve, t, u + 1)
                    for j in range(G):
                        bank = 4 * u + (2, 0)[j % 2]
                        if G * u + j >= 2 * G - NORM_PARTS:
                            next_norm(G * u + j - (2 * G - NORM_PARTS))
                        s["out_ps"].wait(dve, t, G * u + j + 1)
                        for e in range(4):
                            if e:
                                s["x"].wait(dve, t, 4 * (G * u + j) + e)
                            dve.scalar_tensor_tensor(
                                out=xj[u][j], in0=ps[:, bank, 128 * e:128 * e + 128],
                                scalar=wf[:, u, j, e:e + 1], in1=xj[u][j], op0=ALU.mult,
                                op1=ALU.add).then_inc(s["x"].sem, 1)

            turns(dve, lambda t, part: norm_turn(dve, nm, s, t, part, k, xn), body, NORM_PARTS)


def setup_kernel(nc, w, ps, k, start_loads):
    N, NA, NB = 64, 8, 16
    M = NA + NB + NA + 1
    PI = 3.14159265358979
    TWO_PI = (6.28125, 1.9340515136718750e-3, 1.2556659146e-6)
    ROUND = 1.5 * 2.0 ** 23
    with ExitStack() as ctx:
        def tmp(name, shape, dt=F32):
            return ctx.enter_context(nc.sbuf_tensor("s4_" + name, shape, dt))

        sem = ctx.enter_context(OneTime(nc, "s4_"))

        nat = tmp("nat", [128, 4, 2, N])
        par = tmp("par", [128, 4, 128])
        ldt, drow = tmp("ldt", [128, 128]), tmp("drow", [1, 128])
        mi, mf = tmp("mi", [128, M], I32), tmp("mf", [128, M])
        ph = tmp("ph", [128, 2])
        sgn = tmp("sgn", [128, 1])
        dta = tmp("dta", [128, 2, 128])
        arg, kk, ex = tmp("arg", [128, 128, M]), tmp("kk", [128, 128, M]), tmp("ex", [128, 128, M])
        tt = kk
        sm = tmp("sm", [128, 12, 128])
        pq, pq2 = tmp("pq", [128, 128, NA]), tmp("pq2", [128, 128, NA])
        spare = k.x3[:].rearrange("p c b -> p (c b)")
        k2 = spare[0:NA, 0:128 * NB].rearrange("p (d b) -> p d b", b=NB)
        zero = spare[:, 128 * NB:128 * NB + 127]
        loads, consts, turned, kps = sem("loads"), sem("consts"), sem("turned"), sem("kps")
        act_dt, vec_arg, act_ex, vec_red, act_sin = (sem(n) for n in ("act_dt", "vec_arg", "act_ex", "vec_red",
                                                                     "act_sin"))
        chain, vec_pq, vec_k2, stored = sem("chain"), sem("vec_pq"), sem("vec_k2"), sem("stored")
        block = ctx.enter_context(nc.Block())

        @block.sync
        def _(sp):
            for i, name in enumerate(("A_re", "A_im", "C_re", "C_im")):
                for h in range(2):
                    sp.dma_start(nat[:, i, h, :], w["L1_xattn_" + name]).then_inc(loads, 16)
            sp.dma_start(ldt[:], row_of(w["L1_xattn_log_dt"]).broadcast_to([128, 128])).then_inc(loads, 16)
            sp.dma_start(drow[:], row_of(w["L1_xattn_D_skip"])).then_inc(loads, 16)
            start_loads(sp)
            sp.wait_ge(consts, 9)
            sp.dma_start(k.kpad[:, 0:127], zero[:]).then_inc(stored, 16)
            sp.wait_ge(vec_k2, 1)
            sp.dma_start(k.kpad[:, 127:255].rearrange("d (a b) -> a d b", b=NB), k2[:]).then_inc(stored, 16)
            sp.wait_ge(stored, 32)

        @block.gpsimd
        def _(pool):
            pool.iota(mi[:, 0:8], pattern=[[16, 8]], base=0, channel_multiplier=0).then_inc(consts, 1)
            pool.iota(mi[:, 8:24], pattern=[[1, 16]], base=0, channel_multiplier=0).then_inc(consts, 1)
            pool.iota(mi[:, 24:32], pattern=[[16, 8]], base=0, channel_multiplier=0).then_inc(consts, 1)
            pool.iota(mi[:, 32:33], pattern=[[1, 1]], base=1, channel_multiplier=0).then_inc(consts, 1)
            pool.memset(ph[:], 0.0).then_inc(consts, 1)
            pool.memset(sgn[:], 1.0).then_inc(consts, 1)
            pool.wait_ge(consts, 6)
            pool.memset(ph[0:N, 0:1], PI / 2).then_inc(consts, 1)
            pool.wait_ge(consts, 7)
            pool.memset(ph[N:128, 1:2], PI / 2).then_inc(consts, 1)
            pool.wait_ge(consts, 8)
            pool.memset(zero[:], 0.0).then_inc(consts, 1)
            pool.wait_ge(consts, 9)
            pool.memset(sgn[N:128], -1.0).then_inc(consts, 1)

        @block.tensor
        def _(pe):
            pe.wait_ge(loads, 160)
            for i in range(4):
                m = pe.transpose(ps[:, 0, 128 * i:128 * i + 128], nat[:, i].rearrange("p h n -> p (h n)"), k.ident[:])
            m.then_inc(turned, 1)
            pe.wait_ge(vec_pq, 1)
            for d in range(128):
                m = pe.matmul(ps[0:NA, 1 + d // 32, NB * (d % 32):NB * (d % 32) + NB], pq[:, d, :],
                              tt[:, d, NA:NA + NB], start=True, stop=True)
            m.then_inc(kps, 1)

        @block.scalar
        def _(act):
            act.wait_ge(loads, 160)
            act.activation(ldt[:], ldt[:], ACT.Exp).then_inc(act_dt, 1)
            act.wait_ge(vec_arg, 1)
            act.activation(ex[:], ex[:], ACT.Exp).then_inc(act_ex, 1)
            act.wait_ge(vec_red, 1)
            act.activation(tt[:], arg[:], ACT.Sin).then_inc(act_sin, 1)

        @block.vector
        def _(dve):
            n = [0]

            def link(ins):
                n[0] += 1
                ins.then_inc(chain, 1)
                dve.wait_ge(chain, n[0])

            dve.wait_ge(consts, 10)
            link(dve.tensor_copy(mf[:], mi[:]))
            dve.wait_ge(turned, 1)
            link(dve.tensor_copy(par[:].rearrange("p i d -> p (i d)"), ps[:, 0, :]))
            dve.wait_ge(act_dt, 1)
            for i in range(2):
                link(dve.tensor_tensor(dta[:, i, :], par[:, i, :], ldt[:], ALU.mult))
            mb = mf[:].rearrange("p (o m) -> p o m", o=1).broadcast_to([128, 128, M])

            def per_channel(t):
                return t.rearrange("p (d o) -> p d o", o=1)

            dve.tensor_tensor(ex[:], per_channel(dta[:, 0, :]).broadcast_to([128, 128, M]), mb,
                              ALU.mult).then_inc(vec_arg, 1)
            link(dve.tensor_tensor(arg[:], per_channel(dta[:, 1, :]).broadcast_to([128, 128, M]), mb, ALU.mult))
            for lo, hi, i in ((0, 24, 0), (24, M, 1)):
                a, q = arg[:, :, lo:hi], kk[:, :, lo:hi]
                link(dve.tensor_scalar(q, a, ph[:, i:i + 1], 1 / (2 * PI), ALU.add, ALU.mult))
                link(dve.tensor_scalar(q, q, ROUND, ROUND, ALU.add, ALU.subtract))
            for c in TWO_PI:
                link(dve.scalar_tensor_tensor(out=arg[:], in0=kk[:], scalar=-c, in1=arg[:], op0=ALU.mult,
                                              op1=ALU.add))
            for lo, hi, i in ((0, 24, 0), (24, M, 1)):
                a = arg[:, :, lo:hi]
                link(dve.tensor_scalar(a, a, ph[:, i:i + 1], 3.1415925, ALU.add, ALU.min))
            dve.tensor_scalar(arg[:], arg[:], -3.1415925, None, ALU.max).then_inc(vec_red, 1)
            dve.wait_ge(act_sin, 1)
            dve.wait_ge(act_ex, 1)
            cos, sin = sm[:, 0, :], sm[:, 1, :]
            dve.tensor_copy(sm[0:N, 0, :], tt[0:N, :, NA + 1])
            dve.tensor_copy(sm[N:128, 0, :], tt[N:128, :, M - 1])
            dve.tensor_copy(sm[0:N, 1, :], tt[0:N, :, M - 1])
            link(dve.tensor_copy(sm[N:128, 1, :], tt[N:128, :, NA + 1]))
            link(dve.tensor_tensor(tt[:], tt[:], ex[:], ALU.mult))
            e1 = ex[:, :, M - 1]
            ar, ai, cr, ci = (par[:, i, :] for i in range(4))
            r = [sm[:, i, :] for i in range(12)]

            def tt_(out, a, b, op):
                link(dve.tensor_tensor(out, a, b, op))

            tt_(r[2], cos, e1, ALU.mult)
            link(dve.tensor_scalar(r[2], r[2], 1.0, None, ALU.subtract))
            tt_(r[3], sin, e1, ALU.mult)
            tt_(r[4], cr, r[2], ALU.mult)
            tt_(r[5], ci, r[3], ALU.mult)
            tt_(r[4], r[4], r[5], ALU.subtract)
            tt_(r[5], cr, r[3], ALU.mult)
            tt_(r[6], ci, r[2], ALU.mult)
            tt_(r[5], r[5], r[6], ALU.add)
            tt_(r[6], ar, ar, ALU.mult)
            tt_(r[7], ai, ai, ALU.mult)
            tt_(r[6], r[6], r[7], ALU.add)
            link(dve.reciprocal(r[6], r[6]))
            tt_(r[7], r[4], ar, ALU.mult)
            tt_(r[8], r[5], ai, ALU.mult)
            tt_(r[7], r[7], r[8], ALU.add)
            tt_(r[8], r[5], ar, ALU.mult)
            tt_(r[9], r[4], ai, ALU.mult)
            tt_(r[8], r[8], r[9], ALU.subtract)
            tt_(r[7], r[7], r[6], ALU.mult)
            tt_(r[8], r[8], r[6], ALU.mult)
            link(dve.tensor_scalar(r[7], r[7], sgn[:, 0:1], 2.0, ALU.mult, ALU.mult))
            link(dve.tensor_scalar(r[8], r[8], 2.0, None, ALU.mult))
            tt_(pq[:], tt[:, :, 0:NA], per_channel(r[7]).broadcast_to([128, 128, NA]), ALU.mult)
            tt_(pq2[:], tt[:, :, NA + NB:NA + NB + NA], per_channel(r[8]).broadcast_to([128, 128, NA]), ALU.mult)
            dve.tensor_tensor(pq[:], pq[:], pq2[:], ALU.subtract).then_inc(vec_pq, 1)
            dve.wait_ge(kps, 1)
            for b in range(4):
                link(dve.tensor_copy(k2[:, 32 * b:32 * b + 32, :].rearrange("p d b -> p (d b)"),
                                     ps[0:NA, 1 + b, :]))
            dve.tensor_tensor(k2[0:1, :, 0], k2[0:1, :, 0], drow[:], ALU.add).then_inc(vec_k2, 1)


CH = 16
CHUNKS = D // CH
EARLY = CHUNKS // 2


def load_toeplitz(sp, k, c, dst):
    src = bass.AP(tensor=k.kpad.tensor, offset=256 * CH * c, ap=[[1, 128], [256, CH], [1, 128]])
    sp.dma_start(dst, src).then_inc(k.toep_in[c], 16)


def stage_film(nc, w, ps, k):
    with ExitStack() as ctx:
        k.toep = ctx.enter_context(nc.sbuf_tensor("v_toep", [128, EARLY, CH, 128], F32))
        once = ctx.enter_context(OneTime(nc, "v_in_"))
        k.toep_in = [once(f"toep_in{i}") for i in range(CHUNKS)]
        film_in(nc, w, ps, k)
        convolve(nc, w, ps, k)
    film_out(nc, w, ps, k)


def film_in(nc, w, ps, k):
    H, DH, ROUNDS = 4, 32, 4
    SCALE = DH ** -0.5
    TAKEN = -3e38
    NB_ = PAIR
    AHEAD = 4
    LAG = 4
    with ExitStack() as ctx:
        def tmp(name, shape, dt=F32):
            return ctx.enter_context(nc.sbuf_tensor("c_" + name, shape, dt))

        nm = Norm(lambda n, s: ctx.enter_context(nc.sbuf_tensor(n, s, F32)), "c")
        xn, xnT = tmp("xn", [128, 2, G, 128]), tmp("xnT", [128, 2, W])
        rstd2 = tmp("rstd2", [128, NB_])
        x2 = tmp("x2", [128, NB_, 128])
        cx = tmp("cx", [128, 2, C])
        qT, kT = tmp("qT", [128, 2, W]), tmp("kT", [128, 2, W])
        hmask = tmp("hmask", [128, H])
        km = tmp("km", [128, AHEAD, H, 128])
        sc, left, ex = tmp("sc", [128, 2, H, 128]), tmp("left", [128, 2, H, 128]), tmp("ex", [128, 2, H, 128])
        first, top = tmp("first", [128, 2, H, 8]), tmp("top", [128, 2, H, 8])
        shift, total = tmp("shift", [128, 2, H]), tmp("total", [128, 2, H])
        share = tmp("share", [128, 2, H])
        part, half_sum, mean_w = tmp("part", [128, H, 128]), tmp("half_sum", [128, 2, 128]), tmp("mean_w", [128, 2, 128])
        wT, aT = tmp("wT", [128, 128]), tmp("aT", [C + 1, 128])
        fo = tmp("fo", [128, 2, 512])
        s = signals(nc, k, "c", **NORM, rr=1, vr=1, ve2=1, rstd2=1, kept=2, xnT_ps=2, xnT=2, x2a=1, x2b=1, x2c=1,
                    qk_ps=2, qT=2, kT=2, km=NB_, sc_ps=NB_, sc=NB_, top=NB_ * H * ROUNDS, left=NB_ * H * ROUNDS,
                    shift=NB_, ex=NB_ * H, keep=NB_ * H, rtot=NB_, share=NB_, part=NB_, half_sum=NB_, mean_w=NB_,
                    cx0=NB_ * 8, cx1=NB_ * 8, wT_ps=NB_, wT=NB_, aT_ps=NB_, aT=NB_, film_ps=NB_, fo=NB_,
                    filmed=NB_, x3=NB_, fo_out0=NB_ * 8, fo_out1=NB_ * 8)
        consts = ctx.enter_context(OneTime(nc, "c_"))("consts")
        block = ctx.enter_context(nc.Block())
        c_dram = w["ctx_768"].rearrange("b s c -> s b c")

        @block.sync
        def _(sp):
            def body(t, _):
                for i in range(NB_):
                    a = i % 2
                    s["aT_ps"].wait(sp, t, max(i - 1, 0) if i >= 2 else 0)
                    sp.dma_start(cx[:, a], c_dram[:, bass.ds(t * NB_ + i, 1), :].rearrange("s b c -> s (b c)")
                                 ).then_inc(s[f"cx{a}"].sem, 16)
                    if i >= 1:
                        put(t, i - 1)
                put(t, NB_ - 1)

            def put(t, i):
                s["fo"].wait(sp, t, i + 1)
                sp.dma_start(k.fo_dram[:, bass.ds(t * NB_ + i, 1), :].rearrange("s b c -> s (b c)"),
                             fo[:, i % 2, 256:512]).then_inc(s[f"fo_out{i % 2}"].sem, 16)

            for c in range(EARLY):
                load_toeplitz(sp, k, c, k.toep[:, c])
            turns(sp, lambda t: None, body)
            for a in range(2):
                s[f"fo_out{a}"].wait(sp, TURNS - 1, NB_ * 8)

        @block.gpsimd
        def _(pool):
            pool.memset(aT[C:C + 1], 1.0).then_inc(consts, 1)
            pool.wait_ge(consts, 1)
            pool.memset(hmask[:], 0.0).then_inc(consts, 1)
            for h in range(H):
                pool.wait_ge(consts, 2 + h)
                pool.memset(hmask[DH * h:DH * h + DH, h:h + 1], 1.0).then_inc(consts, 1)
            pool.wait_ge(consts, 2 + H)

            def masked_k(t, i):
                s["kT"].wait(pool, t, i // G + 1)
                s["sc_ps"].wait(pool, t, max(i - AHEAD + 1, 0))
                pool.tensor_tensor(km[:, i % AHEAD],
                                   kT[:, i // G, (i % G) * S:(i % G) * S + S].rearrange("p (h t) -> p h t", h=1)
                                   .broadcast_to([128, H, 128]),
                                   hmask[:].rearrange("p (h o) -> p h o", o=1).broadcast_to([128, H, 128]),
                                   ALU.mult).then_inc(s["km"].sem, 1)

            def powers(t):
                norm_rstd(pool, nm, s, t, k.half[:])
                s["ve2"].wait(pool, t, 1)
                pool.tensor_tensor(rstd2[:], rstd2[:], k.half[:], ALU.pow).then_inc(s["rstd2"].sem, 1)

            def opening(t):
                s["rstd2"].wait(pool, t, 1)
                s["xn"].wait(pool, t, NB_)
                s["x3"].wait(pool, t, 0)
                xr = xn[:].rearrange("p u j d -> p (u j) d")

                def rows(v):
                    return v[:].rearrange("p (j d) -> p j d", j=1).broadcast_to([128, NB_, 128])

                pool.tensor_tensor(x2[:], xr, rstd2[:].rearrange("p (j o) -> p j o", o=1).broadcast_to([128, NB_, 128]),
                                   ALU.mult).then_inc(s["x2a"].sem, 1)
                s["x2a"].wait(pool, t, 1)
                pool.tensor_tensor(x2[:], x2[:], rows(k.gin1), ALU.mult).then_inc(s["x2b"].sem, 1)
                s["x2b"].wait(pool, t, 1)
                pool.tensor_tensor(x2[:], x2[:], rows(k.bin1), ALU.add).then_inc(s["x2c"].sem, 1)

            def film(t, i):
                x3 = k.x3[:, :, bass.ds(t * NB_ + i, 1)]
                f = fo[:, i % 2, :]
                s["fo"].wait(pool, t, i + 1)
                s["x2c"].wait(pool, t, 1)
                pool.tensor_tensor(x2[:, i], x2[:, i], f[:, 0:128], ALU.mult).then_inc(s["filmed"].sem, 1)
                s["filmed"].wait_apart(pool, t, i + 1)
                pool.tensor_tensor(x3, x2[:, i].rearrange("p (c o) -> p c o", o=1),
                                   f[:, 128:256].rearrange("p (c o) -> p c o", o=1), ALU.add).then_inc(s["x3"].sem, 1)

            def body(t, next_powers, next_masked, next_opening):
                for n in range(NB_ + 2):
                    if n == NB_ - 4:
                        next_powers()
                    if n == NB_ - 2:
                        next_masked()
                    if n + AHEAD < NB_:
                        masked_k(t, n + AHEAD)
                    if n < NB_:
                        a = n % 2
                        s["share"].wait(pool, t, n + 1)
                        if n:
                            s["half_sum"].wait(pool, t, n)
                        pool.tensor_tensor(part[:], ex[:, a], share[:, a, :].rearrange("p (h o) -> p h o", o=1)
                                           .broadcast_to([128, H, 128]), ALU.mult).then_inc(s["part"].sem, 1)
                        s["part"].wait(pool, t, n + 1)
                        if n:
                            s["mean_w"].wait(pool, t, n)
                        pool.tensor_tensor(half_sum[:], part[:, 0:2], part[:, 2:4], ALU.add).then_inc(s["half_sum"].sem, 1)
                        s["half_sum"].wait(pool, t, n + 1)
                        s["wT_ps"].wait(pool, t, max(n - 1, 0))
                        pool.tensor_tensor(mean_w[:, a], half_sum[:, 0], half_sum[:, 1],
                                           ALU.add).then_inc(s["mean_w"].sem, 1)
                    if n >= 2:
                        film(t, n - 2)
                next_opening()

            def first_masked(t):
                for i in range(AHEAD):
                    masked_k(t, i)

            powers(0)
            first_masked(0)
            opening(0)
            with pool.Fori(0, TURNS - 1) as t:
                body(t, lambda: powers(t + 1), lambda: first_masked(t + 1), lambda: opening(t + 1))
            body(TURNS - 1, lambda: None, lambda: None, lambda: None)

        @block.tensor
        def _(pe):
            pe.wait_ge(consts, 2 + H)

            def turn_xn(t):
                for u in range(2):
                    transpose_tokens(pe, s, t, u, xn, ps[:, 4 + u, :], k.ident[:])

            def project(t):
                for u in range(2):
                    bank = (6, 4)[u]
                    s["xnT"].wait(pe, t, 2)
                    pe.matmul(ps[:, bank, :], k.wq1[:], xnT[:, u], start=True, stop=True)
                    pe.matmul(ps[:, bank + 1, :], k.wk1[:], k.cT[:, bass.ds(t * 2 * W + u * W, W)],
                              start=True, stop=True).then_inc(s["qk_ps"].sem, 1)

            def scores(t, n):
                s["km"].wait(pe, t, n + 1)
                if n in (0, G):
                    s["qT"].wait(pe, t, n // G + 1)
                s["sc"].wait(pe, t, max(n - 1, 0))
                pe.matmul(ps[:, n % 2, :], qT[:, n // G, (n % G) * S:(n % G) * S + S],
                          km[:, n % AHEAD].rearrange("p h t -> p (h t)"),
                          start=True, stop=True).then_inc(s["sc_ps"].sem, 1)

            def opening(t):
                turn_xn(t)
                project(t)

            def first_scores(t):
                for n in range(2):
                    scores(t, n)

            def body(t, next_opening, next_scores):
                for n in range(2, NB_ + LAG):
                    if n < NB_:
                        scores(t, n)
                    if n >= LAG:
                        i = n - LAG
                        if i == NB_ - 4:
                            next_opening()
                        if i == NB_ - 2:
                            next_scores()
                        s["mean_w"].wait(pe, t, i + 1)
                        s["aT"].wait(pe, t, i)
                        pe.transpose(ps[:, 2, 0:128], mean_w[:, i % 2, :], k.ident[:]).then_inc(s["wT_ps"].sem, 1)
                        s["wT"].wait(pe, t, i + 1)
                        s[f"cx{i % 2}"].wait(pe, t, 16 * (i // 2 + 1))
                        pe.matmul(ps[0:C, 2, 128:256], cx[:, i % 2, :], wT[:], start=True,
                                  stop=True).then_inc(s["aT_ps"].sem, 1)
                        s["aT"].wait(pe, t, i + 1)
                        s["fo"].wait(pe, t, i)
                        pe.matmul(ps[:, 3, :], aT[:], k.wfilm[:], start=True, stop=True).then_inc(s["film_ps"].sem, 1)

            opening(0)
            first_scores(0)
            with pe.Fori(0, TURNS - 1) as t:
                body(t, lambda: opening(t + 1), lambda: first_scores(t + 1))
            body(TURNS - 1, lambda: None, lambda: None)

        @block.scalar
        def _(act):
            act.wait_ge(consts, 2 + H)

            def opening(t):
                for u in range(2):
                    s["xnT_ps"].wait(act, t, u + 1)
                    act.activation(xnT[:, u], ps[:, 4 + u, :], ACT.Identity).then_inc(s["xnT"].sem, 1)
                for u in range(2):
                    bank = (6, 4)[u]
                    s["qk_ps"].wait(act, t, u + 1)
                    s["sc_ps"].wait(act, t, 0)
                    act.activation(qT[:, u], ps[:, bank, :], ACT.Identity).then_inc(s["qT"].sem, 1)
                    act.activation(kT[:, u], ps[:, bank + 1, :], ACT.Identity).then_inc(s["kT"].sem, 1)

            def weigh(t, i):
                a = i % 2
                s["shift"].wait(act, t, i + 1)
                s["part"].wait(act, t, max(i - 1, 0))
                for h in range(H):
                    act.activation(ex[:, a, h, :], sc[:, a, h, :], ACT.Exp, bias=shift[:, a, h:h + 1],
                                   scale=SCALE).then_inc(s["ex"].sem, 1)

            def tail(t, i):
                s["wT_ps"].wait(act, t, i + 1)
                act.activation(wT[:], ps[:, 2, 0:128], ACT.Identity).then_inc(s["wT"].sem, 1)
                s["aT_ps"].wait(act, t, i + 1)
                act.activation(aT[0:C], ps[0:C, 2, 128:256], ACT.Identity).then_inc(s["aT"].sem, 1)
                s["film_ps"].wait(act, t, i + 1)
                s["x3"].wait(act, t, max(i - 1, 0))
                s[f"fo_out{i % 2}"].wait(act, t, 16 * (i // 2))
                act.activation(fo[:, i % 2, :], ps[:, 3, :], ACT.Identity).then_inc(s["fo"].sem, 1)

            def body(t, next_opening):
                for n in range(NB_ // 2 + 1):
                    if n < NB_ // 2:
                        weigh(t, 2 * n)
                        weigh(t, 2 * n + 1)
                    if n == NB_ // 2 - 1:
                        next_opening()
                    if n >= 1:
                        tail(t, 2 * n - 2)
                        tail(t, 2 * n - 1)

            turns(act, opening, body)

        @block.vector
        def _(dve):
            def stats(t):
                s["rstd2"].wait(dve, t, 0)
                s["xn"].wait(dve, t, 0)
                norm_stats(dve, nm, s, t,
                           lambda u, j: k.X[:, bass.ds(t * PAIR + u * G + j, 1), :])

            def opening(t):
                xj = [[k.X[:, bass.ds(t * PAIR + u * G + j, 1), :] for j in range(G)] for u in range(2)]
                s["xnT_ps"].wait(dve, t, 0)
                s["x2a"].wait(dve, t, 0)
                for u in range(2):
                    norm_apply(dve, nm, s, t, u, lambda u, j: xj[u][j], xn)
                rs, ve = nm.rstd[:].rearrange("p u j -> p (u j)"), nm.ve[:].rearrange("p u j -> p (u j)")
                dve.tensor_tensor(rstd2[:], rs, rs, ALU.mult).then_inc(s["rr"].sem, 1)
                s["rr"].wait(dve, t, 1)
                dve.scalar_tensor_tensor(out=rstd2[:], in0=ve, scalar=EPS, in1=rstd2[:], op0=ALU.subtract,
                                         op1=ALU.mult).then_inc(s["vr"].sem, 1)
                s["vr"].wait(dve, t, 1)
                dve.tensor_scalar(rstd2[:], rstd2[:], EPS, None, ALU.add).then_inc(s["ve2"].sem, 1)
                dve.tensor_copy(k.mean1[:, bass.ds(t * PAIR, PAIR)],
                                nm.mean[:].rearrange("p u j -> p (u j)")).then_inc(s["kept"].sem, 1)
                dve.tensor_copy(k.rstd1[:, bass.ds(t * PAIR, PAIR)], rs).then_inc(s["kept"].sem, 1)

            def body(t, next_stats, next_opening):
                for pair in range(NB_ // 2):
                    both = (2 * pair, 2 * pair + 1)
                    if pair == NB_ // 2 - 2:
                        next_stats()
                    if pair == NB_ // 2 - 1:
                        next_opening()
                    for i in both:
                        s["sc_ps"].wait(dve, t, i + 1)
                        s["ex"].wait(dve, t, H * max(i - 1, 0))
                        dve.tensor_tensor(sc[:, i % 2], ps[:, i % 2, :].rearrange("p (h t) -> p h t", h=H),
                                          k.vmask[:, bass.ds(t * NB_ + i, 1), :].broadcast_to([128, H, 128]),
                                          ALU.add).then_inc(s["sc"].sem, 1)
                    for r in range(ROUNDS):
                        done = 2 * H * (ROUNDS * pair + r)
                        for a in range(2):
                            if r:
                                s["left"].wait_apart(dve, t, done - 2 * H + H * (a + 1))
                            else:
                                s["sc"].wait_apart(dve, t, both[a] + 1)
                            for h in range(H):
                                dve.max((first if r == 0 else top)[:, a, h, :],
                                        (sc if r == 0 else left)[:, a, h, :]).then_inc(s["top"].sem, 1)
                        for a in range(2):
                            s["top"].wait_apart(dve, t, done + H * (a + 1))
                            if r == 0:
                                dve.tensor_scalar(shift[:, a, :], first[:, a, :, 0], -SCALE, None,
                                                  ALU.mult).then_inc(s["shift"].sem, 1)
                            for h in range(H):
                                dve.match_replace(left[:, a, h, :], (first if r == 0 else top)[:, a, h, :],
                                                  (sc if r == 0 else left)[:, a, h, :],
                                                  TAKEN).then_inc(s["left"].sem, 1)
                    for i in both:
                        a = i % 2
                        s["left"].wait(dve, t, 2 * H * ROUNDS * pair + 2 * H * (ROUNDS - 1) + H * (a + 1))
                        s["ex"].wait(dve, t, H * (i + 1))
                        for h in range(H):
                            dve.scalar_tensor_tensor(out=ex[:, a, h, :], in0=left[:, a, h, :], scalar=TAKEN * 0.5,
                                                     in1=ex[:, a, h, :], op0=ALU.is_le, op1=ALU.mult,
                                                     accum_out=total[:, a, h:h + 1]).then_inc(s["keep"].sem, 1)
                    for i in both:
                        a = i % 2
                        s["keep"].wait(dve, t, H * (i + 1))
                        dve.reciprocal(total[:, a, :], total[:, a, :]).then_inc(s["rtot"].sem, 1)
                    for i in both:
                        a = i % 2
                        s["rtot"].wait(dve, t, i + 1)
                        s["part"].wait(dve, t, max(i - 1, 0))
                        dve.scalar_tensor_tensor(out=share[:, a, :], in0=total[:, a, :], scalar=1.0 / H,
                                                 in1=k.tmask[:, bass.ds(t * NB_ + i, 1)].broadcast_to([128, H]),
                                                 op0=ALU.mult, op1=ALU.mult).then_inc(s["share"].sem, 1)

            stats(0)
            opening(0)
            with dve.Fori(0, TURNS - 1) as t:
                body(t, lambda: stats(t + 1), lambda: opening(t + 1))
            body(TURNS - 1, lambda: None, lambda: None)


def convolve(nc, w, ps, k):
    with ExitStack() as ctx:
        late = ctx.enter_context(nc.sbuf_tensor("v_late", [128, CHUNKS - EARLY, CH, 128], F32))
        once = ctx.enter_context(OneTime(nc, "v_"))
        yT = ctx.enter_context(nc.sbuf_tensor("v_yT", [128, 2, CH // 4, 128], F32))
        flip_ps, flipped, yT_ps, yT_out, y_ps = (once(n) for n in ("flip_ps", "flipped", "yT_ps", "yT_out", "y_ps"))
        block = ctx.enter_context(nc.Block())

        def chunk(c):
            return k.x3[:, CH * c:CH * c + CH, :].rearrange("p c b -> p (c b)")

        @block.sync
        def _(sp):
            for c in range(EARLY, CHUNKS):
                load_toeplitz(sp, k, c, late[:, c - EARLY])

        @block.tensor
        def _(pe):
            for c in range(CHUNKS):
                pe.matmul(ps[:, c, :], k.flip[:], chunk(c), start=True, stop=True).then_inc(flip_ps, 1)
            for n in range(CHUNKS + 1):
                if n < CHUNKS:
                    pe.wait_ge(flipped, n + 1)
                    pe.wait_ge(k.toep_in[n], 16)
                    toep = k.toep[:, n] if n < EARLY else late[:, n - EARLY]
                    for i in range(CH):
                        q, r = i // 4, i % 4
                        m = pe.matmul(ps[B * r:B * r + B, n, 128 * q:128 * q + 128], k.x3[:, CH * n + i, :],
                                      toep[:, i, :], start=True, stop=True)
                    m.then_inc(yT_ps, 1)
                if n >= 1:
                    c = n - 1
                    pe.wait_ge(yT_out, c + 1)
                    for q in range(CH // 4):
                        m = pe.transpose(ps[:, c, 128 * q:128 * q + 128], yT[:, c % 2, q, :], k.ident[:])
                    m.then_inc(y_ps, 1)

        @block.scalar
        def _(act):
            for c in range(CHUNKS):
                act.wait_ge(flip_ps, c + 1)
                act.activation(chunk(c), ps[:, c, :], ACT.Identity).then_inc(flipped, 1)
            for c in range(CHUNKS):
                act.wait_ge(yT_ps, c + 1)
                if c >= 2:
                    act.wait_ge(y_ps, c - 1)
                act.activation(yT[:, c % 2].rearrange("p q t -> p (q t)"), ps[:, c, :],
                               ACT.Identity).then_inc(yT_out, 1)

        @block.vector
        def _(dve):
            for c in range(CHUNKS):
                dve.wait_ge(y_ps, c + 1)
                dve.tensor_copy(chunk(c), ps[:, c, :])


def film_out(nc, w, ps, k):
    with ExitStack() as ctx:
        def tmp(name, shape, dt=F32):
            return ctx.enter_context(nc.sbuf_tensor("d_" + name, shape, dt))

        nm1 = Norm(lambda n, s: ctx.enter_context(nc.sbuf_tensor(n, s, F32)), "d1")
        nm2 = Norm(lambda n, s: ctx.enter_context(nc.sbuf_tensor(n, s, F32)), "d2")
        fo = tmp("fo", [128, 2, G, 256])
        z, xt, last = tmp("z", [128, 2, G, 128]), tmp("xt", [128, 2, G, 128]), tmp("last", [128, 2, G, 128])
        xn, hT = tmp("xn", [128, 2, G, 128]), tmp("hT", [128, 2, W])
        hid = tmp("hid", [128, 2, 4, W])
        s = signals(nc, k, "d", fo_in0=16, fo_in1=16, xt=2 * G, zs=2, zh=2, z=2, xnT_ps=2, hT=2,
                    hid_ps=8, hid=8, mlp_ps=2, zm=2, zb=2, og=2, ob=2, x=2)
        s1 = signals(nc, k, "d1", **GROUP_NORM)
        s2 = {n[3:]: v for n, v in signals(nc, k, "d2", **{"n2_" + n: v for n, v in GROUP_NORM.items()}).items()}
        s1["xnT_ps"] = s["xnT_ps"]
        block = ctx.enter_context(nc.Block())

        @block.sync
        def _(sp):
            with sp.Fori(0, TURNS) as t:
                for u in range(2):
                    s["zh"].wait(sp, t, 0)
                    sp.dma_start(fo[:, u], k.fo_dram[:, bass.ds(t * PAIR + u * G, G), :]).then_inc(s[f"fo_in{u}"].sem, 16)

        def rows(v):
            return v[:].rearrange("p (j d) -> p j d", j=1).broadcast_to([128, G, 128])

        @block.gpsimd
        def _(pool):
            def power(nm, sg, t, u):
                sg["ve"].wait(pool, t, u + 1)
                pool.tensor_tensor(nm.rstd[:, u], nm.ve[:, u], k.half[:, 0:G], ALU.pow).then_inc(sg["rstd"].sem, 1)

            def finish(t, u):
                s2["xn"].wait(pool, t, G * (u + 1))
                pool.tensor_tensor(last[:, u], last[:, u], rows(k.gout1), ALU.mult).then_inc(s["og"].sem, 1)
                s["og"].wait(pool, t, u + 1)
                pool.tensor_tensor(last[:, u], last[:, u], rows(k.bout1), ALU.add).then_inc(s["ob"].sem, 1)

            def body(t, next_power):
                power(nm1, s1, t, 1)
                power(nm2, s2, t, 0)
                finish(t, 0)
                next_power()
                power(nm2, s2, t, 1)
                finish(t, 1)

            turns(pool, lambda t: power(nm1, s1, t, 0), body)

        @block.tensor
        def _(pe):
            with pe.Fori(0, TURNS) as t:
                for u in range(2):
                    s["zm"].wait(pe, t, u)
                    transpose_tokens(pe, s1, t, u, xn, ps[:, 4 * u, :], k.ident[:])
                    s["hT"].wait(pe, t, u + 1)
                    for q in range(4):
                        pe.matmul(ps[:, 4 * u + (q + 1) % 4, :], k.w1_1[:, 128 * q:128 * q + 128], hT[:, u],
                                  start=True, stop=True).then_inc(s["hid_ps"].sem, 1)
                    s["hid"].wait(pe, t, 4 * (u + 1))
                    for j in range(G):
                        for q in range(4):
                            m = pe.matmul(ps[:, 4 * u + 1, j * S:j * S + S], hid[:, u, q, j * S:j * S + S],
                                          k.w2_1[:, q, :], start=q == 0, stop=q == 3)
                    m.then_inc(s["mlp_ps"].sem, 1)

        @block.scalar
        def _(act):
            with act.Fori(0, TURNS) as t:
                for u in range(2):
                    for q in range(4):
                        s["hid_ps"].wait(act, t, 4 * u + q + 1)
                        act.activation(hid[:, u, q, :], ps[:, 4 * u + (q + 1) % 4, :], ACT.Gelu,
                                       bias=k.b1_1[:, q:q + 1]).then_inc(s["hid"].sem, 1)

        @block.vector
        def _(dve):
            def sum_up(t, u):
                if u == 1:
                    s2["xn"].wait(dve, t, 0)
                elif not (isinstance(t, int) and t == 0):
                    s2["xn"].wait(dve, t, -G)
                yg = k.x3[:, :, bass.ds(t * PAIR + u * G, G)].rearrange("p c b -> p b c")
                for j in range(G):
                    b = t * PAIR + u * G + j
                    dve.tensor_scalar(xt[:, u, j, :], k.X[:, bass.ds(b, 1), :], k.mean1[:, bass.ds(b, 1)],
                                      k.rstd1[:, bass.ds(b, 1)], ALU.subtract, ALU.mult).then_inc(s["xt"].sem, 1)
                s[f"fo_in{u}"].wait(dve, t, 16)
                dve.tensor_tensor(z[:, u], yg, fo[:, u, :, 0:128], ALU.mult).then_inc(s["zs"].sem, 1)
                s["zs"].wait(dve, t, u + 1)
                dve.tensor_tensor(z[:, u], z[:, u], fo[:, u, :, 128:256], ALU.add).then_inc(s["zh"].sem, 1)
                s["zh"].wait(dve, t, u + 1)
                s["xt"].wait(dve, t, G * (u + 1))
                dve.tensor_tensor(z[:, u], z[:, u], xt[:, u], ALU.add).then_inc(s["z"].sem, 1)
                s["z"].wait_apart(dve, t, u + 1)
                group_stats(dve, nm1, s1, u, lambda u, j: z[:, u, j, :])
                group_moments(dve, nm1, s1, t, u)

            def enter(t, u):
                group_apply(dve, nm1, s1, t, u, lambda u, j: z[:, u, j, :], xn)

            def turn_in(t, u):
                s["xnT_ps"].wait(dve, t, u + 1)
                dve.tensor_scalar(hT[:, u], ps[:, 4 * u, :], k.gffn1[:], k.bffn1[:], ALU.mult,
                                  ALU.add).then_inc(s["hT"].sem, 1)

            def leave(t, u):
                s["mlp_ps"].wait(dve, t, u + 1)
                dve.tensor_tensor(z[:, u].rearrange("p j d -> p (j d)"), z[:, u].rearrange("p j d -> p (j d)"),
                                  ps[:, 4 * u + 1, :], ALU.add).then_inc(s["zm"].sem, 1)
                s["zm"].wait(dve, t, u + 1)
                dve.tensor_tensor(z[:, u], z[:, u], rows(k.b2_1), ALU.add).then_inc(s["zb"].sem, 1)
                s["zb"].wait_apart(dve, t, u + 1)
                group_stats(dve, nm2, s2, u, lambda u, j: z[:, u, j, :])
                group_moments(dve, nm2, s2, t, u)

            def norm_out(t, u):
                group_apply(dve, nm2, s2, t, u, lambda u, j: z[:, u, j, :], last)

            def residual(t, u):
                xg = k.X[:, bass.ds(t * PAIR + u * G, G), :]
                s["ob"].wait(dve, t, u + 1)
                dve.tensor_tensor(xg, xg, last[:, u], ALU.add).then_inc(s["x"].sem, 1)

            def opening(t, part):
                (sum_up, enter, turn_in)[part](t, 0)

            def body(t, next_opening):
                sum_up(t, 1)
                leave(t, 0)
                enter(t, 1)
                norm_out(t, 0)
                turn_in(t, 1)
                next_opening(0)
                residual(t, 0)
                leave(t, 1)
                next_opening(1)
                norm_out(t, 1)
                next_opening(2)
                residual(t, 1)

            turns(dve, opening, body, 3)


def stage_adapters(nc, w, ps, k):
    R = 64
    NB_ = 2 * G
    with ExitStack() as ctx:
        def tmp(name, shape, dt=F32):
            return ctx.enter_context(nc.sbuf_tensor("e_" + name, shape, dt))

        nm = Norm(lambda n, s: ctx.enter_context(nc.sbuf_tensor(n, s, F32)), "e")
        hx = tmp("hx", [128, 2, G, 514])
        xn = hx[:, :, :, 129:257]
        xnT, sx = tmp("xnT", [128, 2, W]), tmp("sx", [128, NB_])
        loss = tmp("loss", [128, 2, NB_])
        junk = tmp("junk", [128, 2, 257])
        gain, best = tmp("gain", [NB_, 8]), tmp("best", [NB_, 8])
        at, atf = tmp("at", [NB_, 8], U32), tmp("atf", [NB_, 1])
        pick = tmp("pick", [1, NB_], I32)
        a, aT = tmp("a", [128, 2, G, R]), tmp("aT", [R + 1, 2, W])
        s = signals(nc, k, "e", **NORM, xnT_ps=2, xnT=2, sx=2, h_ps=2, hb=NB_, h=NB_, gram_ps=NB_, loss=2 * NB_,
                    sum_ps=1, gain=1, best=1, at=1, atf=1, pick_ps=1, pick=1, a_ps=2, a=2, aT_ps=2, aT=2,
                    out_ps=2, x=2)
        ones = ctx.enter_context(OneTime(nc, "e_"))("ones")
        block = ctx.enter_context(nc.Block())

        @block.gpsimd
        def _(pool):
            pool.memset(hx[:, :, :, 128:129], 1.0).then_inc(ones, 1)
            pool.wait_ge(ones, 1)
            pool.memset(aT[R:R + 1], 1.0).then_inc(ones, 1)
            pool.wait_ge(ones, 2)
            with pool.Fori(0, TURNS) as t:
                norm_rstd(pool, nm, s, t, k.half[:])

        @block.tensor
        def _(pe):
            pe.wait_ge(ones, 2)
            with pe.Fori(0, TURNS) as t:
                for u in range(2):
                    s["x"].wait(pe, t, 0)
                    transpose_tokens(pe, s, t, u, xn, ps[:, 4 * u, :], k.ident[:])
                for u in range(2):
                    s["xnT"].wait(pe, t, u + 1)
                    for j in range(G):
                        m = pe.matmul(ps[:, 4 * u + 1 + j // 2, 256 * (j % 2):256 * (j % 2) + 256],
                                      xnT[:, u, j * S:j * S + S], k.wd1[:].rearrange("p e h -> p (e h)"),
                                      start=True, stop=True)
                    m.then_inc(s["h_ps"].sem, 1)
                for u in range(2):
                    s["hb"].wait(pe, t, G * (u + 1))
                    for j in range(G):
                        s["h"].wait(pe, t, G * u + j + 1)
                        if j >= 2:
                            s["loss"].wait(pe, t, 2 * (G * u + j - 1))
                        for q in range(2):
                            m = pe.matmul(ps[:, 4 * u + ((3, 0), (1, 2))[j % 2][q], 0:257],
                                          hx[:, u, j, 257 * q:257 * q + 128],
                                          hx[:, u, j, 128 * q:128 * q + 257], start=True, stop=True)
                        m.then_inc(s["gram_ps"].sem, 1)
                s["loss"].wait(pe, t, 2 * NB_)
                s["sx"].wait(pe, t, 2)
                pe.matmul(ps[0:NB_, 0, 0:8], loss[:, 0, :], k.indic[:, 0, :], start=True, stop=False)
                pe.matmul(ps[0:NB_, 0, 0:8], loss[:, 1, :], k.indic[:, 1, :], start=False, stop=False)
                pe.matmul(ps[0:NB_, 0, 0:8], sx[:], k.bd2T[:], start=False, stop=False)
                pe.matmul(ps[0:NB_, 0, 0:8], k.ones[:, 0:NB_], k.bd2q[:], start=False,
                          stop=True).then_inc(s["sum_ps"].sem, 1)
                s["atf"].wait_apart(pe, t, 1)
                pe.transpose(ps[0:1, 1, 0:NB_], atf[:], k.ident[0:NB_, 0:NB_]).then_inc(s["pick_ps"].sem, 1)
                s["pick"].wait_apart(pe, t, 1)
                chosen = [pe.value_load(pick[0:1, i:i + 1], min_val=0, max_val=7) for i in range(NB_)]
                for u in range(2):
                    for j in range(G):
                        e = chosen[G * u + j]
                        o = ps[:, 4 * u + 2, R * j:R * j + R]
                        pe.matmul(o, xnT[:, u, j * S:j * S + S],
                                  k.wdown[:, bass.ds(e, 1), :].rearrange("p e r -> p (e r)"), start=True, stop=False)
                        m = pe.matmul(o, k.ones[0:1, :], k.bdown[:, bass.ds(e, 1), :].rearrange("p e r -> p (e r)"),
                                      start=False, stop=True)
                    m.then_inc(s["a_ps"].sem, 1)
                for u in range(2):
                    s["a"].wait_apart(pe, t, u + 1)
                    for j in range(G):
                        m = pe.transpose(ps[0:R, 4 * u + 3, j * S:j * S + S], a[:, u, j, :], k.ident[:])
                    m.then_inc(s["aT_ps"].sem, 1)
                for u in range(2):
                    s["aT"].wait(pe, t, u + 1)
                    for j in range(G):
                        e = chosen[G * u + j]
                        o = ps[:, 4 * u + 2, j * S:j * S + S]
                        pe.matmul(o, xnT[:, u, j * S:j * S + S], k.wbase[:], start=True, stop=False)
                        m = pe.matmul(o, aT[:, u, j * S:j * S + S],
                                      k.wup[:, bass.ds(e, 1), :].rearrange("p e r -> p (e r)"), start=False, stop=True)
                    m.then_inc(s["out_ps"].sem, 1)

        @block.scalar
        def _(act):
            with act.Fori(0, TURNS) as t:
                for u in range(2):
                    s["xnT_ps"].wait(act, t, u + 1)
                    act.activation(xnT[:, u], ps[:, 4 * u, :], ACT.Identity).then_inc(s["xnT"].sem, 1)
                for u in range(2):
                    for j in range(G):
                        s["hb"].wait(act, t, G * u + j + 1)
                        h = hx[:, u, j, :].rearrange("p (q n) -> p q n", q=2)[:, :, 0:128]
                        act.activation(h, h, ACT.Relu).then_inc(s["h"].sem, 1)
                for u in range(2):
                    s["a_ps"].wait(act, t, u + 1)
                    act.activation(a[:, u].rearrange("p j r -> p (j r)"), ps[:, 4 * u + 2, 0:G * R],
                                   ACT.Relu).then_inc(s["a"].sem, 1)
                for u in range(2):
                    s["aT_ps"].wait(act, t, u + 1)
                    act.activation(aT[0:R, u], ps[0:R, 4 * u + 3, :], ACT.Identity).then_inc(s["aT"].sem, 1)

        @block.vector
        def _(dve):
            dve.wait_ge(ones, 2)
            def body(t, next_norm):
                for u in range(2):
                    s["h_ps"].wait(dve, t, u + 1)
                    for j in range(G):
                        h = hx[:, u, j, :].rearrange("p (q n) -> p q n", q=2)[:, :, 0:128]
                        dve.tensor_tensor(h, ps[:, 4 * u + 1 + j // 2, 256 * (j % 2):256 * (j % 2) + 256]
                                          .rearrange("p (q n) -> p q n", q=2),
                                          k.bd1[:].rearrange("p (q n) -> p q n", q=2),
                                          ALU.add).then_inc(s["hb"].sem, 1)
                for u in range(2):
                    s["xnT"].wait(dve, t, u + 1)
                    dve.tensor_reduce(sx[:, G * u:G * u + G], xnT[:, u].rearrange("p (j t) -> p j t", j=G),
                                      AX.X, ALU.add).then_inc(s["sx"].sem, 1)
                for u in range(2):
                    for j in range(G):
                        i = G * u + j
                        s["gram_ps"].wait(dve, t, i + 1)
                        if i:
                            s["loss"].wait(dve, t, 2 * i)
                        if i < 3:
                            next_norm(i)
                        for q in range(2):
                            dve.scalar_tensor_tensor(out=junk[:, q, :], in0=ps[:, 4 * u + ((3, 0), (1, 2))[j % 2][q], 0:257],
                                                     scalar=1.0, in1=k.dcoef[:, q, :], op0=ALU.mult, op1=ALU.mult,
                                                     accum_out=loss[:, q, i:i + 1]).then_inc(s["loss"].sem, 1)
                for part in (3, 4):
                    next_norm(part)
                s["sum_ps"].wait(dve, t, 1)
                dve.tensor_scalar(gain[:], ps[0:NB_, 0, 0:8], -1.0, None, ALU.mult).then_inc(s["gain"].sem, 1)
                s["gain"].wait_apart(dve, t, 1)
                dve.max(best[:], gain[:]).then_inc(s["best"].sem, 1)
                s["best"].wait_apart(dve, t, 1)
                dve.max_index(at[:], best[:], gain[:]).then_inc(s["at"].sem, 1)
                s["at"].wait(dve, t, 1)
                dve.tensor_copy(atf[:], at[:, 0:1]).then_inc(s["atf"].sem, 1)
                s["pick_ps"].wait(dve, t, 1)
                dve.tensor_copy(pick[:], ps[0:1, 1, 0:NB_]).then_inc(s["pick"].sem, 1)
                for u in range(2):
                    s["out_ps"].wait(dve, t, u + 1)
                    xg = k.X[:, bass.ds(t * PAIR + u * G, G), :]
                    dve.scalar_tensor_tensor(out=xg, in0=ps[:, 4 * u + 2, :].rearrange("p (j d) -> p j d", j=G),
                                             scalar=k.tg[:, 5:6], in1=xg, op0=ALU.mult,
                                             op1=ALU.add).then_inc(s["x"].sem, 1)

            turns(dve, lambda t, part: norm_turn(dve, nm, s, t, part, k, xn), body, NORM_PARTS)


def stage_attention16(nc, w, ps, k):
    H, DH = 16, 8
    SCALE = DH ** -0.5
    HU = H // 2
    NB_ = PAIR
    UNITS = 2 * NB_
    AHEAD = 3
    with ExitStack() as ctx:
        def tmp(name, shape, dt=F32):
            return ctx.enter_context(nc.sbuf_tensor("g_" + name, shape, dt))

        nm = Norm(lambda n, s: ctx.enter_context(nc.sbuf_tensor(n, s, F32)), "g")
        xn, xnT, ct = tmp("xn", [128, 2, G, 128]), tmp("xnT", [128, 2, W]), tmp("ct", [C, 2, W])
        qT, kT = tmp("qT", [128, 2, W]), tmp("kT", [128, 2, W])
        hmask = tmp("hmask", [128, H])
        km = tmp("km", [128, AHEAD, H, 128])
        v = tmp("v", [128, NB_, 4, 160])
        sel = tmp("sel", [128, 160])
        top = tmp("top", [128, 2, HU])
        p, pT = tmp("p", [128, 2, HU, 128]), tmp("pT", [128, 2, HU, 128])
        rsum, oT = tmp("rsum", [128, 128]), tmp("oT", [128, 2, 128])
        bo = tmp("bo", [128, 128])
        s = signals(nc, k, "g", **NORM, ct0=16, ct1=16, xnT_ps=2, xnT=2, q_ps=2, q=2, k_ps=2, kT=2, km0=1, km=NB_ - 1,
                    v_ps=2, v=NB_, xb=2, sc_ps=UNITS, top=UNITS, sub=UNITS, p=UNITS, pT_ps=UNITS, pT=2 * UNITS,
                    av_ps=UNITS, rsum=NB_, oT=NB_, out_ps=NB_, x=NB_)
        once = ctx.enter_context(OneTime(nc, "g_"))
        consts, bo_done = once("consts"), once("bo")
        block = ctx.enter_context(nc.Block())

        @block.sync
        def _(sp):
            with sp.Fori(0, TURNS) as t:
                for u in range(2):
                    s["v_ps"].wait(sp, t, 0)
                    s["k_ps"].wait(sp, t, 0)
                    sp.dma_start(ct[:, u], k.cT[:, bass.ds(t * 2 * W + u * W, W)]).then_inc(s[f"ct{u}"].sem, 16)

        @block.gpsimd
        def _(pool):
            pool.memset(v[:], 0.0).then_inc(consts, 1)
            pool.memset(sel[:], 0.0).then_inc(consts, 1)
            pool.memset(hmask[:], 1.0).then_inc(consts, 1)
            pool.wait_ge(consts, 3)
            pool.memset(sel[:].rearrange("p (b x) -> p b x", x=40)[:, :, 0:DH], 1.0).then_inc(consts, 1)
            pool.affine_select(out=hmask[:], in_=hmask[:], compare_op=ALU.is_ge, fill=0.0, base=0,
                               pattern=[[-DH, H]], channel_multiplier=1).then_inc(consts, 1)
            pool.wait_ge(consts, 5)
            pool.affine_select(out=hmask[:], in_=hmask[:], compare_op=ALU.is_ge, fill=0.0, base=DH - 1,
                               pattern=[[DH, H]], channel_multiplier=-1).then_inc(consts, 1)
            pool.wait_ge(consts, 6)
            def body(t, next_rstd):
                for i in range(1, NB_):
                    u, j = i // G, i % G
                    if i == NB_ - 2:
                        next_rstd()
                    s["kT"].wait(pool, t, u + 1)
                    s["sc_ps"].wait(pool, t, 2 * max(i - AHEAD + 1, 0))
                    pool.tensor_tensor(km[:, i % AHEAD],
                                       kT[:, u, j * S:j * S + S].rearrange("p (h t) -> p h t", h=1)
                                       .broadcast_to([128, H, 128]),
                                       hmask[:].rearrange("p (h o) -> p h o", o=1).broadcast_to([128, H, 128]),
                                       ALU.mult).then_inc(s["km"].sem, 1)

            turns(pool, lambda t: norm_rstd(pool, nm, s, t, k.half[:]), body)

        @block.tensor
        def _(pe):
            pe.wait_ge(consts, 6)

            def opening(t, part):
                if part == 0:
                    s["sub"].wait(pe, t, 0)
                    for u in range(2):
                        s[f"ct{u}"].wait(pe, t, 16)
                        pe.matmul(ps[:, u, :], k.wk2[:], ct[:, u], start=True, stop=True).then_inc(s["k_ps"].sem, 1)
                    for u in range(2):
                        for j in range(G):
                            m = pe.matmul(ps[:, 2 + u, j * S:j * S + S], ct[:, u, j * S:j * S + S], k.wv2[:],
                                          start=True, stop=True)
                        m.then_inc(s["v_ps"].sem, 1)
                else:
                    s["pT"].wait(pe, t, 0)
                    for u in range(2):
                        transpose_tokens(pe, s, t, u, xn, ps[:, 4 + u, :], k.ident[:])

            def body(t, next_opening):
                s["x"].wait(pe, t, 0)
                for u in range(2):
                    s["xnT"].wait(pe, t, u + 1)
                    pe.matmul(ps[:, 6 + u, :], k.wq2[:], xnT[:, u], start=True, stop=True).then_inc(s["q_ps"].sem, 1)
                for n in range(UNITS + 3):
                    if n == UNITS + 1:
                        next_opening(0)
                    if n == UNITS + 2:
                        next_opening(1)
                    if n < UNITS:
                        i, half = n // 2, n % 2
                        u, j = i // G, i % G
                        if n % UNITS == 0 or n == UNITS // 2:
                            s["q"].wait(pe, t, u + 1)
                        if n == 0:
                            s["km0"].wait(pe, t, 1)
                        elif half == 0:
                            s["km"].wait(pe, t, i)
                        if n == 0:
                            s["v"].wait(pe, t, NB_)
                        if n >= 2:
                            s["sub"].wait(pe, t, n - 1)
                        for a in range(2):
                            h = HU * half + 4 * a
                            m = pe.matmul(ps[:, 2 * half + a, :], qT[:, u, j * S:j * S + S],
                                          km[:, i % AHEAD, h:h + 4, :].rearrange("p h t -> p (h t)"),
                                          start=True, stop=True)
                        m.then_inc(s["sc_ps"].sem, 1)
                    if n % 2 == 0 and n >= 4:
                        i = n // 2 - 2
                        s["oT"].wait(pe, t, i + 1)
                        if i:
                            s["x"].wait(pe, t, i)
                        else:
                            s["q"].wait(pe, t, 2)
                        pe.matmul(ps[:, 7, 0:128], oT[:, i % 2], k.wo2[:], start=True,
                                  stop=True).then_inc(s["out_ps"].sem, 1)
                    if 1 <= n <= UNITS:
                        s["p"].wait(pe, t, n)
                        if n >= 2:
                            s["pT"].wait(pe, t, 2 * (n - 1))
                        for h in range(HU):
                            m = pe.transpose(ps[:, 4 + h // 4, 128 * (h % 4):128 * (h % 4) + 128],
                                             p[:, (n - 1) % 2, h, :], k.ident[:])
                        m.then_inc(s["pT_ps"].sem, 1)
                    if 2 <= n < UNITS + 2:
                        i, half = (n - 2) // 2, n % 2
                        s["pT"].wait(pe, t, 2 * (n - 1))
                        if half == 0 and i:
                            s["oT"].wait(pe, t, i)
                        for a in (2 * half, 2 * half + 1):
                            o = ps[32 * a:32 * a + 32, 6, :]
                            for b in range(4):
                                pe.matmul(o[:, 0:128], v[:, i, a, 32 * b:32 * b + 32],
                                          pT[:, half, 4 * (a % 2) + b, :], start=b == 0, stop=b == 3)
                            for b in range(4):
                                m = pe.matmul(o[:, 128:256], sel[:, 32 * b:32 * b + 32],
                                              pT[:, half, 4 * (a % 2) + b, :], start=b == 0, stop=b == 3)
                        m.then_inc(s["av_ps"].sem, 1)

            turns(pe, opening, body, 2)

        @block.scalar
        def _(act):
            with act.Fori(0, TURNS) as t:
                for u in range(2):
                    s["k_ps"].wait(act, t, u + 1)
                    act.activation(kT[:, u], ps[:, u, :], ACT.Identity, bias=k.bk2[:]).then_inc(s["kT"].sem, 1)
                for u in range(2):
                    s["xnT_ps"].wait(act, t, u + 1)
                    act.activation(xnT[:, u], ps[:, 4 + u, :], ACT.Identity).then_inc(s["xnT"].sem, 1)
                for u in range(2):
                    s["q_ps"].wait(act, t, u + 1)
                    act.activation(qT[:, u], ps[:, 6 + u, :], ACT.Identity, bias=k.bq2[:]).then_inc(s["q"].sem, 1)
                for n in range(UNITS + 1):
                    if n >= 1:
                        s["pT_ps"].wait(act, t, n)
                        if n >= 3:
                            s["av_ps"].wait(act, t, n - 2)
                        for a in range(2):
                            act.activation(pT[:, (n - 1) % 2, 4 * a:4 * a + 4, :].rearrange("p a b -> p (a b)"),
                                           ps[:, 4 + a, :], ACT.Identity).then_inc(s["pT"].sem, 1)
                    if n < UNITS:
                        s["sub"].wait(act, t, n + 1)
                        act.activation(p[:, n % 2], p[:, n % 2], ACT.Exp, scale=SCALE).then_inc(s["p"].sem, 1)

        @block.vector
        def _(dve):
            dve.tensor_scalar(bo[:], k.bo2[:], k.tg[:, 2:3], None, ALU.mult).then_inc(bo_done, 1)
            dve.wait_ge(bo_done, 1)
            dve.wait_ge(consts, 6)
            def body(t, next_norm):
                s["kT"].wait(dve, t, 1)
                s["sc_ps"].wait(dve, t, 0)
                dve.tensor_tensor(km[:, 0], kT[:, 0, 0:S].rearrange("p (h t) -> p h t", h=1)
                                  .broadcast_to([128, H, 128]),
                                  hmask[:].rearrange("p (h o) -> p h o", o=1).broadcast_to([128, H, 128]),
                                  ALU.mult).then_inc(s["km0"].sem, 1)
                for i in range(NB_):
                    u, j = i // G, i % G
                    if j == 0:
                        s["v_ps"].wait(dve, t, u + 1)
                    dve.tensor_tensor(v[:, i].rearrange("p a (b x) -> p a b x", x=40)[:, :, :, 0:DH],
                                      ps[:, 2 + u, j * S:j * S + S].rearrange("p (a b d) -> p a b d", a=4, b=4),
                                      k.bv2[:].rearrange("p (a b d) -> p a b d", a=4, b=4),
                                      ALU.add).then_inc(s["v"].sem, 1)
                s["xn"].wait(dve, t, 2 * G)
                for u in range(2):
                    xg = k.X[:, bass.ds(t * PAIR + u * G, G), :]
                    dve.tensor_tensor(xg, xg, bo[:].rearrange("p (j d) -> p j d", j=1).broadcast_to([128, G, 128]),
                                      ALU.add).then_inc(s["xb"].sem, 1)
                s["xb"].wait(dve, t, 2)
                for n in range(UNITS + 3):
                    if n in (4, 5, 7, 9, 11):
                        next_norm((4, 5, 7, 9, 11).index(n))
                    done = n // 2 - 2 if n % 2 == 0 and n >= 4 else None
                    if done is not None:
                        s["av_ps"].wait(dve, t, 2 * done + 2)
                        dve.reciprocal(rsum[:], ps[:, 6, 128:256]).then_inc(s["rsum"].sem, 1)
                        s["rsum"].wait(dve, t, done + 1)
                        dve.tensor_tensor(oT[:, done % 2], ps[:, 6, 0:128], rsum[:], ALU.mult).then_inc(s["oT"].sem, 1)
                    if n < UNITS:
                        half = n % 2
                        sc = ps[:, 2 * half:2 * half + 2, :].rearrange("p a (b c) -> p (a b) c", b=4)
                        s["sc_ps"].wait(dve, t, n + 1)
                        dve.tensor_reduce(top[:, half, :], sc, AX.X, ALU.max).then_inc(s["top"].sem, 1)
                        s["top"].wait(dve, t, n + 1)
                        if n >= 2:
                            s["pT_ps"].wait(dve, t, n - 1)
                        dve.tensor_tensor(p[:, half], sc, top[:, half, :].rearrange("p (h o) -> p h o", o=1)
                                          .broadcast_to([128, HU, 128]), ALU.subtract).then_inc(s["sub"].sem, 1)
                    if done is not None:
                        s["out_ps"].wait(dve, t, done + 1)
                        x_ = k.X[:, bass.ds(t * PAIR + done, 1), :].rearrange("p o d -> p (o d)")
                        dve.scalar_tensor_tensor(out=x_, in0=ps[:, 7, 0:128], scalar=k.tg[:, 2:3], in1=x_,
                                                 op0=ALU.mult, op1=ALU.add).then_inc(s["x"].sem, 1)

            turns(dve, lambda t, part: norm_turn(dve, nm, s, t, part, k, xn), body, NORM_PARTS)


def stage_fp8(nc, w, ps, k):
    with ExitStack() as ctx:
        k.amax = ctx.enter_context(nc.sbuf_tensor("h_amax", [128, 2], F32))
        k.scale = ctx.enter_context(nc.sbuf_tensor("h_scale", [128, 2], F32))
        k.unscale = ctx.enter_context(nc.sbuf_tensor("h_unscale", [128, 1], F32))
        k.wqT = ctx.enter_context(nc.sbuf_tensor("h_wqT", [128, 128], BF16))
        k.identb = ctx.enter_context(nc.sbuf_tensor("h_identb", [128, 128], BF16))
        k.bias8t = ctx.enter_context(nc.sbuf_tensor("h_bias8t", [128, 128], F32))
        norm_all(nc, w, ps, k)
        fp8_scales(nc, w, ps, k)
        fp8_product(nc, w, ps, k)


def norm_all(nc, w, ps, k):
    with ExitStack() as ctx:
        nm = Norm(lambda n, s: ctx.enter_context(nc.sbuf_tensor(n, s, F32)), "h")
        xall = k.x3[:].rearrange("p a b -> p (a b)").rearrange("p (b c) -> p b c", b=B)
        now = ctx.enter_context(nc.sbuf_tensor("h_now", [128, PAIR], F32))
        most = ctx.enter_context(nc.sbuf_tensor("h_most", [128, PAIR], F32))
        s = signals(nc, k, "h", **NORM, now=1, most=1)
        once = ctx.enter_context(OneTime(nc, "h_"))
        zeroed, final = once("zeroed"), once("final")
        block = ctx.enter_context(nc.Block())

        @block.gpsimd
        def _(pool):
            with pool.Fori(0, TURNS) as t:
                norm_rstd(pool, nm, s, t, k.half[:])

        @block.vector
        def _(dve):
            dve.memset(most[:], 0.0).then_inc(zeroed, 1)
            dve.wait_ge(zeroed, 1)
            with dve.Fori(0, TURNS) as t:
                xj = [[k.X[:, bass.ds(t * PAIR + u * G + j, 1), :] for j in range(G)] for u in range(2)]
                norm_stats(dve, nm, s, t, lambda u, j: xj[u][j])
                s["rstd"].wait(dve, t, 1)
                s["mean"].wait(dve, t, 1)
                for u in range(2):
                    for j in range(G):
                        dve.tensor_scalar(xall[:, bass.ds(t * PAIR + u * G + j, 1), :], xj[u][j],
                                          nm.mean[:, u, j:j + 1], nm.rstd[:, u, j:j + 1], ALU.subtract,
                                          ALU.mult).then_inc(s["xn"].sem, 1)
                s["most"].wait(dve, t, 0)
                s["xn"].wait_apart(dve, t, 2 * G)
                dve.tensor_reduce(now[:], xall[:, bass.ds(t * PAIR, PAIR), :], AX.X, ALU.max,
                                  apply_absolute_value=True).then_inc(s["now"].sem, 1)
                s["now"].wait(dve, t, 1)
                dve.tensor_tensor(most[:], most[:], now[:], ALU.max).then_inc(s["most"].sem, 1)
            s["most"].wait(dve, TURNS - 1, 1)
            dve.tensor_reduce(k.amax[:, 0:1], most[:], AX.X, ALU.max).then_inc(final, 1)
            dve.tensor_reduce(k.amax[:, 1:2], k.wq8[:], AX.X, ALU.max, apply_absolute_value=True).then_inc(final, 1)


E4M3 = dict(top=448.0, least=2.0 ** -6, magic=1.5 * 2.0 ** 20, exponent=0x7F800000)


def fp8_scales(nc, w, ps, k):
    with ExitStack() as ctx:
        def tmp(name, shape, dt=F32):
            return ctx.enter_context(nc.sbuf_tensor("i_" + name, shape, dt))

        row, inv = tmp("row", [1, 2]), tmp("inv", [128, 2])
        q, mag, wq = tmp("q", [128, 128]), tmp("mag", [128, 128]), tmp("wq", [128, 128], BF16)
        once = ctx.enter_context(OneTime(nc, "i_"))
        chain, amax_T, rows, amax_b, wq_done, wT = (once(n) for n in (
            "chain", "amax_T", "rows", "amax_b", "wq_done", "wT"))
        block = ctx.enter_context(nc.Block())

        @block.tensor
        def _(pe):
            for i in range(2):
                m = pe.transpose(ps[0:1, 0, 128 * i:128 * i + 128], k.amax[:, i:i + 1], k.ident[:])
            m.then_inc(amax_T, 1)
            pe.wait_ge(rows, 1)
            pe.matmul(ps[:, 1, 0:2], k.ones[0:1, :], row[:], start=True, stop=True).then_inc(amax_b, 1)
            pe.wait_ge(wq_done, 1)
            pe.transpose(ps[:, 2, 0:64].bitcast(BF16), wq[:], k.identb[:]).then_inc(wT, 1)

        @block.vector
        def _(dve):
            n = [0]

            def link(ins):
                n[0] += 1
                ins.then_inc(chain, 1)
                dve.wait_ge(chain, n[0])

            dve.wait_ge(amax_T, 1)
            dve.tensor_reduce(row[:], ps[0:1, 0, 0:256].rearrange("p (a b) -> p a b", a=2), AX.X,
                              ALU.max).then_inc(rows, 1)
            link(dve.tensor_copy(k.identb[:], k.ident[:]))
            dve.tensor_scalar(k.bias8t[:], k.bias8[:], k.tg[:, 6:7], None, ALU.mult)
            dve.wait_ge(amax_b, 1)
            link(dve.tensor_scalar(k.scale[:], ps[:, 1, 0:2], 1e-12, None, ALU.max))
            link(dve.reciprocal(inv[:], k.scale[:]))
            link(dve.tensor_scalar(k.scale[:], inv[:], E4M3["top"], None, ALU.mult))
            link(dve.reciprocal(inv[:], k.scale[:]))
            link(dve.tensor_tensor(k.unscale[:], inv[:, 0:1], inv[:, 1:2], ALU.mult))
            link(dve.tensor_tensor(k.unscale[:], k.tg[:, 6:7], k.unscale[:], ALU.mult))
            link(dve.tensor_scalar(q[:], k.wq8[:], k.scale[:, 1:2], None, ALU.mult))
            link(dve.tensor_scalar(mag[:].bitcast(I32), q[:].bitcast(I32), E4M3["exponent"], None, ALU.bitwise_and))
            link(dve.tensor_scalar(mag[:], mag[:], E4M3["least"], E4M3["magic"], ALU.max, ALU.mult))
            link(dve.tensor_tensor(q[:], q[:], mag[:], ALU.add))
            dve.tensor_tensor(wq[:], q[:], mag[:], ALU.subtract).then_inc(wq_done, 1)
            dve.wait_ge(wT, 1)
            dve.tensor_copy(k.wqT[:], ps[:, 2, 0:64].bitcast(BF16))


def fp8_product(nc, w, ps, k):
    with ExitStack() as ctx:
        def tmp(name, shape, dt=F32):
            return ctx.enter_context(nc.sbuf_tensor("j_" + name, shape, dt))

        xall = k.x3[:].rearrange("p a b -> p (a b)").rearrange("p (b c) -> p b c", b=B)
        q, mag = tmp("q", [128, 2, W]), tmp("mag", [128, 2, W])
        xq, xqT = tmp("xq", [128, 2, W], BF16), tmp("xqT", [128, 2, W], BF16)
        s = signals(nc, k, "j", q=2, exponent=2, magic=2, sum=2, xq=2, xqT_ps=2, xqT=2, out_ps=2, x=2, xb=2)
        block = ctx.enter_context(nc.Block())

        @block.tensor
        def _(pe):
            with pe.Fori(0, TURNS) as t:
                for u in range(2):
                    s["xq"].wait(pe, t, u + 1)
                    s["xqT"].wait(pe, t, 0)
                    for j in range(G):
                        m = pe.transpose(ps[:, 4 * u, 64 * j:64 * j + 64].bitcast(BF16), xq[:, u, j * S:j * S + S],
                                         k.identb[:])
                    m.then_inc(s["xqT_ps"].sem, 1)
                for u in range(2):
                    s["xqT"].wait(pe, t, u + 1)
                    s["x"].wait(pe, t, 0)
                    for j in range(G):
                        m = pe.matmul(ps[:, 4 * u + 1, j * S:j * S + S], xqT[:, u, j * S:j * S + S], k.wqT[:],
                                      start=True, stop=True)
                    m.then_inc(s["out_ps"].sem, 1)

        @block.scalar
        def _(act):
            with act.Fori(0, TURNS) as t:
                for u in range(2):
                    s["xqT_ps"].wait(act, t, u + 1)
                    s["out_ps"].wait(act, t, 0)
                    act.activation(xqT[:, u], ps[:, 4 * u, 0:256].bitcast(BF16), ACT.Identity).then_inc(s["xqT"].sem, 1)

        @block.vector
        def _(dve):
            with dve.Fori(0, TURNS) as t:
                for u in range(2):
                    s["xqT_ps"].wait(dve, t, 0)
                    s["xq"].wait(dve, t, 0)
                    dve.tensor_scalar(q[:, u].rearrange("p (j c) -> p j c", j=G),
                                      xall[:, bass.ds(t * PAIR + u * G, G), :], k.scale[:, 0:1], None,
                                      ALU.mult).then_inc(s["q"].sem, 1)
                for u in range(2):
                    s["q"].wait(dve, t, u + 1)
                    dve.tensor_scalar(mag[:, u].bitcast(I32), q[:, u].bitcast(I32), E4M3["exponent"], None,
                                      ALU.bitwise_and).then_inc(s["exponent"].sem, 1)
                for u in range(2):
                    s["exponent"].wait(dve, t, u + 1)
                    dve.tensor_scalar(mag[:, u], mag[:, u], E4M3["least"], E4M3["magic"], ALU.max,
                                      ALU.mult).then_inc(s["magic"].sem, 1)
                for u in range(2):
                    s["magic"].wait(dve, t, u + 1)
                    dve.tensor_tensor(q[:, u], q[:, u], mag[:, u], ALU.add).then_inc(s["sum"].sem, 1)
                for u in range(2):
                    s["sum"].wait(dve, t, u + 1)
                    dve.tensor_tensor(xq[:, u], q[:, u], mag[:, u], ALU.subtract).then_inc(s["xq"].sem, 1)
                for u in range(2):
                    s["out_ps"].wait(dve, t, u + 1)
                    xg = k.X[:, bass.ds(t * PAIR + u * G, G), :]
                    dve.scalar_tensor_tensor(out=xg, in0=ps[:, 4 * u + 1, :].rearrange("p (j d) -> p j d", j=G),
                                             scalar=k.unscale[:, 0:1], in1=xg, op0=ALU.mult,
                                             op1=ALU.add).then_inc(s["x"].sem, 1)
                for u in range(2):
                    s["x"].wait(dve, t, u + 1)
                    xg = k.X[:, bass.ds(t * PAIR + u * G, G), :]
                    dve.tensor_tensor(xg, xg, k.bias8t[:].rearrange("p (j d) -> p j d", j=1)
                                      .broadcast_to([128, G, 128]), ALU.add).then_inc(s["xb"].sem, 1)


def stage_attention8(nc, w, ps, k):
    H, DH = 8, 64
    SCALE = DH ** -0.5
    NB_ = PAIR
    K1_BANKS, Q0_BANKS = (6, 7, 0, 1), (2, 3, 4, 5)
    with ExitStack() as ctx:
        def tmp(name, shape, dt=F32):
            return ctx.enter_context(nc.sbuf_tensor("l_" + name, shape, dt))

        nm = Norm(lambda n, s: ctx.enter_context(nc.sbuf_tensor(n, s, F32)), "l")
        xn, xnT, ct = tmp("xn", [128, 2, G, 128]), tmp("xnT", [128, 2, W]), tmp("ct", [C, 2, W])
        qT, km = tmp("qT", [128, 2, 4, W]), tmp("km", [128, 2, 4, G, 2, 128])
        v = tmp("v", [128, 3, H * DH])
        shift, total, top = tmp("shift", [128, 2, H]), tmp("total", [128, 2, H]), tmp("top", [128, 2, H])
        p, pT = tmp("p", [128, 2, H, 128]), tmp("pT", [128, H, 128])
        oT = tmp("oT", [128, 4, 128])
        bo = tmp("bo", [128, 128])
        s = signals(nc, k, "l", **NORM, ct0=16, ct1=16, xnT_ps=2, xnT=2, q_ps=8, q0=4, q1=4, k_ps=8, kT0=8, kT1=8,
                    xb=2, sc_ps=NB_, top=NB_, shift=NB_, p=NB_ * H, rsum=NB_, share=NB_, v_ps=NB_, v=NB_,
                    pT_ps=NB_, pT=2 * NB_, av_ps=NB_, oT=NB_, out_ps=NB_, x=NB_)
        once = ctx.enter_context(OneTime(nc, "l_"))
        zeroed, bo_done = once("zeroed"), once("bo")
        block = ctx.enter_context(nc.Block())

        @block.sync
        def _(sp):
            with sp.Fori(0, TURNS) as t:
                for u in range(2):
                    s["v_ps"].wait(sp, t, 0)
                    sp.dma_start(ct[:, u], k.cT[:, bass.ds(t * 2 * W + u * W, W)]).then_inc(s[f"ct{u}"].sem, 16)

        @block.gpsimd
        def _(pool):
            pool.memset(km[:], 0.0).then_inc(zeroed, 1)
            with pool.Fori(0, TURNS) as t:
                norm_rstd(pool, nm, s, t, k.half[:])

        @block.tensor
        def _(pe):
            def opening(t, part):
                if part == 0:
                    s["p"].wait(pe, t, 0)
                    s["ct0"].wait(pe, t, 16)
                    for b in range(4):
                        pe.matmul(ps[:, b, :], k.wk3[:, 128 * b:128 * b + 128], ct[:, 0], start=True,
                                  stop=True).then_inc(s["k_ps"].sem, 1)
                else:
                    s["pT"].wait(pe, t, 0)
                    for u in range(2):
                        transpose_tokens(pe, s, t, u, xn, ps[:, 4 + u, :], k.ident[:])

            def body(t, next_opening):
                s["x"].wait(pe, t, 0)
                s["ct1"].wait(pe, t, 16)
                for b in range(4):
                    if b >= 2:
                        s["kT0"].wait(pe, t, 2 * (b - 1))
                    pe.matmul(ps[:, K1_BANKS[b], :], k.wk3[:, 128 * b:128 * b + 128], ct[:, 1], start=True,
                              stop=True).then_inc(s["k_ps"].sem, 1)
                for b in range(4):
                    if b < 2:
                        s["kT0"].wait(pe, t, 2 * (b + 3))
                    s["xnT"].wait(pe, t, 2)
                    pe.matmul(ps[:, Q0_BANKS[b], :], k.wq3[:, 128 * b:128 * b + 128], xnT[:, 0], start=True,
                              stop=True).then_inc(s["q_ps"].sem, 1)
                for b in range(4):
                    s["kT1"].wait(pe, t, 2 * (b + 1))
                    pe.matmul(ps[:, K1_BANKS[b], :], k.wq3[:, 128 * b:128 * b + 128], xnT[:, 1], start=True,
                              stop=True).then_inc(s["q_ps"].sem, 1)
                for n in range(NB_ + 3):
                    if n == NB_ + 1:
                        next_opening(0)
                    if n == NB_ + 2:
                        next_opening(1)
                    if n < NB_:
                        u, j = n // G, n % G
                        if n == 0:
                            s["q0"].wait(pe, t, 4)
                            s["q1"].wait(pe, t, 4)
                        if n >= 2:
                            s["p"].wait(pe, t, H * (n - 1))
                        for b in range(4):
                            m = pe.matmul(ps[:, 2 * (n % 2) + b // 2, 256 * (b % 2):256 * (b % 2) + 256],
                                          qT[:, u, b, j * S:j * S + S], km[:, u, b, j].rearrange("p h t -> p (h t)"),
                                          start=True, stop=True)
                        m.then_inc(s["sc_ps"].sem, 1)
                    if n >= 3:
                        s["oT"].wait(pe, t, n - 2)
                        if n <= NB_:
                            s["v"].wait(pe, t, n)
                        else:
                            s["x"].wait(pe, t, n - 3)
                        for b in range(4):
                            m = pe.matmul(ps[:, 7, 0:128], oT[:, b, :], k.wo3[:, b, :], start=b == 0, stop=b == 3)
                        m.then_inc(s["out_ps"].sem, 1)
                    if n < NB_:
                        if 1 <= n < 3:
                            s["v"].wait(pe, t, n)
                        elif n:
                            s["x"].wait(pe, t, n - 2)
                        pe.matmul(ps[:, 7, :], ct[:, u, j * S:j * S + S], k.wv3[:], start=True,
                                  stop=True).then_inc(s["v_ps"].sem, 1)
                    if 2 <= n < NB_ + 2:
                        i = n - 2
                        s["pT"].wait(pe, t, 2 * (i + 1))
                        s["v"].wait(pe, t, i + 1)
                        if i:
                            s["oT"].wait(pe, t, i)
                        for h in range(H):
                            r = DH * (h % 2)
                            m = pe.matmul(ps[r:r + DH, 6, 128 * (h // 2):128 * (h // 2) + 128],
                                          v[:, i % 3, DH * h:DH * h + DH], pT[:, h, :], start=True, stop=True)
                        m.then_inc(s["av_ps"].sem, 1)
                    if 1 <= n <= NB_:
                        i = n - 1
                        s["share"].wait(pe, t, i + 1)
                        if i:
                            s["pT"].wait(pe, t, 2 * i)
                        for h in range(H):
                            m = pe.transpose(ps[:, 4 + h // 4, 128 * (h % 4):128 * (h % 4) + 128], p[:, i % 2, h, :],
                                             k.ident[:])
                        m.then_inc(s["pT_ps"].sem, 1)

            turns(pe, opening, body, 2)

        @block.scalar
        def _(act):
            act.wait_ge(zeroed, 1)
            with act.Fori(0, TURNS) as t:
                for b in range(4):
                    s["k_ps"].wait(act, t, b + 1)
                    for a in range(2):
                        r = slice(DH * a, DH * a + DH)
                        act.activation(km[r, 0, b, :, a, :], ps[r, b, :].rearrange("p (j t) -> p j t", j=G),
                                       ACT.Identity).then_inc(s["kT0"].sem, 1)
                for u in range(2):
                    s["xnT_ps"].wait(act, t, u + 1)
                    act.activation(xnT[:, u], ps[:, 4 + u, :], ACT.Identity).then_inc(s["xnT"].sem, 1)
                for b in range(4):
                    s["q_ps"].wait(act, t, b + 1)
                    act.activation(qT[:, 0, b, :], ps[:, Q0_BANKS[b], :], ACT.Identity).then_inc(s["q0"].sem, 1)
                for n in range(NB_ + 2):
                    if n >= 2:
                        i = n - 2
                        s["pT_ps"].wait(act, t, i + 1)
                        if i:
                            s["av_ps"].wait(act, t, i)
                        for a in range(2):
                            act.activation(pT[:, 4 * a:4 * a + 4, :].rearrange("p a b -> p (a b)"), ps[:, 4 + a, :],
                                           ACT.Identity).then_inc(s["pT"].sem, 1)
                    if n < NB_:
                        s["shift"].wait(act, t, n + 1)
                        if n >= 2:
                            s["pT_ps"].wait(act, t, n - 1)
                        for h in range(H):
                            act.activation(p[:, n % 2, h, :],
                                           ps[:, 2 * (n % 2) + h // 4, 128 * (h % 4):128 * (h % 4) + 128], ACT.Exp,
                                           bias=shift[:, n % 2, h:h + 1], scale=SCALE,
                                           accum_out=total[:, n % 2, h:h + 1]).then_inc(s["p"].sem, 1)
                    if n >= 2:
                        s["av_ps"].wait(act, t, i + 1)
                        if i:
                            s["out_ps"].wait(act, t, i)
                        act.activation(oT[:].rearrange("p a b -> p (a b)"), ps[:, 6, :],
                                       ACT.Identity).then_inc(s["oT"].sem, 1)

        @block.vector
        def _(dve):
            dve.tensor_scalar(bo[:], k.bo3[:], k.tg[:, 3:4], None, ALU.mult).then_inc(bo_done, 1)
            dve.wait_ge(bo_done, 1)
            dve.wait_ge(zeroed, 1)
            def body(t, next_norm):
                for b in range(4):
                    s["k_ps"].wait(dve, t, 5 + b)
                    for a in range(2):
                        r = slice(DH * a, DH * a + DH)
                        dve.tensor_copy(km[r, 1, b, :, a, :],
                                        ps[r, K1_BANKS[b], :].rearrange("p (j t) -> p j t", j=G)).then_inc(s["kT1"].sem, 1)
                s["xn"].wait(dve, t, 2 * G)
                for u in range(2):
                    xg = k.X[:, bass.ds(t * PAIR + u * G, G), :]
                    dve.tensor_tensor(xg, xg, bo[:].rearrange("p (j d) -> p j d", j=1).broadcast_to([128, G, 128]),
                                      ALU.add).then_inc(s["xb"].sem, 1)
                for b in range(4):
                    s["q_ps"].wait(dve, t, 5 + b)
                    dve.tensor_copy(qT[:, 1, b, :], ps[:, K1_BANKS[b], :]).then_inc(s["q1"].sem, 1)
                s["xb"].wait(dve, t, 2)
                for n in range(NB_ + 3):
                    if 2 <= n < 2 + NORM_PARTS:
                        next_norm(n - 2)
                    if 1 <= n <= NB_:
                        i, a = n - 1, (n - 1) % 2
                        s["p"].wait(dve, t, H * (i + 1))
                        dve.reciprocal(total[:, a, :], total[:, a, :]).then_inc(s["rsum"].sem, 1)
                        s["rsum"].wait(dve, t, i + 1)
                        dve.tensor_tensor(p[:, a], p[:, a], total[:, a, :].rearrange("p (h o) -> p h o", o=1)
                                          .broadcast_to([128, H, 128]), ALU.mult).then_inc(s["share"].sem, 1)
                    if n < NB_:
                        a = n % 2
                        s["sc_ps"].wait(dve, t, n + 1)
                        dve.tensor_reduce(top[:, a, :],
                                          ps[:, 2 * a:2 * a + 2, :].rearrange("p a (b c) -> p (a b) c", b=4),
                                          AX.X, ALU.max).then_inc(s["top"].sem, 1)
                        s["top"].wait(dve, t, n + 1)
                        dve.tensor_scalar(shift[:, a, :], top[:, a, :], -SCALE, None,
                                          ALU.mult).then_inc(s["shift"].sem, 1)
                    if n >= 3:
                        i = n - 3
                        s["out_ps"].wait(dve, t, i + 1)
                        x_ = k.X[:, bass.ds(t * PAIR + i, 1), :].rearrange("p o d -> p (o d)")
                        dve.scalar_tensor_tensor(out=x_, in0=ps[:, 7, 0:128], scalar=k.tg[:, 3:4], in1=x_,
                                                 op0=ALU.mult, op1=ALU.add).then_inc(s["x"].sem, 1)
                    if n < NB_:
                        s["v_ps"].wait(dve, t, n + 1)
                        if n >= 3:
                            s["av_ps"].wait(dve, t, n - 2)
                        dve.tensor_copy(v[:, n % 3], ps[:, 7, :]).then_inc(s["v"].sem, 1)

            turns(dve, lambda t, part: norm_turn(dve, nm, s, t, part, k, xn), body, NORM_PARTS)


def stage_moe(nc, w, ps, k):
    E, TEMP, TINY = 8, 5.0, 1e-9
    with ExitStack() as ctx:
        def tmp(name, shape, dt=F32):
            return ctx.enter_context(nc.sbuf_tensor("m_" + name, shape, dt))

        nm = Norm(lambda n, s: ctx.enter_context(nc.sbuf_tensor(n, s, F32)), "m")
        xn, xnT = tmp("xn", [128, 2, G, 128]), tmp("xnT", [128, 2, W])
        lg, pr, top = tmp("lg", [128, 2, G, E]), tmp("pr", [128, 2, G, E]), tmp("top", [128, 2, G, 8])
        big, tot = tmp("big", [128, 2, G]), tmp("tot", [128, 2, G])
        at, atf = tmp("at", [128, 2, G, 8], U32), tmp("atf", [128, 2, G, 2])
        hit, gt = tmp("hit", [128, 2, G, 2, E]), tmp("gt", [128, 2, G, E])
        gtT = tmp("gtT", [E, 2, W])
        hid = tmp("hid", [128, 2, 2, W])
        s = signals(nc, k, "m", **NORM, xnT_ps=2, xnT=2, lg_ps=2, lg=2, big=2, less=2, ex=2, tot=2, rtot=2,
                    pr=2, top=2 * G, at=2 * G, atf=2, pair=2, rpair=4, two=2, hit=4, whit=4, gt=2, gT_ps=2, gT=2,
                    hid_ps=4 * E, hid=4 * E, out_ps=2 * E, x=2 * G * E, b_ps=2, xb=2)
        block = ctx.enter_context(nc.Block())

        @block.gpsimd
        def _(pool):
            with pool.Fori(0, TURNS) as t:
                norm_rstd(pool, nm, s, t, k.half[:])

        @block.tensor
        def _(pe):
            with pe.Fori(0, TURNS) as t:
                for u in range(2):
                    s["xb"].wait(pe, t, 0)
                    transpose_tokens(pe, s, t, u, xn, ps[:, 4 * u, :], k.ident[:])
                for u in range(2):
                    s["xnT"].wait(pe, t, u + 1)
                    for j in range(G):
                        m = pe.matmul(ps[:, 4 * u + 3, E * j:E * j + E], xnT[:, u, j * S:j * S + S], k.wg3[:],
                                      start=True, stop=True)
                    m.then_inc(s["lg_ps"].sem, 1)
                s["lg"].wait(pe, t, 2)
                for n in range(2 * E + 2):
                    if n < 2 * E:
                        e, u = n // 2, n % 2
                        for q in range(2):
                            if e:
                                s["hid"].wait(pe, t, 4 * (e - 1) + 2 * u + q + 1)
                            pe.matmul(ps[:, 4 * u + q, :], k.w1_3[:, e, 128 * q:128 * q + 128], xnT[:, u], start=True,
                                      stop=True).then_inc(s["hid_ps"].sem, 1)
                    if n >= 2:
                        e, u = (n - 2) // 2, n % 2
                        s["hid"].wait(pe, t, 4 * e + 2 * u + 2)
                        if e >= 2:
                            s["x"].wait(pe, t, G * (2 * (e - 2) + u + 1))
                        for j in range(G):
                            for q in range(2):
                                m = pe.matmul(ps[:, 4 * u + 2 + e % 2, j * S:j * S + S], hid[:, u, q, j * S:j * S + S],
                                              k.w2_3[:, e, q, :], start=q == 0, stop=q == 1)
                        m.then_inc(s["out_ps"].sem, 1)
                for u in range(2):
                    s["gt"].wait(pe, t, u + 1)
                    for j in range(G):
                        m = pe.transpose(ps[0:E, 4 * u, j * S:j * S + S], gt[:, u, j, :], k.ident[:])
                    m.then_inc(s["gT_ps"].sem, 1)
                for u in range(2):
                    s["gT"].wait(pe, t, u + 1)
                    for j in range(G):
                        m = pe.matmul(ps[:, 4 * u + 1, j * S:j * S + S], gtT[:, u, j * S:j * S + S], k.b2_3[:],
                                      start=True, stop=True)
                    m.then_inc(s["b_ps"].sem, 1)

        @block.scalar
        def _(act):
            with act.Fori(0, TURNS) as t:
                for u in range(2):
                    s["xnT_ps"].wait(act, t, u + 1)
                    act.activation(xnT[:, u], ps[:, 4 * u, :], ACT.Identity).then_inc(s["xnT"].sem, 1)
                for u in range(2):
                    s["less"].wait(act, t, u + 1)
                    act.activation(pr[:, u], lg[:, u], ACT.Exp, scale=1.0 / TEMP).then_inc(s["ex"].sem, 1)
                for n in range(2 * E):
                    e, u = n // 2, n % 2
                    for q in range(2):
                        s["hid_ps"].wait(act, t, 2 * n + q + 1)
                        if e:
                            s["out_ps"].wait(act, t, n - 1)
                        act.activation(hid[:, u, q, :], ps[:, 4 * u + q, :], ACT.Gelu,
                                       bias=k.b1_3[:, 2 * e + q:2 * e + q + 1]).then_inc(s["hid"].sem, 1)
                for u in range(2):
                    s["gT_ps"].wait(act, t, u + 1)
                    act.activation(gtT[:, u], ps[0:E, 4 * u, :], ACT.Identity).then_inc(s["gT"].sem, 1)

        @block.vector
        def _(dve):
            def body(t, next_norm):
                xj = [[k.X[:, bass.ds(t * PAIR + u * G + j, 1), :] for j in range(G)] for u in range(2)]

                def each(ap):
                    return ap.rearrange("p (j o) -> p j o", o=1).broadcast_to([128, G, E])

                for u in range(2):
                    s["lg_ps"].wait(dve, t, u + 1)
                    dve.tensor_tensor(lg[:, u], ps[:, 4 * u + 3, 0:E * G].rearrange("p (j e) -> p j e", e=E),
                                      k.bg3[:].rearrange("p (j e) -> p j e", j=1).broadcast_to([128, G, E]),
                                      ALU.add).then_inc(s["lg"].sem, 1)
                    s["lg"].wait(dve, t, u + 1)
                    dve.tensor_reduce(big[:, u], lg[:, u], AX.X, ALU.max).then_inc(s["big"].sem, 1)
                    s["big"].wait(dve, t, u + 1)
                    dve.tensor_tensor(lg[:, u], lg[:, u], each(big[:, u]), ALU.subtract).then_inc(s["less"].sem, 1)
                for u in range(2):
                    s["ex"].wait(dve, t, u + 1)
                    dve.tensor_reduce(tot[:, u], pr[:, u], AX.X, ALU.add).then_inc(s["tot"].sem, 1)
                    s["tot"].wait(dve, t, u + 1)
                    dve.reciprocal(tot[:, u], tot[:, u]).then_inc(s["rtot"].sem, 1)
                    s["rtot"].wait(dve, t, u + 1)
                    dve.tensor_tensor(pr[:, u], pr[:, u], each(tot[:, u]), ALU.mult).then_inc(s["pr"].sem, 1)
                    s["pr"].wait_apart(dve, t, u + 1)
                    for j in range(G):
                        dve.max(top[:, u, j, :], pr[:, u, j, :]).then_inc(s["top"].sem, 1)
                    s["top"].wait_apart(dve, t, G * (u + 1))
                    for j in range(G):
                        dve.max_index(at[:, u, j, :], top[:, u, j, :], pr[:, u, j, :]).then_inc(s["at"].sem, 1)
                    dve.tensor_tensor(tot[:, u], top[:, u, :, 0], top[:, u, :, 1], ALU.add).then_inc(s["pair"].sem, 1)
                    s["pair"].wait(dve, t, u + 1)
                    dve.tensor_scalar(tot[:, u], tot[:, u], TINY, None, ALU.add).then_inc(s["rpair"].sem, 1)
                    s["rpair"].wait(dve, t, 2 * u + 1)
                    dve.reciprocal(tot[:, u], tot[:, u]).then_inc(s["rpair"].sem, 1)
                    s["rpair"].wait(dve, t, 2 * u + 2)
                    dve.scalar_tensor_tensor(out=top[:, u, :, 0:2], in0=top[:, u, :, 0:2], scalar=k.tg[:, 7:8],
                                             in1=tot[:, u].rearrange("p (j o) -> p j o", o=1).broadcast_to([128, G, 2]),
                                             op0=ALU.mult, op1=ALU.mult).then_inc(s["two"].sem, 1)
                    s["at"].wait(dve, t, G * (u + 1))
                    dve.tensor_copy(atf[:, u], at[:, u, :, 0:2]).then_inc(s["atf"].sem, 1)
                    s["atf"].wait(dve, t, u + 1)
                    for i in range(2):
                        dve.tensor_tensor(hit[:, u, :, i, :],
                                          k.iota8[:].rearrange("p (j e) -> p j e", j=1).broadcast_to([128, G, E]),
                                          atf[:, u, :, i:i + 1].broadcast_to([128, G, E]),
                                          ALU.is_equal).then_inc(s["hit"].sem, 1)
                    s["hit"].wait(dve, t, 2 * u + 2)
                    s["two"].wait(dve, t, u + 1)
                    for i in range(2):
                        dve.tensor_tensor(hit[:, u, :, i, :], hit[:, u, :, i, :],
                                          top[:, u, :, i:i + 1].broadcast_to([128, G, E]),
                                          ALU.mult).then_inc(s["whit"].sem, 1)
                    s["whit"].wait(dve, t, 2 * u + 2)
                    dve.tensor_tensor(gt[:, u], hit[:, u, :, 0, :], hit[:, u, :, 1, :], ALU.add).then_inc(s["gt"].sem, 1)
                s["gt"].wait(dve, t, 2)
                for n in range(2 * E):
                    if n >= 4 and n % 2 == 0 and (n - 4) // 2 < NORM_PARTS:
                        next_norm((n - 4) // 2)
                    e, u = n // 2, n % 2
                    s["out_ps"].wait(dve, t, n + 1)
                    if e:
                        s["x"].wait(dve, t, G * (n - 1))
                    for j in range(G):
                        dve.scalar_tensor_tensor(out=xj[u][j], in0=ps[:, 4 * u + 2 + e % 2, j * S:j * S + S],
                                                 scalar=gt[:, u, j, e:e + 1], in1=xj[u][j], op0=ALU.mult,
                                                 op1=ALU.add).then_inc(s["x"].sem, 1)
                s["x"].wait(dve, t, 2 * G * E)
                for u in range(2):
                    s["b_ps"].wait(dve, t, u + 1)
                    xg = k.X[:, bass.ds(t * PAIR + u * G, G), :]
                    dve.tensor_tensor(xg, xg, ps[:, 4 * u + 1, :].rearrange("p (j d) -> p j d", j=G),
                                      ALU.add).then_inc(s["xb"].sem, 1)

            turns(dve, lambda t, part: norm_turn(dve, nm, s, t, part, k, xn), body, NORM_PARTS)


class Kept:

    def __init__(self, keep):
        self.X = keep("X", [128, B, 128])
        self.cT = keep("cT", [C, B * S])
        self.ident = keep("ident", [128, 128])
        self.flip = keep("flip", [128, 128])
        self.half = keep("half", [128, 8])
        self.ones = keep("ones", [128, 128])
        self.iota8 = keep("iota8", [128, 8])
        self.tg = keep("tg", [128, 8])
        self.tmask = keep("tmask", [128, B])
        self.wv0T = keep("wv0T", [128, 64])
        self.wt0T = keep("wt0T", [C, 64])
        self.bv0 = keep("bv0", [64, 1])
        self.bt0 = keep("bt0", [64, 1])
        self.gateT = keep("gateT", [128, 8])
        self.expT = keep("expT", [128, 8, 128])
        self.wq1 = keep("wq1", [128, 128])
        self.wk1 = keep("wk1", [C, 128])
        self.wfilm = keep("wfilm", [C + 1, 512])
        self.gin1 = keep("gin1", [128, 128])
        self.bin1 = keep("bin1", [128, 128])
        self.w1_1 = keep("w1_1", [128, 512])
        self.w2_1 = keep("w2_1", [128, 4, 128])
        self.b1_1 = keep("b1_1", [128, 4])
        self.gffn1 = keep("gffn1", [128, 1])
        self.bffn1 = keep("bffn1", [128, 1])
        self.b2_1 = keep("b2_1", [128, 128])
        self.gout1 = keep("gout1", [128, 128])
        self.bout1 = keep("bout1", [128, 128])
        self.wbase = keep("wbase", [128, 128])
        self.wd1 = keep("wd1", [128, 8, 32])
        self.bd1 = keep("bd1", [128, 256])
        self.dcoef = keep("dcoef", [128, 2, 257])
        self.indic = keep("indic", [128, 2, 8])
        self.bd2T = keep("bd2T", [128, 8])
        self.bd2q = keep("bd2q", [128, 8])
        self.wdown = keep("wdown", [128, 8, 64])
        self.bdown = keep("bdown", [1, 8, 64])
        self.wup = keep("wup", [65, 8, 128])
        self.wq2 = keep("wq2", [128, 128])
        self.wk2 = keep("wk2", [C, 128])
        self.bq2 = keep("bq2", [128, 1])
        self.bk2 = keep("bk2", [128, 1])
        self.wv2 = keep("wv2", [C, 128])
        self.bv2 = keep("bv2", [128, 128])
        self.wo2 = keep("wo2", [128, 128])
        self.bo2 = keep("bo2", [128, 128])
        self.wq8 = keep("wq8", [128, 128])
        self.bias8 = keep("bias8", [128, 128])
        self.wq3 = keep("wq3", [128, 512])
        self.wk3 = keep("wk3", [C, 512])
        self.wv3 = keep("wv3", [C, 512])
        self.wo3 = keep("wo3", [128, 4, 128])
        self.bo3 = keep("bo3", [128, 128])
        self.wg3 = keep("wg3", [128, 8])
        self.bg3 = keep("bg3", [128, 8])
        self.w1_3 = keep("w1_3", [128, 8, 256])
        self.w2_3 = keep("w2_3", [128, 8, 2, 128])
        self.b1_3 = keep("b1_3", [128, 16])
        self.b2_3 = keep("b2_3", [8, 128])
        self.x3 = keep("x3", [128, 128, B])
        self.mean1 = keep("mean1", [128, B])
        self.rstd1 = keep("rstd1", [128, B])


def build(nc, w, out):
    with ExitStack() as ctx:
        def keep(name, shape, dt=F32):
            return ctx.enter_context(nc.sbuf_tensor("k_" + name, shape, dt))

        k = Kept(keep)
        k.ctx, k.sems, k.apart = ctx, {}, ctx.enter_context(nc.semaphore("apart"))
        k.vmask = keep("vmask", [128, B, S], BF16)
        k.kpad = nc.dram_tensor("kpad", (128, 256), F32, kind="Internal").ap()
        ps = ctx.enter_context(nc.psum_tensor("ps", [128, 8, 512], F32))

        k.fo_dram = nc.dram_tensor("fo_dram", (128, B, 256), F32, kind="Internal").ap()
        setup_weights(nc, w, ps, k)
        stages = [stage_cosine, stage_experts, stage_film, stage_adapters, stage_attention16, stage_fp8,
                  stage_attention8, stage_moe]
        for stage in stages:
            stage(nc, w, ps, k)
        store(nc, k, out)


def store(nc, k, out):
    with ExitStack() as ctx:
        stored = ctx.enter_context(OneTime(nc, ""))("stored")
        block = ctx.enter_context(nc.Block())

        @block.sync
        def _(sp):
            o = out.rearrange("b s d -> s b d")
            for i in range(4):
                sp.dma_start(o[:, 8 * i:8 * i + 8, :], k.X[:, 8 * i:8 * i + 8, :]).then_inc(stored, 16)
            sp.wait_ge(stored, 64)


def kernel(**inputs):
    import numpy as np
    import concourse.bacc as bacc
    from concourse.bass_utils import run_bass_kernel_spmd

    nc = bacc.Bacc("TRN2", target_bir_lowering=False, num_devices=1)
    arrays, aps = {}, {}
    for name, value in inputs.items():
        a = np.ascontiguousarray(value)
        if a.ndim == 0:
            a = a.reshape(1, 1)
        arrays["in_" + name] = a
        aps[name] = nc.dram_tensor("in_" + name, a.shape, mybir.dt.from_np(a.dtype), kind="ExternalInput").ap()
    out = nc.dram_tensor("out", (B, S, D), F32, kind="ExternalOutput").ap()
    build(nc, aps, out)
    r = run_bass_kernel_spmd(nc, [arrays], core_ids=[0])
    return r.results[0]["out"]
```
